# Optimizing a Trainium2 kernel written in Bass

```python
import numpy as np
import jax
import jax.numpy as jnp

def _softmax(x, axis=-1):
    return jax.nn.softmax(x, axis=axis)

def _gelu(x):
    return jax.nn.gelu(x, approximate=True)

def _silu(x):
    return jax.nn.silu(x)

def _sigmoid(x):
    return jax.nn.sigmoid(x)

def _layernorm(x, axis=-1, eps=1e-05):
    m = jnp.mean(x, axis=axis, keepdims=True)
    v = jnp.var(x, axis=axis, keepdims=True)
    return (x - m) / jnp.sqrt(v + eps)

def _scatter_add(tgt, idx, src, axis=0):
    return tgt.at[idx].add(src)

def _segment_sum(src, seg, n):
    return jax.ops.segment_sum(src, seg, n)
kernel_name = 'mk_seq_preln_d4_jaxref_r8_f6d837'

def setup_inputs(seed: int=0):
    np.random.seed(seed)
    _w = jnp.asarray

    def _L0_attn_setup():
        import jax, jax.numpy as jnp
        import numpy as np
        LN_EPS = 1e-05
        D_HEAD = 64

        def _layernorm(x, w, b):
            x = x - jnp.mean(x, axis=-1, keepdims=True)
            scale = jnp.sqrt(jnp.mean(x * x, axis=-1, keepdims=True) + LN_EPS)
            return x / scale * w + b
        key = jax.random.key(seed)
        ks = jax.random.split(key, 6)
        B, S, D, H, Dh = (2, 256, 128, 16, D_HEAD)
        std = 0.02
        return {'resid_pre': jax.random.normal(ks[0], (B, S, D), dtype=jnp.float32), 'W_Q': jax.random.normal(ks[1], (H, D, Dh), dtype=jnp.float32) * std, 'b_Q': jnp.zeros((H, Dh), dtype=jnp.float32), 'W_K': jax.random.normal(ks[2], (H, D, Dh), dtype=jnp.float32) * std, 'b_K': jnp.zeros((H, Dh), dtype=jnp.float32), 'W_V': jax.random.normal(ks[3], (H, D, Dh), dtype=jnp.float32) * std, 'b_V': jnp.zeros((H, Dh), dtype=jnp.float32), 'W_O': jax.random.normal(ks[4], (H, Dh, D), dtype=jnp.float32) * std, 'b_O': jnp.zeros((D,), dtype=jnp.float32), 'ln1_w': jnp.ones((D,), dtype=jnp.float32), 'ln1_b': jnp.zeros((D,), dtype=jnp.float32), 'ln2_w': jnp.ones((D,), dtype=jnp.float32), 'ln2_b': jnp.zeros((D,), dtype=jnp.float32)}
    _L0_attn_in = _L0_attn_setup()

    def _L0_ffn_setup():
        import jax, jax.numpy as jnp
        import numpy as np
        H = 8
        KD = 128
        TOPK = 8
        NUM_KEYS = 32
        N_EXPERTS = NUM_KEYS * NUM_KEYS
        N_DIM = 128
        BN_EPS = 1e-05

        def gelu_new(x):
            c = jnp.sqrt(jnp.asarray(2.0 / jnp.pi, x.dtype))
            return 0.5 * x * (1.0 + jnp.tanh(c * (x + 0.044715 * x * x * x)))
        key = jax.random.key(seed)
        ks = jax.random.split(key, 5)
        b, s = (2, 128)
        x = jax.random.normal(ks[0], (b, s, N_DIM), dtype=jnp.float32)
        w_q = jax.random.normal(ks[1], (N_DIM, 2 * H * KD), dtype=jnp.float32) * 0.02
        bn_gamma = jnp.ones((2 * H * KD,), dtype=jnp.float32)
        bn_beta = jnp.zeros((2 * H * KD,), dtype=jnp.float32)
        keys = jax.random.normal(ks[2], (H, NUM_KEYS, 2, KD), dtype=jnp.float32) * 0.02
        down_embed = jax.random.normal(ks[3], (N_EXPERTS, N_DIM), dtype=jnp.float32) * 0.02
        up_embed = jax.random.normal(ks[4], (N_EXPERTS, N_DIM), dtype=jnp.float32) * 0.02
        return {'x': x, 'w_q': w_q, 'bn_gamma': bn_gamma, 'bn_beta': bn_beta, 'keys': keys, 'down_embed': down_embed, 'up_embed': up_embed}
    _L0_ffn_in = _L0_ffn_setup()

    def _L1_attn_setup():
        import jax, jax.numpy as jnp
        import numpy as np
        D = 128
        H = 16
        G = 4
        HD = D // H
        HPG = H // G
        THETA = 10000.0
        EPS = 1e-10

        def _l2_qk_norm(t):
            return t / (jnp.sqrt(jnp.sum(t * t, axis=-1, keepdims=True)) + EPS)

        def _rope(t):
            T = t.shape[1]
            half = HD // 2
            inv_freq = 1.0 / THETA ** (jnp.arange(half, dtype=jnp.float32) / half)
            ang = jnp.arange(T, dtype=jnp.float32)[:, None] * inv_freq[None, :]
            cos = jnp.cos(ang)[None, :, None, :]
            sin = jnp.sin(ang)[None, :, None, :]
            x1, x2 = (t[..., :half], t[..., half:])
            return jnp.concatenate([x1 * cos - x2 * sin, x2 * cos + x1 * sin], axis=-1)
        key = jax.random.key(seed)
        k1, k2, k3 = jax.random.split(key, 3)
        x = jax.random.normal(k1, (1, 512, D), jnp.float32)
        w_qkv = jax.random.normal(k2, (D, H * HD + 2 * G * HD), jnp.float32) * 0.02
        w_o = jax.random.normal(k3, (D, D), jnp.float32) * 0.02
        return {'x': x, 'w_qkv': w_qkv, 'w_o': w_o}
    _L1_attn_in = _L1_attn_setup()

    def _L1_ffn_setup():
        import jax, jax.numpy as jnp
        import numpy as np
        NUM_EXPERTS_TOTAL = 9
        TOP_K = 2
        key = jax.random.key(seed)
        k0, k1, k2, k3, k4 = jax.random.split(key, 5)
        B, S, H, I = (2, 256, 128, 352)
        E = NUM_EXPERTS_TOTAL
        x = jax.random.normal(k0, (B, S, H), dtype=jnp.float32)
        Wr = jax.random.normal(k1, (H, E), dtype=jnp.float32) * 0.02
        Wg = jax.random.normal(k2, (E, H, I), dtype=jnp.float32) * 0.02
        Wu = jax.random.normal(k3, (E, H, I), dtype=jnp.float32) * 0.02
        Wd = jax.random.normal(k4, (E, I, H), dtype=jnp.float32) * 0.02
        return {'x': x, 'Wr': Wr, 'Wg': Wg, 'Wu': Wu, 'Wd': Wd}
    _L1_ffn_in = _L1_ffn_setup()

    def _L2_attn_setup():
        import jax, jax.numpy as jnp
        import numpy as np
        B, T, DM, H, D = (2, 512, 128, 16, 64)
        HD = H * D
        PHASE_SCALE = 10.0

        def _multiscale_phasors(num_heads, head_dim):
            d = np.arange(head_dim, dtype=np.float32) / head_dim
            base = 10000.0 ** (-d)
            head_scale = 2.0 ** (-np.arange(num_heads, dtype=np.float32))
            return jnp.asarray(2.0 * np.pi * head_scale[:, None] * base[None, :], dtype=jnp.float32)

        def _holo_fused_step(v, binder, probe):
            mem = jnp.cumsum(v * binder, axis=1)
            t = v.shape[1]
            scale = jnp.sqrt(jnp.arange(1, t + 1, dtype=jnp.float32))[None, :, None, None]
            return jnp.real(mem * probe) / scale
        key = jax.random.key(seed)
        k0, k1, k2, k3 = jax.random.split(key, 4)
        x = jax.random.normal(k0, (B, T, DM), jnp.float32)
        Wk = jax.random.normal(k1, (DM, HD), jnp.float32) / np.float32(np.sqrt(DM))
        Wv = jax.random.normal(k2, (DM, HD), jnp.float32) / np.float32(np.sqrt(DM))
        Wo = jax.random.normal(k3, (HD, DM), jnp.float32) / np.float32(np.sqrt(HD))
        gate = jnp.full((H, 2), 0.5, jnp.float32)
        freqs = _multiscale_phasors(H, D)
        return {'x': x, 'Wk': Wk, 'Wv': Wv, 'Wo': Wo, 'gate': gate, 'freqs': freqs}
    _L2_attn_in = _L2_attn_setup()

    def _L2_ffn_setup():
        import jax, jax.numpy as jnp
        import numpy as np
        DIM = 128
        DEPTH = 2
        HEADS = 8
        DIM_HEAD = 64
        WINDOW = 64
        INNER = HEADS * DIM_HEAD
        HID = int(DIM * 4 * 2 / 3)
        B, N = (2, 1024)
        QK_SCALE = 8.0

        def shift_token(t):
            t1, t2 = jnp.split(t, 2, axis=-1)
            t2 = jnp.pad(t2, ((0, 0), (1, 0), (0, 0)))[:, :-1]
            return jnp.concatenate([t1, t2], axis=-1)

        def l2norm(t):
            return t / jnp.clip(jnp.linalg.norm(t, axis=-1, keepdims=True), 1e-12)

        def rotate_half(x):
            x1, x2 = jnp.split(x, 2, axis=-1)
            return jnp.concatenate([-x2, x1], axis=-1)

        def rotary_xpos(q, k):
            n = q.shape[-2]
            half_idx = jnp.arange(0, DIM_HEAD, 2, dtype=jnp.float32)
            inv_freq = 1.0 / 10000.0 ** (half_idx / DIM_HEAD)
            t = jnp.arange(n, dtype=jnp.float32)
            freqs = t[:, None] * inv_freq[None, :]
            freqs = jnp.concatenate([freqs, freqs], axis=-1)
            base = (half_idx + 0.4 * DIM_HEAD) / (1.4 * DIM_HEAD)
            power = (t - n // 2) / float(WINDOW // 2)
            scale = base[None, :] ** power[:, None]
            scale = jnp.concatenate([scale, scale], axis=-1)
            cos, sin = (jnp.cos(freqs), jnp.sin(freqs))
            q = q * cos * scale + rotate_half(q) * sin * scale
            k = k * cos / scale + rotate_half(k) * sin / scale
            return (q, k)

        def local_attention(q, k, v):
            b, h, n, d = q.shape
            w = n // WINDOW
            bq = q.reshape(b, h, w, WINDOW, d) * QK_SCALE
            bk = k.reshape(b, h, w, WINDOW, d)
            bv = v.reshape(b, h, w, WINDOW, d)

            def look_around(t):
                p = jnp.pad(t, ((0, 0), (0, 0), (1, 0), (0, 0), (0, 0)))
                return jnp.concatenate([p[:, :, :w], p[:, :, 1:]], axis=3)
            bk, bv = (look_around(bk), look_around(bv))
            bt = jnp.arange(n).reshape(w, WINDOW)
            btp = jnp.pad(bt, ((1, 0), (0, 0)), constant_values=-1)
            btk = jnp.concatenate([btp[:w], btp[1:]], axis=1)
            sim = jnp.einsum('bhwid,bhwjd->bhwij', bq, bk)
            i = bt[:, :, None]
            j = btk[:, None, :]
            mask = (i < j) | (i > j + WINDOW) | (j == -1)
            sim = jnp.where(mask, -jnp.finfo(sim.dtype).max, sim)
            attn = jax.nn.softmax(sim, axis=-1)
            out = jnp.einsum('bhwij,bhwjd->bhwid', attn, bv)
            return out.reshape(b, h, n, d)

        def _layer(x, wqkv, qs, ksc, wo, lg, lb, w1, b1, w2, b2):
            b, n, _ = x.shape
            h = shift_token(x)
            qkv = h @ wqkv
            q, k, v = jnp.split(qkv, 3, axis=-1)
            to_heads = lambda t: t.reshape(b, n, HEADS, DIM_HEAD).transpose(0, 2, 1, 3)
            q, k, v = (to_heads(q), to_heads(k), to_heads(v))
            q = l2norm(q) * qs
            k = l2norm(k) * ksc
            q, k = rotary_xpos(q, k)
            o = local_attention(q, k, v)
            o = o.transpose(0, 2, 1, 3).reshape(b, n, INNER)
            x = x + o @ wo
            h = shift_token(x)
            mu = h.mean(-1, keepdims=True)
            var = h.var(-1, keepdims=True)
            h = (h - mu) / jnp.sqrt(var + 1e-05) * lg + lb
            h = h @ w1 + b1
            a, g = jnp.split(h, 2, axis=-1)
            h = a * jax.nn.gelu(g, approximate=False)
            x = x + h @ w2 + b2
            return x
        key = jax.random.key(seed)
        ks = jax.random.split(key, 6)
        return {'x': jax.random.normal(ks[0], (B, N, DIM), jnp.float32), 'wqkv': jax.random.normal(ks[1], (DEPTH, DIM, 3 * INNER), jnp.float32) * 0.02, 'q_scale': jnp.ones((DEPTH, DIM_HEAD), jnp.float32), 'k_scale': jnp.ones((DEPTH, DIM_HEAD), jnp.float32), 'wo': jax.random.normal(ks[2], (DEPTH, INNER, DIM), jnp.float32) * 0.02, 'ln_g': jnp.ones((DEPTH, DIM), jnp.float32), 'ln_b': jnp.zeros((DEPTH, DIM), jnp.float32), 'w1': jax.random.normal(ks[3], (DEPTH, DIM, 2 * HID), jnp.float32) * 0.02, 'b1': jnp.zeros((DEPTH, 2 * HID), jnp.float32), 'w2': jax.random.normal(ks[4], (DEPTH, HID, DIM), jnp.float32) * 0.02, 'b2': jnp.zeros((DEPTH, DIM), jnp.float32)}
    _L2_ffn_in = _L2_ffn_setup()

    def _L3_attn_setup():
        import jax, jax.numpy as jnp
        import numpy as np
        import math
        N_STATE = 64
        H_MODEL = 128
        D_CONV = 16
        EXPAND = 2
        D_INNER = EXPAND * H_MODEL
        HEADDIM = H_MODEL // 4
        NHEADS = D_INNER // HEADDIM
        NGROUPS = 1
        CONV_DIM = D_INNER + 2 * NGROUPS * N_STATE
        D_IN_PROJ = 2 * D_INNER + 2 * NGROUPS * N_STATE + NHEADS
        BATCH, SEQLEN = (4, 256)

        def _mamba2(x, W_in, conv_w, conv_b, dt_bias, A_log, D, init_states, norm_w, W_out):
            b, l, _ = x.shape
            zxbcdt = x @ W_in
            z = zxbcdt[..., :D_INNER]
            xBC = zxbcdt[..., D_INNER:D_INNER + CONV_DIM]
            dt = jax.nn.softplus(zxbcdt[..., -NHEADS:] + dt_bias)
            kernel = conv_w.T[:, None, :]
            xBC = jax.lax.conv_general_dilated(xBC, kernel, window_strides=(1,), padding=[(D_CONV - 1, 0)], dimension_numbers=('NWC', 'WIO', 'NWC'), feature_group_count=CONV_DIM) + conv_b
            xBC = jax.nn.silu(xBC)
            xs = xBC[..., :D_INNER].reshape(b, l, NHEADS, HEADDIM)
            Bm = xBC[..., D_INNER:D_INNER + N_STATE]
            Cm = xBC[..., D_INNER + N_STATE:]
            A = -jnp.exp(A_log)
            dA = jnp.exp(dt * A)
            h0 = jnp.broadcast_to(init_states, (b, NHEADS, HEADDIM, N_STATE))

            def step(h, inp):
                dA_t, x_t, dt_t, B_t, C_t = inp
                dBx = jnp.einsum('bh,bhp,bn->bhpn', dt_t, x_t, B_t)
                h = h * dA_t[:, :, None, None] + dBx
                y_t = jnp.einsum('bhpn,bn->bhp', h, C_t)
                return (h, y_t)
            scan_in = (jnp.moveaxis(dA, 1, 0), jnp.moveaxis(xs, 1, 0), jnp.moveaxis(dt, 1, 0), jnp.moveaxis(Bm, 1, 0), jnp.moveaxis(Cm, 1, 0))
            _, ys = jax.lax.scan(step, h0, scan_in)
            y = jnp.moveaxis(ys, 0, 1) + D[None, None, :, None] * xs
            y = y.reshape(b, l, D_INNER)
            y = y * jax.nn.silu(z)
            y = y * jax.lax.rsqrt(jnp.mean(y * y, axis=-1, keepdims=True) + 1e-05) * norm_w
            return y @ W_out
        key = jax.random.key(seed)
        ks = jax.random.split(key, 10)
        x = jax.random.normal(ks[0], (BATCH, SEQLEN, H_MODEL), jnp.float32)
        W_in = jax.random.normal(ks[1], (H_MODEL, D_IN_PROJ), jnp.float32) * H_MODEL ** (-0.5)
        conv_w = jax.random.normal(ks[2], (CONV_DIM, D_CONV), jnp.float32) * D_CONV ** (-0.5)
        conv_b = jnp.zeros((CONV_DIM,), jnp.float32)
        dt0 = jnp.exp(jax.random.uniform(ks[3], (NHEADS,), minval=math.log(0.001), maxval=math.log(0.1)))
        dt_bias = jnp.log(jnp.expm1(dt0))
        A_log = jnp.log(jax.random.uniform(ks[4], (NHEADS,), minval=1.0, maxval=16.0))
        D = jnp.ones((NHEADS,), jnp.float32)
        init_states = jax.random.normal(ks[5], (NHEADS, HEADDIM, N_STATE), jnp.float32) * 0.01
        norm_w = jnp.ones((D_INNER,), jnp.float32)
        W_out = jax.random.normal(ks[6], (D_INNER, H_MODEL), jnp.float32) * D_INNER ** (-0.5)
        W_nl = jax.random.normal(ks[7], (H_MODEL, H_MODEL), jnp.float32) * H_MODEL ** (-0.5)
        b_nl = jnp.zeros((H_MODEL,), jnp.float32)
        return dict(x=x, W_in=W_in, conv_w=conv_w, conv_b=conv_b, dt_bias=dt_bias, A_log=A_log, D=D, init_states=init_states, norm_w=norm_w, W_out=W_out, W_nl=W_nl, b_nl=b_nl)
    _L3_attn_in = _L3_attn_setup()

    def _L3_ffn_setup():
        import jax, jax.numpy as jnp
        import numpy as np
        N_EMBD = 128
        NUM_EXPERTS = 8
        TOP_K = 2
        D_FF = 4 * N_EMBD
        B, S = (4, 256)
        key = jax.random.key(seed)
        ks = jax.random.split(key, 7)
        scale = lambda fan_in: 1.0 / np.sqrt(fan_in)
        x = jax.random.normal(ks[0], (B, S, N_EMBD), dtype=jnp.float32)
        W_router = jax.random.normal(ks[1], (N_EMBD, NUM_EXPERTS), dtype=jnp.float32) * scale(N_EMBD)
        b_router = jnp.zeros((NUM_EXPERTS,), dtype=jnp.float32)
        W1 = jax.random.normal(ks[2], (NUM_EXPERTS, N_EMBD, D_FF), dtype=jnp.float32) * scale(N_EMBD)
        b1 = jnp.zeros((NUM_EXPERTS, D_FF), dtype=jnp.float32)
        W2 = jax.random.normal(ks[3], (NUM_EXPERTS, D_FF, N_EMBD), dtype=jnp.float32) * scale(D_FF)
        b2 = jnpp = jnp.zeros((NUM_EXPERTS, N_EMBD), dtype=jnp.float32)
        return {'x': x, 'W_router': W_router, 'b_router': b_router, 'W1': W1, 'b1': b1, 'W2': W2, 'b2': b2}
    _L3_ffn_in = _L3_ffn_setup()
    _d = {'L0_attn_resid_pre': _L0_attn_in['resid_pre'], 'L0_attn_W_Q': _L0_attn_in['W_Q'], 'L0_attn_b_Q': _L0_attn_in['b_Q'], 'L0_attn_W_K': _L0_attn_in['W_K'], 'L0_attn_b_K': _L0_attn_in['b_K'], 'L0_attn_W_V': _L0_attn_in['W_V'], 'L0_attn_b_V': _L0_attn_in['b_V'], 'L0_attn_W_O': _L0_attn_in['W_O'], 'L0_attn_b_O': _L0_attn_in['b_O'], 'L0_attn_ln1_w': _L0_attn_in['ln1_w'], 'L0_attn_ln1_b': _L0_attn_in['ln1_b'], 'L0_attn_ln2_w': _L0_attn_in['ln2_w'], 'L0_attn_ln2_b': _L0_attn_in['ln2_b'], 'L0_ffn_w_q': _L0_ffn_in['w_q'], 'L0_ffn_bn_gamma': _L0_ffn_in['bn_gamma'], 'L0_ffn_bn_beta': _L0_ffn_in['bn_beta'], 'L0_ffn_keys': _L0_ffn_in['keys'], 'L0_ffn_down_embed': _L0_ffn_in['down_embed'], 'L0_ffn_up_embed': _L0_ffn_in['up_embed'], 'L1_attn_w_qkv': _L1_attn_in['w_qkv'], 'L1_attn_w_o': _L1_attn_in['w_o'], 'L1_ffn_Wr': _L1_ffn_in['Wr'], 'L1_ffn_Wg': _L1_ffn_in['Wg'], 'L1_ffn_Wu': _L1_ffn_in['Wu'], 'L1_ffn_Wd': _L1_ffn_in['Wd'], 'L2_attn_Wk': _L2_attn_in['Wk'], 'L2_attn_Wv': _L2_attn_in['Wv'], 'L2_attn_Wo': _L2_attn_in['Wo'], 'L2_attn_gate': _L2_attn_in['gate'], 'L2_attn_freqs': _L2_attn_in['freqs'], 'L2_ffn_wqkv': _L2_ffn_in['wqkv'], 'L2_ffn_q_scale': _L2_ffn_in['q_scale'], 'L2_ffn_k_scale': _L2_ffn_in['k_scale'], 'L2_ffn_wo': _L2_ffn_in['wo'], 'L2_ffn_ln_g': _L2_ffn_in['ln_g'], 'L2_ffn_ln_b': _L2_ffn_in['ln_b'], 'L2_ffn_w1': _L2_ffn_in['w1'], 'L2_ffn_b1': _L2_ffn_in['b1'], 'L2_ffn_w2': _L2_ffn_in['w2'], 'L2_ffn_b2': _L2_ffn_in['b2'], 'L3_attn_W_in': _L3_attn_in['W_in'], 'L3_attn_conv_w': _L3_attn_in['conv_w'], 'L3_attn_conv_b': _L3_attn_in['conv_b'], 'L3_attn_dt_bias': _L3_attn_in['dt_bias'], 'L3_attn_A_log': _L3_attn_in['A_log'], 'L3_attn_D': _L3_attn_in['D'], 'L3_attn_init_states': _L3_attn_in['init_states'], 'L3_attn_norm_w': _L3_attn_in['norm_w'], 'L3_attn_W_out': _L3_attn_in['W_out'], 'L3_attn_W_nl': _L3_attn_in['W_nl'], 'L3_attn_b_nl': _L3_attn_in['b_nl'], 'L3_ffn_W_router': _L3_ffn_in['W_router'], 'L3_ffn_b_router': _L3_ffn_in['b_router'], 'L3_ffn_W1': _L3_ffn_in['W1'], 'L3_ffn_b1': _L3_ffn_in['b1'], 'L3_ffn_W2': _L3_ffn_in['W2'], 'L3_ffn_b2': _L3_ffn_in['b2']}
    _x0 = _d['L0_attn_resid_pre']
    _d['L0_attn_resid_pre'] = jax.random.normal(jax.random.fold_in(jax.random.key(seed), 1), (1, 2048, 128), dtype=_x0.dtype)
    del _x0
    return _d

def reference(L0_attn_resid_pre, L0_attn_W_Q, L0_attn_b_Q, L0_attn_W_K, L0_attn_b_K, L0_attn_W_V, L0_attn_b_V, L0_attn_W_O, L0_attn_b_O, L0_attn_ln1_w, L0_attn_ln1_b, L0_attn_ln2_w, L0_attn_ln2_b, L0_ffn_w_q, L0_ffn_bn_gamma, L0_ffn_bn_beta, L0_ffn_keys, L0_ffn_down_embed, L0_ffn_up_embed, L1_attn_w_qkv, L1_attn_w_o, L1_ffn_Wr, L1_ffn_Wg, L1_ffn_Wu, L1_ffn_Wd, L2_attn_Wk, L2_attn_Wv, L2_attn_Wo, L2_attn_gate, L2_attn_freqs, L2_ffn_wqkv, L2_ffn_q_scale, L2_ffn_k_scale, L2_ffn_wo, L2_ffn_ln_g, L2_ffn_ln_b, L2_ffn_w1, L2_ffn_b1, L2_ffn_w2, L2_ffn_b2, L3_attn_W_in, L3_attn_conv_w, L3_attn_conv_b, L3_attn_dt_bias, L3_attn_A_log, L3_attn_D, L3_attn_init_states, L3_attn_norm_w, L3_attn_W_out, L3_attn_W_nl, L3_attn_b_nl, L3_ffn_W_router, L3_ffn_b_router, L3_ffn_W1, L3_ffn_b1, L3_ffn_W2, L3_ffn_b2):

    def _L0_attn_ref(resid_pre, W_Q, b_Q, W_K, b_K, W_V, b_V, W_O, b_O, ln1_w, ln1_b, ln2_w, ln2_b):
        import jax, jax.numpy as jnp
        import numpy as np
        LN_EPS = 1e-05
        D_HEAD = 64

        def _layernorm(x, w, b):
            x = x - jnp.mean(x, axis=-1, keepdims=True)
            scale = jnp.sqrt(jnp.mean(x * x, axis=-1, keepdims=True) + LN_EPS)
            return x / scale * w + b
        x = _layernorm(resid_pre, ln1_w, ln1_b)
        q = jnp.einsum('hdk,bsd->bshk', W_Q, x) + b_Q
        k = jnp.einsum('hdk,bsd->bshk', W_K, x) + b_K
        v = jnp.einsum('hdk,bsd->bshk', W_V, x) + b_V
        scores = jnp.einsum('bqhk,bphk->bhqp', q, k) / jnp.sqrt(jnp.asarray(D_HEAD, dtype=q.dtype))
        S = scores.shape[-1]
        causal = jnp.tril(jnp.ones((S, S), dtype=bool))
        scores = jnp.where(causal, scores, jnp.asarray(0.0, dtype=scores.dtype))
        pattern = jax.nn.softmax(scores, axis=-1)
        z = jnp.einsum('bhqp,bphk->bqhk', pattern, v)
        attn_out = jnp.einsum('bqhk,hkd->bqd', z, W_O) + b_O
        resid_mid = resid_pre + attn_out
        resid_post = resid_mid + _layernorm(resid_mid, ln2_w, ln2_b)
        return resid_post

    def _L0_ffn_ref(x, w_q, bn_gamma, bn_beta, keys, down_embed, up_embed):
        import jax, jax.numpy as jnp
        import numpy as np
        H = 8
        KD = 128
        TOPK = 8
        NUM_KEYS = 32
        N_EXPERTS = NUM_KEYS * NUM_KEYS
        N_DIM = 128
        BN_EPS = 1e-05

        def gelu_new(x):
            c = jnp.sqrt(jnp.asarray(2.0 / jnp.pi, x.dtype))
            return 0.5 * x * (1.0 + jnp.tanh(c * (x + 0.044715 * x * x * x)))
        b, n, d = x.shape
        q = jnp.einsum('bnd,de->bne', x, w_q)
        mean = jnp.mean(q, axis=(0, 1))
        var = jnp.var(q, axis=(0, 1))
        q = (q - mean) * jax.lax.rsqrt(var + BN_EPS) * bn_gamma + bn_beta
        q = q.reshape(b, n, 2, H, KD).transpose(2, 0, 1, 3, 4)
        sim = jnp.einsum('pbnhd,hkpd->pbnhk', q, keys)
        sx, ix = jax.lax.top_k(sim[0], TOPK)
        sy, iy = jax.lax.top_k(sim[1], TOPK)
        all_scores = (sx[..., :, None] + sy[..., None, :]).reshape(b, n, H, TOPK * TOPK)
        all_indices = (ix[..., :, None] * NUM_KEYS + iy[..., None, :]).reshape(b, n, H, TOPK * TOPK)
        scores, pk = jax.lax.top_k(all_scores, TOPK)
        indices = jnp.take_along_axis(all_indices, pk, axis=-1)
        wd = down_embed[indices]
        wu = up_embed[indices]
        h = jnp.einsum('bnd,bnhkd->bnhk', x, wd)
        h = gelu_new(h)
        h = jax.nn.softmax(scores, axis=-1) * h
        out = jnp.einsum('bnhk,bnhkd->bnd', h, wu)
        return out

    def _L1_attn_ref(x, w_qkv, w_o):
        import jax, jax.numpy as jnp
        import numpy as np
        D = 128
        H = 16
        G = 4
        HD = D // H
        HPG = H // G
        THETA = 10000.0
        EPS = 1e-10

        def _l2_qk_norm(t):
            return t / (jnp.sqrt(jnp.sum(t * t, axis=-1, keepdims=True)) + EPS)

        def _rope(t):
            T = t.shape[1]
            half = HD // 2
            inv_freq = 1.0 / THETA ** (jnp.arange(half, dtype=jnp.float32) / half)
            ang = jnp.arange(T, dtype=jnp.float32)[:, None] * inv_freq[None, :]
            cos = jnp.cos(ang)[None, :, None, :]
            sin = jnp.sin(ang)[None, :, None, :]
            x1, x2 = (t[..., :half], t[..., half:])
            return jnp.concatenate([x1 * cos - x2 * sin, x2 * cos + x1 * sin], axis=-1)
        B, T, _ = x.shape
        qkv = x @ w_qkv
        q, k, v = jnp.split(qkv, [H * HD, H * HD + G * HD], axis=-1)
        q = q.reshape(B, T, H, HD)
        k = k.reshape(B, T, G, HD)
        v = v.reshape(B, T, G, HD)
        q = _l2_qk_norm(q)
        k = _l2_qk_norm(k)
        q = _rope(q)
        k = _rope(k)
        k = jnp.repeat(k, HPG, axis=2)
        v = jnp.repeat(v, HPG, axis=2)
        q = jnp.transpose(q, (0, 2, 1, 3))
        k = jnp.transpose(k, (0, 2, 1, 3))
        v = jnp.transpose(v, (0, 2, 1, 3))
        scale = 1.0 / np.sqrt(HD).astype(np.float32)
        scores = jnp.einsum('bhqd,bhkd->bhqk', q, k) * scale
        causal = jnp.tril(jnp.ones((T, T), dtype=bool))
        scores = jnp.where(causal[None, None], scores, jnp.float32(-1e+30))
        attn = jax.nn.softmax(scores, axis=-1)
        out = jnp.einsum('bhqk,bhkd->bhqd', attn, v)
        out = jnp.transpose(out, (0, 2, 1, 3)).reshape(B, T, H * HD)
        return out @ w_o

    def _L1_ffn_ref(x, Wr, Wg, Wu, Wd):
        import jax, jax.numpy as jnp
        import numpy as np
        NUM_EXPERTS_TOTAL = 9
        TOP_K = 2
        B, S, H = x.shape
        E = NUM_EXPERTS_TOTAL
        T = B * S
        logits = jnp.einsum('bsh,he->bse', x, Wr)
        probs = jax.nn.softmax(logits, axis=-1)
        topk_w, topk_idx = jax.lax.top_k(probs, TOP_K)
        topk_w = topk_w / jnp.sum(topk_w, axis=-1, keepdims=True)
        xf = x.reshape(T, H)
        wf = topk_w.reshape(T, TOP_K)
        idxf = topk_idx.reshape(T, TOP_K)
        cw = jnp.zeros((T, E), dtype=x.dtype).at[jnp.arange(T)[:, None], idxf].add(wf)
        gate = jax.nn.silu(jnp.einsum('th,ehi->tei', xf, Wg))
        hidden = gate * jnp.einsum('th,ehi->tei', xf, Wu)
        out = jnp.einsum('tei,eih,te->th', hidden, Wd, cw)
        return out.reshape(B, S, H)

    def _L2_attn_ref(x, Wk, Wv, Wo, gate, freqs):
        import jax, jax.numpy as jnp
        import numpy as np
        B, T, DM, H, D = (2, 512, 128, 16, 64)
        HD = H * D
        PHASE_SCALE = 10.0

        def _multiscale_phasors(num_heads, head_dim):
            d = np.arange(head_dim, dtype=np.float32) / head_dim
            base = 10000.0 ** (-d)
            head_scale = 2.0 ** (-np.arange(num_heads, dtype=np.float32))
            return jnp.asarray(2.0 * np.pi * head_scale[:, None] * base[None, :], dtype=jnp.float32)

        def _holo_fused_step(v, binder, probe):
            mem = jnp.cumsum(v * binder, axis=1)
            t = v.shape[1]
            scale = jnp.sqrt(jnp.arange(1, t + 1, dtype=jnp.float32))[None, :, None, None]
            return jnp.real(mem * probe) / scale
        Bb, Tt, _ = x.shape
        k_real = (x @ Wk).reshape(Bb, Tt, H, D)
        v = (x @ Wv).reshape(Bb, Tt, H, D).astype(jnp.complex64)
        k = jnp.exp(1j * (k_real * PHASE_SCALE))
        t = jnp.arange(Tt, dtype=jnp.float32)
        rotors = jnp.exp(1j * (t[:, None, None] * freqs))[None]
        out_pos = _holo_fused_step(v, rotors, jnp.conj(rotors))
        k_shifted = jnp.roll(k, 1, axis=1).at[:, 0].set(0.0)
        out_assoc = _holo_fused_step(v, jnp.conj(k_shifted), k)
        g_pos = gate[:, 0][None, None, :, None]
        g_assoc = gate[:, 1][None, None, :, None]
        out = out_pos * g_pos + out_assoc * g_assoc
        return out.reshape(Bb, Tt, HD) @ Wo

    def _L2_ffn_ref(x, wqkv, q_scale, k_scale, wo, ln_g, ln_b, w1, b1, w2, b2):
        import jax, jax.numpy as jnp
        import numpy as np
        DIM = 128
        DEPTH = 2
        HEADS = 8
        DIM_HEAD = 64
        WINDOW = 64
        INNER = HEADS * DIM_HEAD
        HID = int(DIM * 4 * 2 / 3)
        B, N = (2, 1024)
        QK_SCALE = 8.0

        def shift_token(t):
            t1, t2 = jnp.split(t, 2, axis=-1)
            t2 = jnp.pad(t2, ((0, 0), (1, 0), (0, 0)))[:, :-1]
            return jnp.concatenate([t1, t2], axis=-1)

        def l2norm(t):
            return t / jnp.clip(jnp.linalg.norm(t, axis=-1, keepdims=True), 1e-12)

        def rotate_half(x):
            x1, x2 = jnp.split(x, 2, axis=-1)
            return jnp.concatenate([-x2, x1], axis=-1)

        def rotary_xpos(q, k):
            n = q.shape[-2]
            half_idx = jnp.arange(0, DIM_HEAD, 2, dtype=jnp.float32)
            inv_freq = 1.0 / 10000.0 ** (half_idx / DIM_HEAD)
            t = jnp.arange(n, dtype=jnp.float32)
            freqs = t[:, None] * inv_freq[None, :]
            freqs = jnp.concatenate([freqs, freqs], axis=-1)
            base = (half_idx + 0.4 * DIM_HEAD) / (1.4 * DIM_HEAD)
            power = (t - n // 2) / float(WINDOW // 2)
            scale = base[None, :] ** power[:, None]
            scale = jnp.concatenate([scale, scale], axis=-1)
            cos, sin = (jnp.cos(freqs), jnp.sin(freqs))
            q = q * cos * scale + rotate_half(q) * sin * scale
            k = k * cos / scale + rotate_half(k) * sin / scale
            return (q, k)

        def local_attention(q, k, v):
            b, h, n, d = q.shape
            w = n // WINDOW
            bq = q.reshape(b, h, w, WINDOW, d) * QK_SCALE
            bk = k.reshape(b, h, w, WINDOW, d)
            bv = v.reshape(b, h, w, WINDOW, d)

            def look_around(t):
                p = jnp.pad(t, ((0, 0), (0, 0), (1, 0), (0, 0), (0, 0)))
                return jnp.concatenate([p[:, :, :w], p[:, :, 1:]], axis=3)
            bk, bv = (look_around(bk), look_around(bv))
            bt = jnp.arange(n).reshape(w, WINDOW)
            btp = jnp.pad(bt, ((1, 0), (0, 0)), constant_values=-1)
            btk = jnp.concatenate([btp[:w], btp[1:]], axis=1)
            sim = jnp.einsum('bhwid,bhwjd->bhwij', bq, bk)
            i = bt[:, :, None]
            j = btk[:, None, :]
            mask = (i < j) | (i > j + WINDOW) | (j == -1)
            sim = jnp.where(mask, -jnp.finfo(sim.dtype).max, sim)
            attn = jax.nn.softmax(sim, axis=-1)
            out = jnp.einsum('bhwij,bhwjd->bhwid', attn, bv)
            return out.reshape(b, h, n, d)

        def _layer(x, wqkv, qs, ksc, wo, lg, lb, w1, b1, w2, b2):
            b, n, _ = x.shape
            h = shift_token(x)
            qkv = h @ wqkv
            q, k, v = jnp.split(qkv, 3, axis=-1)
            to_heads = lambda t: t.reshape(b, n, HEADS, DIM_HEAD).transpose(0, 2, 1, 3)
            q, k, v = (to_heads(q), to_heads(k), to_heads(v))
            q = l2norm(q) * qs
            k = l2norm(k) * ksc
            q, k = rotary_xpos(q, k)
            o = local_attention(q, k, v)
            o = o.transpose(0, 2, 1, 3).reshape(b, n, INNER)
            x = x + o @ wo
            h = shift_token(x)
            mu = h.mean(-1, keepdims=True)
            var = h.var(-1, keepdims=True)
            h = (h - mu) / jnp.sqrt(var + 1e-05) * lg + lb
            h = h @ w1 + b1
            a, g = jnp.split(h, 2, axis=-1)
            h = a * jax.nn.gelu(g, approximate=False)
            x = x + h @ w2 + b2
            return x
        for l in range(DEPTH):
            x = _layer(x, wqkv[l], q_scale[l], k_scale[l], wo[l], ln_g[l], ln_b[l], w1[l], b1[l], w2[l], b2[l])
        return x

    def _L3_attn_ref(x, W_in, conv_w, conv_b, dt_bias, A_log, D, init_states, norm_w, W_out, W_nl, b_nl):
        import jax, jax.numpy as jnp
        import numpy as np
        import math
        N_STATE = 64
        H_MODEL = 128
        D_CONV = 16
        EXPAND = 2
        D_INNER = EXPAND * H_MODEL
        HEADDIM = H_MODEL // 4
        NHEADS = D_INNER // HEADDIM
        NGROUPS = 1
        CONV_DIM = D_INNER + 2 * NGROUPS * N_STATE
        D_IN_PROJ = 2 * D_INNER + 2 * NGROUPS * N_STATE + NHEADS
        BATCH, SEQLEN = (4, 256)

        def _mamba2(x, W_in, conv_w, conv_b, dt_bias, A_log, D, init_states, norm_w, W_out):
            b, l, _ = x.shape
            zxbcdt = x @ W_in
            z = zxbcdt[..., :D_INNER]
            xBC = zxbcdt[..., D_INNER:D_INNER + CONV_DIM]
            dt = jax.nn.softplus(zxbcdt[..., -NHEADS:] + dt_bias)
            kernel = conv_w.T[:, None, :]
            xBC = jax.lax.conv_general_dilated(xBC, kernel, window_strides=(1,), padding=[(D_CONV - 1, 0)], dimension_numbers=('NWC', 'WIO', 'NWC'), feature_group_count=CONV_DIM) + conv_b
            xBC = jax.nn.silu(xBC)
            xs = xBC[..., :D_INNER].reshape(b, l, NHEADS, HEADDIM)
            Bm = xBC[..., D_INNER:D_INNER + N_STATE]
            Cm = xBC[..., D_INNER + N_STATE:]
            A = -jnp.exp(A_log)
            dA = jnp.exp(dt * A)
            h0 = jnp.broadcast_to(init_states, (b, NHEADS, HEADDIM, N_STATE))

            def step(h, inp):
                dA_t, x_t, dt_t, B_t, C_t = inp
                dBx = jnp.einsum('bh,bhp,bn->bhpn', dt_t, x_t, B_t)
                h = h * dA_t[:, :, None, None] + dBx
                y_t = jnp.einsum('bhpn,bn->bhp', h, C_t)
                return (h, y_t)
            scan_in = (jnp.moveaxis(dA, 1, 0), jnp.moveaxis(xs, 1, 0), jnp.moveaxis(dt, 1, 0), jnp.moveaxis(Bm, 1, 0), jnp.moveaxis(Cm, 1, 0))
            _, ys = jax.lax.scan(step, h0, scan_in)
            y = jnp.moveaxis(ys, 0, 1) + D[None, None, :, None] * xs
            y = y.reshape(b, l, D_INNER)
            y = y * jax.nn.silu(z)
            y = y * jax.lax.rsqrt(jnp.mean(y * y, axis=-1, keepdims=True) + 1e-05) * norm_w
            return y @ W_out
        y = _mamba2(x, W_in, conv_w, conv_b, dt_bias, A_log, D, init_states, norm_w, W_out)
        t = y / jnp.sqrt(1.0 + y * y)
        return t @ W_nl + b_nl + x

    def _L3_ffn_ref(x, W_router, b_router, W1, b1, W2, b2):
        import jax, jax.numpy as jnp
        import numpy as np
        N_EMBD = 128
        NUM_EXPERTS = 8
        TOP_K = 2
        D_FF = 4 * N_EMBD
        B, S = (4, 256)
        Bv, Sv, D = x.shape
        flat_x = x.reshape(-1, D)
        T = flat_x.shape[0]
        logits = flat_x @ W_router + b_router
        top_vals, top_idx = jax.lax.top_k(logits, TOP_K)
        neg_inf = jnp.full_like(logits, -jnp.inf)
        sparse_logits = neg_inf.at[jnp.arange(T)[:, None], top_idx].set(top_vals)
        router_weights = jax.nn.softmax(sparse_logits, axis=-1)
        final_output = jnp.zeros_like(flat_x)
        for e in range(NUM_EXPERTS):
            expert_mask = jnp.any(top_idx == e, axis=-1)
            h = jax.nn.relu(flat_x @ W1[e] + b1[e])
            y = h @ W2[e] + b2[e]
            w = router_weights[:, e] * expert_mask.astype(x.dtype)
            final_output = final_output + y * w[:, None]
        return final_output.reshape(Bv, Sv, D)
    x = L0_attn_resid_pre
    x = x + _L0_attn_ref(_layernorm(x, axis=-1), L0_attn_W_Q, L0_attn_b_Q, L0_attn_W_K, L0_attn_b_K, L0_attn_W_V, L0_attn_b_V, L0_attn_W_O, L0_attn_b_O, L0_attn_ln1_w, L0_attn_ln1_b, L0_attn_ln2_w, L0_attn_ln2_b)
    x = x + _L0_ffn_ref(_layernorm(x, axis=-1), L0_ffn_w_q, L0_ffn_bn_gamma, L0_ffn_bn_beta, L0_ffn_keys, L0_ffn_down_embed, L0_ffn_up_embed)
    x = x + _L1_attn_ref(_layernorm(x, axis=-1), L1_attn_w_qkv, L1_attn_w_o)
    x = x + _L1_ffn_ref(_layernorm(x, axis=-1), L1_ffn_Wr, L1_ffn_Wg, L1_ffn_Wu, L1_ffn_Wd)
    x = x + _L2_attn_ref(_layernorm(x, axis=-1), L2_attn_Wk, L2_attn_Wv, L2_attn_Wo, L2_attn_gate, L2_attn_freqs)
    x = x + _L2_ffn_ref(_layernorm(x, axis=-1), L2_ffn_wqkv, L2_ffn_q_scale, L2_ffn_k_scale, L2_ffn_wo, L2_ffn_ln_g, L2_ffn_ln_b, L2_ffn_w1, L2_ffn_b1, L2_ffn_w2, L2_ffn_b2)
    x = x + _L3_attn_ref(_layernorm(x, axis=-1), L3_attn_W_in, L3_attn_conv_w, L3_attn_conv_b, L3_attn_dt_bias, L3_attn_A_log, L3_attn_D, L3_attn_init_states, L3_attn_norm_w, L3_attn_W_out, L3_attn_W_nl, L3_attn_b_nl)
    x = x + _L3_ffn_ref(_layernorm(x, axis=-1), L3_ffn_W_router, L3_ffn_b_router, L3_ffn_W1, L3_ffn_b1, L3_ffn_W2, L3_ffn_b2)
    return x

_drawn_inputs = setup_inputs


def setup_inputs(seed=0):
    import zlib

    import numpy as np

    out = dict(_drawn_inputs(seed))
    spreads = {'L0_attn_b_Q': (0.0, 0.8),
     'L0_attn_b_K': (0.0, 2.0),
     'L0_attn_b_V': (0.0, 0.1),
     'L0_attn_b_O': (0.0, 0.1),
     'L0_attn_ln1_w': (1.0, 0.6),
     'L0_attn_ln1_b': (0.0, 0.1),
     'L0_attn_ln2_w': (1.0, 0.2),
     'L0_attn_ln2_b': (0.0, 0.1),
     'L0_ffn_bn_gamma': (1.0, 0.6),
     'L0_ffn_bn_beta': (0.0, 0.8),
     'L2_attn_gate': (0.5, 0.2),
     'L2_ffn_q_scale': (1.0, 0.6),
     'L2_ffn_k_scale': (1.0, 0.6),
     'L2_ffn_ln_g': (1.0, 0.6),
     'L2_ffn_ln_b': (0.0, 0.8),
     'L2_ffn_b1': (0.0, 0.8),
     'L2_ffn_b2': (0.0, 0.8),
     'L3_attn_conv_b': (0.0, 2.0),
     'L3_attn_D': (1.0, 0.6),
     'L3_attn_norm_w': (1.0, 0.6),
     'L3_attn_b_nl': (0.0, 2.0),
     'L3_ffn_b_router': (0.0, 2.0),
     'L3_ffn_b1': (0.0, 2.0),
     'L3_ffn_b2': (0.0, 2.0)}
    factors = {'L0_attn_W_Q': 8.0,
     'L0_attn_W_K': 8.0,
     'L0_ffn_w_q': 8.0,
     'L0_ffn_keys': 8.0,
     'L0_ffn_down_embed': 8.0,
     'L0_ffn_up_embed': 8.0,
     'L1_attn_w_qkv': 6.568,
     'L1_attn_w_o': 7.293,
     'L1_ffn_Wr': 8.0,
     'L1_ffn_Wg': 8.0,
     'L1_ffn_Wu': 8.0,
     'L1_ffn_Wd': 8.0,
     'L2_ffn_wqkv': 3.956,
     'L2_ffn_wo': 3.762,
     'L2_ffn_w1': 8.0,
     'L2_ffn_w2': 8.0,
     'L3_attn_A_log': 21.928,
     'L3_attn_init_states': 64.0,
     'L3_attn_W_in': 2.868,
     'L3_attn_conv_w': 3.179,
     'L3_attn_dt_bias': 8.0,
     'L3_attn_W_out': 2.734,
     'L3_attn_W_nl': 2.747,
     'L3_ffn_W_router': 2.691,
     'L3_ffn_W1': 3.88}
    for name, (base, spread) in spreads.items():
        noise = np.random.default_rng([zlib.crc32(name.encode()), seed]).standard_normal(out[name].shape)
        drawn = base * np.exp(spread * noise) if base else spread * noise
        out[name] = jnp.asarray(drawn.astype(out[name].dtype))
    for name, factor in factors.items():
        out[name] = (out[name] * factor).astype(out[name].dtype)
    return out
```

```python
import itertools
from contextlib import ExitStack, contextmanager

import concourse.bass as bass
import concourse.mybir as mybir
import numpy as np

F32 = mybir.dt.float32
BF16 = mybir.dt.bfloat16
I32 = mybir.dt.int32
U32 = mybir.dt.uint32
ALU = mybir.AluOpType
ACT = mybir.ActivationFunctionType
AX_X = mybir.AxisListType.X

STAGES = (0, 8)

P = 128
T = 2048
NT = T // P
D = 128
BANK = 512
NB = T // BANK
TPB = BANK // P
LN_EPS = 1e-5
COUNT = itertools.count()


def bcast(ap, shape):
    return ap.broadcast_to(shape)


@contextmanager
def sublayer(nc):
    sems = []
    with ExitStack() as ctx:
        class Space:
            def sb(self, name, shape, dt=F32):
                return ctx.enter_context(nc.sbuf_tensor(f"{name}_{next(COUNT)}", shape, dt))

            def ps(self, name, shape, dt=F32):
                return ctx.enter_context(nc.psum_tensor(f"{name}_{next(COUNT)}", shape, dt))

            def sem(self, name):
                s = nc.alloc_semaphore(f"{name}_{next(COUNT)}")
                sems.append(s)
                return s
        yield Space()
    nc.clear_and_free_semaphores(sems)
    nc.all_engine_barrier()


def scoped(f):
    def run(nc, *args):
        with sublayer(nc) as sp:
            f(nc, sp, *args)
    return run


@scoped
def layernorm(nc, sp, K, src, dst):
    stats = sp.sb("ln_stats", [P, NT, 6])
    moments = sp.sb("ln_moments", [P, NT, 2])
    std = sp.sb("ln_std", [P, NT])
    rstd = sp.sb("ln_rstd", [P, NT])
    stats_ready = sp.sem("ln_stats_ready")
    moments_ready = sp.sem("ln_moments_ready")
    std_ready = sp.sem("ln_std_ready")
    rstd_ready = sp.sem("ln_rstd_ready")
    with nc.Block() as block:
        @block.vector
        def _(dve):
            for t in range(NT):
                nc.vector.bn_stats(stats[:, t, :], src[:, t, :]).then_inc(stats_ready, 1)
            dve.wait_ge(stats_ready, NT)
            for t in range(NT):
                nc.vector.bn_aggr(moments[:, t, :], stats[:, t, :]).then_inc(moments_ready, 1)
            dve.wait_ge(std_ready, 1)
            nc.vector.reciprocal(rstd[:, :], std[:, :]).then_inc(rstd_ready, 1)
            dve.wait_ge(rstd_ready, 1)
            for t in range(NT):
                nc.vector.tensor_scalar(dst[:, t, :], src[:, t, :], moments[:, t, 0:1], rstd[:, t:t + 1],
                                        ALU.subtract, ALU.mult)

        @block.scalar
        def _(act):
            act.wait_ge(moments_ready, NT)
            nc.scalar.activation(std[:, :], moments[:, :, 1], ACT.Sqrt, bias=K.eps[:, 0:1]).then_inc(std_ready, 1)


@scoped
def transpose_tokens(nc, sp, K, src, dst, scale=None, bias=None):
    turned = sp.ps("turned", [P, 2, BANK])
    turned_ready = sp.sem("turned_ready")
    turned_used = sp.sem("turned_used")
    with nc.Block() as block:
        @block.tensor
        def _(pe):
            for b in range(NB):
                if b >= 2:
                    pe.wait_ge(turned_used, b - 1)
                for j in range(TPB):
                    last = nc.tensor.transpose(turned[:, b % 2, j * P:(j + 1) * P], src[:, b * TPB + j, :], K.ident[:, :])
                last.then_inc(turned_ready, 1)

        @block.vector
        def _(dve):
            for b in range(NB):
                dve.wait_ge(turned_ready, b + 1)
                out = dst[:, b * BANK:(b + 1) * BANK]
                if scale is None:
                    nc.vector.tensor_copy(out, turned[:, b % 2, :]).then_inc(turned_used, 1)
                else:
                    nc.vector.tensor_scalar(out, turned[:, b % 2, :], scale, bias, ALU.mult, ALU.add).then_inc(turned_used, 1)


def l0_attention(nc, X, K, W):
    H, DH = 16, 64
    PAIRS = H // 2
    UNITS = 2 * NT
    NBLK = [t // TPB + 1 for t in range(NT)]
    first = [0]
    for u in range(UNITS):
        first.append(first[-1] + NBLK[u // 2])
    with sublayer(nc) as sp:
        R = sp.sb("resid_pre", [P, NT, D])
        xhat = sp.sb("xhat", [P, NT, D])
        xT = sp.sb("xT", [P, T])
        vecs = sp.sb("ln1_vecs", [P, 2])
        wq = sp.sb("wq", [P, H * DH])
        wk = sp.sb("wk", [P, H * DH])
        wv = sp.sb("wv", [P, H * DH])
        wo = sp.sb("wo", [P, PAIRS, D])
        bq = sp.sb("bq", [P, PAIRS])
        bk = sp.sb("bk", [P, PAIRS])
        bv = sp.sb("bv", [P, H * DH])
        rows = sp.sb("rows", [P, 3, D])
        loaded = sp.sem("weights_loaded")
        layernorm(nc, K, X, R)
        layernorm(nc, K, R, xhat)
        with nc.Block() as block:
            @block.sync
            def _(sync):
                def load(dst, src):
                    sync.dma_start(dst, src).then_inc(loaded, 16)
                load(vecs[:, 0:1], W["L0_attn_ln1_w"].rearrange("(d a) -> d a", a=1))
                load(vecs[:, 1:2], W["L0_attn_ln1_b"].rearrange("(d a) -> d a", a=1))
                for dst, name in ((wq, "L0_attn_W_Q"), (wk, "L0_attn_W_K"), (wv, "L0_attn_W_V")):
                    load(dst[:, :].rearrange("d (h k) -> d h k", k=DH), W[name].rearrange("h d k -> d h k"))
                load(wo[:, :, :], W["L0_attn_W_O"].rearrange("(g a) k n -> (a k) g n", a=2))
                load(bq[:, :], W["L0_attn_b_Q"])
                load(bk[:, :], W["L0_attn_b_K"])
                load(bv[:, :], W["L0_attn_b_V"].rearrange("h k -> (h k)").partition_broadcast(P))
                for j, name in enumerate(("L0_attn_b_O", "L0_attn_ln2_w", "L0_attn_ln2_b")):
                    load(rows[:, j, :], W[name].partition_broadcast(P))
                sync.wait_ge(loaded, 16 * 12)
        transpose_tokens(nc, K, xhat, xT, vecs[:, 0:1], vecs[:, 1:2])
        acc = xhat
        wqs = sp.sb("wq_pair", [P, P])
        wks = sp.sb("wk_pair", [P, P])
        qT = sp.sb("qT", [P, T])
        kT = sp.sb("kT", [P, T])
        V = sp.sb("V", [P, NT, P])
        tot = sp.sb("v_totals", [P, NT, P])
        suf = sp.sb("v_suffix", [P, NT, P])
        prob = sp.sb("prob", [P, 2, T])
        probT = sp.sb("probT", [P, 2, NT, P])
        bmax = sp.sb("bank_max", [P, 2, 1 + NB])
        nmax = sp.sb("neg_max", [P, 2])
        e0 = sp.sb("exp_masked", [P, 2])
        rsum = sp.sb("bank_sums", [P, 2, NB])
        den = sp.sb("den", [P, 2, 3])
        ztmp = sp.sb("ztmp", [P, 2, DH])
        z = sp.sb("z", [P, 2, P])
        zT = sp.sb("zT", [P, P])
        psS = sp.ps("scores", [P, 4, BANK])
        psT = sp.ps("turned", [P, 2, BANK])
        psM = sp.ps("z", [P, BANK])
        psO = sp.ps("zT_and_out", [P, BANK])
        names = ("w_ready proj_ready dve_proj act_proj tot_ready suf_step qk_done masked bank_max_ready row_max max_ready "
                 "exp_done e0_ready trans_done dve_evac act_evac pv_done fin_a fin_b fin_c fin_d z_ready zt_done zt_evac out_done "
                 "out_added acc_init").split()
        S = {n: sp.sem(n) for n in names}
        with nc.Block() as block:
            @block.vector
            def _(dve):
                nc.vector.memset(bmax[:, :, :], 0.0)
                nc.vector.memset(suf[:, NT - 1, :], 0.0)
                nc.vector.tensor_tensor(acc[:, :, :], R[:, :, :], bcast(rows[:, 0:1, :], [P, NT, D]), ALU.add)

        def rows_of(h):
            return slice(DH * h, DH * h + DH)

        with nc.Fori(0, PAIRS) as g:
            with nc.Block() as block:
                @block.tensor
                def _(pe):
                    pe.wait_ge(S["w_ready"], 2)
                    for n in range(4 * NB):
                        ps = psS[:, n % 4, :]
                        if n >= 4:
                            pe.wait_ge(S["dve_proj" if n % 2 == 0 else "act_proj"], (n - 4) // 2 + 1)
                        b = n // 2 % NB
                        if n < 2 * NB:
                            nc.tensor.matmul(ps, (wqs if n % 2 == 0 else wks)[:, :], xT[:, b * BANK:(b + 1) * BANK],
                                             start=True, stop=True).then_inc(S["proj_ready"], 1)
                        elif n % 2 == 0:
                            for j in range(TPB):
                                t = b * TPB + j
                                last = nc.tensor.matmul(ps[:, j * P:(j + 1) * P], xT[:, t * P:(t + 1) * P], wv[:, bass.ds(g * P, P)],
                                                        start=True, stop=True)
                            last.then_inc(S["proj_ready"], 1)
                        else:
                            pe.wait_ge(S["dve_proj"], NB + b + 1)
                            nc.tensor.matmul(ps, K.ones[:, :], V[:, b * TPB:(b + 1) * TPB, :].rearrange("p t n -> p (t n)"),
                                             start=True, stop=True).then_inc(S["proj_ready"], 1)
                    pe.wait_ge(S["dve_proj"], 2 * NB)
                    pe.wait_ge(S["act_proj"], 2 * NB)

                    def qk(u):
                        t, h = u // 2, u % 2
                        for j in range(NBLK[t]):
                            n = first[u] + j
                            if n >= 4:
                                pe.wait_ge(S["exp_done"], n - 3)
                            w = min(BANK, (t + 1) * P - j * BANK)
                            nc.tensor.matmul(psS[:, n % 4, 0:w], qT[rows_of(h), t * P:(t + 1) * P], kT[rows_of(h), j * BANK:j * BANK + w],
                                             start=True, stop=True).then_inc(S["qk_done"], 1)

                    def out(t):
                        pe.wait_ge(S["zt_evac"], t + 1)
                        nc.tensor.matmul(psO[:, P:2 * P], zT[:, :], wo[:, bass.ds(g, 1), :].rearrange("p a n -> p (a n)"),
                                         start=True, stop=True).then_inc(S["out_done"], 1)

                    def trans(u):
                        t = u // 2
                        for j in range(NBLK[t]):
                            n = first[u] + j
                            if n >= 2:
                                pe.wait_ge(S["dve_evac" if n % 2 == 0 else "act_evac"], (n - 2) // 2 + 1)
                            pe.wait_ge(S["exp_done"], n + 1)
                            for k in range(j * TPB, min(j * TPB + TPB, t + 1)):
                                last = nc.tensor.transpose(psT[:, n % 2, (k % TPB) * P:(k % TPB + 1) * P],
                                                           prob[:, u % 2, k * P:(k + 1) * P], K.ident[:, :])
                            last.then_inc(S["trans_done"], 1)

                    def pv(u):
                        t, h = u // 2, u % 2
                        if u >= 1:
                            pe.wait_ge(S["z_ready"], u)
                        n = first[u + 1]
                        pe.wait_ge(S["dve_evac"], (n + 1) // 2)
                        pe.wait_ge(S["act_evac"], n // 2)
                        for k in range(t + 1):
                            last = nc.tensor.matmul(psM[:, rows_of(h)], probT[:, u % 2, k, :], V[:, k, rows_of(h)],
                                                    start=(k == 0), stop=(k == t))
                        last.then_inc(S["pv_done"], 1)

                    for s in range(UNITS + 5):
                        if s >= 5 and s % 2 == 1 and s - 5 < UNITS:
                            t = (s - 5) // 2
                            pe.wait_ge(S["z_ready"], 2 * t + 2)
                            if t >= 1:
                                pe.wait_ge(S["out_added"], t)
                            nc.tensor.transpose(psO[:, 0:P], z[:, t % 2, :], K.ident[:, :]).then_inc(S["zt_done"], 1)
                        if s >= 6 and s % 2 == 0 and s - 6 < UNITS:
                            out((s - 6) // 2)
                        if s < UNITS:
                            qk(s)
                        if 0 <= s - 2 < UNITS:
                            pv(s - 2)
                        if 0 <= s - 1 < UNITS:
                            trans(s - 1)

                @block.scalar
                def _(act):
                    nc.scalar.copy(wqs[:, :], wq[:, bass.ds(g * P, P)]).then_inc(S["w_ready"], 1)
                    nc.scalar.copy(wks[:, :], wk[:, bass.ds(g * P, P)]).then_inc(S["w_ready"], 1)
                    for n in range(1, 4 * NB, 2):
                        act.wait_ge(S["proj_ready"], n + 1)
                        b = n // 2 % NB
                        if n < 2 * NB:
                            nc.scalar.activation(kT[:, b * BANK:(b + 1) * BANK], psS[:, n % 4, :], ACT.Identity,
                                                 bias=bk[:, bass.ds(g, 1)]).then_inc(S["act_proj"], 1)
                        else:
                            nc.scalar.copy(tot[:, b * TPB:(b + 1) * TPB, :].rearrange("p t n -> p (t n)"), psS[:, n % 4, :]).then_inc(S["act_proj"], 1)

                    def exps(u):
                        t = u // 2
                        act.wait_ge(S["max_ready"], u + 1)
                        if u >= 2:
                            act.wait_ge(S["trans_done"], first[u - 1])
                            act.wait_ge(S["z_ready"], u - 1)
                        for j in range(NBLK[t]):
                            n = first[u] + j
                            w = min(BANK, (t + 1) * P - j * BANK)
                            nc.scalar.activation(prob[:, u % 2, j * BANK:j * BANK + w], psS[:, n % 4, 0:w], ACT.Exp, bias=nmax[:, u % 2:u % 2 + 1],
                                                 accum_out=rsum[:, u % 2, j:j + 1]).then_inc(S["exp_done"], 1)
                        nc.scalar.activation(e0[:, u % 2:u % 2 + 1], nmax[:, u % 2:u % 2 + 1], ACT.Exp).then_inc(S["e0_ready"], 1)

                    for s in range(UNITS + 5):
                        if s < UNITS:
                            exps(s)
                        if 0 <= s - 1 < UNITS:
                            u = s - 1
                            if u >= 2:
                                act.wait_ge(S["pv_done"], u - 1)
                            for n in range(first[u], first[u + 1]):
                                if n % 2 == 1:
                                    act.wait_ge(S["trans_done"], n + 1)
                                    k = (n - first[u]) * TPB
                                    w = min(TPB, u // 2 + 1 - k)
                                    nc.scalar.copy(probT[:, u % 2, k:k + w, :].rearrange("p t n -> p (t n)"),
                                                   psT[:, n % 2, 0:w * P]).then_inc(S["act_evac"], 1)
                        if s >= 5 and s % 2 == 1 and s - 5 < UNITS:
                            act.wait_ge(S["zt_done"], (s - 5) // 2 + 1)
                            nc.scalar.copy(zT[:, :], psO[:, 0:P]).then_inc(S["zt_evac"], 1)

                @block.gpsimd
                def _(pool):
                    pool.wait_ge(S["act_proj"], 2 * NB)
                    for i, t in enumerate(range(NT - 2, -1, -1)):
                        if i >= 1:
                            pool.wait_ge(S["suf_step"], i)
                        nc.gpsimd.tensor_tensor(suf[:, t, :], suf[:, t + 1, :], tot[:, t + 1, :], ALU.add).then_inc(S["suf_step"], 1)

                @block.vector
                def _(dve):
                    for n in range(0, 4 * NB, 2):
                        dve.wait_ge(S["proj_ready"], n + 1)
                        b = n // 2 % NB
                        if n < 2 * NB:
                            nc.vector.tensor_scalar(qT[:, b * BANK:(b + 1) * BANK], psS[:, n % 4, :], bq[:, bass.ds(g, 1)], DH ** -0.5,
                                                    ALU.add, ALU.mult).then_inc(S["dve_proj"], 1)
                        else:
                            nc.vector.tensor_tensor(V[:, b * TPB:(b + 1) * TPB, :], psS[:, n % 4, :].rearrange("p (t n) -> p t n", n=P),
                                                    bcast(bv[:, bass.ds(g * P, P)].unsqueeze(1), [P, TPB, P]), ALU.add).then_inc(S["dve_proj"], 1)

                    def maxima(u):
                        t = u // 2
                        for j in range(NBLK[t]):
                            n = first[u] + j
                            w = min(BANK, (t + 1) * P - j * BANK)
                            dve.wait_ge(S["qk_done"], n + 1)
                            if j == NBLK[t] - 1:
                                diag = psS[:, n % 4, w - P:w]
                                nc.vector.tensor_tensor(diag, diag, K.causal_q[:, :], ALU.mult).then_inc(S["masked"], 1)
                                dve.wait_ge(S["masked"], u + 1)
                            if j == 0 and u >= 2:
                                dve.wait_ge(S["e0_ready"], u - 1)
                            nc.vector.reduce_max(bmax[:, u % 2, 1 + j:2 + j], psS[:, n % 4, 0:w], axis=AX_X).then_inc(S["bank_max_ready"], 1)
                        dve.wait_ge(S["bank_max_ready"], first[u + 1])
                        lo = 0 if t < NT - 1 else 1
                        nc.vector.tensor_reduce(nmax[:, u % 2:u % 2 + 1], bmax[:, u % 2, lo:1 + NBLK[t]], axis=AX_X, op=ALU.max,
                                                negate=True).then_inc(S["max_ready"], 1)

                    def add_out(t):
                        dve.wait_ge(S["out_done"], t + 1)
                        nc.vector.tensor_tensor(acc[:, t, :], acc[:, t, :], psO[:, P:2 * P], ALU.add).then_inc(S["out_added"], 1)

                    def finish(u):
                        t, h = u // 2, u % 2
                        later = T - (t + 1) * P
                        dve.wait_ge(S["e0_ready"], u + 1)
                        nc.vector.tensor_reduce(den[:, h, 0:1], rsum[:, u % 2, 0:NBLK[t]], axis=AX_X, op=ALU.add).then_inc(S["fin_a"], 1)
                        dve.wait_ge(S["fin_a"], u + 1)
                        if later:
                            nc.vector.scalar_tensor_tensor(out=den[:, h, 1:2], in0=e0[:, u % 2:u % 2 + 1], scalar=float(later), in1=den[:, h, 0:1],
                                                           op0=ALU.mult, op1=ALU.add).then_inc(S["fin_b"], 1)
                            dve.wait_ge(S["fin_b"], u + 1)
                        nc.vector.reciprocal(den[:, h, 2:3], den[:, h, 1:2] if later else den[:, h, 0:1]).then_inc(S["fin_c"], 1)
                        dve.wait_ge(S["pv_done"], u + 1)
                        src = psM[:, rows_of(h)]
                        if later:
                            dve.wait_ge(S["suf_step"], NT - 1 - t)
                            nc.vector.scalar_tensor_tensor(out=ztmp[:, h, :], in0=suf[:, t, rows_of(h)], scalar=e0[:, u % 2:u % 2 + 1], in1=src,
                                                           op0=ALU.mult, op1=ALU.add).then_inc(S["fin_d"], 1)
                            dve.wait_ge(S["fin_d"], u + 1)
                            src = ztmp[:, h, :]
                        dve.wait_ge(S["fin_c"], u + 1)
                        if t >= 2:
                            dve.wait_ge(S["zt_done"], t - 1)
                        nc.vector.tensor_scalar(z[:, t % 2, rows_of(h)], src, den[:, h, 2:3], None, ALU.mult).then_inc(S["z_ready"], 1)

                    for s in range(UNITS + 5):
                        if s < UNITS:
                            maxima(s)
                        if 0 <= s - 2 < UNITS:
                            finish(s - 2)
                        if 0 <= s - 1 < UNITS:
                            u = s - 1
                            if u >= 2:
                                dve.wait_ge(S["pv_done"], u - 1)
                            for n in range(first[u], first[u + 1]):
                                if n % 2 == 0:
                                    dve.wait_ge(S["trans_done"], n + 1)
                                    k = (n - first[u]) * TPB
                                    w = min(TPB, u // 2 + 1 - k)
                                    nc.vector.tensor_copy(probT[:, u % 2, k:k + w, :].rearrange("p t n -> p (t n)"),
                                                          psT[:, n % 2, 0:w * P]).then_inc(S["dve_evac"], 1)
                        if s >= 6 and s % 2 == 0 and s - 6 < UNITS:
                            t = (s - 6) // 2
                            add_out(t)

            nc.gpsimd.sem_clear(sem_range(S))
            nc.all_engine_barrier()
        layernorm(nc, K, acc, R)
        with nc.Block() as block:
            @block.vector
            def _(dve):
                half = NT // 2
                nc.vector.tensor_tensor(R[:, :, :], R[:, :, :], bcast(rows[:, 1:2, :], [P, NT, D]), ALU.mult).then_inc(S["fin_a"], 1)
                nc.vector.tensor_tensor(X[:, :, :], X[:, :, :], acc[:, :, :], ALU.add).then_inc(S["fin_b"], 1)
                dve.wait_ge(S["fin_a"], 1)
                nc.vector.tensor_tensor(R[:, :, :], R[:, :, :], bcast(rows[:, 2:3, :], [P, NT, D]), ALU.add).then_inc(S["fin_c"], 1)
                dve.wait_ge(S["fin_b"], 1)
                dve.wait_ge(S["fin_c"], 1)
                nc.vector.tensor_tensor(X[:, :, :], X[:, :, :], R[:, :, :], ALU.add)


def l0_experts(nc, X, K, W):
    H, KD, NK, TOP = 8, 128, 32, 8
    C = 2 * H
    EC = NK * NK // P
    with sublayer(nc) as sp:
        xn = sp.sb("xn", [P, NT, D])
        xT = sp.sb("xT", [P, T])
        keysT = sp.sb("keysT", [P, C, NK])
        bn = sp.sb("bn", [P, 2, C])
        downT = sp.sb("downT", [P, EC * P])
        up = sp.sb("up", [P, EC, D])
        G = sp.sb("gelu_hidden", [P, EC, T])
        sim = sp.sb("sim", [P, NT, C, NK])
        loaded = sp.sem("weights_loaded")
        with nc.Block() as block:
            @block.sync
            def _(sync):
                sync.dma_start(keysT[:, :, :], W["L0_ffn_keys"].rearrange("c k n -> k c n")).then_inc(loaded, 16)
                sync.dma_start(bn[:, 0, :], W["L0_ffn_bn_gamma"]).then_inc(loaded, 16)
                sync.dma_start(bn[:, 1, :], W["L0_ffn_bn_beta"]).then_inc(loaded, 16)
                sync.dma_start(downT[:, :], W["L0_ffn_down_embed"]).then_inc(loaded, 16)
                sync.dma_start(up[:, :, :], W["L0_ffn_up_embed"].rearrange("(c e) d -> e c d", e=P)).then_inc(loaded, 16)
                sync.wait_ge(loaded, 16 * 5)
        layernorm(nc, K, X, xn)
        transpose_tokens(nc, K, xn, xT)
        l0_hidden(nc, xT, downT, G, EC)
        l0_queries(nc, K, W, xT, keysT, bn, sim, C, NK)
        l0_select(nc, X, K, sim, G, up, H, NK, TOP, EC)


@scoped
def l0_hidden(nc, sp, xT, downT, G, EC):
    ps = sp.ps("hidden", [P, 8, BANK])
    hidden_ready = sp.sem("hidden_ready")
    gelu_done = sp.sem("gelu_done")
    with nc.Block() as block:
        @block.tensor
        def _(pe):
            for n in range(EC * NB):
                if n >= 8:
                    pe.wait_ge(gelu_done, n - 7)
                nc.tensor.matmul(ps[:, n % 8, :], downT[:, (n // NB) * P:(n // NB + 1) * P], xT[:, (n % NB) * BANK:(n % NB + 1) * BANK],
                                 start=True, stop=True).then_inc(hidden_ready, 1)

        @block.scalar
        def _(act):
            for n in range(EC * NB):
                act.wait_ge(hidden_ready, n + 1)
                nc.scalar.activation(G[:, n // NB, (n % NB) * BANK:(n % NB + 1) * BANK], ps[:, n % 8, :], ACT.Gelu_apprx_tanh).then_inc(gelu_done, 1)


@scoped
def l0_queries(nc, sp, K, W, xT, keysT, bn, sim, C, NK):
    wq = sp.sb("wq_chunk", [P, P])
    qn = sp.sb("queries", [P, T])
    stats = sp.sb("bn_stats", [P, NB, 6])
    mv = sp.sb("bn_moments", [P, 2])
    std = sp.sb("bn_std", [P, 1])
    rstd = sp.sb("bn_rstd", [P, 1])
    ab = sp.sb("bn_affine", [P, 3])
    psQ = sp.ps("queries", [P, NB, BANK])
    psK = sp.ps("sims", [P, BANK])
    S = {n: sp.sem(n) for n in "wq_loaded q_ready stats_ready mv_ready std_ready rstd_ready a_ready ma_ready b_ready q_normed sim_ready".split()}
    with nc.Fori(0, C) as c:
        with nc.Block() as block:
            @block.sync
            def _(sync):
                sync.dma_start(wq[:, :], W["L0_ffn_w_q"][:, bass.ds(c * P, P)]).then_inc(S["wq_loaded"], 16)

            @block.tensor
            def _(pe):
                pe.wait_ge(S["wq_loaded"], 16)
                for b in range(NB):
                    nc.tensor.matmul(psQ[:, b, :], wq[:, :], xT[:, b * BANK:(b + 1) * BANK], start=True, stop=True).then_inc(S["q_ready"], 1)
                for t in range(NT):
                    if t % TPB == 0:
                        pe.wait_ge(S["q_normed"], t // TPB + 1)
                    last = nc.tensor.matmul(psK[:, t * NK:(t + 1) * NK], qn[:, t * P:(t + 1) * P],
                                            keysT[:, bass.ds(c, 1), :].rearrange("p a n -> p (a n)"), start=True, stop=True)
                last.then_inc(S["sim_ready"], 1)

            @block.vector
            def _(dve):
                for b in range(NB):
                    dve.wait_ge(S["q_ready"], b + 1)
                    nc.vector.bn_stats(stats[:, b, :], psQ[:, b, :]).then_inc(S["stats_ready"], 1)
                dve.wait_ge(S["stats_ready"], NB)
                nc.vector.bn_aggr(mv[:, :], stats[:, :, :].rearrange("p b s -> p (b s)")).then_inc(S["mv_ready"], 1)
                dve.wait_ge(S["std_ready"], 1)
                nc.vector.reciprocal(rstd[:, :], std[:, :]).then_inc(S["rstd_ready"], 1)
                dve.wait_ge(S["rstd_ready"], 1)
                nc.vector.tensor_tensor(ab[:, 0:1], rstd[:, :], bn[:, 0, bass.ds(c, 1)], ALU.mult).then_inc(S["a_ready"], 1)
                dve.wait_ge(S["a_ready"], 1)
                nc.vector.tensor_tensor(ab[:, 2:3], mv[:, 0:1], ab[:, 0:1], ALU.mult).then_inc(S["ma_ready"], 1)
                dve.wait_ge(S["ma_ready"], 1)
                nc.vector.tensor_tensor(ab[:, 1:2], bn[:, 1, bass.ds(c, 1)], ab[:, 2:3], ALU.subtract).then_inc(S["b_ready"], 1)
                dve.wait_ge(S["sim_ready"], 1)
                nc.vector.tensor_copy(sim[:, :, bass.ds(c, 1), :], psK[:, :].rearrange("p (t a n) -> p t a n", a=1, n=NK))

            @block.scalar
            def _(act):
                act.wait_ge(S["mv_ready"], 1)
                nc.scalar.activation(std[:, :], mv[:, 1:2], ACT.Sqrt, bias=K.eps[:, 0:1]).then_inc(S["std_ready"], 1)
                act.wait_ge(S["b_ready"], 1)
                for b in range(NB):
                    nc.scalar.activation(qn[:, b * BANK:(b + 1) * BANK], psQ[:, b, :], ACT.Identity, scale=ab[:, 0:1],
                                         bias=ab[:, 1:2]).then_inc(S["q_normed"], 1)
        nc.gpsimd.sem_clear(sem_range(S))
        nc.all_engine_barrier()


@scoped
def l0_select(nc, sp, X, K, sim, G, up, H, NK, TOP, EC):
    simt = sp.sb("sim_tile", [P, 2 * H, NK])
    top = sp.sb("top_keys", [P, 2 * H, TOP])
    pairs = sp.sb("pair_sums", [P, H, TOP, TOP])
    best = sp.sb("best", [P, H, TOP])
    nmax = sp.sb("neg_best", [P, H])
    shifted = sp.sb("best_shifted", [P, H, TOP])
    expd = sp.sb("best_exp", [P, H, TOP])
    z = sp.sb("z", [P, 2, H])
    sums = sp.sb("all_sums", [P, 2, NK * NK])
    exps = sp.sb("all_exps", [P, 2, NK * NK])
    picked = sp.sb("picked", [P, 2, NK * NK])
    diag = sp.sb("diag_rz", [P, H, P])
    weighted = sp.sb("weighted_hidden", [P, EC, P])
    psW = sp.ps("weights", [P, EC // TPB, BANK])
    psY = sp.ps("out", [P, BANK])
    names = ("tile_ready top_ready pairs_ready best_ready nmax_ready shifted_ready exp8_ready z_ready rz_ready diag_ready "
             "sums_ready exps_ready picked_ready added weighted_ready out_ready").split()
    S = {n: sp.sem(n) for n in names}
    with nc.Fori(0, NT) as t:
        with nc.Block() as block:
            @block.gpsimd
            def _(pool):
                for h in range(H):
                    if h == 0:
                        pool.wait_ge(S["tile_ready"], 1)
                    if h >= 2:
                        pool.wait_ge(S["picked_ready"], h - 1)
                        pool.wait_ge(S["exps_ready"], h - 1)
                    nc.gpsimd.tensor_tensor(sums[:, h % 2, :].rearrange("p (i j) -> p i j", j=NK),
                                            bcast(simt[:, h, :].unsqueeze(2), [P, NK, NK]),
                                            bcast(simt[:, H + h, :].unsqueeze(1), [P, NK, NK]), ALU.add).then_inc(S["sums_ready"], 1)

            @block.scalar
            def _(act):
                nc.scalar.copy(simt[:, :, :], sim[:, bass.ds(t, 1), :, :].rearrange("p a c n -> p (a c) n")).then_inc(S["tile_ready"], 1)
                act.wait_ge(S["shifted_ready"], 2)
                nc.scalar.activation(expd[:, :, :], shifted[:, :, :], ACT.Exp).then_inc(S["exp8_ready"], 1)
                for h in range(H):
                    act.wait_ge(S["sums_ready"], h + 1)
                    if h >= 2:
                        act.wait_ge(S["picked_ready"], h - 1)
                    nc.scalar.activation(exps[:, h % 2, :], sums[:, h % 2, :], ACT.Exp, bias=nmax[:, h:h + 1]).then_inc(S["exps_ready"], 1)

            @block.vector
            def _(dve):
                dve.wait_ge(S["tile_ready"], 1)
                for c in range(2 * H):
                    last = nc.vector.max(top[:, c, :], simt[:, c, :])
                last.then_inc(S["top_ready"], 1)
                dve.wait_ge(S["top_ready"], 1)
                nc.vector.tensor_tensor(pairs[:, :, :, :], bcast(top[:, 0:H, :].unsqueeze(3), [P, H, TOP, TOP]),
                                        bcast(top[:, H:2 * H, :].unsqueeze(2), [P, H, TOP, TOP]), ALU.add).then_inc(S["pairs_ready"], 1)
                dve.wait_ge(S["pairs_ready"], 1)
                for h in range(H):
                    last = nc.vector.max(best[:, h, :], pairs[:, h, :, :].rearrange("p i j -> p (i j)"))
                last.then_inc(S["best_ready"], 1)
                dve.wait_ge(S["best_ready"], 1)
                nc.vector.tensor_tensor(shifted[:, :, :], best[:, :, :], bcast(best[:, :, 0:1], [P, H, TOP]), ALU.subtract).then_inc(S["shifted_ready"], 1)
                nc.vector.tensor_scalar(nmax[:, :], best[:, :, 0], -1.0, None, ALU.mult).then_inc(S["shifted_ready"], 1)
                dve.wait_ge(S["exp8_ready"], 1)
                nc.vector.tensor_reduce(z[:, 0, :], expd[:, :, :], axis=AX_X, op=ALU.add).then_inc(S["z_ready"], 1)
                dve.wait_ge(S["z_ready"], 1)
                nc.vector.reciprocal(z[:, 1, :], z[:, 0, :]).then_inc(S["rz_ready"], 1)
                dve.wait_ge(S["rz_ready"], 1)
                for h in range(H):
                    nc.vector.tensor_scalar(diag[:, h, :], K.ident[:, :], z[:, 1, h:h + 1], None, ALU.mult).then_inc(S["diag_ready"], 1)
                for h in range(H):
                    dve.wait_ge(S["exps_ready"], h + 1)
                    if h >= 2:
                        dve.wait_ge(S["added"], h - 1)
                    nc.vector.scalar_tensor_tensor(out=picked[:, h % 2, :], in0=sums[:, h % 2, :], scalar=best[:, h, TOP - 1:TOP],
                                                   in1=exps[:, h % 2, :], op0=ALU.is_ge, op1=ALU.mult).then_inc(S["picked_ready"], 1)
                dve.wait_ge(S["added"], H)
                nc.vector.tensor_tensor(weighted[:, :, :], psW[:, :, :].rearrange("p b (c n) -> p (b c) n", n=P),
                                        G[:, :, bass.ds(t * P, P)], ALU.mult).then_inc(S["weighted_ready"], 1)
                dve.wait_ge(S["out_ready"], 1)
                xt = X[:, bass.ds(t, 1), :].rearrange("p a n -> p (a n)")
                nc.vector.tensor_tensor(xt, xt, psY[:, 0:D], ALU.add)

            @block.tensor
            def _(pe):
                for h in range(H):
                    pe.wait_ge(S["diag_ready"], h + 1)
                    pe.wait_ge(S["picked_ready"], h + 1)
                    for e in range(EC):
                        last = nc.tensor.matmul(psW[:, e // TPB, (e % TPB) * P:(e % TPB + 1) * P], picked[:, h % 2, e * P:(e + 1) * P],
                                                diag[:, h, :], start=(h == 0 and e % TPB == 0), stop=(h == H - 1), skip_group_check=True)
                    last.then_inc(S["added"], 1)
                pe.wait_ge(S["weighted_ready"], 1)
                for e in range(EC):
                    last = nc.tensor.matmul(psY[:, 0:D], weighted[:, e, :], up[:, e, :], start=(e == 0), stop=(e == EC - 1))
                last.then_inc(S["out_ready"], 1)
        nc.gpsimd.sem_clear(sem_range(S))
        nc.all_engine_barrier()


def l1_attention(nc, X, K, W):
    H, G, HD = 16, 4, 8
    with sublayer(nc) as sp:
        QS = sp.sb("q_stackT", [72, H, T], BF16)
        KS = sp.sb("k_stackT", [72, G, T], BF16)
        V1 = sp.sb("v_and_one", [P, NT, G, HD + 1])
        Z = sp.sb("z", [P, NT, D])
        l1_qkv(nc, X, K, W, QS, KS, V1, Z, H, G, HD)
        l1_core(nc, K, QS, KS, V1, Z, H, G, HD)
        project_add(nc, K, Z, W["L1_attn_w_o"], X)


@scoped
def project_add(nc, sp, K, Z, w_dram, X):
    w = sp.sb("w", [P, D])
    ZT = sp.sb("ZT", [P, T])
    psY = sp.ps("y", [P, 2, BANK])
    w_loaded = sp.sem("w_loaded")
    y_ready = sp.sem("y_ready")
    y_added = sp.sem("y_added")
    transpose_tokens(nc, K, Z, ZT)
    with nc.Block() as block:
        @block.sync
        def _(sync):
            sync.dma_start(w[:, :], w_dram).then_inc(w_loaded, 16)

        @block.tensor
        def _(pe):
            pe.wait_ge(w_loaded, 16)
            for b in range(NB):
                if b >= 2:
                    pe.wait_ge(y_added, b - 1)
                for j in range(TPB):
                    t = b * TPB + j
                    last = nc.tensor.matmul(psY[:, b % 2, j * D:(j + 1) * D], ZT[:, t * P:(t + 1) * P], w[:, :], start=True, stop=True)
                last.then_inc(y_ready, 1)

        @block.vector
        def _(dve):
            for b in range(NB):
                dve.wait_ge(y_ready, b + 1)
                xb = X[:, b * TPB:(b + 1) * TPB, :].rearrange("p t d -> p (t d)")
                nc.vector.tensor_tensor(xb, xb, psY[:, b % 2, :], ALU.add).then_inc(y_added, 1)


@scoped
def l1_qkv(nc, sp, X, K, W, QS, KS, V1, xn, H, G, HD):
    N = H + G
    HALF = HD // 2
    xT = sp.sb("xT", [P, T])
    layernorm(nc, K, X, xn)
    transpose_tokens(nc, K, xn, xT)
    w = sp.sb("w_qkv", [P, (N + G) * HD])
    trig = sp.sb("rope", [P, 2, NT, HALF])
    qk = sp.sb("qk", [P, NT, N, HD])
    sq = sp.sb("squares", [P, NT, N, HD])
    nrm = sp.sb("norms", [P, 2, NT * N])
    rot = sp.sb("rotated", [P, NT, N, HD])
    parts = sp.sb("parts", [P, 3, NT * N, HD], BF16)
    stack = sp.sb("stack", [P, NT * N, 9, HD], BF16)
    tmp = stack[:, 0:2 * NT * N // 9 + 1, :, :].rearrange("p a i d -> p (a i d)")[:, 0:2 * NT * N * HD].bitcast(F32).rearrange(
        "p (t n d) -> p t n d", t=NT, n=N)
    identb = sp.sb("identb", [P, P], BF16)
    psP = sp.ps("qkv", [P, 4, BANK])
    psT = sp.ps("turned", [72, 4, 2 * BANK], BF16)
    names = ("loaded qkv_ready qkv_copied one_set sq_ready ss_ready nrm_ready eps_added rn_ready normed "
             "c_ready s_ready rotated part1 rest1 part2 rest2 part3 stacked identb_ready turned_ready dve_copied act_copied").split()
    S = {n: sp.sem(n) for n in names}
    with nc.Block() as block:
        @block.sync
        def _(sync):
            sync.dma_start(w[:, :], W["L1_attn_w_qkv"]).then_inc(S["loaded"], 16)
            sync.dma_start(trig[:, :, :, :], W["rope8"]).then_inc(S["loaded"], 16)

        @block.tensor
        def _(pe):
            pe.wait_ge(S["loaded"], 32)
            WD = (N + G) * HD
            for n in range(NT // 2):
                if n >= 4:
                    pe.wait_ge(S["qkv_copied"], 2 * (n - 3))
                for j in range(2):
                    t = 2 * n + j
                    last = nc.tensor.matmul(psP[:, n % 4, j * WD:(j + 1) * WD], xT[:, t * P:(t + 1) * P], w[:, :], start=True, stop=True)
                last.then_inc(S["qkv_ready"], 1)
            pe.wait_ge(S["identb_ready"], 1)
            pe.wait_ge(S["stacked"], 3)
            st = stack[:, :, :, :].rearrange("p (t n) i d -> p t n (i d)", n=N)
            for n in range(2 * N):
                if n >= 4:
                    pe.wait_ge(S["dve_copied" if n % 2 == 0 else "act_copied"], (n - 4) // 2 + 1)
                for j in range(8):
                    last = nc.tensor.transpose(psT[:, n % 4, j * P:(j + 1) * P], st[:, (n % 2) * 8 + j, n // 2, :], identb[:, :])
                last.then_inc(S["turned_ready"], 1)

        def stack_out(n):
            h, half = n // 2, n % 2
            return (QS[:, h, half * 1024:(half + 1) * 1024] if h < H else KS[:, h - H, half * 1024:(half + 1) * 1024])

        @block.scalar
        def _(act):
            for n in range(NT // 2):
                act.wait_ge(S["qkv_ready"], n + 1)
                src = psP[:, n % 4, 0:2 * (N + G) * HD].rearrange("p (t c) -> p t c", t=2)
                nc.scalar.copy(qk[:, 2 * n:2 * n + 2, :, :].rearrange("p t n d -> p t (n d)"), src[:, :, 0:N * HD]).then_inc(S["qkv_copied"], 1)
                if n == 0:
                    act.wait_ge(S["one_set"], 1)
                nc.scalar.copy(V1[:, 2 * n:2 * n + 2, :, 0:HD], src[:, :, N * HD:].rearrange("p t (g d) -> p t g d", d=HD)).then_inc(S["qkv_copied"], 1)
            act.wait_ge(S["ss_ready"], 1)
            nc.scalar.activation(nrm[:, 1, :], nrm[:, 0, :], ACT.Sqrt).then_inc(S["nrm_ready"], 1)
            for i, done in enumerate(("part1", "part2", "part3")):
                act.wait_ge(S[done], 1)
                p4 = parts[:, i, :, :].rearrange("p (t n) d -> p t n d", n=N)
                s5 = stack[:, :, :, :].rearrange("p (t n) i d -> p t n i d", n=N)
                for t in range(NT):
                    nc.scalar.copy(s5[:, t, 0:H, 3 * i:3 * i + 3, :], bcast(p4[:, t, 0:H, :].unsqueeze(2), [P, H, 3, HD]))
                    last = nc.scalar.copy(s5[:, t, H:N, i:9:3, :], bcast(p4[:, t, H:N, :].unsqueeze(2), [P, G, 3, HD]))
                last.then_inc(S["stacked"], 1)
            for n in range(1, 2 * N, 2):
                act.wait_ge(S["turned_ready"], n + 1)
                nc.scalar.copy(stack_out(n), psT[:, n % 4, :]).then_inc(S["act_copied"], 1)

        @block.gpsimd
        def _(pool):
            nc.gpsimd.memset(V1[:, :, :, :], 1.0).then_inc(S["one_set"], 1)
            nc.gpsimd.tensor_copy(identb[:, :], K.ident[:, :]).then_inc(S["identb_ready"], 1)

        @block.vector
        def _(dve):
            dve.wait_ge(S["qkv_copied"], NT)
            flat = "p t n d -> p (t n d)"
            nc.vector.tensor_tensor(sq[:, :, :, :].rearrange(flat), qk[:, :, :, :].rearrange(flat), qk[:, :, :, :].rearrange(flat), ALU.mult).then_inc(S["sq_ready"], 1)
            dve.wait_ge(S["sq_ready"], 1)
            nc.vector.tensor_reduce(nrm[:, 0, :], sq[:, :, :, :].rearrange("p t n d -> p (t n) d"), axis=AX_X, op=ALU.add).then_inc(S["ss_ready"], 1)
            dve.wait_ge(S["nrm_ready"], 1)
            nc.vector.tensor_scalar(nrm[:, 0, :], nrm[:, 1, :], 1e-10, None, ALU.add).then_inc(S["eps_added"], 1)
            dve.wait_ge(S["eps_added"], 1)
            nc.vector.reciprocal(nrm[:, 1, :], nrm[:, 0, :]).then_inc(S["rn_ready"], 1)
            dve.wait_ge(S["rn_ready"], 1)
            nc.vector.tensor_tensor(sq[:, :, :, :].rearrange("p t n d -> p (t n) d"), qk[:, :, :, :].rearrange("p t n d -> p (t n) d"),
                                    bcast(nrm[:, 1, :].unsqueeze(2), [P, NT * N, HD]), ALU.mult).then_inc(S["normed"], 1)
            dve.wait_ge(S["normed"], 1)
            dve.wait_ge(S["loaded"], 32)
            sh = [P, NT, N, HALF]
            cos, sin = (bcast(trig[:, i, :, :].unsqueeze(2), sh) for i in range(2))
            x1, x2 = sq[:, :, :, 0:HALF], sq[:, :, :, HALF:HD]
            nc.vector.tensor_tensor(rot[:, :, :, 0:HALF], x1, cos, ALU.mult).then_inc(S["c_ready"], 1)
            nc.vector.tensor_tensor(rot[:, :, :, HALF:HD], x2, cos, ALU.mult).then_inc(S["c_ready"], 1)
            nc.vector.tensor_tensor(tmp[:, :, :, 0:HALF], x2, sin, ALU.mult).then_inc(S["s_ready"], 1)
            nc.vector.tensor_tensor(tmp[:, :, :, HALF:HD], x1, sin, ALU.mult).then_inc(S["s_ready"], 1)
            dve.wait_ge(S["c_ready"], 2)
            dve.wait_ge(S["s_ready"], 2)
            nc.vector.tensor_tensor(qk[:, :, :, 0:HALF], rot[:, :, :, 0:HALF], tmp[:, :, :, 0:HALF], ALU.subtract).then_inc(S["rotated"], 1)
            nc.vector.tensor_tensor(qk[:, :, :, HALF:HD], rot[:, :, :, HALF:HD], tmp[:, :, :, HALF:HD], ALU.add).then_inc(S["rotated"], 1)
            dve.wait_ge(S["rotated"], 2)
            v, rest = qk[:, :, :, :].rearrange(flat), rot[:, :, :, :].rearrange(flat)
            part = [parts[:, i, :, :].rearrange("p n d -> p (n d)") for i in range(3)]
            nc.vector.tensor_copy(part[0], v).then_inc(S["part1"], 1)
            dve.wait_ge(S["part1"], 1)
            nc.vector.tensor_tensor(rest, v, part[0], ALU.subtract).then_inc(S["rest1"], 1)
            dve.wait_ge(S["rest1"], 1)
            nc.vector.tensor_copy(part[1], rest).then_inc(S["part2"], 1)
            dve.wait_ge(S["part2"], 1)
            nc.vector.tensor_tensor(v, rest, part[1], ALU.subtract).then_inc(S["rest2"], 1)
            dve.wait_ge(S["rest2"], 1)
            nc.vector.tensor_copy(part[2], v).then_inc(S["part3"], 1)
            for n in range(0, 2 * N, 2):
                dve.wait_ge(S["turned_ready"], n + 1)
                nc.vector.tensor_copy(stack_out(n), psT[:, n % 4, :]).then_inc(S["dve_copied"], 1)


@scoped
def l1_core(nc, sp, K, QS, KS, V1, Z, H, G, HD):
    HPG = H // G
    prob = sp.sb("prob", [P, 3, 2 * BANK])
    rden = sp.sb("rden", [P, 2, TPB])
    psS = sp.ps("scores", [P, 3, 2 * BANK])
    psO = sp.ps("outs", [P, 2, BANK])
    items = []
    for b in range(NB):
        for j in range(HPG):
            for i in range(2 * b):
                items.append((b, j, [(2 * i, 0, BANK), (2 * i + 1, BANK, BANK)]))
            items.append((b, j, [(TPB * b, 0, BANK), (TPB * b + 1, BANK, 3 * P)]))
            items.append((b, j, [(TPB * b + 2, 0, 2 * P), (TPB * b + 3, 2 * P, P)]))
    diagonal = [tiles[0][0] >= TPB * b for b, j, tiles in items]
    masks_to = [sum(diagonal[:n + 1]) for n in range(len(items))]
    names = "qk_done exp_done mask_done pv_done out_ready rden_ready z_done".split()
    S = {n: sp.sem(n) for n in names}
    with nc.Fori(0, G) as g:
        with nc.Block() as block:
            @block.tensor
            def _(pe):
                def qk(n):
                    b, j, tiles = items[n]
                    if n >= 3:
                        pe.wait_ge(S["exp_done"], n - 2)
                    for t, col, w in tiles:
                        last = nc.tensor.matmul(psS[:, n % 3, col:col + w], KS[:, bass.ds(g, 1), t * P:(t + 1) * P].rearrange("p a n -> p (a n)"),
                                                QS[:, bass.ds(g * HPG + j, 1), (b + 1) * BANK - w:(b + 1) * BANK].rearrange("p a n -> p (a n)"),
                                                start=True, stop=True)
                    last.then_inc(S["qk_done"], 1)

                def pv(n):
                    b, j, tiles = items[n]
                    o = b * HPG + j
                    if tiles[0][0] == 0 and o >= 2:
                        pe.wait_ge(S["z_done"], o - 1)
                    pe.wait_ge(S["exp_done"], n + 1)
                    if diagonal[n]:
                        pe.wait_ge(S["mask_done"], masks_to[n])
                    for t, col, w in tiles:
                        for c in range(w // P):
                            q = TPB - w // P + c
                            last = nc.tensor.matmul(psO[:, o % 2, q * 16:q * 16 + HD + 1], prob[:, n % 3, col + c * P:col + (c + 1) * P],
                                                    V1[:, t, bass.ds(g, 1), :].rearrange("p a n -> p (a n)"),
                                                    start=(t == 0 and q == 0), stop=(t == TPB * b + q), skip_group_check=True)
                    last.then_inc(S["pv_done"], 1)
                    if tiles[-1][0] == TPB * b + TPB - 1:
                        pe.wait_ge(S["pv_done"], n + 1)
                        pe.sem_inc(S["out_ready"], 1)

                for s in range(len(items) + 2):
                    if s < len(items):
                        qk(s)
                    if s >= 2:
                        pv(s - 2)

            @block.scalar
            def _(act):
                for n, (b, j, tiles) in enumerate(items):
                    act.wait_ge(S["qk_done"], n + 1)
                    if n >= 3:
                        act.wait_ge(S["pv_done"], n - 2)
                    w = tiles[1][1] + tiles[1][2]
                    nc.scalar.activation(prob[:, n % 3, 0:w], psS[:, n % 3, 0:w], ACT.Exp, scale=HD ** -0.5).then_inc(S["exp_done"], 1)

            @block.gpsimd
            def _(pool):
                for n, (b, j, tiles) in enumerate(items):
                    if diagonal[n]:
                        pool.wait_ge(S["exp_done"], n + 1)
                        d = tiles[1][1]
                        v = prob[:, n % 3, 0:2 * d].rearrange("p (a c) -> p a c", a=2)[:, :, 0:P]
                        nc.gpsimd.tensor_tensor(v, v, bcast(K.causal_k[:, :].unsqueeze(1), [P, 2, P]), ALU.mult).then_inc(S["mask_done"], 1)

            @block.vector
            def _(dve):
                for o in range(NB * HPG):
                    b, j = o // HPG, o % HPG
                    out = psO[:, o % 2, 0:16 * TPB].rearrange("p (q c) -> p q c", c=16)
                    dve.wait_ge(S["out_ready"], o + 1)
                    nc.vector.reciprocal(rden[:, o % 2, :], out[:, :, HD]).then_inc(S["rden_ready"], 1)
                    dve.wait_ge(S["rden_ready"], o + 1)
                    nc.vector.tensor_tensor(Z[:, b * TPB:(b + 1) * TPB, bass.ds((g * HPG + j) * HD, HD)], out[:, :, 0:HD],
                                            bcast(rden[:, o % 2, :].unsqueeze(2), [P, TPB, HD]), ALU.mult).then_inc(S["z_done"], 1)
        nc.gpsimd.sem_clear(sem_range(S))
        nc.all_engine_barrier()


@scoped
def route_top2(nc, sp, K, xT, wr_dram, br_dram, E, cw):
    wr = sp.sb("w_router", [P, E])
    br = sp.sb("b_router", [P, E])
    logit = sp.sb("logits", [P, NT, E])
    best = sp.sb("best", [P, NT, 8])
    ex = sp.sb("exp_logits", [P, NT, E])
    zz = sp.sb("z", [P, 2, NT])
    ps = sp.ps("logits", [P, NT, 16])
    S = {n: sp.sem(n) for n in "loaded logits_ready copied best_ready shifted exp_done masked sum_ready rz_ready".split()}
    with nc.Block() as block:
        @block.sync
        def _(sync):
            sync.dma_start(wr[:, :], wr_dram).then_inc(S["loaded"], 16)
            if br_dram is not None:
                sync.dma_start(br[:, :], br_dram.partition_broadcast(P)).then_inc(S["loaded"], 16)

        @block.tensor
        def _(pe):
            pe.wait_ge(S["loaded"], 16 if br_dram is None else 32)
            for t in range(NT):
                last = nc.tensor.matmul(ps[:, t, 0:E], xT[:, t * P:(t + 1) * P], wr[:, :], start=True, stop=True)
            last.then_inc(S["logits_ready"], 1)

        @block.vector
        def _(dve):
            dve.wait_ge(S["logits_ready"], 1)
            if br_dram is None:
                nc.vector.tensor_copy(logit[:, :, :], ps[:, :, 0:E]).then_inc(S["copied"], 1)
            else:
                dve.wait_ge(S["loaded"], 32)
                nc.vector.tensor_tensor(logit[:, :, :], ps[:, :, 0:E], bcast(br[:, :].unsqueeze(1), [P, NT, E]), ALU.add).then_inc(S["copied"], 1)
            dve.wait_ge(S["copied"], 1)
            for t in range(NT):
                nc.vector.max(best[:, t, :], logit[:, t, :]).then_inc(S["best_ready"], 1)
            dve.wait_ge(S["best_ready"], NT)
            nc.vector.tensor_tensor(ex[:, :, :], logit[:, :, :], bcast(best[:, :, 0:1], [P, NT, E]), ALU.subtract).then_inc(S["shifted"], 1)
            nc.vector.tensor_tensor(logit[:, :, :], logit[:, :, :], bcast(best[:, :, 1:2], [P, NT, E]), ALU.is_ge).then_inc(S["shifted"], 1)
            dve.wait_ge(S["shifted"], 2)
            dve.wait_ge(S["exp_done"], 1)
            nc.vector.tensor_tensor(cw[:, :, :], ex[:, :, :], logit[:, :, :], ALU.mult).then_inc(S["masked"], 1)
            dve.wait_ge(S["masked"], 1)
            nc.vector.tensor_reduce(zz[:, 0, :], cw[:, :, :], axis=AX_X, op=ALU.add).then_inc(S["sum_ready"], 1)
            dve.wait_ge(S["sum_ready"], 1)
            nc.vector.reciprocal(zz[:, 1, :], zz[:, 0, :]).then_inc(S["rz_ready"], 1)
            dve.wait_ge(S["rz_ready"], 1)
            nc.vector.tensor_tensor(cw[:, :, :], cw[:, :, :], bcast(zz[:, 1, :].unsqueeze(2), [P, NT, E]), ALU.mult)

        @block.scalar
        def _(act):
            act.wait_ge(S["shifted"], 1)
            nc.scalar.activation(ex[:, :, :], ex[:, :, :], ACT.Exp).then_inc(S["exp_done"], 1)


@scoped
def expert_mlps(nc, sp, X, K, xT, cw, E, F, up_drams, down_dram, b1_dram):
    gated = len(up_drams) == 2
    FC = -(-F // P)
    rows = [min(P, F - c * P) for c in range(FC)]
    NW = len(up_drams)
    w1_all = sp.sb("w1_all", [P, NW, E * F])
    w2_all = sp.sb("w2_all", [P, FC, E, D])
    b1 = None if gated else sp.sb("b1", [P, FC, E])
    w1 = sp.sb("w1_expert", [P, NW, F])
    gate = sp.sb("silu", [P, 2, BANK])
    gate2 = sp.sb("sigmoid", [P, 2, BANK])
    hid = sp.sb("hidden", [P, 2, FC, BANK])
    psG = sp.ps("gate", [P, 2, BANK])
    psU = sp.ps("up", [P, 2, BANK]) if gated else psG
    psY = sp.ps("y", [P, 2, BANK])
    S = {n: sp.sem(n) for n in "w_ready gu_ready silu_done sig_done hid_done y_ready y_added".split()}
    loaded = sp.sem("loaded")
    with nc.Block() as block:
        @block.sync
        def _(sync):
            for i, w in enumerate(up_drams):
                sync.dma_start(w1_all[:, i, :].rearrange("d (e f) -> d e f", e=E), w.rearrange("e d f -> d e f")).then_inc(loaded, 16)
            for c in range(FC):
                sync.dma_start(w2_all[0:rows[c], c, :, :], down_dram[:, c * P:c * P + rows[c], :].rearrange("e f n -> f e n")).then_inc(loaded, 16)
            if not gated:
                sync.dma_start(b1[:, :, :], b1_dram).then_inc(loaded, 16)
            sync.wait_ge(loaded, 16 * (NW + FC + (not gated)))
    n_items = NB * FC
    with nc.Fori(0, E) as e:
        with nc.Block() as block:
            @block.tensor
            def _(pe):
                def hidden(n):
                    b, c = n // FC, n % FC
                    if n == 0:
                        pe.wait_ge(S["w_ready"], 1)
                    if n >= 2:
                        pe.wait_ge(S["hid_done"], n - 1)
                    for i in range(NW):
                        last = nc.tensor.matmul((psG, psU)[i][0:rows[c], n % 2, :], w1[:, i, c * P:c * P + rows[c]], xT[:, b * BANK:(b + 1) * BANK],
                                                start=True, stop=True)
                    last.then_inc(S["gu_ready"], 1)

                def down(b):
                    pe.wait_ge(S["hid_done"], (b + 1) * FC)
                    if b >= 2:
                        pe.wait_ge(S["y_added"], TPB * (b - 1))
                    for j in range(TPB):
                        for c in range(FC):
                            last = nc.tensor.matmul(psY[:, b % 2, j * D:(j + 1) * D], hid[0:rows[c], b % 2, c, j * P:(j + 1) * P],
                                                    w2_all[0:rows[c], c, bass.ds(e, 1), :].rearrange("p a n -> p (a n)"),
                                                    start=(c == 0), stop=(c == FC - 1))
                    last.then_inc(S["y_ready"], 1)

                for n in range(n_items + 1):
                    if n < n_items:
                        hidden(n)
                    if n >= FC and (n - 1) % FC == 0 and n > 1 or n == n_items:
                        down((n - 1) // FC if n == n_items else (n - 1) // FC - 1)

            @block.scalar
            def _(act):
                nc.scalar.copy(w1[:, :, :], w1_all[:, :, bass.ds(e * F, F)]).then_inc(S["w_ready"], 1)
                for n in range(n_items):
                    b, c = n // FC, n % FC
                    act.wait_ge(S["gu_ready"], n + 1)
                    if gated:
                        if n >= 2:
                            act.wait_ge(S["silu_done"], n - 1)
                        nc.scalar.activation(gate2[0:rows[c], n % 2, :], psG[0:rows[c], n % 2, :], ACT.Sigmoid).then_inc(S["sig_done"], 1)
                    else:
                        if c == 0 and b >= 2:
                            act.wait_ge(S["y_ready"], b - 1)
                        nc.scalar.activation(hid[:, b % 2, c, :], psG[:, n % 2, :], ACT.Relu, bias=b1[:, c, bass.ds(e, 1)]).then_inc(S["hid_done"], 1)

            @block.vector
            def _(dve):
                def add(b):
                    dve.wait_ge(S["y_ready"], b + 1)
                    for j in range(TPB):
                        t = b * TPB + j
                        nc.vector.scalar_tensor_tensor(out=X[:, t, :], in0=psY[:, b % 2, j * D:(j + 1) * D], scalar=cw[:, t, bass.ds(e, 1)], in1=X[:, t, :],
                                                       op0=ALU.mult, op1=ALU.add).then_inc(S["y_added"], 1)

                for n in range(n_items if gated else 0):
                    b, c = n // FC, n % FC
                    dve.wait_ge(S["sig_done"], n + 1)
                    nc.vector.tensor_tensor(gate[0:rows[c], n % 2, :], gate2[0:rows[c], n % 2, :], psG[0:rows[c], n % 2, :], ALU.mult).then_inc(S["silu_done"], 1)
                    dve.wait_ge(S["silu_done"], n + 1)
                    if c == 0 and b >= 2:
                        dve.wait_ge(S["y_ready"], b - 1)
                    nc.vector.tensor_tensor(hid[0:rows[c], b % 2, c, :], gate[0:rows[c], n % 2, :], psU[0:rows[c], n % 2, :], ALU.mult).then_inc(S["hid_done"], 1)
                    if c == FC - 1 and b >= 1:
                        add(b - 1)
                for b in range(NB - 1 if gated else 0, NB):
                    add(b)
        nc.gpsimd.sem_clear(sem_range(S))
        nc.all_engine_barrier()


def l1_experts(nc, X, K, W):
    E, F = 9, 352
    with sublayer(nc) as sp:
        xn = sp.sb("xn", [P, NT, D])
        xT = sp.sb("xT", [P, T])
        cw = sp.sb("expert_weights", [P, NT, E])
        layernorm(nc, K, X, xn)
        transpose_tokens(nc, K, xn, xT)
        route_top2(nc, K, xT, W["L1_ffn_Wr"], None, E, cw)
        expert_mlps(nc, X, K, xT, cw, E, F, [W["L1_ffn_Wg"], W["L1_ffn_Wu"]], W["L1_ffn_Wd"], None)


def l3_experts(nc, X, K, W):
    E, F = 8, 512
    with sublayer(nc) as sp:
        xn = sp.sb("xn", [P, NT, D])
        xT = sp.sb("xT", [P, T])
        cw = sp.sb("expert_weights", [P, NT, E])
        layernorm(nc, K, X, xn)
        transpose_tokens(nc, K, xn, xT)
        route_top2(nc, K, xT, W["L3_ffn_W_router"], W["L3_ffn_b_router"], E, cw)
        expert_mlps(nc, X, K, xT, cw, E, F, [W["L3_ffn_W1"]], W["L3_ffn_W2"], W["L3_ffn_b1"])
        with nc.Block() as block:
            @block.vector
            def _(dve):
                nc.vector.memset(xn[:, :, E:], 0.0)
                nc.vector.tensor_copy(xn[:, :, 0:E], cw[:, :, :])
        project_add(nc, K, xn, W["L3_ffn_b2"], X)


def l2_attention(nc, X, K, W):
    with sublayer(nc) as sp:
        xn = sp.sb("xn", [P, NT, D])
        xT = sp.sb("xT", [P, T])
        layernorm(nc, K, X, xn)
        transpose_tokens(nc, K, xn, xT)
        l2_memories(nc, X, K, W, xT, xn)


@scoped
def l2_memories(nc, sp, X, K, W, xT, Y):
    C = 8
    TWO_PI_HI = 6.28125
    TWO_PI_LO = float(2 * np.pi - TWO_PI_HI)
    ROUND = 12582912.0
    PI = float(np.nextafter(np.float32(np.pi), np.float32(0)))
    PHASE_SCALE = 10.0
    pos = sp.sb("positions", [P, T])
    posi = sp.sb("positions_int", [P, BANK], I32)
    consts = sp.sb("round_and_half_pi", [P, 2])
    gate = sp.sb("gate", [P, 2, C])
    freq = sp.sb("freqs", [P, C])
    rs = sp.sb("rsqrt_t", [P, NT])
    wo = sp.sb("wo", [P, C, D])
    wk = sp.sb("wk_chunk", [P, P])
    wv = sp.sb("wv_chunk", [P, P])
    ang = [sp.sb(n, [P, T]) for n in ("angle_pos", "angle_key")]
    turns = [sp.sb(n, [P, T]) for n in ("turns_pos", "turns_key")]
    v = sp.sb("v", [P, T])
    cs = [[sp.sb(f"{n}_{m}", [P, 1 + T]) for n in ("cos", "sin")] for m in ("pos", "key")]
    prod = [sp.sb(f"prod{i}", [P, T]) for i in range(4)]
    mem = [sp.sb(f"mem{i}", [P, T]) for i in range(4)]
    psK = sp.ps("k", [P, 2, BANK])
    psV = sp.ps("v", [P, 2, BANK])
    psY = sp.ps("y", [P, 4, BANK])
    loaded = sp.sem("loaded")
    setup = sp.sem("setup")
    names = ("w_loaded kv_ready v_copied ang_pos ang_key rounded_pos rounded_key turns_pos turns_key "
             "red1 red2 red3 abs_pos abs_key trig_pos trig_key prods mems finals y_ready").split()
    S = {n: sp.sem(n) for n in names}
    blocks = [slice(b * BANK, (b + 1) * BANK) for b in range(NB)]

    with nc.Block() as block:
        @block.sync
        def _(sync):
            sync.dma_start(gate[:, :, :], W["L2_attn_gate"]).then_inc(loaded, 16)
            sync.dma_start(freq[:, :], W["L2_attn_freqs"]).then_inc(loaded, 16)
            sync.dma_start(rs[:, :], W["rsqrt_t"]).then_inc(loaded, 16)
            sync.dma_start(wo[:, :, :], W["L2_attn_Wo"].rearrange("(c f) n -> f c n", f=P)).then_inc(loaded, 16)
            sync.wait_ge(loaded, 64)

        @block.gpsimd
        def _(pool):
            for b in range(NB):
                if b:
                    pool.wait_ge(setup, 2 * b)
                nc.gpsimd.iota(posi[:, :], pattern=[[1, BANK]], base=b * BANK, channel_multiplier=0).then_inc(setup, 1)
                pool.wait_ge(setup, 2 * b + 1)
                nc.gpsimd.tensor_copy(pos[:, blocks[b]], posi[:, :]).then_inc(setup, 1)

        @block.vector
        def _(dve):
            nc.vector.memset(consts[:, 0:1], ROUND)
            nc.vector.memset(consts[:, 1:2], float(np.pi / 2))
            nc.vector.memset(cs[1][0][:, 0:1], 0.0)
            nc.vector.memset(cs[1][1][:, 0:1], 0.0)
            nc.vector.memset(Y[:, :, :], 0.0)

    with nc.Fori(0, C) as c:
        with nc.Block() as block:
            @block.sync
            def _(sync):
                sync.dma_start(wk[:, :], W["L2_attn_Wk"][:, bass.ds(c * P, P)]).then_inc(S["w_loaded"], 16)
                sync.dma_start(wv[:, :], W["L2_attn_Wv"][:, bass.ds(c * P, P)]).then_inc(S["w_loaded"], 16)

            @block.tensor
            def _(pe):
                pe.wait_ge(S["w_loaded"], 32)
                for b in range(NB):
                    if b >= 2:
                        pe.wait_ge(S["ang_key"], b - 1)
                        pe.wait_ge(S["v_copied"], b - 1)
                    nc.tensor.matmul(psK[:, b % 2, :], wk[:, :], xT[:, blocks[b]], start=True, stop=True)
                    nc.tensor.matmul(psV[:, b % 2, :], wv[:, :], xT[:, blocks[b]], start=True, stop=True).then_inc(S["kv_ready"], 1)
                for b in range(NB):
                    pe.wait_ge(S["finals"], 4 * (b + 1))
                    for j in range(TPB):
                        t = b * TPB + j
                        for i in range(4):
                            last = nc.tensor.matmul(psY[:, b, j * D:(j + 1) * D], prod[i][:, t * P:(t + 1) * P],
                                                    wo[:, bass.ds(c, 1), :].rearrange("p a n -> p (a n)"), start=(i == 0), stop=(i == 3))
                    last.then_inc(S["y_ready"], 1)

            @block.scalar
            def _(act):
                def angles(b):
                    nc.scalar.activation(ang[0][:, blocks[b]], pos[:, blocks[b]], ACT.Identity, scale=freq[:, bass.ds(c, 1)]).then_inc(S["ang_pos"], 1)
                    act.wait_ge(S["kv_ready"], b + 1)
                    nc.scalar.mul(ang[1][:, blocks[b]], psK[:, b % 2, :], PHASE_SCALE).then_inc(S["ang_key"], 1)
                    nc.scalar.copy(v[:, blocks[b]], psV[:, b % 2, :]).then_inc(S["v_copied"], 1)
                    for i, (made, done) in enumerate((("ang_pos", "rounded_pos"), ("ang_key", "rounded_key"))):
                        act.wait_ge(S[made], b + 1)
                        nc.scalar.activation(turns[i][:, blocks[b]], ang[i][:, blocks[b]], ACT.Identity, scale=float(1 / (2 * np.pi)),
                                             bias=consts[:, 0:1]).then_inc(S[done], 1)

                def trig(b):
                    for i, (absd, done) in enumerate((("abs_pos", "trig_pos"), ("abs_key", "trig_key"))):
                        act.wait_ge(S["red3"], 2 * b + i + 1)
                        sh = slice(1 + b * BANK, 1 + (b + 1) * BANK)
                        nc.scalar.activation(turns[i][:, blocks[b]], ang[i][:, blocks[b]], ACT.Abs).then_inc(S[absd], 1)
                        nc.scalar.activation(cs[i][1][:, sh], ang[i][:, blocks[b]], ACT.Sin).then_inc(S[done], 1)
                        act.wait_ge(S[absd], b + 1)
                        nc.scalar.activation(cs[i][0][:, sh], turns[i][:, blocks[b]], ACT.Sin, scale=-1.0, bias=consts[:, 1:2]).then_inc(S[done], 1)

                angles(0)
                for b in range(NB):
                    if b + 1 < NB:
                        angles(b + 1)
                    trig(b)

            @block.gpsimd
            def _(pool):
                def turn(b):
                    for i, (rounded, done) in enumerate((("rounded_pos", "turns_pos"), ("rounded_key", "turns_key"))):
                        pool.wait_ge(S[rounded], b + 1)
                        nc.gpsimd.tensor_scalar(turns[i][:, blocks[b]], turns[i][:, blocks[b]], -ROUND, 1.0, ALU.add, ALU.mult).then_inc(S[done], 1)

                turn(0)
                for b in range(NB):
                    if b + 1 < NB:
                        turn(b + 1)
                    pool.wait_ge(S["v_copied"], b + 1)
                    for i in range(4):
                        if i % 2 == 0:
                            pool.wait_ge(S["trig_pos" if i == 0 else "trig_key"], 2 * (b + 1))
                        src = slice(1 + b * BANK, 1 + (b + 1) * BANK) if i < 2 else blocks[b]
                        nc.gpsimd.tensor_tensor(prod[i][:, blocks[b]], v[:, blocks[b]], cs[i // 2][i % 2][:, src], ALU.mult).then_inc(S["prods"], 1)

            @block.vector
            def _(dve):
                def add(b):
                    dve.wait_ge(S["y_ready"], b + 1)
                    yb = Y[:, b * TPB:(b + 1) * TPB, :].rearrange("p t n -> p (t n)")
                    nc.vector.tensor_tensor(yb, yb, psY[:, b, :], ALU.add)

                def reduce(b):
                    n = 2 * b
                    for i, made in enumerate(("turns_pos", "turns_key")):
                        dve.wait_ge(S[made], b + 1)
                        a = ang[i][:, blocks[b]]
                        nc.vector.scalar_tensor_tensor(out=a, in0=turns[i][:, blocks[b]], scalar=-TWO_PI_HI, in1=a, op0=ALU.mult, op1=ALU.add).then_inc(S["red1"], 1)
                    for i in range(2):
                        dve.wait_ge(S["red1"], n + i + 1)
                        a = ang[i][:, blocks[b]]
                        nc.vector.scalar_tensor_tensor(out=a, in0=turns[i][:, blocks[b]], scalar=-TWO_PI_LO, in1=a, op0=ALU.mult, op1=ALU.add).then_inc(S["red2"], 1)
                    for i in range(2):
                        dve.wait_ge(S["red2"], n + i + 1)
                        a = ang[i][:, blocks[b]]
                        nc.vector.tensor_scalar(a, a, PI, -PI, ALU.min, ALU.max).then_inc(S["red3"], 1)

                reduce(0)
                for b in range(NB):
                    if b + 1 < NB:
                        reduce(b + 1)
                    for i in range(4):
                        dve.wait_ge(S["prods"], 4 * b + i + 1)
                        if b:
                            dve.wait_ge(S["mems"], 4 * (b - 1) + i + 1)
                        nc.vector.tensor_tensor_scan(mem[i][:, blocks[b]], bcast(K.ones[:, 0:1], [P, BANK]), prod[i][:, blocks[b]],
                                                     0.0 if b == 0 else mem[i][:, b * BANK - 1:b * BANK], ALU.mult, ALU.add).then_inc(S["mems"], 1)
                    for i in range(4):
                        dve.wait_ge(S["mems"], 4 * b + i + 1)
                        src = slice(1 + b * BANK, 1 + (b + 1) * BANK)
                        nc.vector.scalar_tensor_tensor(out=prod[i][:, blocks[b]], in0=mem[i][:, blocks[b]], scalar=gate[:, i // 2, bass.ds(c, 1)],
                                                       in1=cs[i // 2][i % 2][:, src], op0=ALU.mult, op1=ALU.mult).then_inc(S["finals"], 1)
                    if b >= 1:
                        add(b - 1)
                add(NB - 1)

        nc.gpsimd.sem_clear(sem_range(S))
        nc.all_engine_barrier()
    with nc.Block() as block:
        @block.vector
        def _(dve):
            for t in range(NT):
                nc.vector.scalar_tensor_tensor(out=X[:, t, :], in0=Y[:, t, :], scalar=rs[:, t:t + 1], in1=X[:, t, :], op0=ALU.mult, op1=ALU.add)


@scoped
def shift_tokens(nc, sp, src, dst):
    HF = D // 2
    zeroed = sp.sem("zeroed")
    shifted = sp.sem("shifted")
    with nc.Block() as block:
        @block.sync
        def _(sync):
            sync.dma_start(dst[1:P, :, HF:D], src[0:P - 1, :, HF:D]).then_inc(shifted, 16)
            sync.dma_start(dst[0:1, 1:NT, HF:D], src[P - 1:P, 0:NT - 1, HF:D]).then_inc(shifted, 16)
            sync.wait_ge(shifted, 32)

        @block.vector
        def _(dve):
            nc.vector.memset(dst[0:1, 0, HF:D], 0.0)

        @block.scalar
        def _(act):
            nc.scalar.copy(dst[:, :, 0:HF], src[:, :, 0:HF])


def l2_transformer(nc, X, K, W):
    DEPTH = 2
    with sublayer(nc) as sp:
        Y = sp.sb("y", [P, NT, D])
        layernorm(nc, K, X, Y)
        with nc.Fori(0, DEPTH) as l:
            with sublayer(nc) as inner:
                qT = inner.sb("qT", [P, 4, T])
                kT = inner.sb("kT", [P, 4, T])
                V = inner.sb("V", [P, NT, 512])
                rn = inner.sb("rnorm", [P, NT, 16])
                l2_qkv(nc, K, W, l, Y, qT, kT, V, rn)
                l2_window_attention(nc, K, W, l, Y, qT, kT, V, rn)
            l2_geglu(nc, K, W, l, Y)
        with nc.Block() as block:
            @block.vector
            def _(dve):
                nc.vector.tensor_tensor(X[:, :, :], X[:, :, :], Y[:, :, :], ALU.add)


@scoped
def l2_qkv(nc, sp, K, W, l, Y, qT, kT, V, rn):
    DH = 64
    HD2 = DH // 2
    h = sp.sb("shifted", [P, NT, D])
    hT = sp.sb("hT", [P, T])
    shift_tokens(nc, Y, h)
    transpose_tokens(nc, K, h, hT)
    w = sp.sb("wqkv", [P, 3 * 512])
    tab = sp.sb("rope_tables", [P, 2, NT, 2, DH])
    scl = sp.sb("qk_scales", [P, 2, 2, DH])
    sq = sp.sb("squares", [P, 2, 16, DH])
    ss = sp.sb("sums", [P, 3, 2, 16])
    m1 = sp.sb("cos_terms", [P, 2, 2, 8, DH])
    m2 = sp.sb("sin_terms", [P, 2, 2, 8, DH])
    psA = sp.ps("qkv", [P, 2, 3, BANK])
    psT = sp.ps("turned", [P, 2, BANK])
    names = ("loaded tables_ready qkv_ready sq_ready v_copied ss_ready root_ready clamped rn_ready cos_ready sin_ready "
             "summed k_normed turned_ready q_copied k_copied").split()
    S = {n: sp.sem(n) for n in names}
    with nc.Block() as block:
        @block.sync
        def _(sync):
            sync.dma_start(w[:, :], W["L2_ffn_wqkv"][bass.ds(l, 1), :, :].rearrange("a d n -> (a d) n")).then_inc(S["loaded"], 16)
            sync.dma_start(tab[:, :, :, :, :], W["xpos"]).then_inc(S["loaded"], 16)
            for i, name in enumerate(("L2_ffn_q_scale", "L2_ffn_k_scale")):
                src = W[name][bass.ds(l, 1), :].rearrange("a d -> (a d)")
                sync.dma_start(scl[:, 0, i, :], src.partition_broadcast(P)).then_inc(S["loaded"], 16)
                sync.dma_start(scl[:, 1, i, 0:HD2], src[HD2:DH].partition_broadcast(P)).then_inc(S["loaded"], 16)
                sync.dma_start(scl[:, 1, i, HD2:DH], src[0:HD2].partition_broadcast(P)).then_inc(S["loaded"], 16)

        @block.tensor
        def _(pe):
            pe.wait_ge(S["loaded"], 16 * 8)
            for t in range(NT + 1):
                if t < NT:
                    if t >= 2:
                        pe.wait_ge(S["sin_ready"], 2 * (t - 1))
                        pe.wait_ge(S["cos_ready"], t - 1)
                        pe.wait_ge(S["sq_ready"], t - 1)
                        pe.wait_ge(S["v_copied"], t - 1)
                    for i in range(3):
                        last = nc.tensor.matmul(psA[:, t % 2, i, :], hT[:, t * P:(t + 1) * P], w[:, i * 512:(i + 1) * 512], start=True, stop=True)
                    last.then_inc(S["qkv_ready"], 1)
                if t >= 1:
                    u = t - 1
                    pe.wait_ge(S["summed"], u + 1)
                    pe.wait_ge(S["k_normed"], u + 1)
                    if u >= 1:
                        pe.wait_ge(S["q_copied"], u)
                        pe.wait_ge(S["k_copied"], u)
                    for i in range(2):
                        for j in range(4):
                            last = nc.tensor.transpose(psT[:, i, j * P:(j + 1) * P], m1[:, u % 2, i, 2 * j:2 * j + 2, :].rearrange("p h d -> p (h d)"), K.ident[:, :])
                    last.then_inc(S["turned_ready"], 1)

        @block.scalar
        def _(act):
            for t in range(NT + 1):
                if t < NT:
                    act.wait_ge(S["qkv_ready"], t + 1)
                    if t >= 2:
                        act.wait_ge(S["ss_ready"], t - 1)
                    nc.scalar.activation(sq[:, t % 2, :, :].rearrange("p h d -> p (h d)"), psA[:, t % 2, 0:2, :].rearrange("p i n -> p (i n)"), ACT.Square).then_inc(S["sq_ready"], 1)
                    nc.scalar.copy(V[:, t, :], psA[:, t % 2, 2, :]).then_inc(S["v_copied"], 1)
                    act.wait_ge(S["ss_ready"], t + 1)
                    nc.scalar.activation(ss[:, 1, t % 2, :], ss[:, 0, t % 2, :], ACT.Sqrt).then_inc(S["root_ready"], 1)
                if t >= 1:
                    act.wait_ge(S["turned_ready"], t)
                    nc.scalar.copy(qT[:, :, (t - 1) * P:t * P], psT[:, 0, :].rearrange("p (j n) -> p j n", n=P)).then_inc(S["q_copied"], 1)

        @block.gpsimd
        def _(pool):
            for t in range(NT):
                pool.wait_ge(S["cos_ready"], t + 1)
                pool.wait_ge(S["sin_ready"], 2 * (t + 1))
                a = m1[:, t % 2, :, :, :].rearrange("p i h d -> p (i h d)")
                nc.gpsimd.tensor_tensor(a, a, m2[:, t % 2, :, :, :].rearrange("p i h d -> p (i h d)"), ALU.add).then_inc(S["summed"], 1)
                pool.wait_ge(S["summed"], t + 1)
                pool.wait_ge(S["rn_ready"], t + 1)
                k = m1[:, t % 2, 1, :, :]
                nc.gpsimd.tensor_tensor(k, k, bcast(rn[:, t, 8:16].unsqueeze(2), [P, 8, DH]), ALU.mult).then_inc(S["k_normed"], 1)

        @block.vector
        def _(dve):
            dve.wait_ge(S["loaded"], 16 * 8)
            for i in range(2):
                nc.vector.tensor_tensor(tab[:, i, :, :, :], tab[:, i, :, :, :], bcast(scl[:, i, :, :].unsqueeze(1), [P, NT, 2, DH]), ALU.mult).then_inc(S["tables_ready"], 1)
            dve.wait_ge(S["tables_ready"], 2)
            for t in range(NT + 1):
                if t < NT:
                    dve.wait_ge(S["sq_ready"], t + 1)
                    if t >= 2:
                        dve.wait_ge(S["root_ready"], t - 1)
                    nc.vector.tensor_reduce(ss[:, 0, t % 2, :], sq[:, t % 2, :, :], axis=AX_X, op=ALU.add).then_inc(S["ss_ready"], 1)
                    if t >= 2:
                        dve.wait_ge(S["turned_ready"], t - 1)
                        dve.wait_ge(S["summed"], t - 1)
                    dve.wait_ge(S["v_copied"], t + 1)
                    x = psA[:, t % 2, 0:2, :].rearrange("p i (h d) -> p i h d", d=DH)
                    nc.vector.tensor_tensor(m1[:, t % 2, :, :, :], x, bcast(tab[:, 0, t, :, :].unsqueeze(2), [P, 2, 8, DH]), ALU.mult).then_inc(S["cos_ready"], 1)
                    for o, i in ((0, HD2), (HD2, 0)):
                        nc.vector.tensor_tensor(m2[:, t % 2, :, :, o:o + HD2], x[:, :, :, i:i + HD2],
                                                bcast(tab[:, 1, t, :, o:o + HD2].unsqueeze(2), [P, 2, 8, HD2]), ALU.mult).then_inc(S["sin_ready"], 1)
                    dve.wait_ge(S["root_ready"], t + 1)
                    nc.vector.tensor_scalar(ss[:, 2, t % 2, :], ss[:, 1, t % 2, :], 1e-12, None, ALU.max).then_inc(S["clamped"], 1)
                    dve.wait_ge(S["clamped"], t + 1)
                    nc.vector.reciprocal(rn[:, t, :], ss[:, 2, t % 2, :]).then_inc(S["rn_ready"], 1)
                if t >= 1:
                    dve.wait_ge(S["turned_ready"], t)
                    nc.vector.tensor_copy(kT[:, :, (t - 1) * P:t * P], psT[:, 1, :].rearrange("p (j n) -> p j n", n=P)).then_inc(S["k_copied"], 1)


@scoped
def l2_window_attention(nc, sp, K, W, l, Y, qT, kT, V, rn):
    DH, H = 64, 8
    KW = P + 64
    LOW = -3.0e38
    wo = sp.sb("wo", [P, 4, D])
    mask = sp.sb("mask", [P, 2, KW])
    sm = sp.sb("masked_scores", [P, 2, H, KW])
    mx = sp.sb("max", [P, 2, H])
    nb = sp.sb("neg_max", [P, 2, H])
    den = sp.sb("den", [P, 2, H])
    rden = sp.sb("rden", [P, 2, H])
    prob = sp.sb("prob", [P, 2, H, 2 * P])
    probT = sp.sb("probT", [P, 2, 2 * H, P])
    z = sp.sb("z", [P, 2, H, DH])
    zT = sp.sb("zT", [P, 4, P])
    psS = sp.ps("scores", [P, 4, BANK])
    psT = sp.ps("turned", [P, 2, BANK])
    psZ = sp.ps("z", [P, BANK])
    psO = sp.ps("zT_and_out", [P, BANK])
    names = ("loaded mask_ready zeroed qk_done masked max_ready nb_ready exp_done trans_done dve_evac act_evac pv_done rden_ready z_ready "
             "zt_done zt_evac out_done out_added").split()
    S = {n: sp.sem(n) for n in names}
    head = [2 * (m % 4) + m // 4 for m in range(H)]
    with nc.Block() as block:
        @block.sync
        def _(sync):
            sync.dma_start(wo[:, :, :], W["L2_ffn_wo"][bass.ds(l, 1), :, :].rearrange("a (c f) n -> f (a c) n", f=P)).then_inc(S["loaded"], 16)

        @block.gpsimd
        def _(pool):
            nc.gpsimd.memset(mask[:, :, :], 0.0).then_inc(S["zeroed"], 1)
            nc.gpsimd.memset(prob[:, :, :, 0:64], 0.0).then_inc(S["zeroed"], 1)
            pool.wait_ge(S["zeroed"], 2)
            nc.gpsimd.affine_select(out=mask[:, :, :], in_=mask[:, :, :], compare_op=ALU.is_ge, fill=LOW, base=0,
                                    pattern=[[0, 2], [1, KW]], channel_multiplier=-1).then_inc(S["zeroed"], 1)
            pool.wait_ge(S["zeroed"], 3)
            nc.gpsimd.affine_select(out=mask[:, :, :], in_=mask[:, :, :], compare_op=ALU.is_ge, fill=LOW, base=64,
                                    pattern=[[0, 2], [-1, KW]], channel_multiplier=1).then_inc(S["zeroed"], 1)
            pool.wait_ge(S["zeroed"], 4)
            nc.gpsimd.affine_select(out=mask[:, 0, :], in_=mask[:, 0, :], compare_op=ALU.is_ge, fill=LOW, base=-64,
                                    pattern=[[1, KW]], channel_multiplier=0).then_inc(S["mask_ready"], 1)

        @block.tensor
        def _(pe):
            def scores(t):
                if t >= 1:
                    pe.wait_ge(S["masked"], t)
                lo = 64 if t == 0 else 0
                for m in range(H):
                    r = slice((m // 4) * DH, (m // 4) * DH + DH)
                    last = nc.tensor.matmul(psS[:, m // 2, (m % 2) * KW + lo:(m % 2 + 1) * KW], qT[r, m % 4, t * P:(t + 1) * P],
                                            kT[r, m % 4, t * P - 64 + lo:(t + 1) * P], start=True, stop=True)
                last.then_inc(S["qk_done"], 1)

            def trans(t):
                for j in range(4):
                    n = 4 * t + j
                    if n >= 2:
                        pe.wait_ge(S["dve_evac" if n % 2 == 0 else "act_evac"], (n - 2) // 2 + 1)
                    pe.wait_ge(S["exp_done"], H * t + 2 * j + 2)
                    for i in range(4):
                        last = nc.tensor.transpose(psT[:, n % 2, i * P:(i + 1) * P], prob[:, t % 2, 2 * j + i // 2, (i % 2) * P:(i % 2 + 1) * P], K.ident[:, :])
                    last.then_inc(S["trans_done"], 1)

            def pv(t):
                pe.wait_ge(S["dve_evac"], 2 * (t + 1))
                pe.wait_ge(S["act_evac"], 2 * (t + 1))
                if t >= 1:
                    pe.wait_ge(S["z_ready"], t)
                for m in range(H):
                    hs = slice(head[m] * DH, head[m] * DH + DH)
                    if t >= 1:
                        nc.tensor.matmul(psZ[:, hs], probT[:, t % 2, 2 * m, :], V[:, t - 1, hs], start=True, stop=False)
                    last = nc.tensor.matmul(psZ[:, hs], probT[:, t % 2, 2 * m + 1, :], V[:, t, hs], start=(t == 0), stop=True)
                last.then_inc(S["pv_done"], 1)

            def turn_z(t):
                pe.wait_ge(S["z_ready"], t + 1)
                if t >= 1:
                    pe.wait_ge(S["out_added"], t)
                for j in range(4):
                    last = nc.tensor.transpose(psO[:, j * P:(j + 1) * P], z[:, t % 2, 2 * j:2 * j + 2, :].rearrange("p h d -> p (h d)"), K.ident[:, :])
                last.then_inc(S["zt_done"], 1)

            def project(t):
                pe.wait_ge(S["zt_evac"], t + 1)
                for j in range(4):
                    last = nc.tensor.matmul(psO[:, 0:D], zT[:, j, :], wo[:, j, :], start=(j == 0), stop=(j == 3))
                last.then_inc(S["out_done"], 1)

            pe.wait_ge(S["loaded"], 16)
            for s in range(NT + 3):
                if s < NT:
                    scores(s)
                if 0 <= s - 3 < NT:
                    turn_z(s - 3)
                if 0 <= s - 2 < NT:
                    pv(s - 2)
                if 0 <= s - 3 < NT:
                    project(s - 3)
                if 0 <= s - 1 < NT:
                    trans(s - 1)

        def evacuate(eng, t, odd):
            if t >= 2:
                eng.wait_ge(S["pv_done"], t - 1)
            for j in range(odd, 4, 2):
                n = 4 * t + j
                eng.wait_ge(S["trans_done"], n + 1)
                out, src = probT[:, t % 2, 4 * j:4 * j + 4, :].rearrange("p a n -> p (a n)"), psT[:, n % 2, :]
                if odd:
                    nc.scalar.copy(out, src).then_inc(S["act_evac"], 1)
                else:
                    nc.vector.tensor_copy(out, src).then_inc(S["dve_evac"], 1)

        @block.scalar
        def _(act):
            for s in range(NT + 3):
                if s < NT:
                    act.wait_ge(S["nb_ready"], s + 1)
                    if s >= 2:
                        act.wait_ge(S["trans_done"], 4 * (s - 1))
                        act.wait_ge(S["rden_ready"], s - 1)
                    if s < 2:
                        act.wait_ge(S["zeroed"], 2)
                    for m in range(H):
                        nc.scalar.activation(prob[:, s % 2, m, 64:2 * P], sm[:, s % 2, m, :], ACT.Exp, scale=rn[:, s, head[m]:head[m] + 1],
                                             bias=nb[:, s % 2, m:m + 1], accum_out=den[:, s % 2, m:m + 1]).then_inc(S["exp_done"], 1)
                if 0 <= s - 3 < NT:
                    act.wait_ge(S["zt_done"], s - 2)
                    nc.scalar.copy(zT[:, :, :].rearrange("p j n -> p (j n)"), psO[:, :]).then_inc(S["zt_evac"], 1)
                if 0 <= s - 1 < NT:
                    evacuate(act, s - 1, 1)

        @block.vector
        def _(dve):
            dve.wait_ge(S["mask_ready"], 1)
            for s in range(NT + 3):
                if s < NT:
                    dve.wait_ge(S["qk_done"], s + 1)
                    if s >= 2:
                        dve.wait_ge(S["exp_done"], H * (s - 1))
                    smv = sm[:, s % 2, :, :].rearrange("p (b a) k -> p b a k", a=2)
                    lo = 64 if s == 0 else 0
                    if s == 0:
                        nc.vector.tensor_copy(sm[:, 0, :, 0:64], bcast(mask[:, 0:1, 0:64], [P, H, 64]))
                    nc.vector.tensor_tensor(smv[:, :, :, lo:], psS[:, :, 0:2 * KW].rearrange("p b (a k) -> p b a k", a=2)[:, :, :, lo:],
                                            bcast(mask[:, min(s, 1), lo:].unsqueeze(1).unsqueeze(1), [P, 4, 2, KW - lo]), ALU.add).then_inc(S["masked"], 1)
                    dve.wait_ge(S["masked"], s + 1)
                    nc.vector.tensor_reduce(mx[:, s % 2, :], sm[:, s % 2, :, :], axis=AX_X, op=ALU.max).then_inc(S["max_ready"], 1)
                    dve.wait_ge(S["max_ready"], s + 1)
                    nc.vector.scalar_tensor_tensor(out=nb[:, s % 2, :].rearrange("p (o a) -> p o a", o=2), in0=mx[:, s % 2, :].rearrange("p (o a) -> p o a", o=2),
                                                   scalar=-1.0, in1=rn[:, s, 0:H].rearrange("p (a o) -> p o a", o=2), op0=ALU.mult, op1=ALU.mult).then_inc(S["nb_ready"], 1)
                if 0 <= s - 2 < NT:
                    t = s - 2
                    dve.wait_ge(S["exp_done"], H * (t + 1))
                    nc.vector.reciprocal(rden[:, t % 2, :].rearrange("p (a o) -> p o a", o=2), den[:, t % 2, :].rearrange("p (o a) -> p o a", o=2)).then_inc(S["rden_ready"], 1)
                    dve.wait_ge(S["rden_ready"], t + 1)
                    dve.wait_ge(S["pv_done"], t + 1)
                    if t >= 2:
                        dve.wait_ge(S["zt_done"], t - 1)
                    nc.vector.tensor_tensor(z[:, t % 2, :, :], psZ[:, :].rearrange("p (h d) -> p h d", d=DH), bcast(rden[:, t % 2, :].unsqueeze(2), [P, H, DH]),
                                            ALU.mult).then_inc(S["z_ready"], 1)
                if 0 <= s - 1 < NT:
                    evacuate(dve, s - 1, 0)
                if 0 <= s - 3 < NT:
                    t = s - 3
                    dve.wait_ge(S["out_done"], t + 1)
                    nc.vector.tensor_tensor(Y[:, t, :], Y[:, t, :], psO[:, 0:D], ALU.add).then_inc(S["out_added"], 1)


@scoped
def l2_geglu(nc, sp, K, W, l, Y):
    HID = 341
    FC = 3
    rows = [min(P, HID - c * P) for c in range(FC)]
    h = sp.sb("shifted", [P, NT, D])
    hn = sp.sb("normed", [P, NT, D])
    hT = sp.sb("hT", [P, T])
    w1 = sp.sb("w1", [P, 2 * HID])
    w2 = sp.sb("w2", [P, FC, D])
    b1 = sp.sb("b1", [P, 2, FC])
    b2 = sp.sb("b2", [P, D])
    ln = sp.sb("ln", [P, 2])
    g = sp.sb("gelu", [P, 2, BANK])
    hid = sp.sb("hidden", [P, 2, FC, BANK])
    loaded = sp.sem("loaded")
    with nc.Block() as block:
        @block.sync
        def _(sync):
            sync.dma_start(w1[:, :], W["L2_ffn_w1"][bass.ds(l, 1), :, :].rearrange("a d n -> (a d) n")).then_inc(loaded, 16)
            for c in range(FC):
                sync.dma_start(w2[0:rows[c], c, :], W["L2_ffn_w2"][bass.ds(l, 1), c * P:c * P + rows[c], :].rearrange("a f n -> (a f) n")).then_inc(loaded, 16)
            sync.dma_start(b1[:, :, :], W["L2_ffn_b1"][bass.ds(l, 1), :, :, :].rearrange("a p g c -> (a p) g c")).then_inc(loaded, 16)
            sync.dma_start(b2[:, :], W["L2_ffn_b2"][bass.ds(l, 1), :].rearrange("a d -> (a d)").partition_broadcast(P)).then_inc(loaded, 16)
            sync.dma_start(ln[:, :], W["l2_ln"][bass.ds(l, 1), :, :].rearrange("a d g -> (a d) g")).then_inc(loaded, 16)
            sync.wait_ge(loaded, 16 * 7)
    shift_tokens(nc, Y, h)
    layernorm(nc, K, h, hn)
    transpose_tokens(nc, K, hn, hT, ln[:, 0:1], ln[:, 1:2])
    psA = sp.ps("a", [P, 2, BANK])
    psG = sp.ps("g", [P, 2, BANK])
    psY = sp.ps("y", [P, 2, BANK])
    S = {n: sp.sem(n) for n in "ag_ready gelu_done hid_done y_ready b2_added y_added".split()}
    n_items = NB * FC
    with nc.Block() as block:
        @block.tensor
        def _(pe):
            def down(b):
                pe.wait_ge(S["hid_done"], (b + 1) * FC)
                if b >= 2:
                    pe.wait_ge(S["y_added"], b - 1)
                for j in range(TPB):
                    for c in range(FC):
                        last = nc.tensor.matmul(psY[:, b % 2, j * D:(j + 1) * D], hid[0:rows[c], b % 2, c, j * P:(j + 1) * P], w2[0:rows[c], c, :],
                                                start=(c == 0), stop=(c == FC - 1))
                last.then_inc(S["y_ready"], 1)

            for n in range(n_items):
                b, c = n // FC, n % FC
                if n >= 2:
                    pe.wait_ge(S["hid_done"], n - 1)
                for i, ps in enumerate((psA, psG)):
                    last = nc.tensor.matmul(ps[0:rows[c], n % 2, :], w1[:, i * HID + c * P:i * HID + c * P + rows[c]], hT[:, b * BANK:(b + 1) * BANK],
                                            start=True, stop=True)
                last.then_inc(S["ag_ready"], 1)
                if c == 0 and b >= 1:
                    down(b - 1)
            down(NB - 1)

        @block.scalar
        def _(act):
            for n in range(n_items):
                c = n % FC
                act.wait_ge(S["ag_ready"], n + 1)
                if n >= 2:
                    act.wait_ge(S["hid_done"], n - 1)
                nc.scalar.activation(g[0:rows[c], n % 2, :], psG[0:rows[c], n % 2, :], ACT.Gelu, bias=b1[0:rows[c], 1, c:c + 1]).then_inc(S["gelu_done"], 1)

        @block.vector
        def _(dve):
            def add(b):
                yb = Y[:, b * TPB:(b + 1) * TPB, :]
                nc.vector.tensor_tensor(yb, yb, bcast(b2[:, :].unsqueeze(1), [P, TPB, D]), ALU.add).then_inc(S["b2_added"], 1)
                dve.wait_ge(S["b2_added"], b + 1)
                dve.wait_ge(S["y_ready"], b + 1)
                nc.vector.tensor_tensor(yb, yb, psY[:, b % 2, :].rearrange("p (t n) -> p t n", n=D), ALU.add).then_inc(S["y_added"], 1)

            for n in range(n_items):
                b, c = n // FC, n % FC
                dve.wait_ge(S["gelu_done"], n + 1)
                if c == 0 and b >= 2:
                    dve.wait_ge(S["y_ready"], b - 1)
                nc.vector.scalar_tensor_tensor(out=hid[0:rows[c], b % 2, c, :], in0=psA[0:rows[c], n % 2, :], scalar=b1[0:rows[c], 0, c:c + 1],
                                               in1=g[0:rows[c], n % 2, :], op0=ALU.add, op1=ALU.mult).then_inc(S["hid_done"], 1)
                if c == 0 and b >= 1:
                    add(b - 1)
            add(NB - 1)


def l3_mixer(nc, X, K, W):
    DI, NS, NH, HD = 256, 64, 8, 32
    with sublayer(nc) as sp:
        xn = sp.sb("xn", [P, NT, D])
        Yo = sp.sb("mixed", [P, NT, DI])
        with sublayer(nc) as inner:
            xT = inner.sb("xT", [P, T])
            w_in = inner.sb("w_in", [P, 648])
            layernorm(nc, K, X, xn)
            transpose_tokens(nc, K, xn, xT)
            gate = inner.sb("silu_z", [P, NT, DI])
            dt = inner.sb("dt", [P, NT, NH])
            a = inner.sb("log_decay", [P, NT, NH])
            xs = inner.sb("x_tokens", [P, NT, DI])
            Bt = inner.sb("B_tokens", [P, NT, NS])
            BC = inner.sb("BC", [P, T])
            CT = inner.sb("CT", [NS, T])
            l3_gate_dt(nc, K, W, xT, w_in, gate, dt, a, NH)
            with sublayer(nc) as conv:
                xc = [conv.sb(f"x_conv{i}", [P, T]) for i in range(2)] + [BC]
                l3_conv(nc, K, W, xT, w_in, xc)
                l3_turn(nc, K, xc, xs, Bt, CT)
            l3_scan(nc, K, W, dt, a, xs, Bt, BC, CT, Yo, NS, NH, HD)
            with nc.Block() as block:
                @block.vector
                def _(dve):
                    nc.vector.tensor_tensor(Yo[:, 0:NT // 2, :], Yo[:, 0:NT // 2, :], gate[:, 0:NT // 2, :], ALU.mult)

                @block.gpsimd
                def _(pool):
                    nc.gpsimd.tensor_tensor(Yo[:, NT // 2:, :], Yo[:, NT // 2:, :], gate[:, NT // 2:, :], ALU.mult)
        Z = sp.sb("squashed", [P, NT, D])
        l3_out(nc, K, W, Yo, Z)
        rows = sp.sb("b_nl", [P, D])
        loaded = sp.sem("b_loaded")
        added = sp.sem("x_added")
        with nc.Block() as block:
            @block.sync
            def _(sync):
                sync.dma_start(rows[:, :], W["L3_attn_b_nl"].partition_broadcast(P)).then_inc(loaded, 16)

            @block.vector
            def _(dve):
                nc.vector.tensor_tensor(X[:, :, :], X[:, :, :], xn[:, :, :], ALU.add).then_inc(added, 1)
                dve.wait_ge(added, 1)
                dve.wait_ge(loaded, 16)
                nc.vector.tensor_tensor(X[:, :, :], X[:, :, :], bcast(rows[:, :].unsqueeze(1), [P, NT, D]), ALU.add)
        project_add(nc, K, Z, W["L3_attn_W_nl"], X)


@scoped
def l3_gate_dt(nc, sp, K, W, xT, w_in, gate, dt, a, NH):
    SERIES = [1.0 / (2 * i + 1) for i in range(8)]
    rows = sp.sb("bias_and_alog", [P, 2, NH])
    nexpA = sp.sb("exp_A_log", [P, NH])
    N = NT * NH
    d = {n: sp.sb(n, [P, N]) for n in "raw absd u den rden z z2 acc lin pos".split()}
    sig = sp.sb("sigmoid", [P, 2, 2, 256])
    psZ = sp.ps("z", [P, 2, BANK])
    psD = sp.ps("dt", [P, BANK])
    S = {n: sp.sem(n) for n in "loaded z_ready sig_done gate_done d_ready raw_ready abs_done u_done expA_done step".split()}
    with nc.Block() as block:
        @block.sync
        def _(sync):
            sync.dma_start(w_in[:, :], W["L3_attn_W_in"]).then_inc(S["loaded"], 16)
            sync.dma_start(rows[:, 0, :], W["L3_attn_dt_bias"].partition_broadcast(P)).then_inc(S["loaded"], 16)
            sync.dma_start(rows[:, 1, :], W["L3_attn_A_log"].partition_broadcast(P)).then_inc(S["loaded"], 16)

        @block.tensor
        def _(pe):
            pe.wait_ge(S["loaded"], 48)
            for t in range(NT):
                last = nc.tensor.matmul(psD[:, t * NH:(t + 1) * NH], xT[:, t * P:(t + 1) * P], w_in[:, 640:648], start=True, stop=True)
            last.then_inc(S["d_ready"], 1)
            for n in range(NT // 2):
                if n >= 2:
                    pe.wait_ge(S["gate_done"], n - 1)
                for j in range(2):
                    t = 2 * n + j
                    last = nc.tensor.matmul(psZ[:, n % 2, j * 256:(j + 1) * 256], xT[:, t * P:(t + 1) * P], w_in[:, 0:256], start=True, stop=True)
                last.then_inc(S["z_ready"], 1)

        @block.scalar
        def _(act):
            act.wait_ge(S["loaded"], 48)
            nc.scalar.activation(nexpA[:, :], rows[:, 1, :], ACT.Exp).then_inc(S["expA_done"], 1)
            act.wait_ge(S["raw_ready"], 1)
            nc.scalar.activation(d["absd"][:, :], d["raw"][:, :], ACT.Abs).then_inc(S["abs_done"], 1)
            act.wait_ge(S["abs_done"], 1)
            nc.scalar.activation(d["u"][:, :], d["absd"][:, :], ACT.Exp, scale=-1.0).then_inc(S["u_done"], 1)
            for n in range(NT // 2):
                act.wait_ge(S["z_ready"], n + 1)
                if n >= 2:
                    act.wait_ge(S["gate_done"], n - 1)
                nc.scalar.activation(sig[:, n % 2, :, :].rearrange("p t n -> p (t n)"), psZ[:, n % 2, :], ACT.Sigmoid).then_inc(S["sig_done"], 1)

        @block.vector
        def _(dve):
            steps = [0]

            def done(ins):
                steps[0] += 1
                ins.then_inc(S["step"], 1)
                dve.wait_ge(S["step"], steps[0])

            V = nc.vector
            dve.wait_ge(S["d_ready"], 1)
            dve.wait_ge(S["loaded"], 48)
            V.tensor_tensor(d["raw"][:, :].rearrange("p (t h) -> p t h", h=NH), psD[:, 0:N].rearrange("p (t h) -> p t h", h=NH),
                            bcast(rows[:, 0:1, :], [P, NT, NH]), ALU.add).then_inc(S["raw_ready"], 1)
            dve.wait_ge(S["u_done"], 1)
            done(V.tensor_scalar(d["den"][:, :], d["u"][:, :], 2.0, None, ALU.add))
            done(V.reciprocal(d["rden"][:, :], d["den"][:, :]))
            done(V.tensor_tensor(d["z"][:, :], d["u"][:, :], d["rden"][:, :], ALU.mult))
            done(V.tensor_tensor(d["z2"][:, :], d["z"][:, :], d["z"][:, :], ALU.mult))
            done(V.tensor_scalar(d["acc"][:, :], d["z2"][:, :], SERIES[7], SERIES[6], ALU.mult, ALU.add))
            for c in SERIES[5::-1]:
                done(V.tensor_tensor(d["lin"][:, :], d["acc"][:, :], d["z2"][:, :], ALU.mult))
                done(V.tensor_scalar(d["acc"][:, :], d["lin"][:, :], c, None, ALU.add))
            done(V.scalar_tensor_tensor(out=d["lin"][:, :], in0=d["acc"][:, :], scalar=2.0, in1=d["z"][:, :], op0=ALU.mult, op1=ALU.mult))
            done(V.tensor_scalar(d["pos"][:, :], d["raw"][:, :], 0.0, None, ALU.max))
            flat = dt[:, :, :].rearrange("p t h -> p (t h)")
            done(V.tensor_tensor(flat, d["pos"][:, :], d["lin"][:, :], ALU.add))
            dve.wait_ge(S["expA_done"], 1)
            V.scalar_tensor_tensor(out=a[:, :, :], in0=dt[:, :, :], scalar=-1.0, in1=bcast(nexpA[:, :].unsqueeze(1), [P, NT, NH]), op0=ALU.mult, op1=ALU.mult)
            for n in range(NT // 2):
                dve.wait_ge(S["sig_done"], n + 1)
                V.tensor_tensor(gate[:, 2 * n:2 * n + 2, :].rearrange("p t n -> p (t n)"), sig[:, n % 2, :, :].rearrange("p t n -> p (t n)"), psZ[:, n % 2, :],
                                ALU.mult).then_inc(S["gate_done"], 1)


@scoped
def l3_conv(nc, sp, K, W, xT, w_in, xc):
    TAPS = 16
    PAD = TAPS - 1
    cw = sp.sb("conv_w", [P, 3, TAPS])
    cb = sp.sb("conv_b", [P, 3])
    diag = sp.sb("tap_diagonals", [P, 2, TAPS, P])
    xp = [sp.sb(f"padded{c}", [P, PAD + T]) for c in range(3)]
    acc = sp.sb("acc", [P, 2, T])
    sig = sp.sb("sigmoid", [P, 2, BANK])
    sig2 = acc[:, TAPS % 2, :]
    psP = sp.ps("proj", [P, 4, BANK])
    psC = sp.ps("conv", [P, 4, BANK])
    S = {n: sp.sem(n) for n in "loaded padded proj_ready act_copied dve_copied diag_ready conv_ready sig_done silu_done tap bc_sig".split()}
    order = [2, 0, 1]
    with nc.Block() as block:
        @block.sync
        def _(sync):
            sync.dma_start(cw[:, :, :], W["L3_attn_conv_w"].rearrange("(c p) k -> p c k", p=P)).then_inc(S["loaded"], 16)
            sync.dma_start(cb[:, :], W["L3_attn_conv_b"]).then_inc(S["loaded"], 16)

        @block.tensor
        def _(pe):
            for n in range(3 * NB):
                c, b = order[n // NB], n % NB
                if n >= 4:
                    pe.wait_ge(S["act_copied"], n - 3)
                nc.tensor.matmul(psP[:, n % 4, :], w_in[:, 256 + c * P:256 + (c + 1) * P], xT[:, b * BANK:(b + 1) * BANK], start=True, stop=True).then_inc(S["proj_ready"], 1)
            for n in range(2 * NB):
                c, b = n // NB, n % NB
                pe.wait_ge(S["act_copied"], NB + n + 1)
                pe.wait_ge(S["diag_ready"], TAPS * (c + 1))
                if n >= 4:
                    pe.wait_ge(S["silu_done"], n - 3)
                for k in range(TAPS):
                    last = nc.tensor.matmul(psC[:, n % 4, :], diag[:, c, k, :], xp[c][:, k + b * BANK:k + (b + 1) * BANK], start=(k == 0), stop=(k == TAPS - 1))
                last.then_inc(S["conv_ready"], 1)

        @block.gpsimd
        def _(pool):
            for c in range(3):
                last = nc.gpsimd.memset(xp[c][:, 0:PAD], 0.0)
            last.then_inc(S["padded"], 1)
            pool.wait_ge(S["loaded"], 32)
            for c in range(2):
                for k in range(TAPS):
                    nc.gpsimd.tensor_scalar(diag[:, c, k, :], K.ident[:, :], cw[:, c, k:k + 1], 1.0, ALU.mult, ALU.mult).then_inc(S["diag_ready"], 1)

        @block.scalar
        def _(act):
            act.wait_ge(S["padded"], 1)
            for n in range(3 * NB):
                c, b = order[n // NB], n % NB
                act.wait_ge(S["proj_ready"], n + 1)
                nc.scalar.copy(xp[c][:, PAD + b * BANK:PAD + (b + 1) * BANK], psP[:, n % 4, :]).then_inc(S["act_copied"], 1)
            act.wait_ge(S["loaded"], 32)
            for n in range(2 * NB):
                act.wait_ge(S["conv_ready"], n + 1)
                if n >= 2:
                    act.wait_ge(S["silu_done"], n - 1)
                if n == 4:
                    act.wait_ge(S["tap"], TAPS)
                    nc.scalar.activation(sig2, acc[:, (TAPS - 1) % 2, :], ACT.Sigmoid, bias=cb[:, 2:3]).then_inc(S["bc_sig"], 1)
                nc.scalar.activation(sig[:, n % 2, :], psC[:, n % 4, :], ACT.Sigmoid, bias=cb[:, n // NB:n // NB + 1]).then_inc(S["sig_done"], 1)

        @block.vector
        def _(dve):
            dve.wait_ge(S["loaded"], 32)
            dve.wait_ge(S["act_copied"], NB)
            for k in range(TAPS):
                src = xp[2][:, k:k + T]
                if k == 0:
                    nc.vector.tensor_scalar(acc[:, 0, :], src, cw[:, 2, 0:1], None, ALU.mult).then_inc(S["tap"], 1)
                else:
                    dve.wait_ge(S["tap"], k)
                    nc.vector.scalar_tensor_tensor(out=acc[:, k % 2, :], in0=src, scalar=cw[:, 2, k:k + 1], in1=acc[:, (k - 1) % 2, :],
                                                   op0=ALU.mult, op1=ALU.add).then_inc(S["tap"], 1)
            for n in range(2 * NB):
                c, b = n // NB, n % NB
                dve.wait_ge(S["sig_done"], n + 1)
                nc.vector.scalar_tensor_tensor(out=xc[c][:, b * BANK:(b + 1) * BANK], in0=psC[:, n % 4, :], scalar=cb[:, c:c + 1], in1=sig[:, n % 2, :],
                                               op0=ALU.add, op1=ALU.mult).then_inc(S["silu_done"], 1)
            dve.wait_ge(S["bc_sig"], 1)
            nc.vector.scalar_tensor_tensor(out=xc[2][:, :], in0=acc[:, (TAPS - 1) % 2, :], scalar=cb[:, 2:3], in1=sig2, op0=ALU.add, op1=ALU.mult)


@scoped
def l3_turn(nc, sp, K, xc, xs, Bt, CT):
    NS = 64
    ps = sp.ps("turned", [P, 2, BANK])
    S = {n: sp.sem(n) for n in "c_moved turned copied".split()}
    with nc.Block() as block:
        @block.sync
        def _(sync):
            sync.dma_start(CT[:, :], xc[2][NS:P, :]).then_inc(S["c_moved"], 16)
            sync.wait_ge(S["c_moved"], 16)

        @block.tensor
        def _(pe):
            for t in range(NT):
                if t >= 2:
                    pe.wait_ge(S["copied"], 2 * (t - 1))
                for c in range(3):
                    last = nc.tensor.transpose(ps[:, t % 2, c * P:(c + 1) * P], xc[c][:, t * P:(t + 1) * P], K.ident[:, :])
                last.then_inc(S["turned"], 1)

        @block.vector
        def _(dve):
            for t in range(NT):
                dve.wait_ge(S["turned"], t + 1)
                nc.vector.tensor_copy(xs[:, t, :], ps[:, t % 2, 0:256]).then_inc(S["copied"], 1)
                nc.vector.tensor_copy(Bt[:, t, :], ps[:, t % 2, 256:256 + NS]).then_inc(S["copied"], 1)


@scoped
def l3_scan(nc, sp, K, W, dt, a, xs, Bt, BC, CT, Y, NS, NH, HD):
    DI = NH * HD
    after = sp.sb("after", [P, P])
    drow = sp.sb("D", [P, NH])
    state = sp.sb("state", [NS, 2, DI])
    decayed = sp.sb("state_decayed", [NS, DI])
    aU = sp.sb("a_upto", [P, 2, NH, P])
    E = sp.sb("decays", [P, 2, NH, P])
    MT = sp.sb("mixing", [P, 2, NH, P])
    Gm = sp.sb("CB_masked", [P, 2, P])
    ecum = sp.sb("decay_from_start", [P, 2, NH])
    edec = sp.sb("chunk_decay", [NS, 2, NH])
    xdt = sp.sb("x_dt", [P, 2, DI])
    xw = sp.sb("x_dt_to_end", [P, 2, DI])
    off = sp.sb("from_state", [P, 2, DI])
    psE = sp.ps("sums_between", [P, 2, 2, BANK])
    psG = sp.ps("CB_and_sums", [P, BANK])
    psD = sp.ps("within", [P, BANK])
    psO = sp.ps("from_state", [P, BANK])
    psS = sp.ps("state", [P, BANK])
    names = ("loaded after_ready aU_ready xdt_ready skip_ready seg_ready g_ready e_done small_exp gm_ready mt_ready xw_ready within_ready off_ready "
             "state_ready off_scaled off_added within_added decayed updated").split()
    S = {n: sp.sem(n) for n in names}
    heads = "p (h d) -> p h d"
    with nc.Block() as block:
        @block.sync
        def _(sync):
            sync.dma_start(drow[:, :], W["L3_attn_D"].partition_broadcast(P)).then_inc(S["loaded"], 16)
            sync.dma_start(state[:, 0, :], W["L3_attn_init_states"]).then_inc(S["loaded"], 16)

        @block.gpsimd
        def _(pool):
            nc.gpsimd.affine_select(out=after[:, :], in_=K.ones[:, :], compare_op=ALU.is_gt, fill=0.0, base=0, pattern=[[-1, P]],
                                    channel_multiplier=1).then_inc(S["after_ready"], 1)
            pool.wait_ge(S["loaded"], 32)
            for q in range(NT):
                if q >= 2:
                    pool.wait_ge(S["seg_ready"], q - 1)
                nc.gpsimd.tensor_tensor(aU[:, q % 2, :, :], bcast(K.causal_k[:, :].unsqueeze(1), [P, NH, P]), bcast(a[:, q, :].unsqueeze(2), [P, NH, P]),
                                        ALU.mult).then_inc(S["aU_ready"], 1)
                if q >= 2:
                    pool.wait_ge(S["within_ready"], q - 1)
                    pool.wait_ge(S["xw_ready"], q - 1)
                nc.gpsimd.tensor_tensor(xdt[:, q % 2, :].rearrange(heads, h=NH), xs[:, q, :].rearrange(heads, h=NH), bcast(dt[:, q, :].unsqueeze(2), [P, NH, HD]),
                                        ALU.mult).then_inc(S["xdt_ready"], 1)
                nc.gpsimd.tensor_tensor(Y[:, q, :].rearrange(heads, h=NH), xs[:, q, :].rearrange(heads, h=NH), bcast(drow[:, :].unsqueeze(2), [P, NH, HD]),
                                        ALU.mult).then_inc(S["skip_ready"], 1)

        @block.tensor
        def _(pe):
            pe.wait_ge(S["after_ready"], 1)
            pe.wait_ge(S["loaded"], 32)

            def sums(q):
                pe.wait_ge(S["aU_ready"], q + 1)
                if q >= 2:
                    pe.wait_ge(S["e_done"], q - 1)
                for i in range(2):
                    last = nc.tensor.matmul(psE[:, q % 2, i, :], after[:, :], aU[:, q % 2, 4 * i:4 * i + 4, :].rearrange("p h t -> p (h t)"), start=True, stop=True)
                last.then_inc(S["seg_ready"], 1)
                if q >= 1:
                    pe.wait_ge(S["gm_ready"], q)
                    pe.wait_ge(S["small_exp"], 2 * q)
                cols = slice(q * P, (q + 1) * P)
                nc.tensor.matmul(psG[:, 0:P], BC[0:NS, cols], CT[:, cols], start=True, stop=True)
                nc.tensor.matmul(psG[:, P:P + NH], K.causal_k[:, :], a[:, q, :], start=True, stop=True)
                nc.tensor.matmul(psG[0:NS, P + 16:P + 16 + NH], K.ones[:, 0:NS], a[:, q, :], start=True, stop=True).then_inc(S["g_ready"], 1)

            def outputs(q):
                cols = slice(q * P, (q + 1) * P)
                if q >= 1:
                    pe.wait_ge(S["updated"], q)
                    pe.wait_ge(S["off_scaled"], q)
                nc.tensor.matmul(psO[:, 0:DI], CT[:, cols], state[:, q % 2, :], start=True, stop=True).then_inc(S["off_ready"], 1)
                pe.wait_ge(S["xw_ready"], q + 1)
                nc.tensor.matmul(psS[0:NS, 0:DI], Bt[:, q, :], xw[:, q % 2, :], start=True, stop=True).then_inc(S["state_ready"], 1)
                pe.wait_ge(S["mt_ready"], q + 1)
                if q >= 1:
                    pe.wait_ge(S["within_added"], q)
                for h in range(NH):
                    last = nc.tensor.matmul(psD[:, h * HD:(h + 1) * HD], MT[:, q % 2, h, :], xdt[:, q % 2, h * HD:(h + 1) * HD], start=True, stop=True)
                last.then_inc(S["within_ready"], 1)

            for s in range(NT + 1):
                if s < NT:
                    sums(s)
                if s >= 1:
                    outputs(s - 1)

        @block.scalar
        def _(act):
            for q in range(NT):
                act.wait_ge(S["seg_ready"], q + 1)
                if q >= 2:
                    act.wait_ge(S["mt_ready"], q - 1)
                    act.wait_ge(S["xw_ready"], q - 1)
                nc.scalar.activation(E[:, q % 2, :, :].rearrange("p h t -> p (h t)"), psE[:, q % 2, :, :].rearrange("p i n -> p (i n)"), ACT.Exp).then_inc(S["e_done"], 1)
                act.wait_ge(S["g_ready"], q + 1)
                act.wait_ge(S["gm_ready"], q + 1)
                if q >= 2:
                    act.wait_ge(S["off_scaled"], q - 1)
                    act.wait_ge(S["decayed"], q - 1)
                nc.scalar.activation(ecum[:, q % 2, :], psG[:, P:P + NH], ACT.Exp).then_inc(S["small_exp"], 1)
                nc.scalar.activation(edec[:, q % 2, :], psG[0:NS, P + 16:P + 16 + NH], ACT.Exp).then_inc(S["small_exp"], 1)

        @block.vector
        def _(dve):
            for q in range(NT):
                dve.wait_ge(S["g_ready"], q + 1)
                nc.vector.tensor_tensor(Gm[:, q % 2, :], psG[:, 0:P], K.causal_k[:, :], ALU.mult).then_inc(S["gm_ready"], 1)
                dve.wait_ge(S["e_done"], q + 1)
                dve.wait_ge(S["xdt_ready"], q + 1)
                nc.vector.tensor_tensor(xw[:, q % 2, :].rearrange(heads, h=NH), xdt[:, q % 2, :].rearrange(heads, h=NH),
                                        bcast(E[:, q % 2, :, P - 1:P], [P, NH, HD]), ALU.mult).then_inc(S["xw_ready"], 1)
                dve.wait_ge(S["gm_ready"], q + 1)
                if q >= 2:
                    dve.wait_ge(S["within_ready"], q - 1)
                nc.vector.tensor_tensor(MT[:, q % 2, :, :], E[:, q % 2, :, :], bcast(Gm[:, q % 2, :].unsqueeze(1), [P, NH, P]), ALU.mult).then_inc(S["mt_ready"], 1)
                dve.wait_ge(S["small_exp"], 2 * (q + 1))
                nc.vector.tensor_tensor(decayed[:, :].rearrange(heads, h=NH), state[:, q % 2, :].rearrange(heads, h=NH),
                                        bcast(edec[:, q % 2, :].unsqueeze(2), [NS, NH, HD]), ALU.mult).then_inc(S["decayed"], 1)
                dve.wait_ge(S["decayed"], q + 1)
                dve.wait_ge(S["state_ready"], q + 1)
                nc.vector.tensor_tensor(state[:, (q + 1) % 2, :], decayed[:, :], psS[0:NS, 0:DI], ALU.add).then_inc(S["updated"], 1)
                dve.wait_ge(S["off_ready"], q + 1)
                nc.vector.tensor_tensor(off[:, q % 2, :].rearrange(heads, h=NH), psO[:, 0:DI].rearrange(heads, h=NH),
                                        bcast(ecum[:, q % 2, :].unsqueeze(2), [P, NH, HD]), ALU.mult).then_inc(S["off_scaled"], 1)
                dve.wait_ge(S["off_scaled"], q + 1)
                dve.wait_ge(S["skip_ready"], q + 1)
                nc.vector.tensor_tensor(Y[:, q, :], Y[:, q, :], off[:, q % 2, :], ALU.add).then_inc(S["off_added"], 1)
                dve.wait_ge(S["off_added"], q + 1)
                dve.wait_ge(S["within_ready"], q + 1)
                nc.vector.tensor_tensor(Y[:, q, :], Y[:, q, :], psD[:, 0:DI], ALU.add).then_inc(S["within_added"], 1)


@scoped
def l3_out(nc, sp, K, W, Y, Z):
    DI = 256
    wo = sp.sb("w_out", [P, 2, D])
    nw = sp.sb("norm_w", [P, 2])
    sq = sp.sb("squares", [P, 2, DI])
    ms = sp.sb("mean_square", [P, 3, NT])
    yT = sp.sb("yT", [P, 2, 2, P])
    y = sp.sb("y", [P, NT, D])
    q = sp.sb("y_squares", [P, NT * D])
    root = sp.sb("root", [P, NT * D])
    psT = sp.ps("turned", [P, 2, BANK])
    psY = sp.ps("y", [P, 2, BANK])
    S = {n: sp.sem(n) for n in "loaded ms_ready root_ready r_ready turned copied y_ready y_scaled sq_done sqrt_done recip_done".split()}
    with nc.Block() as block:
        @block.sync
        def _(sync):
            sync.dma_start(wo[:, :, :], W["L3_attn_W_out"].rearrange("(c f) n -> f c n", f=P)).then_inc(S["loaded"], 16)
            sync.dma_start(nw[:, :], W["L3_attn_norm_w"]).then_inc(S["loaded"], 16)

        @block.tensor
        def _(pe):
            pe.wait_ge(S["loaded"], 32)

            def out(t):
                pe.wait_ge(S["copied"], 2 * (t + 1))
                if t >= 2:
                    pe.wait_ge(S["y_scaled"], t - 1)
                for c in range(2):
                    last = nc.tensor.matmul(psY[:, t % 2, 0:D], yT[:, t % 2, c, :], wo[:, c, :], start=(c == 0), stop=(c == 1))
                last.then_inc(S["y_ready"], 1)

            for t in range(NT):
                if t >= 2:
                    pe.wait_ge(S["copied"], 2 * (t - 1))
                for c in range(2):
                    last = nc.tensor.transpose(psT[:, t % 2, c * P:(c + 1) * P], Y[:, t, c * P:(c + 1) * P], K.ident[:, :])
                last.then_inc(S["turned"], 1)
                if t >= 1:
                    out(t - 1)
            out(NT - 1)

        @block.scalar
        def _(act):
            for t in range(NT):
                if t >= 2:
                    act.wait_ge(S["ms_ready"], t - 1)
                nc.scalar.activation(sq[:, t % 2, :], Y[:, t, :], ACT.Square, accum_out=ms[:, 0, t:t + 1]).then_inc(S["ms_ready"], 1)
            act.wait_ge(S["ms_ready"], NT)
            nc.scalar.activation(ms[:, 1, :], ms[:, 0, :], ACT.Sqrt, scale=1.0 / DI, bias=K.eps[:, 0:1]).then_inc(S["root_ready"], 1)
            act.wait_ge(S["r_ready"], 1)
            for t in range(NT):
                act.wait_ge(S["y_ready"], t + 1)
                nc.scalar.activation(y[:, t, :], psY[:, t % 2, 0:D], ACT.Copy, scale=ms[:, 2, t:t + 1]).then_inc(S["y_scaled"], 1)
            act.wait_ge(S["y_scaled"], NT)
            nc.scalar.activation(q[:, :], y[:, :, :].rearrange("p t n -> p (t n)"), ACT.Square).then_inc(S["sq_done"], 1)
            act.wait_ge(S["sq_done"], 1)
            nc.scalar.activation(root[:, :], q[:, :], ACT.Sqrt, bias=K.ones[:, 0:1]).then_inc(S["sqrt_done"], 1)

        @block.vector
        def _(dve):
            dve.wait_ge(S["root_ready"], 1)
            nc.vector.reciprocal(ms[:, 2, :], ms[:, 1, :]).then_inc(S["r_ready"], 1)
            dve.wait_ge(S["loaded"], 32)
            for t in range(NT):
                dve.wait_ge(S["turned"], t + 1)
                if t >= 2:
                    dve.wait_ge(S["y_ready"], t - 1)
                for c in range(2):
                    nc.vector.tensor_scalar(yT[:, t % 2, c, :], psT[:, t % 2, c * P:(c + 1) * P], nw[:, c:c + 1], None, ALU.mult).then_inc(S["copied"], 1)
            dve.wait_ge(S["sqrt_done"], 1)
            nc.vector.reciprocal(q[:, :], root[:, :]).then_inc(S["recip_done"], 1)
            dve.wait_ge(S["recip_done"], 1)
            nc.vector.tensor_tensor(Z[:, :, :].rearrange("p t n -> p (t n)"), y[:, :, :].rearrange("p t n -> p (t n)"), q[:, :], ALU.mult)


def by_tile(a):
    return a.reshape(NT, P, -1).transpose(1, 0, 2)


def shape_constants():
    f = np.float32
    pos = np.arange(T, dtype=f)
    inv = f(1.0) / f(10000.0) ** (np.arange(4, dtype=f) / f(4))
    ang = pos[:, None] * inv[None, :]
    rope8 = np.stack([by_tile(np.cos(ang)), by_tile(np.sin(ang))], axis=1)
    rsqrt_t = by_tile(f(1) / np.sqrt(np.arange(1, T + 1, dtype=f)))[:, :, 0]
    half = np.arange(0, 64, 2, dtype=f)
    fr = pos[:, None] * (f(1.0) / f(10000.0) ** (half / f(64)))[None, :]
    base = (half + f(0.4 * 64)) / f(1.4 * 64)
    scale = base[None, :] ** ((pos - f(T // 2)) / f(32))[:, None]
    fr, scale = np.concatenate([fr, fr], 1), np.concatenate([scale, scale], 1)
    sign = np.concatenate([-np.ones(32, f), np.ones(32, f)])
    tabs = [np.stack([by_tile(x * scale * f(8)), by_tile(x / scale)], axis=2) for x in (np.cos(fr), np.sin(fr) * sign)]
    xpos = np.ascontiguousarray(np.stack(tabs, axis=1), dtype=f)
    return {"xpos": xpos, "rope8": np.ascontiguousarray(rope8, dtype=f), "rsqrt_t": np.ascontiguousarray(rsqrt_t)}


LAYOUT = {
    "L0_attn_b_Q": lambda a: a.reshape(8, P).T,
    "L0_attn_b_K": lambda a: a.reshape(8, P).T,
    "L0_ffn_keys": lambda a: a.transpose(2, 0, 3, 1).reshape(16, 128, 32),
    "L0_ffn_bn_gamma": lambda a: a.reshape(16, P).T,
    "L0_ffn_bn_beta": lambda a: a.reshape(16, P).T,
    "L0_ffn_down_embed": lambda a: a.T,
    "L2_attn_gate": lambda a: np.repeat(a, 64, axis=0).reshape(8, P, 2).transpose(1, 2, 0),
    "L2_attn_freqs": lambda a: a.reshape(8, P).T,
    "L3_attn_conv_b": lambda a: a.reshape(3, P).T,
    "L3_attn_norm_w": lambda a: a.reshape(2, P).T,
    "L3_attn_init_states": lambda a: a.reshape(256, 64).T,
    "L2_ffn_b1": lambda a: np.concatenate([a.reshape(2, 2, 341), np.zeros((2, 2, 43), a.dtype)], axis=2).reshape(2, 2, 3, P).transpose(0, 3, 1, 2),
    "L3_ffn_b1": lambda a: a.reshape(8, 4, P).transpose(2, 1, 0),
    "L3_ffn_b2": lambda a: np.concatenate([a, np.zeros((D - 8, D), a.dtype)]),
}

SUBLAYERS = [l0_attention, l0_experts, l1_attention, l1_experts, l2_attention, l2_transformer, l3_mixer, l3_experts]


class Constants:
    pass


def sem_range(S):
    nums = sorted(s.num for s in S.values())
    assert nums[-1] - nums[0] == len(nums) - 1
    return range(nums[0], nums[-1] + 1)


def build_constants(nc, ctx):
    K = Constants()
    K.ident = ctx.enter_context(nc.sbuf_tensor("ident", [P, P], F32))
    K.ones = ctx.enter_context(nc.sbuf_tensor("ones", [P, P], F32))
    K.causal_q = ctx.enter_context(nc.sbuf_tensor("causal_q", [P, P], F32))
    K.causal_k = ctx.enter_context(nc.sbuf_tensor("causal_k", [P, P], F32))
    K.eps = ctx.enter_context(nc.sbuf_tensor("eps", [P, 1], F32))
    filled = nc.alloc_semaphore("constants_filled")
    with nc.Block() as block:
        @block.gpsimd
        def _(pool):
            nc.gpsimd.memset(K.ident[:, :], 0.0).then_inc(filled, 1)
            nc.gpsimd.memset(K.ones[:, :], 1.0).then_inc(filled, 1)
            nc.gpsimd.memset(K.eps[:, :], LN_EPS).then_inc(filled, 1)
            pool.wait_ge(filled, 3)
            nc.gpsimd.affine_select(out=K.ident[:, :], in_=K.ident[:, :], compare_op=ALU.not_equal, fill=1.0, base=0,
                                    pattern=[[-1, P]], channel_multiplier=1)
            nc.gpsimd.affine_select(out=K.causal_q[:, :], in_=K.ones[:, :], compare_op=ALU.is_ge, fill=0.0, base=0,
                                    pattern=[[-1, P]], channel_multiplier=1)
            nc.gpsimd.affine_select(out=K.causal_k[:, :], in_=K.ones[:, :], compare_op=ALU.is_ge, fill=0.0, base=0,
                                    pattern=[[1, P]], channel_multiplier=-1)
    return K


def program(nc, W, out):
    with ExitStack() as ctx:
        X = ctx.enter_context(nc.sbuf_tensor("X", [P, NT, D], F32))
        K = build_constants(nc, ctx)
        x_moved = nc.alloc_semaphore("x_moved")
        with nc.Block() as block:
            @block.sync
            def _(sync):
                sync.dma_start(X[:, :, :], W["L0_attn_resid_pre"].rearrange("b (t p) d -> p (b t) d", p=P)).then_inc(x_moved, 16)
                sync.wait_ge(x_moved, 16)
        for stage in SUBLAYERS[STAGES[0]:STAGES[1]]:
            stage(nc, X, K, W)
        with nc.Block() as block:
            @block.sync
            def _(sync):
                sync.dma_start(out.rearrange("b (t p) d -> p (b t) d", p=P), X[:, :, :]).then_inc(x_moved, 16)
                sync.wait_ge(x_moved, 32)


def kernel(**inputs):
    import concourse.bacc as _bacc
    from concourse.bass_utils import run_bass_kernel_spmd as _run

    nc = _bacc.Bacc("TRN2", target_bir_lowering=False, num_devices=1)
    arrays, W = {}, {}
    for name in list(inputs):
        a = np.ascontiguousarray(LAYOUT[name](np.asarray(inputs[name])) if name in LAYOUT else inputs[name])
        arrays[f"in_{name}"] = a
        W[name] = nc.dram_tensor(f"in_{name}", a.shape, mybir.dt.from_np(a.dtype), kind="ExternalInput").ap()
    for name, a in shape_constants().items():
        arrays[f"const_{name}"] = a
        W[name] = nc.dram_tensor(f"const_{name}", a.shape, mybir.dt.from_np(a.dtype), kind="ExternalInput").ap()
    ln = np.ascontiguousarray(np.stack([inputs["L2_ffn_ln_g"], inputs["L2_ffn_ln_b"]], axis=2))
    arrays["in_l2_ln"] = ln
    W["l2_ln"] = nc.dram_tensor("in_l2_ln", ln.shape, F32, kind="ExternalInput").ap()
    out = nc.dram_tensor("out_0", (1, T, D), F32, kind="ExternalOutput").ap()
    program(nc, W, out)
    r = _run(nc, [arrays], core_ids=[0])
    return r.results[0]["out_0"]
```

```python
import itertools
from contextlib import ExitStack, contextmanager

import concourse.bass as bass
import concourse.mybir as mybir
import numpy as np

F32 = mybir.dt.float32
BF16 = mybir.dt.bfloat16
I32 = mybir.dt.int32
U32 = mybir.dt.uint32
ALU = mybir.AluOpType
ACT = mybir.ActivationFunctionType
AX_X = mybir.AxisListType.X

STAGES = (0, 8)

P = 128
T = 2048
NT = T // P
D = 128
BANK = 512
NB = T // BANK
TPB = BANK // P
LN_EPS = 1e-5
COUNT = itertools.count()


def bcast(ap, shape):
    return ap.broadcast_to(shape)


@contextmanager
def sublayer(nc):
    sems = []
    with ExitStack() as ctx:
        class Space:
            def sb(self, name, shape, dt=F32):
                return ctx.enter_context(nc.sbuf_tensor(f"{name}_{next(COUNT)}", shape, dt))

            def ps(self, name, shape, dt=F32):
                return ctx.enter_context(nc.psum_tensor(f"{name}_{next(COUNT)}", shape, dt))

            def sem(self, name):
                s = nc.alloc_semaphore(f"{name}_{next(COUNT)}")
                sems.append(s)
                return s
        yield Space()
    nc.clear_and_free_semaphores(sems)
    nc.all_engine_barrier()


def scoped(f):
    def run(nc, *args):
        with sublayer(nc) as sp:
            f(nc, sp, *args)
    return run


@scoped
def layernorm(nc, sp, K, src, dst):
    stats = sp.sb("ln_stats", [P, NT, 6])
    moments = sp.sb("ln_moments", [P, NT, 2])
    std = sp.sb("ln_std", [P, NT])
    rstd = sp.sb("ln_rstd", [P, NT])
    stats_ready = sp.sem("ln_stats_ready")
    moments_ready = sp.sem("ln_moments_ready")
    std_ready = sp.sem("ln_std_ready")
    rstd_ready = sp.sem("ln_rstd_ready")
    with nc.Block() as block:
        @block.vector
        def _(dve):
            for t in range(NT):
                nc.vector.bn_stats(stats[:, t, :], src[:, t, :]).then_inc(stats_ready, 1)
            dve.wait_ge(stats_ready, NT)
            for t in range(NT):
                nc.vector.bn_aggr(moments[:, t, :], stats[:, t, :]).then_inc(moments_ready, 1)
            dve.wait_ge(std_ready, 1)
            nc.vector.reciprocal(rstd[:, :], std[:, :]).then_inc(rstd_ready, 1)
            dve.wait_ge(rstd_ready, 1)
            for t in range(NT):
                nc.vector.tensor_scalar(dst[:, t, :], src[:, t, :], moments[:, t, 0:1], rstd[:, t:t + 1],
                                        ALU.subtract, ALU.mult)

        @block.scalar
        def _(act):
            act.wait_ge(moments_ready, NT)
            nc.scalar.activation(std[:, :], moments[:, :, 1], ACT.Sqrt, bias=K.eps[:, 0:1]).then_inc(std_ready, 1)


@scoped
def transpose_tokens(nc, sp, K, src, dst, scale=None, bias=None):
    turned = sp.ps("turned", [P, 2, BANK])
    turned_ready = sp.sem("turned_ready")
    turned_used = sp.sem("turned_used")
    with nc.Block() as block:
        @block.tensor
        def _(pe):
            for b in range(NB):
                if b >= 2:
                    pe.wait_ge(turned_used, b - 1)
                for j in range(TPB):
                    last = nc.tensor.transpose(turned[:, b % 2, j * P:(j + 1) * P], src[:, b * TPB + j, :], K.ident[:, :])
                last.then_inc(turned_ready, 1)

        @block.vector
        def _(dve):
            for b in range(NB):
                dve.wait_ge(turned_ready, b + 1)
                out = dst[:, b * BANK:(b + 1) * BANK]
                if scale is None:
                    nc.vector.tensor_copy(out, turned[:, b % 2, :]).then_inc(turned_used, 1)
                else:
                    nc.vector.tensor_scalar(out, turned[:, b % 2, :], scale, bias, ALU.mult, ALU.add).then_inc(turned_used, 1)


def l0_attention(nc, X, K, W):
    H, DH = 16, 64
    DA = DH + 1
    PAIRS = H // 2
    items = [(b, h, k) for b in range(NB - 1, -1, -1) for h in range(2) for k in range(TPB * (b + 1))]
    NI = len(items)
    last_of = {(b, h): n for n, (b, h, k) in enumerate(items)}
    outputs = list(last_of)
    on_diagonal = [k >= TPB * b for b, h, k in items]
    masks_to = [sum(on_diagonal[:n + 1]) for n in range(NI)]

    def width(b, k):
        return min(BANK, (b + 1) * BANK - k * P)

    proj = ([(kind, 0, b) for b in range(NB) for kind in ("q", "k")] + [("V", b) for b in range(NB)]
            + [(kind, 1, b) for b in range(NB) for kind in ("q", "k")] + [("suffix", b) for b in range(NB)])
    maxi = [[("max", h, t, j) for t in range(NT - 1, -1, -1) for j in range(t // TPB + 1)] for h in range(2)]
    rows_ = [[("row", h)] for h in range(2)]
    next_units = proj + maxi[0] + maxi[1][:6] + rows_[0] + maxi[1][6:] + rows_[1]
    STEPS_A = NI - 8

    def timeline(do_b, do_a):
        if not do_b:
            return [[u] for u in next_units]
        steps = [[] for _ in range(NI + 8)]
        if do_a:
            for i, u in enumerate(next_units):
                steps[i * STEPS_A // len(next_units)].append(u)
        for b in range(NB):
            steps[last_of[b, 1] + 4].append(("turn", b))
            steps[last_of[b, 1] + 6].append(("out", b))
        return steps

    reader = {"q": "dve", "k": "dve", "V": "dve", "suffix": "dve", "max": "dve", "row": "act", "turn": "act", "out": "dve"}

    with sublayer(nc) as sp:
        sufB = sp.sb("suffix_weighed", [P, NT, 2, DA])
        R = sufB[:, :, :, :].rearrange("p t a n -> p (t a n)")[:, 0:NT * D].rearrange("p (t n) -> p t n", t=NT)
        xhat = sp.sb("xhat", [P, NT, D])
        xT = sp.sb("xT", [P, T])
        xsufT = sp.sb("x_suffixT", [P, T])
        wq = sp.sb("wq", [P, H * DH])
        wk = sp.sb("wk", [P, H * DH])
        wv = sp.sb("wv", [P, H * DH])
        wo = sp.sb("wo", [P, PAIRS, D])
        bq = sp.sb("bq", [P, H])
        bk = sp.sb("bk", [P, H])
        bv = sp.sb("bv", [P, H * DH])
        behind = sp.sb("keys_behind", [P, NT])
        rows = sp.sb("rows", [P, 5, D])
        loaded = sp.sem("weights_loaded")
        layernorm(nc, K, X, R)
        layernorm(nc, K, R, xhat)
        with nc.Block() as block:
            @block.sync
            def _(sync):
                def load(dst, src):
                    sync.dma_start(dst, src).then_inc(loaded, 16)
                for dst, name in ((wq, "L0_attn_W_Q"), (wk, "L0_attn_W_K"), (wv, "L0_attn_W_V")):
                    load(dst[:, :].rearrange("d (h k) -> d h k", k=DH), W[name].rearrange("h d k -> d h k"))
                load(wo[:, :, :], W["L0_attn_W_O"].rearrange("(g a) k n -> (a k) g n", a=2))
                for half in (slice(0, DH), slice(DH, P)):
                    load(bq[half, :], W["L0_attn_b_Q"])
                    load(bk[half, :], W["L0_attn_b_K"])
                load(behind[:, :], W["keys_behind"])
                load(bv[:, :], W["L0_attn_b_V"].rearrange("h k -> (h k)").partition_broadcast(P))
                for j, name in enumerate(("L0_attn_b_O", "L0_attn_ln2_w", "L0_attn_ln2_b", "L0_attn_ln1_w", "L0_attn_ln1_b")):
                    load(rows[:, j, :], W[name].partition_broadcast(P))
                sync.wait_ge(loaded, 16 * 15)
        acc = xhat
        wqs = sp.sb("wq_pair", [P, 2, 2, DH])
        wks = sp.sb("wk_pair", [P, 2, 2, DH])
        strict = sp.sb("strict", [P, P])
        qN = sp.sb("q_next", [DA, 2, T])
        kN = sp.sb("k_next", [DH, 2, T])
        q16 = sp.sb("q_hi_mid", [P, 2, T], BF16)
        k16h = sp.sb("k_hi_hi", [P, 2, T], BF16)
        k16m = sp.sb("k_mid_mid", [P, 2, T], BF16)
        VN = sp.sb("v_next", [P, NT, 2, DH])
        sufN = sp.sb("suffix_next", [P, NT, 2, DA])
        qB = sp.sb("q_and_negmax", [DA, 2, T])
        kB = sp.sb("k_and_one", [DA, 2, T])
        VB = sp.sb("v_and_one", [P, NT, 2, DA])
        bmax = sp.sb("bank_max", [P, 2, NT, 1 + NB])
        nmax = sp.sb("neg_max", [P, 2, NT])
        nmaxT = sp.sb("neg_maxT", [NT, 2, P])
        e0 = sp.sb("exp_masked", [P, 2, NT])
        prob = sp.sb("prob", [P, 3, BANK])
        zsum = sp.sb("z_sum", [P, 2, TPB, DA])
        rden = sp.sb("rden", [P, 2, TPB])
        z = sp.sb("z", [P, NT, 2 * DH])
        zT = sp.sb("zT", [P, BANK])
        psS = sp.ps("scores", [P, 3, BANK])
        psO = sp.ps("outs", [P, 2, BANK])
        psR = sp.ps("ring", [P, 3, BANK])
        names = ("w_ready ring_ready dve_used act_used hi_ready masked row_max row_moved "
                 "qk_done exp_done mask_done pv_done z_read rden_ready z_ready "
                 "later_step weighed fin_a fin_b fin_c").split()
        S = {n: sp.sem(n) for n in names}
        x = VN[:, :, :, :].rearrange("p t a n -> p t (a n)")
        later = z
        with nc.Block() as block:
            @block.vector
            def _(dve):
                nc.vector.memset(bmax[:, :, :, :], 0.0).then_inc(S["fin_a"], 1)
                dve.wait_ge(S["fin_a"], 1)
                nc.vector.memset(bmax[:, :, NT - 1, NB:], -3e38)
                nc.vector.memset(VB[:, :, :, :], 1.0)
                nc.vector.memset(kB[:, :, :], 1.0)
                nc.vector.tensor_scalar(bq[:, :], bq[:, :], DH ** -0.5, None, ALU.mult)
                nc.vector.tensor_tensor(strict[:, :], K.ones[:, :], K.causal_k[:, :], ALU.subtract)
                nc.vector.tensor_tensor(x[:, :, :], xhat[:, :, :], bcast(rows[:, 3:4, :], [P, NT, D]), ALU.mult).then_inc(S["fin_b"], 1)
                dve.wait_ge(S["fin_b"], 1)
                nc.vector.tensor_tensor(x[:, :, :], x[:, :, :], bcast(rows[:, 4:5, :], [P, NT, D]), ALU.add)
                nc.vector.tensor_tensor(acc[:, :, :], R[:, :, :], bcast(rows[:, 0:1, :], [P, NT, D]), ALU.add)

            @block.gpsimd
            def _(pool):
                nc.gpsimd.memset(later[:, NT - 1, :], 0.0)
                for h in range(2):
                    nc.gpsimd.tensor_copy(sufN[:, :, h, DH:DA], behind[:, :].unsqueeze(2))

        with nc.Block() as block:
            @block.gpsimd
            def _(pool):
                for i, t in enumerate(range(NT - 2, -1, -1)):
                    if i >= 1:
                        pool.wait_ge(S["later_step"], i)
                    nc.gpsimd.tensor_tensor(later[:, t, :], later[:, t + 1, :], x[:, t + 1, :], ALU.add).then_inc(S["later_step"], 1)

            @block.tensor
            def _(pe):
                for n in range(2 * NB):
                    b = n if n < NB else 2 * NB - 1 - n
                    if n >= 3:
                        pe.wait_ge(S["dve_used"], n - 2)
                    if n >= NB:
                        pe.wait_ge(S["later_step"], NT - 1 - b * TPB)
                    for j in range(TPB):
                        t = b * TPB + j
                        out = psR[:, n % 3, j * P:(j + 1) * P]
                        if n < NB:
                            last = nc.tensor.transpose(out, x[:, t, :], K.ident[:, :])
                        else:
                            nc.tensor.matmul(out, x[:, t, :], strict[:, :], start=True, stop=False)
                            last = nc.tensor.matmul(out, later[:, t, :], K.ones[:, :], start=False, stop=True)
                    last.then_inc(S["ring_ready"], 1)

            @block.vector
            def _(dve):
                for n in range(2 * NB):
                    b = n if n < NB else 2 * NB - 1 - n
                    dve.wait_ge(S["ring_ready"], n + 1)
                    nc.vector.tensor_copy((xT if n < NB else xsufT)[:, b * BANK:(b + 1) * BANK], psR[:, n % 3, :]).then_inc(S["dve_used"], 1)

        def heads_pass(pair, nxt, do_b, do_a):
            steps = timeline(do_b, do_a)
            units = [u for st in steps for u in st]
            number = {u: n for n, u in enumerate(units)}

            def used_to(n, engine):
                return sum(reader[u[0]] == engine for u in units[:n + 1])

            def bank(u):
                return psR[:, number[u] % 3, :]

            def wait_read(eng, u):
                who = reader[u[0]]
                eng.wait_ge(S[who + "_used"], used_to(number[u], who))

            used = {"dve": S["dve_used"], "act": S["act_used"]}
            with nc.Block() as block:
                @block.tensor
                def _(pe):
                    def qk(n):
                        b, h, k = items[n]
                        w = width(b, k)
                        if n >= 3:
                            pe.wait_ge(S["exp_done"], n - 2)
                        nc.tensor.matmul(psS[:, n % 3, 0:w], kB[:, h, k * P:(k + 1) * P], qB[:, h, (b + 1) * BANK - w:(b + 1) * BANK],
                                         start=True, stop=True).then_inc(S["qk_done"], 1)

                    def pv(n):
                        b, h, k = items[n]
                        o = outputs.index((b, h))
                        if k == 0 and o >= 2:
                            pe.wait_ge(S["z_read"], o - 1)
                        if on_diagonal[n]:
                            pe.wait_ge(S["mask_done"], masks_to[n])
                        else:
                            pe.wait_ge(S["exp_done"], n + 1)
                        w = width(b, k)
                        for c in range(w // P):
                            q = TPB - w // P + c
                            last = nc.tensor.matmul(psO[:, o % 2, q * P:q * P + DA], prob[:, n % 3, c * P:(c + 1) * P], VB[:, k, h, :],
                                                    start=(k == 0 and q == 0), stop=(k == TPB * b + q), skip_group_check=True)
                        last.then_inc(S["pv_done"], 1)

                    def unit(u):
                        n, kind, b, ps = number[u], u[0], u[-1], bank(u)
                        if n >= 3:
                            wait_read(pe, units[n - 3])
                        if kind in "qk":
                            h = u[1]
                            if n == 0:
                                pe.wait_ge(S["w_ready"], 2)
                            last = nc.tensor.matmul(ps, (wqs if kind == "q" else wks)[:, h, :, :].rearrange("p a n -> p (a n)"),
                                                    xT[:, b * BANK:(b + 1) * BANK], start=True, stop=True)
                        elif kind in ("V", "suffix"):
                            xs = xT if kind == "V" else xsufT
                            for j in range(TPB):
                                t = b * TPB + j
                                last = nc.tensor.matmul(ps[:, j * P:(j + 1) * P], xs[:, t * P:(t + 1) * P], wv[:, bass.ds(nxt * P, P)],
                                                        start=True, stop=True)
                        elif kind == "max":
                            _, h, t, j = u
                            if j == 0 and t == NT - 1:
                                wait_read(pe, ("k", h, NB - 1))
                            w = min(BANK, (t + 1) * P - j * BANK)
                            for k16, first in ((k16h, True), (k16m, False)):
                                last = nc.tensor.matmul(ps[:, 0:w], q16[:, h, t * P:(t + 1) * P], k16[:, h, j * BANK:j * BANK + w],
                                                        start=first, stop=not first)
                        elif kind == "row":
                            h = u[1]
                            pe.wait_ge(S["row_max"], h + 1)
                            last = nc.tensor.transpose(ps[0:NT, 0:P], nmax[:, h, :], K.ident[:, :])
                        elif kind == "turn":
                            pe.wait_ge(S["z_ready"], outputs.index((b, 1)) + 1)
                            for j in range(TPB):
                                last = nc.tensor.transpose(ps[:, j * P:(j + 1) * P], z[:, b * TPB + j, :], K.ident[:, :])
                        else:
                            wait_read(pe, ("turn", b))
                            for j in range(TPB):
                                last = nc.tensor.matmul(ps[:, j * P:(j + 1) * P], zT[:, j * P:(j + 1) * P],
                                                        wo[:, bass.ds(pair, 1), :].rearrange("p a n -> p (a n)"), start=True, stop=True)
                        last.then_inc(S["ring_ready"], 1)

                    for s, todo in enumerate(steps):
                        if do_b and s < NI:
                            qk(s)
                        for u in todo:
                            unit(u)
                        if do_b and 0 <= s - 2 < NI:
                            pv(s - 2)

                @block.scalar
                def _(act):
                    if do_a:
                        for ws, w, scale in ((wqs, wq, DH ** -0.5), (wks, wk, 1.0)):
                            pair_w = w[:, bass.ds(nxt * P, P)].rearrange("p (a n) -> p a n", a=2).unsqueeze(2)
                            nc.scalar.activation(ws[:, :, :, :], bcast(pair_w, [P, 2, 2, DH]), ACT.Identity, scale=scale).then_inc(S["w_ready"], 1)

                    def exps(n):
                        b, h, k = items[n]
                        w = width(b, k)
                        act.wait_ge(S["qk_done"], n + 1)
                        if n >= 3:
                            act.wait_ge(S["pv_done"], n - 2)
                        nc.scalar.activation(prob[:, n % 3, 0:w], psS[:, n % 3, 0:w], ACT.Exp).then_inc(S["exp_done"], 1)

                    def copy_out(u):
                        kind, b, ps = u[0], u[-1], bank(u)
                        act.wait_ge(S["ring_ready"], number[u] + 1)
                        if kind in "qk":
                            blk = slice(b * BANK, (b + 1) * BANK)
                            full, hi, bias = (qN[0:DH], q16, bq) if kind == "q" else (kN, k16h, bk)
                            col = bass.ds(nxt * 2 + u[1], 1)
                            nc.scalar.activation(full[:, u[1], blk], ps[0:DH, :], ACT.Identity, bias=bias[0:DH, col])
                            nc.scalar.activation(hi[:, u[1], blk], ps, ACT.Identity, bias=bias[:, col]).then_inc(S["hi_ready"], 1)
                        elif kind == "row":
                            nc.scalar.copy(nmaxT[:, u[1], :], ps[0:NT, 0:P]).then_inc(S["act_used"], 1)
                        else:
                            if b < NB - 1:
                                act.wait_ge(S["ring_ready"], number["out", b + 1] + 1)
                            nc.scalar.copy(zT[:, :], ps).then_inc(S["act_used"], 1)

                    for s, todo in enumerate(steps):
                        if do_b and s < NI:
                            exps(s)
                        for u in todo:
                            if reader[u[0]] == "act" or u[0] in "qk":
                                copy_out(u)
                    if do_a:
                        if do_b:
                            act.wait_ge(S["qk_done"], NI)
                        nc.scalar.copy(kB[0:DH, 1, :], kN[:, 1, :])
                        act.wait_ge(S["row_max"], 2)
                        if do_b:
                            act.wait_ge(S["weighed"], 2)
                        nc.scalar.activation(e0[:, :, :], nmax[:, :, :], ACT.Exp)
                        act.wait_ge(S["row_moved"], 32)
                        nc.scalar.copy(qB[:, 1, :], qN[:, 1, :])

                @block.gpsimd
                def _(pool):
                    if do_b:
                        for h in range(2):
                            nc.gpsimd.tensor_tensor(sufB[:, :, h, :], sufN[:, :, h, :], bcast(e0[:, h, :].unsqueeze(2), [P, NT, DA]),
                                                    ALU.mult).then_inc(S["weighed"], 1)

                    for s in range(len(steps)):
                        if do_b and s < NI and on_diagonal[s]:
                            pool.wait_ge(S["exp_done"], s + 1)
                            v = prob[:, s % 3, 0:P]
                            nc.gpsimd.affine_select(out=v, in_=v, compare_op=ALU.is_ge, fill=0.0, base=0, pattern=[[1, P]],
                                                    channel_multiplier=-1).then_inc(S["mask_done"], 1)
                    if do_a:
                        wait_read(pool, ("V", NB - 1))
                        if do_b:
                            pool.wait_ge(S["pv_done"], NI)
                        nc.gpsimd.tensor_copy(VB[:, :, 0, 0:DH], VN[:, :, 0, :])

                @block.sync
                def _(sync):
                    if do_a:
                        for h in range(2):
                            wait_read(sync, ("row", h))
                            sync.dma_start(qN[DH:DA, h, :], nmaxT[:, h, :]).then_inc(S["row_moved"], 16)

                @block.vector
                def _(dve):
                    def read(u):
                        kind, b, ps = u[0], u[-1], bank(u)
                        dve.wait_ge(S["ring_ready"], number[u] + 1)
                        if kind == "V":
                            nc.vector.tensor_tensor(VN[:, b * TPB:(b + 1) * TPB, :, :].rearrange("p t a n -> p t (a n)"), ps.rearrange("p (t n) -> p t n", n=P),
                                                    bcast(bv[:, bass.ds(nxt * P, P)].unsqueeze(1), [P, TPB, P]), ALU.add).then_inc(S["dve_used"], 1)
                        elif kind == "suffix":
                            if do_b and b == 0:
                                dve.wait_ge(S["weighed"], 2)
                            for j in range(TPB):
                                t = b * TPB + j
                                last = nc.vector.scalar_tensor_tensor(
                                    out=sufN[:, t, :, 0:DH], in0=bv[:, bass.ds(nxt * P, P)].rearrange("p (a n) -> p a n", a=2), scalar=behind[:, t:t + 1],
                                    in1=ps[:, j * P:(j + 1) * P].rearrange("p (a n) -> p a n", a=2), op0=ALU.mult, op1=ALU.add)
                            last.then_inc(S["dve_used"], 1)
                        elif kind in "qk":
                            blk, h = slice(b * BANK, (b + 1) * BANK), u[1]
                            dve.wait_ge(S["hi_ready"], sum(v[0] in "qk" for v in units[:number[u] + 1]))
                            half, hi, mid, bias = (slice(DH, P), q16, q16, bq) if kind == "q" else (slice(0, P), k16h, k16m, bk)
                            nc.vector.scalar_tensor_tensor(out=mid[half, h, blk], in0=ps[half, :], scalar=bias[half, bass.ds(nxt * 2 + h, 1)],
                                                           in1=hi[half, h, blk], op0=ALU.add, op1=ALU.subtract).then_inc(S["dve_used"], 1)
                        elif kind == "max":
                            _, h, t, j = u
                            w = min(BANK, (t + 1) * P - j * BANK)
                            if j == t // TPB:
                                diag = ps[:, w - P:w]
                                nc.vector.tensor_tensor(diag, diag, K.causal_q[:, :], ALU.mult).then_inc(S["masked"], 1)
                                dve.wait_ge(S["masked"], h * NT + NT - t)
                            nc.vector.reduce_max(bmax[:, h, t, j:j + 1], ps[:, 0:w], axis=AX_X).then_inc(S["dve_used"], 1)
                            if t == 0:
                                wait_read(dve, u)
                                nc.vector.tensor_reduce(nmax[:, h, :], bmax[:, h, :, :], axis=AX_X, op=ALU.max, negate=True).then_inc(S["row_max"], 1)
                        else:
                            a = acc[:, b * TPB:(b + 1) * TPB, :].rearrange("p t n -> p (t n)")
                            nc.vector.tensor_tensor(a, a, ps, ALU.add).then_inc(S["dve_used"], 1)

                    def finish(o):
                        b, h = outputs[o]
                        ts = slice(b * TPB, (b + 1) * TPB)
                        dve.wait_ge(S["pv_done"], last_of[b, h] + 1)
                        if o < 2:
                            dve.wait_ge(S["weighed"], o + 1)
                        nc.vector.tensor_tensor(zsum[:, o % 2, :, :], psO[:, o % 2, :].rearrange("p (t n) -> p t n", n=P)[:, :, 0:DA], sufB[:, ts, h, :],
                                                ALU.add).then_inc(S["z_read"], 1)
                        dve.wait_ge(S["z_read"], o + 1)
                        nc.vector.reciprocal(rden[:, o % 2, :], zsum[:, o % 2, :, DH]).then_inc(S["rden_ready"], 1)
                        dve.wait_ge(S["rden_ready"], o + 1)
                        nc.vector.tensor_tensor(z[:, ts, h * DH:(h + 1) * DH], zsum[:, o % 2, :, 0:DH], bcast(rden[:, o % 2, :].unsqueeze(2), [P, TPB, DH]),
                                                ALU.mult).then_inc(S["z_ready"], 1)

                    for s, todo in enumerate(steps):
                        if do_b:
                            for o in range(len(outputs)):
                                if last_of[outputs[o]] + 3 == s:
                                    finish(o)
                        for u in todo:
                            if reader[u[0]] == "dve":
                                read(u)
                    if do_a:
                        if do_b:
                            dve.wait_ge(S["qk_done"], NI)
                        nc.vector.tensor_copy(kB[0:DH, 0, :], kN[:, 0, :])
                        dve.wait_ge(S["row_moved"], 32)
                        nc.vector.tensor_copy(qB[:, 0, :], qN[:, 0, :])
                        if do_b:
                            dve.wait_ge(S["pv_done"], NI)
                        nc.vector.tensor_copy(VB[:, :, 1, 0:DH], VN[:, :, 1, :])

            nc.gpsimd.sem_clear(sem_range(S))
            nc.all_engine_barrier()

        nc.gpsimd.sem_clear(sem_range(S))
        nc.all_engine_barrier()
        heads_pass(None, 0, False, True)
        with nc.Fori(0, PAIRS - 1) as g:
            heads_pass(g, g + 1, True, True)
        heads_pass(PAIRS - 1, None, True, False)
        layernorm(nc, K, acc, R)
        with nc.Block() as block:
            @block.vector
            def _(dve):
                half = NT // 2
                nc.vector.tensor_tensor(R[:, :, :], R[:, :, :], bcast(rows[:, 1:2, :], [P, NT, D]), ALU.mult).then_inc(S["fin_a"], 1)
                nc.vector.tensor_tensor(X[:, :, :], X[:, :, :], acc[:, :, :], ALU.add).then_inc(S["fin_b"], 1)
                dve.wait_ge(S["fin_a"], 1)
                nc.vector.tensor_tensor(R[:, :, :], R[:, :, :], bcast(rows[:, 2:3, :], [P, NT, D]), ALU.add).then_inc(S["fin_c"], 1)
                dve.wait_ge(S["fin_b"], 1)
                dve.wait_ge(S["fin_c"], 1)
                nc.vector.tensor_tensor(X[:, :, :], X[:, :, :], R[:, :, :], ALU.add)


def l0_experts(nc, X, K, W):
    H, KD, NK, TOP = 8, 128, 32, 8
    C = 2 * H
    EC = NK * NK // P
    with sublayer(nc) as sp:
        xn = sp.sb("xn", [P, NT, D])
        xT = sp.sb("xT", [P, T])
        keysT = sp.sb("keysT", [P, C, NK])
        bn = sp.sb("bn", [P, 2, C])
        downT = sp.sb("downT", [P, EC * P])
        up = sp.sb("up", [P, EC, D])
        wq = sp.sb("wq", [P, C * KD])
        G = sp.sb("gelu_hidden", [P, EC, T])
        sim = sp.sb("sim", [P, NT, C, NK])
        loaded = sp.sem("weights_loaded")
        with nc.Block() as block:
            @block.sync
            def _(sync):
                sync.dma_start(keysT[:, :, :], W["L0_ffn_keys"].rearrange("c k n -> k c n")).then_inc(loaded, 16)
                sync.dma_start(bn[:, 0, :], W["L0_ffn_bn_gamma"]).then_inc(loaded, 16)
                sync.dma_start(bn[:, 1, :], W["L0_ffn_bn_beta"]).then_inc(loaded, 16)
                sync.dma_start(downT[:, :], W["L0_ffn_down_embed"]).then_inc(loaded, 16)
                sync.dma_start(up[:, :, :], W["L0_ffn_up_embed"].rearrange("(c e) d -> e c d", e=P)).then_inc(loaded, 16)
                sync.dma_start(wq[:, :], W["L0_ffn_w_q"]).then_inc(loaded, 16)
                sync.wait_ge(loaded, 16 * 6)
        layernorm(nc, K, X, xn)
        transpose_tokens(nc, K, xn, xT)
        l0_hidden(nc, xT, downT, G, EC)
        l0_queries(nc, K, wq, xT, keysT, bn, sim, C, NK)
        l0_select(nc, X, K, sim, G, up, H, NK, TOP, EC)


@scoped
def l0_hidden(nc, sp, xT, downT, G, EC):
    ps = sp.ps("hidden", [P, 8, BANK])
    hidden_ready = sp.sem("hidden_ready")
    gelu_done = sp.sem("gelu_done")
    with nc.Block() as block:
        @block.tensor
        def _(pe):
            for n in range(EC * NB):
                if n >= 8:
                    pe.wait_ge(gelu_done, n - 7)
                nc.tensor.matmul(ps[:, n % 8, :], downT[:, (n // NB) * P:(n // NB + 1) * P], xT[:, (n % NB) * BANK:(n % NB + 1) * BANK],
                                 start=True, stop=True).then_inc(hidden_ready, 1)

        @block.scalar
        def _(act):
            for n in range(EC * NB):
                act.wait_ge(hidden_ready, n + 1)
                nc.scalar.activation(G[:, n // NB, (n % NB) * BANK:(n % NB + 1) * BANK], ps[:, n % 8, :], ACT.Gelu_apprx_tanh).then_inc(gelu_done, 1)


@scoped
def l0_queries(nc, sp, K, wq_all, xT, keysT, bn, sim, C, NK):
    U = 4
    RING = 6
    wq = sp.sb("wq_chunks", [P, U * P])
    qn = sp.sb("queries", [P, 2, T])
    stats = sp.sb("bn_stats", [P, 2, NB, 6])
    mv = sp.sb("bn_moments", [P, 2, 2])
    std = sp.sb("bn_std", [P, 2])
    rstd = sp.sb("bn_rstd", [P, 2])
    ab = sp.sb("bn_affine", [P, 2, 3])
    psQ = sp.ps("queries", [P, RING, BANK])
    psK = sp.ps("sims", [P, BANK])
    S = {n: sp.sem(n) for n in "wq_ready q_ready stats_ready mv_ready std_ready rstd_ready a_ready ma_ready b_ready q_normed sim_ready sim_copied".split()}
    with nc.Fori(0, C // U) as c4:
        with nc.Block() as block:
            @block.gpsimd
            def _(pool):
                nc.gpsimd.tensor_copy(wq[:, :], wq_all[:, bass.ds(c4 * (U * P), U * P)]).then_inc(S["wq_ready"], 1)

            @block.tensor
            def _(pe):
                pe.wait_ge(S["wq_ready"], 1)
                for i in range(U + 1):
                    for b in range(NB):
                        if i < U:
                            n = i * NB + b
                            if n >= RING:
                                pe.wait_ge(S["q_normed"], n - RING + 1)
                            nc.tensor.matmul(psQ[:, n % RING, :], wq[:, i * P:(i + 1) * P], xT[:, b * BANK:(b + 1) * BANK],
                                             start=True, stop=True).then_inc(S["q_ready"], 1)
                        if i >= 1:
                            pe.wait_ge(S["q_normed"], (i - 1) * NB + b + 1)
                            if i >= 2 and b == 0:
                                pe.wait_ge(S["sim_copied"], i - 1)
                            for j in range(TPB):
                                t = b * TPB + j
                                last = nc.tensor.matmul(psK[:, t * NK:(t + 1) * NK], qn[:, (i - 1) % 2, t * P:(t + 1) * P],
                                                        keysT[:, bass.ds(c4 * U + (i - 1), 1), :].rearrange("p a n -> p (a n)"), start=True, stop=True)
                    if i >= 1:
                        last.then_inc(S["sim_ready"], 1)

            @block.scalar
            def _(act):
                for i in range(U + 1):
                    if i < U:
                        act.wait_ge(S["mv_ready"], i + 1)
                        nc.scalar.activation(std[:, i % 2:i % 2 + 1], mv[:, i % 2, 1:2], ACT.Sqrt, bias=K.eps[:, 0:1]).then_inc(S["std_ready"], 1)
                    if i >= 1:
                        act.wait_ge(S["sim_ready"], i)
                        nc.scalar.copy(sim[:, :, bass.ds(c4 * U + (i - 1), 1), :],
                                       psK[:, :].rearrange("p (t a n) -> p t a n", a=1, n=NK)).then_inc(S["sim_copied"], 1)

            @block.vector
            def _(dve):
                for i in range(U):
                    c, w = c4 * U + i, i % 2
                    for b in range(NB):
                        n = i * NB + b
                        dve.wait_ge(S["q_ready"], n + 1)
                        nc.vector.bn_stats(stats[:, w, b, :], psQ[:, n % RING, :]).then_inc(S["stats_ready"], 1)
                    dve.wait_ge(S["stats_ready"], (i + 1) * NB)
                    nc.vector.bn_aggr(mv[:, w, :], stats[:, w, :, :].rearrange("p b s -> p (b s)")).then_inc(S["mv_ready"], 1)
                    dve.wait_ge(S["std_ready"], i + 1)
                    nc.vector.reciprocal(rstd[:, w:w + 1], std[:, w:w + 1]).then_inc(S["rstd_ready"], 1)
                    dve.wait_ge(S["rstd_ready"], i + 1)
                    nc.vector.tensor_tensor(ab[:, w, 0:1], rstd[:, w:w + 1], bn[:, 0, bass.ds(c, 1)], ALU.mult).then_inc(S["a_ready"], 1)
                    dve.wait_ge(S["a_ready"], i + 1)
                    nc.vector.tensor_tensor(ab[:, w, 2:3], mv[:, w, 0:1], ab[:, w, 0:1], ALU.mult).then_inc(S["ma_ready"], 1)
                    dve.wait_ge(S["ma_ready"], i + 1)
                    nc.vector.tensor_tensor(ab[:, w, 1:2], bn[:, 1, bass.ds(c, 1)], ab[:, w, 2:3], ALU.subtract).then_inc(S["b_ready"], 1)
                    dve.wait_ge(S["b_ready"], i + 1)
                    if i >= 2:
                        dve.wait_ge(S["sim_ready"], i - 1)
                    for b in range(NB):
                        n = i * NB + b
                        nc.vector.tensor_scalar(qn[:, w, b * BANK:(b + 1) * BANK], psQ[:, n % RING, :], ab[:, w, 0:1], ab[:, w, 1:2],
                                                ALU.mult, ALU.add).then_inc(S["q_normed"], 1)
        nc.gpsimd.sem_clear(sem_range(S))
        nc.all_engine_barrier()


@scoped
def l0_select(nc, sp, X, K, sim, G, up, H, NK, TOP, EC):
    U = 4
    RING = 3
    simt = sp.sb("sim_tile", [P, 2, 2 * H, NK])
    top = sp.sb("top_keys", [P, 2 * H, TOP])
    pairs = sp.sb("pair_sums", [P, H, TOP, TOP])
    best = sp.sb("best", [P, 2, H, TOP])
    nmax = sp.sb("neg_best", [P, 2, H])
    shifted = sp.sb("best_shifted", [P, H, TOP])
    expd = sp.sb("best_exp", [P, H, TOP])
    z = sp.sb("z", [P, H])
    rz = sp.sb("one_over_z", [P, 2, H])
    sums = sp.sb("all_sums", [P, RING, NK * NK])
    exps = sp.sb("all_exps", [P, RING, NK * NK])
    picked = sp.sb("picked", [P, RING, NK * NK])
    diag = sp.sb("diag_rz", [P, RING, P])
    weighted = sp.sb("weighted_hidden", [P, EC, P])
    psW = sp.ps("weights", [P, 2, EC // TPB, BANK])
    psY = sp.ps("out", [P, BANK])
    names = ("tile_ready top_ready pairs_ready best_ready shifted_ready exp8_ready z_ready rz_ready diag_ready "
             "sums_ready exps_ready picked_ready added weighted_ready out_ready y_added").split()
    S = {n: sp.sem(n) for n in names}
    with nc.Fori(0, NT // U) as t4:
        with nc.Block() as block:
            @block.gpsimd
            def _(pool):
                for n in range(U * H):
                    u, h = n // H, n % H
                    if h == 0:
                        pool.wait_ge(S["tile_ready"], u + 1)
                    if n >= RING:
                        pool.wait_ge(S["picked_ready"], n - RING + 1)
                    nc.gpsimd.tensor_tensor(sums[:, n % RING, :].rearrange("p (i j) -> p i j", j=NK),
                                            bcast(simt[:, u % 2, h, :].unsqueeze(2), [P, NK, NK]),
                                            bcast(simt[:, u % 2, H + h, :].unsqueeze(1), [P, NK, NK]), ALU.add).then_inc(S["sums_ready"], 1)

            @block.scalar
            def _(act):
                def fetch(u):
                    nc.scalar.copy(simt[:, u % 2, :, :], sim[:, bass.ds(t4 * U + u, 1), :, :].rearrange("p a c n -> p (a c) n")).then_inc(S["tile_ready"], 1)

                def exp_best(u):
                    act.wait_ge(S["shifted_ready"], 2 * (u + 1))
                    nc.scalar.activation(expd[:, :, :], shifted[:, :, :], ACT.Exp).then_inc(S["exp8_ready"], 1)

                fetch(0)
                exp_best(0)
                for n in range(U * H):
                    u, h = n // H, n % H
                    act.wait_ge(S["sums_ready"], n + 1)
                    if n >= RING:
                        act.wait_ge(S["picked_ready"], n - RING + 1)
                    nc.scalar.activation(exps[:, n % RING, :], sums[:, n % RING, :], ACT.Exp, bias=nmax[:, u % 2, h:h + 1]).then_inc(S["exps_ready"], 1)
                    if h == 0:
                        act.wait_ge(S["rz_ready"], u + 1)
                    if n >= RING:
                        act.wait_ge(S["added"], n - RING + 1)
                    nc.scalar.activation(diag[:, n % RING, :], K.ident[:, :], ACT.Identity, scale=rz[:, u % 2, h:h + 1]).then_inc(S["diag_ready"], 1)
                    if u + 1 < U and h == 0:
                        fetch(u + 1)
                    if u + 1 < U and h == 6:
                        exp_best(u + 1)

            @block.vector
            def _(dve):
                def top_keys(u, part):
                    dve.wait_ge(S["tile_ready"], u + 1)
                    for c in range(part * H // 2, (part + 1) * H // 2):
                        nc.vector.max(top[:, c, :], simt[:, u % 2, c, :]).then_inc(S["top_ready"], 1)

                def pair_sums(u):
                    dve.wait_ge(S["top_ready"], 2 * H * (u + 1))
                    nc.vector.tensor_tensor(pairs[:, :, :, :], bcast(top[:, 0:H, :].unsqueeze(3), [P, H, TOP, TOP]),
                                            bcast(top[:, H:2 * H, :].unsqueeze(2), [P, H, TOP, TOP]), ALU.add).then_inc(S["pairs_ready"], 1)

                def best_sums(u):
                    w = u % 2
                    dve.wait_ge(S["pairs_ready"], u + 1)
                    for h in range(H):
                        last = nc.vector.max(best[:, w, h, :], pairs[:, h, :, :].rearrange("p i j -> p (i j)"))
                    last.then_inc(S["best_ready"], 1)
                    dve.wait_ge(S["best_ready"], u + 1)
                    nc.vector.tensor_tensor(shifted[:, :, :], best[:, w, :, :], bcast(best[:, w, :, 0:1], [P, H, TOP]), ALU.subtract).then_inc(S["shifted_ready"], 1)
                    nc.vector.tensor_scalar(nmax[:, w, :], best[:, w, :, 0], -1.0, None, ALU.mult).then_inc(S["shifted_ready"], 1)

                def one_over_sums(u):
                    dve.wait_ge(S["exp8_ready"], u + 1)
                    nc.vector.tensor_reduce(z[:, :], expd[:, :, :], axis=AX_X, op=ALU.add).then_inc(S["z_ready"], 1)
                    dve.wait_ge(S["z_ready"], u + 1)
                    nc.vector.reciprocal(rz[:, u % 2, :], z[:, :]).then_inc(S["rz_ready"], 1)

                def weigh(u):
                    dve.wait_ge(S["added"], (u + 1) * H)
                    nc.vector.tensor_tensor(weighted[:, :, :], psW[:, u % 2, :, :].rearrange("p b (c n) -> p (b c) n", n=P),
                                            G[:, :, bass.ds((t4 * U + u) * P, P)], ALU.mult).then_inc(S["weighted_ready"], 1)

                def add_out(u):
                    dve.wait_ge(S["out_ready"], u + 1)
                    xt = X[:, bass.ds(t4 * U + u, 1), :].rearrange("p a n -> p (a n)")
                    nc.vector.tensor_tensor(xt, xt, psY[:, 0:D], ALU.add).then_inc(S["y_added"], 1)

                for part in range(4):
                    top_keys(0, part)
                pair_sums(0)
                best_sums(0)
                one_over_sums(0)
                for n in range(U * H):
                    u, h = n // H, n % H
                    dve.wait_ge(S["exps_ready"], n + 1)
                    if n >= RING:
                        dve.wait_ge(S["added"], n - RING + 1)
                    nc.vector.scalar_tensor_tensor(out=picked[:, n % RING, :], in0=sums[:, n % RING, :], scalar=best[:, u % 2, h, TOP - 1:TOP],
                                                   in1=exps[:, n % RING, :], op0=ALU.is_ge, op1=ALU.mult).then_inc(S["picked_ready"], 1)
                    if h == 0 and u >= 1:
                        weigh(u - 1)
                    if h == 3 and u >= 1:
                        add_out(u - 1)
                    if u + 1 < U:
                        if h < 4:
                            top_keys(u + 1, h)
                        if h == 4:
                            pair_sums(u + 1)
                        if h == 5:
                            best_sums(u + 1)
                        if h == 7:
                            one_over_sums(u + 1)
                weigh(U - 1)
                add_out(U - 1)

            @block.tensor
            def _(pe):
                def out(u):
                    pe.wait_ge(S["weighted_ready"], u + 1)
                    if u >= 1:
                        pe.wait_ge(S["y_added"], u)
                    for e in range(EC):
                        last = nc.tensor.matmul(psY[:, 0:D], weighted[:, e, :], up[:, e, :], start=(e == 0), stop=(e == EC - 1))
                    last.then_inc(S["out_ready"], 1)

                for n in range(U * H):
                    u, h = n // H, n % H
                    pe.wait_ge(S["diag_ready"], n + 1)
                    pe.wait_ge(S["picked_ready"], n + 1)
                    for e in range(EC):
                        last = nc.tensor.matmul(psW[:, u % 2, e // TPB, (e % TPB) * P:(e % TPB + 1) * P], picked[:, n % RING, e * P:(e + 1) * P],
                                                diag[:, n % RING, :], start=(h == 0 and e % TPB == 0), stop=(h == H - 1), skip_group_check=True)
                    last.then_inc(S["added"], 1)
                    if h == 1 and u >= 1:
                        out(u - 1)
                out(U - 1)
        nc.gpsimd.sem_clear(sem_range(S))
        nc.all_engine_barrier()


def l1_attention(nc, X, K, W):
    H, G, HD = 16, 4, 8
    with sublayer(nc) as sp:
        QS = sp.sb("q_stackT", [72, H, T], BF16)
        KS = sp.sb("k_stackT", [72, G, T], BF16)
        V = sp.sb("v", [P, NT, G, HD])
        xn = sp.sb("xn", [P, NT, D])
        l1_qkv(nc, X, K, W, QS, KS, V, xn, H, G, HD)
        ZT = sp.sb("zT", [H // G * HD, G, T])
        l1_core(nc, QS, KS, V, ZT, K, H, G, HD)
        l1_project(nc, ZT, W, X, G)


@scoped
def project_add(nc, sp, K, Z, w_dram, X):
    w = sp.sb("w", [P, D])
    ZT = sp.sb("ZT", [P, T])
    psY = sp.ps("y", [P, 2, BANK])
    w_loaded = sp.sem("w_loaded")
    y_ready = sp.sem("y_ready")
    y_added = sp.sem("y_added")
    transpose_tokens(nc, K, Z, ZT)
    with nc.Block() as block:
        @block.sync
        def _(sync):
            sync.dma_start(w[:, :], w_dram).then_inc(w_loaded, 16)

        @block.tensor
        def _(pe):
            pe.wait_ge(w_loaded, 16)
            for b in range(NB):
                if b >= 2:
                    pe.wait_ge(y_added, b - 1)
                for j in range(TPB):
                    t = b * TPB + j
                    last = nc.tensor.matmul(psY[:, b % 2, j * D:(j + 1) * D], ZT[:, t * P:(t + 1) * P], w[:, :], start=True, stop=True)
                last.then_inc(y_ready, 1)

        @block.vector
        def _(dve):
            for b in range(NB):
                dve.wait_ge(y_ready, b + 1)
                xb = X[:, b * TPB:(b + 1) * TPB, :].rearrange("p t d -> p (t d)")
                nc.vector.tensor_tensor(xb, xb, psY[:, b % 2, :], ALU.add).then_inc(y_added, 1)


@scoped
def l1_qkv(nc, sp, X, K, W, QS, KS, V, xn, H, G, HD):
    N = H + G
    HALF = HD // 2
    xT = sp.sb("xT", [P, T])
    layernorm(nc, K, X, xn)
    transpose_tokens(nc, K, xn, xT)
    w = sp.sb("w_qkv", [P, (N + G) * HD])
    trig = sp.sb("rope", [P, 2, NT, HALF])
    qk = sp.sb("qk", [P, NT, N, HD])
    sq = sp.sb("squares", [P, NT, N, HD])
    nrm = sp.sb("norms", [P, 2, NT * N])
    rot = sp.sb("rotated", [P, NT, N, HD])
    parts = sp.sb("parts", [P, 3, NT * N, HD], BF16)
    stack = sp.sb("stack", [P, NT * N, 9, HD], BF16)
    tmp = stack[:, 0:2 * NT * N // 9 + 1, :, :].rearrange("p a i d -> p (a i d)")[:, 0:2 * NT * N * HD].bitcast(F32).rearrange(
        "p (t n d) -> p t n d", t=NT, n=N)
    identb = sp.sb("identb", [P, P], BF16)
    psP = sp.ps("qkv", [P, 4, BANK])
    psT = sp.ps("turned", [72, 4, 2 * BANK], BF16)
    names = ("loaded qkv_ready qkv_copied sq_ready ss_ready nrm_ready eps_added rn_ready normed "
             "c_ready s_ready rotated part1 rest1 part2 rest2 part3 stacked identb_ready turned_ready dve_copied act_copied").split()
    S = {n: sp.sem(n) for n in names}
    with nc.Block() as block:
        @block.sync
        def _(sync):
            sync.dma_start(w[:, :], W["L1_attn_w_qkv"]).then_inc(S["loaded"], 16)
            sync.dma_start(trig[:, :, :, :], W["rope8"]).then_inc(S["loaded"], 16)

        @block.tensor
        def _(pe):
            pe.wait_ge(S["loaded"], 32)
            WD = (N + G) * HD
            for n in range(NT // 2):
                if n >= 4:
                    pe.wait_ge(S["qkv_copied"], 2 * (n - 3))
                for j in range(2):
                    t = 2 * n + j
                    last = nc.tensor.matmul(psP[:, n % 4, j * WD:(j + 1) * WD], xT[:, t * P:(t + 1) * P], w[:, :], start=True, stop=True)
                last.then_inc(S["qkv_ready"], 1)
            pe.wait_ge(S["identb_ready"], 1)
            pe.wait_ge(S["stacked"], 3)
            st = stack[:, :, :, :].rearrange("p (t n) i d -> p t n (i d)", n=N)
            for n in range(2 * N):
                if n >= 4:
                    pe.wait_ge(S["dve_copied" if n % 2 == 0 else "act_copied"], (n - 4) // 2 + 1)
                for j in range(8):
                    last = nc.tensor.transpose(psT[:, n % 4, j * P:(j + 1) * P], st[:, (n % 2) * 8 + j, n // 2, :], identb[:, :])
                last.then_inc(S["turned_ready"], 1)

        def stack_out(n):
            h, half = n // 2, n % 2
            return (QS[:, h, half * 1024:(half + 1) * 1024] if h < H else KS[:, h - H, half * 1024:(half + 1) * 1024])

        @block.scalar
        def _(act):
            for n in range(NT // 2):
                act.wait_ge(S["qkv_ready"], n + 1)
                src = psP[:, n % 4, 0:2 * (N + G) * HD].rearrange("p (t c) -> p t c", t=2)
                nc.scalar.copy(qk[:, 2 * n:2 * n + 2, :, :].rearrange("p t n d -> p t (n d)"), src[:, :, 0:N * HD]).then_inc(S["qkv_copied"], 1)
                nc.scalar.copy(V[:, 2 * n:2 * n + 2, :, :], src[:, :, N * HD:].rearrange("p t (g d) -> p t g d", d=HD)).then_inc(S["qkv_copied"], 1)
            act.wait_ge(S["ss_ready"], 1)
            nc.scalar.activation(nrm[:, 1, :], nrm[:, 0, :], ACT.Sqrt).then_inc(S["nrm_ready"], 1)
            for i, done in enumerate(("part1", "part2", "part3")):
                act.wait_ge(S[done], 1)
                p4 = parts[:, i, :, :].rearrange("p (t n) d -> p t n d", n=N)
                s5 = stack[:, :, :, :].rearrange("p (t n) i d -> p t n i d", n=N)
                for t in range(NT):
                    nc.scalar.copy(s5[:, t, 0:H, 3 * i:3 * i + 3, :], bcast(p4[:, t, 0:H, :].unsqueeze(2), [P, H, 3, HD]))
                    last = nc.scalar.copy(s5[:, t, H:N, i:9:3, :], bcast(p4[:, t, H:N, :].unsqueeze(2), [P, G, 3, HD]))
                last.then_inc(S["stacked"], 1)
            for n in range(1, 2 * N, 2):
                act.wait_ge(S["turned_ready"], n + 1)
                nc.scalar.copy(stack_out(n), psT[:, n % 4, :]).then_inc(S["act_copied"], 1)

        @block.gpsimd
        def _(pool):
            nc.gpsimd.tensor_copy(identb[:, :], K.ident[:, :]).then_inc(S["identb_ready"], 1)

        @block.vector
        def _(dve):
            dve.wait_ge(S["qkv_copied"], NT)
            flat = "p t n d -> p (t n d)"
            nc.vector.tensor_tensor(sq[:, :, :, :].rearrange(flat), qk[:, :, :, :].rearrange(flat), qk[:, :, :, :].rearrange(flat), ALU.mult).then_inc(S["sq_ready"], 1)
            dve.wait_ge(S["sq_ready"], 1)
            nc.vector.tensor_reduce(nrm[:, 0, :], sq[:, :, :, :].rearrange("p t n d -> p (t n) d"), axis=AX_X, op=ALU.add).then_inc(S["ss_ready"], 1)
            dve.wait_ge(S["nrm_ready"], 1)
            nc.vector.tensor_scalar(nrm[:, 0, :], nrm[:, 1, :], 1e-10, None, ALU.add).then_inc(S["eps_added"], 1)
            dve.wait_ge(S["eps_added"], 1)
            nc.vector.reciprocal(nrm[:, 1, :], nrm[:, 0, :]).then_inc(S["rn_ready"], 1)
            dve.wait_ge(S["rn_ready"], 1)
            nc.vector.tensor_tensor(sq[:, :, :, :].rearrange("p t n d -> p (t n) d"), qk[:, :, :, :].rearrange("p t n d -> p (t n) d"),
                                    bcast(nrm[:, 1, :].unsqueeze(2), [P, NT * N, HD]), ALU.mult).then_inc(S["normed"], 1)
            dve.wait_ge(S["normed"], 1)
            dve.wait_ge(S["loaded"], 32)
            sh = [P, NT, N, HALF]
            cos, sin = (bcast(trig[:, i, :, :].unsqueeze(2), sh) for i in range(2))
            x1, x2 = sq[:, :, :, 0:HALF], sq[:, :, :, HALF:HD]
            nc.vector.tensor_tensor(rot[:, :, :, 0:HALF], x1, cos, ALU.mult).then_inc(S["c_ready"], 1)
            nc.vector.tensor_tensor(rot[:, :, :, HALF:HD], x2, cos, ALU.mult).then_inc(S["c_ready"], 1)
            nc.vector.tensor_tensor(tmp[:, :, :, 0:HALF], x2, sin, ALU.mult).then_inc(S["s_ready"], 1)
            nc.vector.tensor_tensor(tmp[:, :, :, HALF:HD], x1, sin, ALU.mult).then_inc(S["s_ready"], 1)
            dve.wait_ge(S["c_ready"], 2)
            dve.wait_ge(S["s_ready"], 2)
            nc.vector.tensor_tensor(qk[:, :, :, 0:HALF], rot[:, :, :, 0:HALF], tmp[:, :, :, 0:HALF], ALU.subtract).then_inc(S["rotated"], 1)
            nc.vector.tensor_tensor(qk[:, :, :, HALF:HD], rot[:, :, :, HALF:HD], tmp[:, :, :, HALF:HD], ALU.add).then_inc(S["rotated"], 1)
            dve.wait_ge(S["rotated"], 2)
            v, rest = qk[:, :, :, :].rearrange(flat), rot[:, :, :, :].rearrange(flat)
            part = [parts[:, i, :, :].rearrange("p n d -> p (n d)") for i in range(3)]
            nc.vector.tensor_copy(part[0], v).then_inc(S["part1"], 1)
            dve.wait_ge(S["part1"], 1)
            nc.vector.tensor_tensor(rest, v, part[0], ALU.subtract).then_inc(S["rest1"], 1)
            dve.wait_ge(S["rest1"], 1)
            nc.vector.tensor_copy(part[1], rest).then_inc(S["part2"], 1)
            dve.wait_ge(S["part2"], 1)
            nc.vector.tensor_tensor(v, rest, part[1], ALU.subtract).then_inc(S["rest2"], 1)
            dve.wait_ge(S["rest2"], 1)
            nc.vector.tensor_copy(part[2], v).then_inc(S["part3"], 1)
            for n in range(0, 2 * N, 2):
                dve.wait_ge(S["turned_ready"], n + 1)
                nc.vector.tensor_copy(stack_out(n), psT[:, n % 4, :]).then_inc(S["dve_copied"], 1)


@scoped
def l1_core(nc, sp, QS, KS, V, ZT, K, H, G, HD):
    HPG = H // G
    GW = HPG * HD
    prob = sp.sb("prob", [P, 3, 2 * BANK])
    VW = sp.sb("v_weights", [P, NT, HPG, 2 * GW])
    rden = sp.sb("rden", [GW, 2, BANK])
    psS = sp.ps("scores", [P, 3, 2 * BANK])
    psO = sp.ps("outs", [2 * GW, 2, BANK])
    items = []
    for b in range(NB):
        for j in range(HPG):
            for i in range(2 * b):
                items.append((b, j, [(2 * i, 0, BANK), (2 * i + 1, BANK, BANK)]))
            items.append((b, j, [(TPB * b, 0, BANK), (TPB * b + 1, BANK, 3 * P)]))
            items.append((b, j, [(TPB * b + 2, 0, 2 * P), (TPB * b + 3, 2 * P, P)]))
    diagonal = [tiles[0][0] >= TPB * b for b, j, tiles in items]
    masks_to = [sum(diagonal[:n + 1]) for n in range(len(items))]
    last_of = {b: n for n, (b, j, tiles) in enumerate(items)}
    names = "v_set v_placed qk_done exp_done mask_done pv_done rden_ready z_done".split()
    S = {n: sp.sem(n) for n in names}
    with nc.Block() as block:
        @block.gpsimd
        def _(pool):
            nc.gpsimd.memset(VW[:, :, :, :], 0.0).then_inc(S["v_set"], 1)
            pool.wait_ge(S["v_set"], 1)
            for j in range(HPG):
                nc.gpsimd.memset(VW[:, :, j, GW + j * HD:GW + (j + 1) * HD], 1.0)
    with nc.Fori(0, G) as g:
        with nc.Block() as block:
            @block.tensor
            def _(pe):
                def qk(n):
                    b, j, tiles = items[n]
                    if n >= 3:
                        pe.wait_ge(S["exp_done"], n - 2)
                    for t, col, w in tiles:
                        last = nc.tensor.matmul(psS[:, n % 3, col:col + w], KS[:, bass.ds(g, 1), t * P:(t + 1) * P].rearrange("p a n -> p (a n)"),
                                                QS[:, bass.ds(g * HPG + j, 1), (b + 1) * BANK - w:(b + 1) * BANK].rearrange("p a n -> p (a n)"),
                                                start=True, stop=True)
                    last.then_inc(S["qk_done"], 1)

                def pv(n):
                    b, j, tiles = items[n]
                    if n == 0:
                        pe.wait_ge(S["v_placed"], HPG)
                    if j == 0 and tiles[0][0] == 0 and b >= 2:
                        pe.wait_ge(S["z_done"], b - 1)
                    if diagonal[n]:
                        pe.wait_ge(S["mask_done"], masks_to[n])
                    else:
                        pe.wait_ge(S["exp_done"], n + 1)
                    for t, col, w in tiles:
                        last = nc.tensor.matmul(psO[:, b % 2, BANK - w:BANK], VW[:, t, j, :], prob[:, n % 3, col:col + w],
                                                start=(j == 0 and t == 0), stop=(j == HPG - 1 and t == TPB * b + TPB - 1), skip_group_check=True)
                    last.then_inc(S["pv_done"], 1)

                for s in range(len(items) + 2):
                    if s < len(items):
                        qk(s)
                    if s >= 2:
                        pv(s - 2)

            @block.scalar
            def _(act):
                for n, (b, j, tiles) in enumerate(items):
                    act.wait_ge(S["qk_done"], n + 1)
                    if n >= 3:
                        act.wait_ge(S["pv_done"], n - 2)
                    w = tiles[1][1] + tiles[1][2]
                    nc.scalar.activation(prob[:, n % 3, 0:w], psS[:, n % 3, 0:w], ACT.Exp, scale=HD ** -0.5).then_inc(S["exp_done"], 1)

            @block.gpsimd
            def _(pool):
                for n, (b, j, tiles) in enumerate(items):
                    if diagonal[n]:
                        pool.wait_ge(S["exp_done"], n + 1)
                        d = tiles[1][1]
                        v = prob[:, n % 3, 0:2 * d].rearrange("p (a c) -> p a c", a=2)[:, :, 0:P]
                        nc.gpsimd.tensor_tensor(v, v, bcast(K.causal_k[:, :].unsqueeze(1), [P, 2, P]), ALU.mult).then_inc(S["mask_done"], 1)

            @block.vector
            def _(dve):
                for j in range(HPG):
                    nc.vector.tensor_copy(VW[:, :, j, j * HD:(j + 1) * HD], V[:, :, bass.ds(g, 1), :].rearrange("p t a n -> p t (a n)")).then_inc(S["v_placed"], 1)
                for b in range(NB):
                    dve.wait_ge(S["pv_done"], last_of[b] + 1)
                    nc.vector.reciprocal(rden[:, b % 2, :], psO[GW:2 * GW, b % 2, :]).then_inc(S["rden_ready"], 1)
                    dve.wait_ge(S["rden_ready"], b + 1)
                    nc.vector.tensor_tensor(ZT[:, bass.ds(g, 1), b * BANK:(b + 1) * BANK].rearrange("p a n -> p (a n)"), psO[0:GW, b % 2, :], rden[:, b % 2, :],
                                            ALU.mult).then_inc(S["z_done"], 1)
        nc.gpsimd.sem_clear(sem_range(S))
        nc.all_engine_barrier()


@scoped
def l1_project(nc, sp, ZT, W, X, G):
    GW = D // G
    w = sp.sb("w_o", [GW, G, D])
    psY = sp.ps("y", [P, 2, BANK])
    w_loaded = sp.sem("w_loaded")
    y_ready = sp.sem("y_ready")
    y_added = sp.sem("y_added")
    with nc.Block() as block:
        @block.sync
        def _(sync):
            sync.dma_start(w[:, :, :], W["L1_attn_w_o"].rearrange("(g c) n -> c g n", g=G)).then_inc(w_loaded, 16)

        @block.tensor
        def _(pe):
            pe.wait_ge(w_loaded, 16)
            for b in range(NB):
                if b >= 2:
                    pe.wait_ge(y_added, b - 1)
                for j in range(TPB):
                    t = b * TPB + j
                    for g in range(G):
                        last = nc.tensor.matmul(psY[:, b % 2, j * D:(j + 1) * D], ZT[:, g, t * P:(t + 1) * P], w[:, g, :],
                                                start=(g == 0), stop=(g == G - 1))
                last.then_inc(y_ready, 1)

        @block.vector
        def _(dve):
            for b in range(NB):
                dve.wait_ge(y_ready, b + 1)
                xb = X[:, b * TPB:(b + 1) * TPB, :].rearrange("p t d -> p (t d)")
                nc.vector.tensor_tensor(xb, xb, psY[:, b % 2, :], ALU.add).then_inc(y_added, 1)


@scoped
def route_top2(nc, sp, K, xT, wr_dram, br_dram, E, cw):
    wr = sp.sb("w_router", [P, E])
    br = sp.sb("b_router", [P, E])
    logit = sp.sb("logits", [P, NT, E])
    best = sp.sb("best", [P, NT, 8])
    ex = sp.sb("exp_logits", [P, NT, E])
    zz = sp.sb("z", [P, 2, NT])
    ps = sp.ps("logits", [P, NT, 16])
    S = {n: sp.sem(n) for n in "loaded logits_ready copied best_ready shifted exp_done masked sum_ready rz_ready".split()}
    with nc.Block() as block:
        @block.sync
        def _(sync):
            sync.dma_start(wr[:, :], wr_dram).then_inc(S["loaded"], 16)
            if br_dram is not None:
                sync.dma_start(br[:, :], br_dram.partition_broadcast(P)).then_inc(S["loaded"], 16)

        @block.tensor
        def _(pe):
            pe.wait_ge(S["loaded"], 16 if br_dram is None else 32)
            for t in range(NT):
                last = nc.tensor.matmul(ps[:, t, 0:E], xT[:, t * P:(t + 1) * P], wr[:, :], start=True, stop=True)
            last.then_inc(S["logits_ready"], 1)

        @block.vector
        def _(dve):
            dve.wait_ge(S["logits_ready"], 1)
            if br_dram is None:
                nc.vector.tensor_copy(logit[:, :, :], ps[:, :, 0:E]).then_inc(S["copied"], 1)
            else:
                dve.wait_ge(S["loaded"], 32)
                nc.vector.tensor_tensor(logit[:, :, :], ps[:, :, 0:E], bcast(br[:, :].unsqueeze(1), [P, NT, E]), ALU.add).then_inc(S["copied"], 1)
            dve.wait_ge(S["copied"], 1)
            for t in range(NT):
                nc.vector.max(best[:, t, :], logit[:, t, :]).then_inc(S["best_ready"], 1)
            dve.wait_ge(S["best_ready"], NT)
            nc.vector.tensor_tensor(ex[:, :, :], logit[:, :, :], bcast(best[:, :, 0:1], [P, NT, E]), ALU.subtract).then_inc(S["shifted"], 1)
            nc.vector.tensor_tensor(logit[:, :, :], logit[:, :, :], bcast(best[:, :, 1:2], [P, NT, E]), ALU.is_ge).then_inc(S["shifted"], 1)
            dve.wait_ge(S["shifted"], 2)
            dve.wait_ge(S["exp_done"], 1)
            nc.vector.tensor_tensor(cw[:, :, :], ex[:, :, :], logit[:, :, :], ALU.mult).then_inc(S["masked"], 1)
            dve.wait_ge(S["masked"], 1)
            nc.vector.tensor_reduce(zz[:, 0, :], cw[:, :, :], axis=AX_X, op=ALU.add).then_inc(S["sum_ready"], 1)
            dve.wait_ge(S["sum_ready"], 1)
            nc.vector.reciprocal(zz[:, 1, :], zz[:, 0, :]).then_inc(S["rz_ready"], 1)
            dve.wait_ge(S["rz_ready"], 1)
            nc.vector.tensor_tensor(cw[:, :, :], cw[:, :, :], bcast(zz[:, 1, :].unsqueeze(2), [P, NT, E]), ALU.mult)

        @block.scalar
        def _(act):
            act.wait_ge(S["shifted"], 1)
            nc.scalar.activation(ex[:, :, :], ex[:, :, :], ACT.Exp).then_inc(S["exp_done"], 1)


@scoped
def expert_mlps(nc, sp, X, K, xT, cw, E, F, up_drams, down_dram, b1_dram):
    gated = len(up_drams) == 2
    FC = -(-F // P)
    rows = [min(P, F - c * P) for c in range(FC)]
    NW = len(up_drams)
    w1_all = sp.sb("w1_all", [P, NW, E * F])
    w2_all = sp.sb("w2_all", [P, FC, E, D])
    b1 = None if gated else sp.sb("b1", [P, FC, E])
    w1 = sp.sb("w1_expert", [P, NW, F])
    gate = sp.sb("silu", [P, 2, BANK])
    gate2 = sp.sb("sigmoid", [P, 2, BANK])
    hid = sp.sb("hidden", [P, 2, FC, BANK])
    psG = sp.ps("gate", [P, 2, BANK])
    psU = sp.ps("up", [P, 2, BANK]) if gated else psG
    psY = sp.ps("y", [P, 2, BANK])
    S = {n: sp.sem(n) for n in "w_ready gu_ready silu_done sig_done hid_done y_ready y_added".split()}
    loaded = sp.sem("loaded")
    with nc.Block() as block:
        @block.sync
        def _(sync):
            for i, w in enumerate(up_drams):
                sync.dma_start(w1_all[:, i, :].rearrange("d (e f) -> d e f", e=E), w.rearrange("e d f -> d e f")).then_inc(loaded, 16)
            for c in range(FC):
                sync.dma_start(w2_all[0:rows[c], c, :, :], down_dram[:, c * P:c * P + rows[c], :].rearrange("e f n -> f e n")).then_inc(loaded, 16)
            if not gated:
                sync.dma_start(b1[:, :, :], b1_dram).then_inc(loaded, 16)
            sync.wait_ge(loaded, 16 * (NW + FC + (not gated)))
    n_items = NB * FC
    with nc.Fori(0, E) as e:
        with nc.Block() as block:
            @block.tensor
            def _(pe):
                def hidden(n):
                    b, c = n // FC, n % FC
                    if n == 0:
                        pe.wait_ge(S["w_ready"], 1)
                    if n >= 2:
                        pe.wait_ge(S["hid_done"], n - 1)
                    for i in range(NW):
                        last = nc.tensor.matmul((psG, psU)[i][0:rows[c], n % 2, :], w1[:, i, c * P:c * P + rows[c]], xT[:, b * BANK:(b + 1) * BANK],
                                                start=True, stop=True)
                    last.then_inc(S["gu_ready"], 1)

                def down(b):
                    pe.wait_ge(S["hid_done"], (b + 1) * FC)
                    if b >= 2:
                        pe.wait_ge(S["y_added"], TPB * (b - 1))
                    for j in range(TPB):
                        for c in range(FC):
                            last = nc.tensor.matmul(psY[:, b % 2, j * D:(j + 1) * D], hid[0:rows[c], b % 2, c, j * P:(j + 1) * P],
                                                    w2_all[0:rows[c], c, bass.ds(e, 1), :].rearrange("p a n -> p (a n)"),
                                                    start=(c == 0), stop=(c == FC - 1))
                    last.then_inc(S["y_ready"], 1)

                for n in range(n_items + 1):
                    if n < n_items:
                        hidden(n)
                    if n >= FC and (n - 1) % FC == 0 and n > 1 or n == n_items:
                        down((n - 1) // FC if n == n_items else (n - 1) // FC - 1)

            @block.scalar
            def _(act):
                nc.scalar.copy(w1[:, :, :], w1_all[:, :, bass.ds(e * F, F)]).then_inc(S["w_ready"], 1)
                for n in range(n_items):
                    b, c = n // FC, n % FC
                    act.wait_ge(S["gu_ready"], n + 1)
                    if gated:
                        if n >= 2:
                            act.wait_ge(S["silu_done"], n - 1)
                        nc.scalar.activation(gate2[0:rows[c], n % 2, :], psG[0:rows[c], n % 2, :], ACT.Sigmoid).then_inc(S["sig_done"], 1)
                    else:
                        if c == 0 and b >= 2:
                            act.wait_ge(S["y_ready"], b - 1)
                        nc.scalar.activation(hid[:, b % 2, c, :], psG[:, n % 2, :], ACT.Relu, bias=b1[:, c, bass.ds(e, 1)]).then_inc(S["hid_done"], 1)

            @block.vector
            def _(dve):
                def add(b):
                    dve.wait_ge(S["y_ready"], b + 1)
                    for j in range(TPB):
                        t = b * TPB + j
                        nc.vector.scalar_tensor_tensor(out=X[:, t, :], in0=psY[:, b % 2, j * D:(j + 1) * D], scalar=cw[:, t, bass.ds(e, 1)], in1=X[:, t, :],
                                                       op0=ALU.mult, op1=ALU.add).then_inc(S["y_added"], 1)

                for n in range(n_items if gated else 0):
                    b, c = n // FC, n % FC
                    dve.wait_ge(S["sig_done"], n + 1)
                    nc.vector.tensor_tensor(gate[0:rows[c], n % 2, :], gate2[0:rows[c], n % 2, :], psG[0:rows[c], n % 2, :], ALU.mult).then_inc(S["silu_done"], 1)
                    dve.wait_ge(S["silu_done"], n + 1)
                    if c == 0 and b >= 2:
                        dve.wait_ge(S["y_ready"], b - 1)
                    nc.vector.tensor_tensor(hid[0:rows[c], b % 2, c, :], gate[0:rows[c], n % 2, :], psU[0:rows[c], n % 2, :], ALU.mult).then_inc(S["hid_done"], 1)
                    if c == FC - 1 and b >= 1:
                        add(b - 1)
                for b in range(NB - 1 if gated else 0, NB):
                    add(b)
        nc.gpsimd.sem_clear(sem_range(S))
        nc.all_engine_barrier()


def l1_experts(nc, X, K, W):
    E, F = 9, 352
    with sublayer(nc) as sp:
        xn = sp.sb("xn", [P, NT, D])
        xT = sp.sb("xT", [P, T])
        cw = sp.sb("expert_weights", [P, NT, E])
        layernorm(nc, K, X, xn)
        transpose_tokens(nc, K, xn, xT)
        route_top2(nc, K, xT, W["L1_ffn_Wr"], None, E, cw)
        expert_mlps(nc, X, K, xT, cw, E, F, [W["L1_ffn_Wg"], W["L1_ffn_Wu"]], W["L1_ffn_Wd"], None)


def l3_experts(nc, X, K, W):
    E, F = 8, 512
    with sublayer(nc) as sp:
        xn = sp.sb("xn", [P, NT, D])
        xT = sp.sb("xT", [P, T])
        cw = sp.sb("expert_weights", [P, NT, E])
        layernorm(nc, K, X, xn)
        transpose_tokens(nc, K, xn, xT)
        route_top2(nc, K, xT, W["L3_ffn_W_router"], W["L3_ffn_b_router"], E, cw)
        expert_mlps(nc, X, K, xT, cw, E, F, [W["L3_ffn_W1"]], W["L3_ffn_W2"], W["L3_ffn_b1"])
        with nc.Block() as block:
            @block.vector
            def _(dve):
                nc.vector.memset(xn[:, :, E:], 0.0)
                nc.vector.tensor_copy(xn[:, :, 0:E], cw[:, :, :])
        project_add(nc, K, xn, W["L3_ffn_b2"], X)


def l2_attention(nc, X, K, W):
    with sublayer(nc) as sp:
        xn = sp.sb("xn", [P, NT, D])
        xT = sp.sb("xT", [P, T])
        layernorm(nc, K, X, xn)
        transpose_tokens(nc, K, xn, xT)
        l2_memories(nc, X, K, W, xT, xn)


@scoped
def l2_memories(nc, sp, X, K, W, xT, Y):
    C = 8
    TWO_PI_HI = 6.28125
    TWO_PI_LO = float(2 * np.pi - TWO_PI_HI)
    ROUND = 12582912.0
    PI = float(np.nextafter(np.float32(np.pi), np.float32(0)))
    PHASE_SCALE = 10.0
    pos = sp.sb("positions", [P, T])
    posi = sp.sb("positions_int", [P, BANK], I32)
    consts = sp.sb("round_and_half_pi", [P, 2])
    gate = sp.sb("gate", [P, 2, C])
    freq = sp.sb("freqs", [P, C])
    rs = sp.sb("rsqrt_t", [P, NT])
    wo = sp.sb("wo", [P, C, D])
    wk = sp.sb("wk_chunk", [P, P])
    wv = sp.sb("wv_chunk", [P, P])
    ang = [sp.sb(n, [P, T]) for n in ("angle_pos", "angle_key")]
    turns = [sp.sb(n, [P, T]) for n in ("turns_pos", "turns_key")]
    v = sp.sb("v", [P, T])
    cs = [[sp.sb(f"{n}_{m}", [P, 1 + T]) for n in ("cos", "sin")] for m in ("pos", "key")]
    prod = [sp.sb(f"prod{i}", [P, T]) for i in range(4)]
    mem = [sp.sb(f"mem{i}", [P, T]) for i in range(4)]
    psK = sp.ps("k", [P, 2, BANK])
    psV = sp.ps("v", [P, 2, BANK])
    psY = sp.ps("y", [P, 4, BANK])
    loaded = sp.sem("loaded")
    setup = sp.sem("setup")
    names = ("w_loaded kv_ready v_copied ang_pos ang_key rounded_pos rounded_key turns_pos turns_key "
             "red1 red2 red3 abs_pos abs_key trig_pos trig_key prods mems finals y_ready").split()
    S = {n: sp.sem(n) for n in names}
    blocks = [slice(b * BANK, (b + 1) * BANK) for b in range(NB)]

    with nc.Block() as block:
        @block.sync
        def _(sync):
            sync.dma_start(gate[:, :, :], W["L2_attn_gate"]).then_inc(loaded, 16)
            sync.dma_start(freq[:, :], W["L2_attn_freqs"]).then_inc(loaded, 16)
            sync.dma_start(rs[:, :], W["rsqrt_t"]).then_inc(loaded, 16)
            sync.dma_start(wo[:, :, :], W["L2_attn_Wo"].rearrange("(c f) n -> f c n", f=P)).then_inc(loaded, 16)
            sync.wait_ge(loaded, 64)

        @block.gpsimd
        def _(pool):
            for b in range(NB):
                if b:
                    pool.wait_ge(setup, 2 * b)
                nc.gpsimd.iota(posi[:, :], pattern=[[1, BANK]], base=b * BANK, channel_multiplier=0).then_inc(setup, 1)
                pool.wait_ge(setup, 2 * b + 1)
                nc.gpsimd.tensor_copy(pos[:, blocks[b]], posi[:, :]).then_inc(setup, 1)

        @block.vector
        def _(dve):
            nc.vector.memset(consts[:, 0:1], ROUND)
            nc.vector.memset(consts[:, 1:2], float(np.pi / 2))
            nc.vector.memset(cs[1][0][:, 0:1], 0.0)
            nc.vector.memset(cs[1][1][:, 0:1], 0.0)
            nc.vector.memset(Y[:, :, :], 0.0)

    with nc.Fori(0, C) as c:
        with nc.Block() as block:
            @block.sync
            def _(sync):
                sync.dma_start(wk[:, :], W["L2_attn_Wk"][:, bass.ds(c * P, P)]).then_inc(S["w_loaded"], 16)
                sync.dma_start(wv[:, :], W["L2_attn_Wv"][:, bass.ds(c * P, P)]).then_inc(S["w_loaded"], 16)

            @block.tensor
            def _(pe):
                pe.wait_ge(S["w_loaded"], 32)
                for b in range(NB):
                    if b >= 2:
                        pe.wait_ge(S["ang_key"], b - 1)
                        pe.wait_ge(S["v_copied"], b - 1)
                    nc.tensor.matmul(psK[:, b % 2, :], wk[:, :], xT[:, blocks[b]], start=True, stop=True)
                    nc.tensor.matmul(psV[:, b % 2, :], wv[:, :], xT[:, blocks[b]], start=True, stop=True).then_inc(S["kv_ready"], 1)
                for b in range(NB):
                    pe.wait_ge(S["finals"], 4 * (b + 1))
                    for j in range(TPB):
                        t = b * TPB + j
                        for i in range(4):
                            last = nc.tensor.matmul(psY[:, b, j * D:(j + 1) * D], prod[i][:, t * P:(t + 1) * P],
                                                    wo[:, bass.ds(c, 1), :].rearrange("p a n -> p (a n)"), start=(i == 0), stop=(i == 3))
                    last.then_inc(S["y_ready"], 1)

            @block.scalar
            def _(act):
                def angles(b):
                    nc.scalar.activation(ang[0][:, blocks[b]], pos[:, blocks[b]], ACT.Identity, scale=freq[:, bass.ds(c, 1)]).then_inc(S["ang_pos"], 1)
                    act.wait_ge(S["kv_ready"], b + 1)
                    nc.scalar.mul(ang[1][:, blocks[b]], psK[:, b % 2, :], PHASE_SCALE).then_inc(S["ang_key"], 1)
                    nc.scalar.copy(v[:, blocks[b]], psV[:, b % 2, :]).then_inc(S["v_copied"], 1)
                    for i, (made, done) in enumerate((("ang_pos", "rounded_pos"), ("ang_key", "rounded_key"))):
                        act.wait_ge(S[made], b + 1)
                        nc.scalar.activation(turns[i][:, blocks[b]], ang[i][:, blocks[b]], ACT.Identity, scale=float(1 / (2 * np.pi)),
                                             bias=consts[:, 0:1]).then_inc(S[done], 1)

                def trig(b):
                    for i, (absd, done) in enumerate((("abs_pos", "trig_pos"), ("abs_key", "trig_key"))):
                        act.wait_ge(S["red3"], 2 * b + i + 1)
                        sh = slice(1 + b * BANK, 1 + (b + 1) * BANK)
                        nc.scalar.activation(turns[i][:, blocks[b]], ang[i][:, blocks[b]], ACT.Abs).then_inc(S[absd], 1)
                        nc.scalar.activation(cs[i][1][:, sh], ang[i][:, blocks[b]], ACT.Sin).then_inc(S[done], 1)
                        act.wait_ge(S[absd], b + 1)
                        nc.scalar.activation(cs[i][0][:, sh], turns[i][:, blocks[b]], ACT.Sin, scale=-1.0, bias=consts[:, 1:2]).then_inc(S[done], 1)

                angles(0)
                for b in range(NB):
                    if b + 1 < NB:
                        angles(b + 1)
                    trig(b)

            @block.gpsimd
            def _(pool):
                def turn(b):
                    for i, (rounded, done) in enumerate((("rounded_pos", "turns_pos"), ("rounded_key", "turns_key"))):
                        pool.wait_ge(S[rounded], b + 1)
                        nc.gpsimd.tensor_scalar(turns[i][:, blocks[b]], turns[i][:, blocks[b]], -ROUND, 1.0, ALU.add, ALU.mult).then_inc(S[done], 1)

                turn(0)
                for b in range(NB):
                    if b + 1 < NB:
                        turn(b + 1)
                    pool.wait_ge(S["v_copied"], b + 1)
                    for i in range(4):
                        if i % 2 == 0:
                            pool.wait_ge(S["trig_pos" if i == 0 else "trig_key"], 2 * (b + 1))
                        src = slice(1 + b * BANK, 1 + (b + 1) * BANK) if i < 2 else blocks[b]
                        nc.gpsimd.tensor_tensor(prod[i][:, blocks[b]], v[:, blocks[b]], cs[i // 2][i % 2][:, src], ALU.mult).then_inc(S["prods"], 1)

            @block.vector
            def _(dve):
                def add(b):
                    dve.wait_ge(S["y_ready"], b + 1)
                    yb = Y[:, b * TPB:(b + 1) * TPB, :].rearrange("p t n -> p (t n)")
                    nc.vector.tensor_tensor(yb, yb, psY[:, b, :], ALU.add)

                def reduce(b):
                    n = 2 * b
                    for i, made in enumerate(("turns_pos", "turns_key")):
                        dve.wait_ge(S[made], b + 1)
                        a = ang[i][:, blocks[b]]
                        nc.vector.scalar_tensor_tensor(out=a, in0=turns[i][:, blocks[b]], scalar=-TWO_PI_HI, in1=a, op0=ALU.mult, op1=ALU.add).then_inc(S["red1"], 1)
                    for i in range(2):
                        dve.wait_ge(S["red1"], n + i + 1)
                        a = ang[i][:, blocks[b]]
                        nc.vector.scalar_tensor_tensor(out=a, in0=turns[i][:, blocks[b]], scalar=-TWO_PI_LO, in1=a, op0=ALU.mult, op1=ALU.add).then_inc(S["red2"], 1)
                    for i in range(2):
                        dve.wait_ge(S["red2"], n + i + 1)
                        a = ang[i][:, blocks[b]]
                        nc.vector.tensor_scalar(a, a, PI, -PI, ALU.min, ALU.max).then_inc(S["red3"], 1)

                reduce(0)
                for b in range(NB):
                    if b + 1 < NB:
                        reduce(b + 1)
                    for i in range(4):
                        dve.wait_ge(S["prods"], 4 * b + i + 1)
                        if b:
                            dve.wait_ge(S["mems"], 4 * (b - 1) + i + 1)
                        nc.vector.tensor_tensor_scan(mem[i][:, blocks[b]], bcast(K.ones[:, 0:1], [P, BANK]), prod[i][:, blocks[b]],
                                                     0.0 if b == 0 else mem[i][:, b * BANK - 1:b * BANK], ALU.mult, ALU.add).then_inc(S["mems"], 1)
                    for i in range(4):
                        dve.wait_ge(S["mems"], 4 * b + i + 1)
                        src = slice(1 + b * BANK, 1 + (b + 1) * BANK)
                        nc.vector.scalar_tensor_tensor(out=prod[i][:, blocks[b]], in0=mem[i][:, blocks[b]], scalar=gate[:, i // 2, bass.ds(c, 1)],
                                                       in1=cs[i // 2][i % 2][:, src], op0=ALU.mult, op1=ALU.mult).then_inc(S["finals"], 1)
                    if b >= 1:
                        add(b - 1)
                add(NB - 1)

        nc.gpsimd.sem_clear(sem_range(S))
        nc.all_engine_barrier()
    with nc.Block() as block:
        @block.vector
        def _(dve):
            for t in range(NT):
                nc.vector.scalar_tensor_tensor(out=X[:, t, :], in0=Y[:, t, :], scalar=rs[:, t:t + 1], in1=X[:, t, :], op0=ALU.mult, op1=ALU.add)


@scoped
def shift_tokens(nc, sp, src, dst):
    HF = D // 2
    zeroed = sp.sem("zeroed")
    shifted = sp.sem("shifted")
    with nc.Block() as block:
        @block.sync
        def _(sync):
            sync.dma_start(dst[1:P, :, HF:D], src[0:P - 1, :, HF:D]).then_inc(shifted, 16)
            sync.dma_start(dst[0:1, 1:NT, HF:D], src[P - 1:P, 0:NT - 1, HF:D]).then_inc(shifted, 16)
            sync.wait_ge(shifted, 32)

        @block.vector
        def _(dve):
            nc.vector.memset(dst[0:1, 0, HF:D], 0.0)

        @block.scalar
        def _(act):
            nc.scalar.copy(dst[:, :, 0:HF], src[:, :, 0:HF])


def l2_transformer(nc, X, K, W):
    DEPTH = 2
    with sublayer(nc) as sp:
        Y = sp.sb("y", [P, NT, D])
        layernorm(nc, K, X, Y)
        with nc.Fori(0, DEPTH) as l:
            with sublayer(nc) as inner:
                qT = inner.sb("qT", [P, 4, T])
                kT = inner.sb("kT", [P, 4, T])
                V = inner.sb("V", [P, NT, 512])
                rn = inner.sb("rnorm", [P, NT, 16])
                l2_qkv(nc, K, W, l, Y, qT, kT, V, rn)
                l2_window_attention(nc, K, W, l, Y, qT, kT, V, rn)
            l2_geglu(nc, K, W, l, Y)
        with nc.Block() as block:
            @block.vector
            def _(dve):
                nc.vector.tensor_tensor(X[:, :, :], X[:, :, :], Y[:, :, :], ALU.add)


@scoped
def l2_qkv(nc, sp, K, W, l, Y, qT, kT, V, rn):
    DH = 64
    HD2 = DH // 2
    h = sp.sb("shifted", [P, NT, D])
    hT = sp.sb("hT", [P, T])
    shift_tokens(nc, Y, h)
    transpose_tokens(nc, K, h, hT)
    w = sp.sb("wqkv", [P, 3 * 512])
    tab = sp.sb("rope_tables", [P, 2, NT, 2, DH])
    scl = sp.sb("qk_scales", [P, 2, 2, DH])
    sq = sp.sb("squares", [P, 2, 16, DH])
    ss = sp.sb("sums", [P, 3, 2, 16])
    m1 = sp.sb("cos_terms", [P, 2, 2, 8, DH])
    m2 = sp.sb("sin_terms", [P, 2, 2, 8, DH])
    psA = sp.ps("qkv", [P, 2, 3, BANK])
    psT = sp.ps("turned", [P, 2, BANK])
    names = ("loaded tables_ready qkv_ready sq_ready v_copied ss_ready root_ready clamped rn_ready cos_ready sin_ready "
             "summed k_normed turned_ready q_copied k_copied").split()
    S = {n: sp.sem(n) for n in names}
    with nc.Block() as block:
        @block.sync
        def _(sync):
            sync.dma_start(w[:, :], W["L2_ffn_wqkv"][bass.ds(l, 1), :, :].rearrange("a d n -> (a d) n")).then_inc(S["loaded"], 16)
            sync.dma_start(tab[:, :, :, :, :], W["xpos"]).then_inc(S["loaded"], 16)
            for i, name in enumerate(("L2_ffn_q_scale", "L2_ffn_k_scale")):
                src = W[name][bass.ds(l, 1), :].rearrange("a d -> (a d)")
                sync.dma_start(scl[:, 0, i, :], src.partition_broadcast(P)).then_inc(S["loaded"], 16)
                sync.dma_start(scl[:, 1, i, 0:HD2], src[HD2:DH].partition_broadcast(P)).then_inc(S["loaded"], 16)
                sync.dma_start(scl[:, 1, i, HD2:DH], src[0:HD2].partition_broadcast(P)).then_inc(S["loaded"], 16)

        @block.tensor
        def _(pe):
            pe.wait_ge(S["loaded"], 16 * 8)
            for t in range(NT + 1):
                if t < NT:
                    if t >= 2:
                        pe.wait_ge(S["sin_ready"], 2 * (t - 1))
                        pe.wait_ge(S["cos_ready"], t - 1)
                        pe.wait_ge(S["sq_ready"], t - 1)
                        pe.wait_ge(S["v_copied"], t - 1)
                    for i in range(3):
                        last = nc.tensor.matmul(psA[:, t % 2, i, :], hT[:, t * P:(t + 1) * P], w[:, i * 512:(i + 1) * 512], start=True, stop=True)
                    last.then_inc(S["qkv_ready"], 1)
                if t >= 1:
                    u = t - 1
                    pe.wait_ge(S["summed"], u + 1)
                    pe.wait_ge(S["k_normed"], u + 1)
                    if u >= 1:
                        pe.wait_ge(S["q_copied"], u)
                        pe.wait_ge(S["k_copied"], u)
                    for i in range(2):
                        for j in range(4):
                            last = nc.tensor.transpose(psT[:, i, j * P:(j + 1) * P], m1[:, u % 2, i, 2 * j:2 * j + 2, :].rearrange("p h d -> p (h d)"), K.ident[:, :])
                    last.then_inc(S["turned_ready"], 1)

        @block.scalar
        def _(act):
            for t in range(NT + 1):
                if t < NT:
                    act.wait_ge(S["qkv_ready"], t + 1)
                    if t >= 2:
                        act.wait_ge(S["ss_ready"], t - 1)
                    nc.scalar.activation(sq[:, t % 2, :, :].rearrange("p h d -> p (h d)"), psA[:, t % 2, 0:2, :].rearrange("p i n -> p (i n)"), ACT.Square).then_inc(S["sq_ready"], 1)
                    nc.scalar.copy(V[:, t, :], psA[:, t % 2, 2, :]).then_inc(S["v_copied"], 1)
                    act.wait_ge(S["ss_ready"], t + 1)
                    nc.scalar.activation(ss[:, 1, t % 2, :], ss[:, 0, t % 2, :], ACT.Sqrt).then_inc(S["root_ready"], 1)
                if t >= 1:
                    act.wait_ge(S["turned_ready"], t)
                    nc.scalar.copy(qT[:, :, (t - 1) * P:t * P], psT[:, 0, :].rearrange("p (j n) -> p j n", n=P)).then_inc(S["q_copied"], 1)

        @block.gpsimd
        def _(pool):
            for t in range(NT):
                pool.wait_ge(S["cos_ready"], t + 1)
                pool.wait_ge(S["sin_ready"], 2 * (t + 1))
                a = m1[:, t % 2, :, :, :].rearrange("p i h d -> p (i h d)")
                nc.gpsimd.tensor_tensor(a, a, m2[:, t % 2, :, :, :].rearrange("p i h d -> p (i h d)"), ALU.add).then_inc(S["summed"], 1)
                pool.wait_ge(S["summed"], t + 1)
                pool.wait_ge(S["rn_ready"], t + 1)
                k = m1[:, t % 2, 1, :, :]
                nc.gpsimd.tensor_tensor(k, k, bcast(rn[:, t, 8:16].unsqueeze(2), [P, 8, DH]), ALU.mult).then_inc(S["k_normed"], 1)

        @block.vector
        def _(dve):
            dve.wait_ge(S["loaded"], 16 * 8)
            for i in range(2):
                nc.vector.tensor_tensor(tab[:, i, :, :, :], tab[:, i, :, :, :], bcast(scl[:, i, :, :].unsqueeze(1), [P, NT, 2, DH]), ALU.mult).then_inc(S["tables_ready"], 1)
            dve.wait_ge(S["tables_ready"], 2)
            for t in range(NT + 1):
                if t < NT:
                    dve.wait_ge(S["sq_ready"], t + 1)
                    if t >= 2:
                        dve.wait_ge(S["root_ready"], t - 1)
                    nc.vector.tensor_reduce(ss[:, 0, t % 2, :], sq[:, t % 2, :, :], axis=AX_X, op=ALU.add).then_inc(S["ss_ready"], 1)
                    if t >= 2:
                        dve.wait_ge(S["turned_ready"], t - 1)
                        dve.wait_ge(S["summed"], t - 1)
                    dve.wait_ge(S["v_copied"], t + 1)
                    x = psA[:, t % 2, 0:2, :].rearrange("p i (h d) -> p i h d", d=DH)
                    nc.vector.tensor_tensor(m1[:, t % 2, :, :, :], x, bcast(tab[:, 0, t, :, :].unsqueeze(2), [P, 2, 8, DH]), ALU.mult).then_inc(S["cos_ready"], 1)
                    for o, i in ((0, HD2), (HD2, 0)):
                        nc.vector.tensor_tensor(m2[:, t % 2, :, :, o:o + HD2], x[:, :, :, i:i + HD2],
                                                bcast(tab[:, 1, t, :, o:o + HD2].unsqueeze(2), [P, 2, 8, HD2]), ALU.mult).then_inc(S["sin_ready"], 1)
                    dve.wait_ge(S["root_ready"], t + 1)
                    nc.vector.tensor_scalar(ss[:, 2, t % 2, :], ss[:, 1, t % 2, :], 1e-12, None, ALU.max).then_inc(S["clamped"], 1)
                    dve.wait_ge(S["clamped"], t + 1)
                    nc.vector.reciprocal(rn[:, t, :], ss[:, 2, t % 2, :]).then_inc(S["rn_ready"], 1)
                if t >= 1:
                    dve.wait_ge(S["turned_ready"], t)
                    nc.vector.tensor_copy(kT[:, :, (t - 1) * P:t * P], psT[:, 1, :].rearrange("p (j n) -> p j n", n=P)).then_inc(S["k_copied"], 1)


@scoped
def l2_window_attention(nc, sp, K, W, l, Y, qT, kT, V, rn):
    DH, H = 64, 8
    KW = P + 64
    LOW = -3.0e38
    wo = sp.sb("wo", [P, 4, D])
    mask = sp.sb("mask", [P, 2, KW])
    sm = sp.sb("masked_scores", [P, 2, H, KW])
    mx = sp.sb("max", [P, 2, H])
    nb = sp.sb("neg_max", [P, 2, H])
    den = sp.sb("den", [P, 2, H])
    rden = sp.sb("rden", [P, 2, H])
    prob = sp.sb("prob", [P, 2, H, 2 * P])
    probT = sp.sb("probT", [P, 2, 2 * H, P])
    z = sp.sb("z", [P, 2, H, DH])
    zT = sp.sb("zT", [P, 4, P])
    psS = sp.ps("scores", [P, 4, BANK])
    psT = sp.ps("turned", [P, 2, BANK])
    psZ = sp.ps("z", [P, BANK])
    psO = sp.ps("zT_and_out", [P, BANK])
    names = ("loaded mask_ready zeroed qk_done masked max_ready nb_ready exp_done trans_done dve_evac act_evac pv_done rden_ready z_ready "
             "zt_done zt_evac out_done out_added").split()
    S = {n: sp.sem(n) for n in names}
    head = [2 * (m % 4) + m // 4 for m in range(H)]
    with nc.Block() as block:
        @block.sync
        def _(sync):
            sync.dma_start(wo[:, :, :], W["L2_ffn_wo"][bass.ds(l, 1), :, :].rearrange("a (c f) n -> f (a c) n", f=P)).then_inc(S["loaded"], 16)

        @block.gpsimd
        def _(pool):
            nc.gpsimd.memset(mask[:, :, :], 0.0).then_inc(S["zeroed"], 1)
            nc.gpsimd.memset(prob[:, :, :, 0:64], 0.0).then_inc(S["zeroed"], 1)
            pool.wait_ge(S["zeroed"], 2)
            nc.gpsimd.affine_select(out=mask[:, :, :], in_=mask[:, :, :], compare_op=ALU.is_ge, fill=LOW, base=0,
                                    pattern=[[0, 2], [1, KW]], channel_multiplier=-1).then_inc(S["zeroed"], 1)
            pool.wait_ge(S["zeroed"], 3)
            nc.gpsimd.affine_select(out=mask[:, :, :], in_=mask[:, :, :], compare_op=ALU.is_ge, fill=LOW, base=64,
                                    pattern=[[0, 2], [-1, KW]], channel_multiplier=1).then_inc(S["zeroed"], 1)
            pool.wait_ge(S["zeroed"], 4)
            nc.gpsimd.affine_select(out=mask[:, 0, :], in_=mask[:, 0, :], compare_op=ALU.is_ge, fill=LOW, base=-64,
                                    pattern=[[1, KW]], channel_multiplier=0).then_inc(S["mask_ready"], 1)

        @block.tensor
        def _(pe):
            def scores(t):
                if t >= 1:
                    pe.wait_ge(S["masked"], t)
                lo = 64 if t == 0 else 0
                for m in range(H):
                    r = slice((m // 4) * DH, (m // 4) * DH + DH)
                    last = nc.tensor.matmul(psS[:, m // 2, (m % 2) * KW + lo:(m % 2 + 1) * KW], qT[r, m % 4, t * P:(t + 1) * P],
                                            kT[r, m % 4, t * P - 64 + lo:(t + 1) * P], start=True, stop=True)
                last.then_inc(S["qk_done"], 1)

            def trans(t):
                for j in range(4):
                    n = 4 * t + j
                    if n >= 2:
                        pe.wait_ge(S["dve_evac" if n % 2 == 0 else "act_evac"], (n - 2) // 2 + 1)
                    pe.wait_ge(S["exp_done"], H * t + 2 * j + 2)
                    for i in range(4):
                        last = nc.tensor.transpose(psT[:, n % 2, i * P:(i + 1) * P], prob[:, t % 2, 2 * j + i // 2, (i % 2) * P:(i % 2 + 1) * P], K.ident[:, :])
                    last.then_inc(S["trans_done"], 1)

            def pv(t):
                pe.wait_ge(S["dve_evac"], 2 * (t + 1))
                pe.wait_ge(S["act_evac"], 2 * (t + 1))
                if t >= 1:
                    pe.wait_ge(S["z_ready"], t)
                for m in range(H):
                    hs = slice(head[m] * DH, head[m] * DH + DH)
                    if t >= 1:
                        nc.tensor.matmul(psZ[:, hs], probT[:, t % 2, 2 * m, :], V[:, t - 1, hs], start=True, stop=False)
                    last = nc.tensor.matmul(psZ[:, hs], probT[:, t % 2, 2 * m + 1, :], V[:, t, hs], start=(t == 0), stop=True)
                last.then_inc(S["pv_done"], 1)

            def turn_z(t):
                pe.wait_ge(S["z_ready"], t + 1)
                if t >= 1:
                    pe.wait_ge(S["out_added"], t)
                for j in range(4):
                    last = nc.tensor.transpose(psO[:, j * P:(j + 1) * P], z[:, t % 2, 2 * j:2 * j + 2, :].rearrange("p h d -> p (h d)"), K.ident[:, :])
                last.then_inc(S["zt_done"], 1)

            def project(t):
                pe.wait_ge(S["zt_evac"], t + 1)
                for j in range(4):
                    last = nc.tensor.matmul(psO[:, 0:D], zT[:, j, :], wo[:, j, :], start=(j == 0), stop=(j == 3))
                last.then_inc(S["out_done"], 1)

            pe.wait_ge(S["loaded"], 16)
            for s in range(NT + 3):
                if s < NT:
                    scores(s)
                if 0 <= s - 3 < NT:
                    turn_z(s - 3)
                if 0 <= s - 2 < NT:
                    pv(s - 2)
                if 0 <= s - 3 < NT:
                    project(s - 3)
                if 0 <= s - 1 < NT:
                    trans(s - 1)

        def evacuate(eng, t, odd):
            if t >= 2:
                eng.wait_ge(S["pv_done"], t - 1)
            for j in range(odd, 4, 2):
                n = 4 * t + j
                eng.wait_ge(S["trans_done"], n + 1)
                out, src = probT[:, t % 2, 4 * j:4 * j + 4, :].rearrange("p a n -> p (a n)"), psT[:, n % 2, :]
                if odd:
                    nc.scalar.copy(out, src).then_inc(S["act_evac"], 1)
                else:
                    nc.vector.tensor_copy(out, src).then_inc(S["dve_evac"], 1)

        @block.scalar
        def _(act):
            for s in range(NT + 3):
                if s < NT:
                    act.wait_ge(S["nb_ready"], s + 1)
                    if s >= 2:
                        act.wait_ge(S["trans_done"], 4 * (s - 1))
                        act.wait_ge(S["rden_ready"], s - 1)
                    if s < 2:
                        act.wait_ge(S["zeroed"], 2)
                    for m in range(H):
                        nc.scalar.activation(prob[:, s % 2, m, 64:2 * P], sm[:, s % 2, m, :], ACT.Exp, scale=rn[:, s, head[m]:head[m] + 1],
                                             bias=nb[:, s % 2, m:m + 1], accum_out=den[:, s % 2, m:m + 1]).then_inc(S["exp_done"], 1)
                if 0 <= s - 3 < NT:
                    act.wait_ge(S["zt_done"], s - 2)
                    nc.scalar.copy(zT[:, :, :].rearrange("p j n -> p (j n)"), psO[:, :]).then_inc(S["zt_evac"], 1)
                if 0 <= s - 1 < NT:
                    evacuate(act, s - 1, 1)

        @block.vector
        def _(dve):
            dve.wait_ge(S["mask_ready"], 1)
            for s in range(NT + 3):
                if s < NT:
                    dve.wait_ge(S["qk_done"], s + 1)
                    if s >= 2:
                        dve.wait_ge(S["exp_done"], H * (s - 1))
                    smv = sm[:, s % 2, :, :].rearrange("p (b a) k -> p b a k", a=2)
                    lo = 64 if s == 0 else 0
                    if s == 0:
                        nc.vector.tensor_copy(sm[:, 0, :, 0:64], bcast(mask[:, 0:1, 0:64], [P, H, 64]))
                    nc.vector.tensor_tensor(smv[:, :, :, lo:], psS[:, :, 0:2 * KW].rearrange("p b (a k) -> p b a k", a=2)[:, :, :, lo:],
                                            bcast(mask[:, min(s, 1), lo:].unsqueeze(1).unsqueeze(1), [P, 4, 2, KW - lo]), ALU.add).then_inc(S["masked"], 1)
                    dve.wait_ge(S["masked"], s + 1)
                    nc.vector.tensor_reduce(mx[:, s % 2, :], sm[:, s % 2, :, :], axis=AX_X, op=ALU.max).then_inc(S["max_ready"], 1)
                    dve.wait_ge(S["max_ready"], s + 1)
                    nc.vector.scalar_tensor_tensor(out=nb[:, s % 2, :].rearrange("p (o a) -> p o a", o=2), in0=mx[:, s % 2, :].rearrange("p (o a) -> p o a", o=2),
                                                   scalar=-1.0, in1=rn[:, s, 0:H].rearrange("p (a o) -> p o a", o=2), op0=ALU.mult, op1=ALU.mult).then_inc(S["nb_ready"], 1)
                if 0 <= s - 2 < NT:
                    t = s - 2
                    dve.wait_ge(S["exp_done"], H * (t + 1))
                    nc.vector.reciprocal(rden[:, t % 2, :].rearrange("p (a o) -> p o a", o=2), den[:, t % 2, :].rearrange("p (o a) -> p o a", o=2)).then_inc(S["rden_ready"], 1)
                    dve.wait_ge(S["rden_ready"], t + 1)
                    dve.wait_ge(S["pv_done"], t + 1)
                    if t >= 2:
                        dve.wait_ge(S["zt_done"], t - 1)
                    nc.vector.tensor_tensor(z[:, t % 2, :, :], psZ[:, :].rearrange("p (h d) -> p h d", d=DH), bcast(rden[:, t % 2, :].unsqueeze(2), [P, H, DH]),
                                            ALU.mult).then_inc(S["z_ready"], 1)
                if 0 <= s - 1 < NT:
                    evacuate(dve, s - 1, 0)
                if 0 <= s - 3 < NT:
                    t = s - 3
                    dve.wait_ge(S["out_done"], t + 1)
                    nc.vector.tensor_tensor(Y[:, t, :], Y[:, t, :], psO[:, 0:D], ALU.add).then_inc(S["out_added"], 1)


@scoped
def l2_geglu(nc, sp, K, W, l, Y):
    HID = 341
    FC = 3
    rows = [min(P, HID - c * P) for c in range(FC)]
    h = sp.sb("shifted", [P, NT, D])
    hn = sp.sb("normed", [P, NT, D])
    hT = sp.sb("hT", [P, T])
    w1 = sp.sb("w1", [P, 2 * HID])
    w2 = sp.sb("w2", [P, FC, D])
    b1 = sp.sb("b1", [P, 2, FC])
    b2 = sp.sb("b2", [P, D])
    ln = sp.sb("ln", [P, 2])
    g = sp.sb("gelu", [P, 2, BANK])
    hid = sp.sb("hidden", [P, 2, FC, BANK])
    loaded = sp.sem("loaded")
    with nc.Block() as block:
        @block.sync
        def _(sync):
            sync.dma_start(w1[:, :], W["L2_ffn_w1"][bass.ds(l, 1), :, :].rearrange("a d n -> (a d) n")).then_inc(loaded, 16)
            for c in range(FC):
                sync.dma_start(w2[0:rows[c], c, :], W["L2_ffn_w2"][bass.ds(l, 1), c * P:c * P + rows[c], :].rearrange("a f n -> (a f) n")).then_inc(loaded, 16)
            sync.dma_start(b1[:, :, :], W["L2_ffn_b1"][bass.ds(l, 1), :, :, :].rearrange("a p g c -> (a p) g c")).then_inc(loaded, 16)
            sync.dma_start(b2[:, :], W["L2_ffn_b2"][bass.ds(l, 1), :].rearrange("a d -> (a d)").partition_broadcast(P)).then_inc(loaded, 16)
            sync.dma_start(ln[:, :], W["l2_ln"][bass.ds(l, 1), :, :].rearrange("a d g -> (a d) g")).then_inc(loaded, 16)
            sync.wait_ge(loaded, 16 * 7)
    shift_tokens(nc, Y, h)
    layernorm(nc, K, h, hn)
    transpose_tokens(nc, K, hn, hT, ln[:, 0:1], ln[:, 1:2])
    psA = sp.ps("a", [P, 2, BANK])
    psG = sp.ps("g", [P, 2, BANK])
    psY = sp.ps("y", [P, 2, BANK])
    S = {n: sp.sem(n) for n in "ag_ready gelu_done hid_done y_ready b2_added y_added".split()}
    n_items = NB * FC
    with nc.Block() as block:
        @block.tensor
        def _(pe):
            def down(b):
                pe.wait_ge(S["hid_done"], (b + 1) * FC)
                if b >= 2:
                    pe.wait_ge(S["y_added"], b - 1)
                for j in range(TPB):
                    for c in range(FC):
                        last = nc.tensor.matmul(psY[:, b % 2, j * D:(j + 1) * D], hid[0:rows[c], b % 2, c, j * P:(j + 1) * P], w2[0:rows[c], c, :],
                                                start=(c == 0), stop=(c == FC - 1))
                last.then_inc(S["y_ready"], 1)

            for n in range(n_items):
                b, c = n // FC, n % FC
                if n >= 2:
                    pe.wait_ge(S["hid_done"], n - 1)
                for i, ps in enumerate((psA, psG)):
                    last = nc.tensor.matmul(ps[0:rows[c], n % 2, :], w1[:, i * HID + c * P:i * HID + c * P + rows[c]], hT[:, b * BANK:(b + 1) * BANK],
                                            start=True, stop=True)
                last.then_inc(S["ag_ready"], 1)
                if c == 0 and b >= 1:
                    down(b - 1)
            down(NB - 1)

        @block.scalar
        def _(act):
            for n in range(n_items):
                c = n % FC
                act.wait_ge(S["ag_ready"], n + 1)
                if n >= 2:
                    act.wait_ge(S["hid_done"], n - 1)
                nc.scalar.activation(g[0:rows[c], n % 2, :], psG[0:rows[c], n % 2, :], ACT.Gelu, bias=b1[0:rows[c], 1, c:c + 1]).then_inc(S["gelu_done"], 1)

        @block.vector
        def _(dve):
            def add(b):
                yb = Y[:, b * TPB:(b + 1) * TPB, :]
                nc.vector.tensor_tensor(yb, yb, bcast(b2[:, :].unsqueeze(1), [P, TPB, D]), ALU.add).then_inc(S["b2_added"], 1)
                dve.wait_ge(S["b2_added"], b + 1)
                dve.wait_ge(S["y_ready"], b + 1)
                nc.vector.tensor_tensor(yb, yb, psY[:, b % 2, :].rearrange("p (t n) -> p t n", n=D), ALU.add).then_inc(S["y_added"], 1)

            for n in range(n_items):
                b, c = n // FC, n % FC
                dve.wait_ge(S["gelu_done"], n + 1)
                if c == 0 and b >= 2:
                    dve.wait_ge(S["y_ready"], b - 1)
                nc.vector.scalar_tensor_tensor(out=hid[0:rows[c], b % 2, c, :], in0=psA[0:rows[c], n % 2, :], scalar=b1[0:rows[c], 0, c:c + 1],
                                               in1=g[0:rows[c], n % 2, :], op0=ALU.add, op1=ALU.mult).then_inc(S["hid_done"], 1)
                if c == 0 and b >= 1:
                    add(b - 1)
            add(NB - 1)


def l3_mixer(nc, X, K, W):
    DI, NS, NH, HD = 256, 64, 8, 32
    with sublayer(nc) as sp:
        xn = sp.sb("xn", [P, NT, D])
        Yo = sp.sb("mixed", [P, NT, DI])
        with sublayer(nc) as inner:
            xT = inner.sb("xT", [P, T])
            w_in = inner.sb("w_in", [P, 648])
            layernorm(nc, K, X, xn)
            transpose_tokens(nc, K, xn, xT)
            gate = inner.sb("silu_z", [P, NT, DI])
            dt = inner.sb("dt", [P, NT, NH])
            a = inner.sb("log_decay", [P, NT, NH])
            xs = inner.sb("x_tokens", [P, NT, DI])
            Bt = inner.sb("B_tokens", [P, NT, NS])
            BC = inner.sb("BC", [P, T])
            CT = inner.sb("CT", [NS, T])
            l3_gate_dt(nc, K, W, xT, w_in, gate, dt, a, NH)
            with sublayer(nc) as conv:
                xc = [conv.sb(f"x_conv{i}", [P, T]) for i in range(2)] + [BC]
                l3_conv(nc, K, W, xT, w_in, xc)
                l3_turn(nc, K, xc, xs, Bt, CT)
            l3_scan(nc, K, W, dt, a, xs, Bt, BC, CT, Yo, NS, NH, HD)
            with nc.Block() as block:
                @block.vector
                def _(dve):
                    nc.vector.tensor_tensor(Yo[:, 0:NT // 2, :], Yo[:, 0:NT // 2, :], gate[:, 0:NT // 2, :], ALU.mult)

                @block.gpsimd
                def _(pool):
                    nc.gpsimd.tensor_tensor(Yo[:, NT // 2:, :], Yo[:, NT // 2:, :], gate[:, NT // 2:, :], ALU.mult)
        Z = sp.sb("squashed", [P, NT, D])
        l3_out(nc, K, W, Yo, Z)
        rows = sp.sb("b_nl", [P, D])
        loaded = sp.sem("b_loaded")
        added = sp.sem("x_added")
        with nc.Block() as block:
            @block.sync
            def _(sync):
                sync.dma_start(rows[:, :], W["L3_attn_b_nl"].partition_broadcast(P)).then_inc(loaded, 16)

            @block.vector
            def _(dve):
                nc.vector.tensor_tensor(X[:, :, :], X[:, :, :], xn[:, :, :], ALU.add).then_inc(added, 1)
                dve.wait_ge(added, 1)
                dve.wait_ge(loaded, 16)
                nc.vector.tensor_tensor(X[:, :, :], X[:, :, :], bcast(rows[:, :].unsqueeze(1), [P, NT, D]), ALU.add)
        project_add(nc, K, Z, W["L3_attn_W_nl"], X)


@scoped
def l3_gate_dt(nc, sp, K, W, xT, w_in, gate, dt, a, NH):
    SERIES = [1.0 / (2 * i + 1) for i in range(8)]
    rows = sp.sb("bias_and_alog", [P, 2, NH])
    nexpA = sp.sb("exp_A_log", [P, NH])
    N = NT * NH
    d = {n: sp.sb(n, [P, N]) for n in "raw absd u den rden z z2 acc lin pos".split()}
    sig = sp.sb("sigmoid", [P, 2, 2, 256])
    psZ = sp.ps("z", [P, 2, BANK])
    psD = sp.ps("dt", [P, BANK])
    S = {n: sp.sem(n) for n in "loaded z_ready sig_done gate_done d_ready raw_ready abs_done u_done expA_done step".split()}
    with nc.Block() as block:
        @block.sync
        def _(sync):
            sync.dma_start(w_in[:, :], W["L3_attn_W_in"]).then_inc(S["loaded"], 16)
            sync.dma_start(rows[:, 0, :], W["L3_attn_dt_bias"].partition_broadcast(P)).then_inc(S["loaded"], 16)
            sync.dma_start(rows[:, 1, :], W["L3_attn_A_log"].partition_broadcast(P)).then_inc(S["loaded"], 16)

        @block.tensor
        def _(pe):
            pe.wait_ge(S["loaded"], 48)
            for t in range(NT):
                last = nc.tensor.matmul(psD[:, t * NH:(t + 1) * NH], xT[:, t * P:(t + 1) * P], w_in[:, 640:648], start=True, stop=True)
            last.then_inc(S["d_ready"], 1)
            for n in range(NT // 2):
                if n >= 2:
                    pe.wait_ge(S["gate_done"], n - 1)
                for j in range(2):
                    t = 2 * n + j
                    last = nc.tensor.matmul(psZ[:, n % 2, j * 256:(j + 1) * 256], xT[:, t * P:(t + 1) * P], w_in[:, 0:256], start=True, stop=True)
                last.then_inc(S["z_ready"], 1)

        @block.scalar
        def _(act):
            act.wait_ge(S["loaded"], 48)
            nc.scalar.activation(nexpA[:, :], rows[:, 1, :], ACT.Exp).then_inc(S["expA_done"], 1)
            act.wait_ge(S["raw_ready"], 1)
            nc.scalar.activation(d["absd"][:, :], d["raw"][:, :], ACT.Abs).then_inc(S["abs_done"], 1)
            act.wait_ge(S["abs_done"], 1)
            nc.scalar.activation(d["u"][:, :], d["absd"][:, :], ACT.Exp, scale=-1.0).then_inc(S["u_done"], 1)
            for n in range(NT // 2):
                act.wait_ge(S["z_ready"], n + 1)
                if n >= 2:
                    act.wait_ge(S["gate_done"], n - 1)
                nc.scalar.activation(sig[:, n % 2, :, :].rearrange("p t n -> p (t n)"), psZ[:, n % 2, :], ACT.Sigmoid).then_inc(S["sig_done"], 1)

        @block.vector
        def _(dve):
            steps = [0]

            def done(ins):
                steps[0] += 1
                ins.then_inc(S["step"], 1)
                dve.wait_ge(S["step"], steps[0])

            V = nc.vector
            dve.wait_ge(S["d_ready"], 1)
            dve.wait_ge(S["loaded"], 48)
            V.tensor_tensor(d["raw"][:, :].rearrange("p (t h) -> p t h", h=NH), psD[:, 0:N].rearrange("p (t h) -> p t h", h=NH),
                            bcast(rows[:, 0:1, :], [P, NT, NH]), ALU.add).then_inc(S["raw_ready"], 1)
            dve.wait_ge(S["u_done"], 1)
            done(V.tensor_scalar(d["den"][:, :], d["u"][:, :], 2.0, None, ALU.add))
            done(V.reciprocal(d["rden"][:, :], d["den"][:, :]))
            done(V.tensor_tensor(d["z"][:, :], d["u"][:, :], d["rden"][:, :], ALU.mult))
            done(V.tensor_tensor(d["z2"][:, :], d["z"][:, :], d["z"][:, :], ALU.mult))
            done(V.tensor_scalar(d["acc"][:, :], d["z2"][:, :], SERIES[7], SERIES[6], ALU.mult, ALU.add))
            for c in SERIES[5::-1]:
                done(V.tensor_tensor(d["lin"][:, :], d["acc"][:, :], d["z2"][:, :], ALU.mult))
                done(V.tensor_scalar(d["acc"][:, :], d["lin"][:, :], c, None, ALU.add))
            done(V.scalar_tensor_tensor(out=d["lin"][:, :], in0=d["acc"][:, :], scalar=2.0, in1=d["z"][:, :], op0=ALU.mult, op1=ALU.mult))
            done(V.tensor_scalar(d["pos"][:, :], d["raw"][:, :], 0.0, None, ALU.max))
            flat = dt[:, :, :].rearrange("p t h -> p (t h)")
            done(V.tensor_tensor(flat, d["pos"][:, :], d["lin"][:, :], ALU.add))
            dve.wait_ge(S["expA_done"], 1)
            V.scalar_tensor_tensor(out=a[:, :, :], in0=dt[:, :, :], scalar=-1.0, in1=bcast(nexpA[:, :].unsqueeze(1), [P, NT, NH]), op0=ALU.mult, op1=ALU.mult)
            for n in range(NT // 2):
                dve.wait_ge(S["sig_done"], n + 1)
                V.tensor_tensor(gate[:, 2 * n:2 * n + 2, :].rearrange("p t n -> p (t n)"), sig[:, n % 2, :, :].rearrange("p t n -> p (t n)"), psZ[:, n % 2, :],
                                ALU.mult).then_inc(S["gate_done"], 1)


@scoped
def l3_conv(nc, sp, K, W, xT, w_in, xc):
    TAPS = 16
    PAD = TAPS - 1
    cw = sp.sb("conv_w", [P, 3, TAPS])
    cb = sp.sb("conv_b", [P, 3])
    diag = sp.sb("tap_diagonals", [P, 2, TAPS, P])
    xp = [sp.sb(f"padded{c}", [P, PAD + T]) for c in range(3)]
    acc = sp.sb("acc", [P, 2, T])
    sig = sp.sb("sigmoid", [P, 2, BANK])
    sig2 = acc[:, TAPS % 2, :]
    psP = sp.ps("proj", [P, 4, BANK])
    psC = sp.ps("conv", [P, 4, BANK])
    S = {n: sp.sem(n) for n in "loaded padded proj_ready act_copied dve_copied diag_ready conv_ready sig_done silu_done tap bc_sig".split()}
    order = [2, 0, 1]
    with nc.Block() as block:
        @block.sync
        def _(sync):
            sync.dma_start(cw[:, :, :], W["L3_attn_conv_w"].rearrange("(c p) k -> p c k", p=P)).then_inc(S["loaded"], 16)
            sync.dma_start(cb[:, :], W["L3_attn_conv_b"]).then_inc(S["loaded"], 16)

        @block.tensor
        def _(pe):
            for n in range(3 * NB):
                c, b = order[n // NB], n % NB
                if n >= 4:
                    pe.wait_ge(S["act_copied"], n - 3)
                nc.tensor.matmul(psP[:, n % 4, :], w_in[:, 256 + c * P:256 + (c + 1) * P], xT[:, b * BANK:(b + 1) * BANK], start=True, stop=True).then_inc(S["proj_ready"], 1)
            for n in range(2 * NB):
                c, b = n // NB, n % NB
                pe.wait_ge(S["act_copied"], NB + n + 1)
                pe.wait_ge(S["diag_ready"], TAPS * (c + 1))
                if n >= 4:
                    pe.wait_ge(S["silu_done"], n - 3)
                for k in range(TAPS):
                    last = nc.tensor.matmul(psC[:, n % 4, :], diag[:, c, k, :], xp[c][:, k + b * BANK:k + (b + 1) * BANK], start=(k == 0), stop=(k == TAPS - 1))
                last.then_inc(S["conv_ready"], 1)

        @block.gpsimd
        def _(pool):
            for c in range(3):
                last = nc.gpsimd.memset(xp[c][:, 0:PAD], 0.0)
            last.then_inc(S["padded"], 1)
            pool.wait_ge(S["loaded"], 32)
            for c in range(2):
                for k in range(TAPS):
                    nc.gpsimd.tensor_scalar(diag[:, c, k, :], K.ident[:, :], cw[:, c, k:k + 1], 1.0, ALU.mult, ALU.mult).then_inc(S["diag_ready"], 1)

        @block.scalar
        def _(act):
            act.wait_ge(S["padded"], 1)
            for n in range(3 * NB):
                c, b = order[n // NB], n % NB
                act.wait_ge(S["proj_ready"], n + 1)
                nc.scalar.copy(xp[c][:, PAD + b * BANK:PAD + (b + 1) * BANK], psP[:, n % 4, :]).then_inc(S["act_copied"], 1)
            act.wait_ge(S["loaded"], 32)
            for n in range(2 * NB):
                act.wait_ge(S["conv_ready"], n + 1)
                if n >= 2:
                    act.wait_ge(S["silu_done"], n - 1)
                if n == 4:
                    act.wait_ge(S["tap"], TAPS)
                    nc.scalar.activation(sig2, acc[:, (TAPS - 1) % 2, :], ACT.Sigmoid, bias=cb[:, 2:3]).then_inc(S["bc_sig"], 1)
                nc.scalar.activation(sig[:, n % 2, :], psC[:, n % 4, :], ACT.Sigmoid, bias=cb[:, n // NB:n // NB + 1]).then_inc(S["sig_done"], 1)

        @block.vector
        def _(dve):
            dve.wait_ge(S["loaded"], 32)
            dve.wait_ge(S["act_copied"], NB)
            for k in range(TAPS):
                src = xp[2][:, k:k + T]
                if k == 0:
                    nc.vector.tensor_scalar(acc[:, 0, :], src, cw[:, 2, 0:1], None, ALU.mult).then_inc(S["tap"], 1)
                else:
                    dve.wait_ge(S["tap"], k)
                    nc.vector.scalar_tensor_tensor(out=acc[:, k % 2, :], in0=src, scalar=cw[:, 2, k:k + 1], in1=acc[:, (k - 1) % 2, :],
                                                   op0=ALU.mult, op1=ALU.add).then_inc(S["tap"], 1)
            for n in range(2 * NB):
                c, b = n // NB, n % NB
                dve.wait_ge(S["sig_done"], n + 1)
                nc.vector.scalar_tensor_tensor(out=xc[c][:, b * BANK:(b + 1) * BANK], in0=psC[:, n % 4, :], scalar=cb[:, c:c + 1], in1=sig[:, n % 2, :],
                                               op0=ALU.add, op1=ALU.mult).then_inc(S["silu_done"], 1)
            dve.wait_ge(S["bc_sig"], 1)
            nc.vector.scalar_tensor_tensor(out=xc[2][:, :], in0=acc[:, (TAPS - 1) % 2, :], scalar=cb[:, 2:3], in1=sig2, op0=ALU.add, op1=ALU.mult)


@scoped
def l3_turn(nc, sp, K, xc, xs, Bt, CT):
    NS = 64
    ps = sp.ps("turned", [P, 2, BANK])
    S = {n: sp.sem(n) for n in "c_moved turned copied".split()}
    with nc.Block() as block:
        @block.sync
        def _(sync):
            sync.dma_start(CT[:, :], xc[2][NS:P, :]).then_inc(S["c_moved"], 16)
            sync.wait_ge(S["c_moved"], 16)

        @block.tensor
        def _(pe):
            for t in range(NT):
                if t >= 2:
                    pe.wait_ge(S["copied"], 2 * (t - 1))
                for c in range(3):
                    last = nc.tensor.transpose(ps[:, t % 2, c * P:(c + 1) * P], xc[c][:, t * P:(t + 1) * P], K.ident[:, :])
                last.then_inc(S["turned"], 1)

        @block.vector
        def _(dve):
            for t in range(NT):
                dve.wait_ge(S["turned"], t + 1)
                nc.vector.tensor_copy(xs[:, t, :], ps[:, t % 2, 0:256]).then_inc(S["copied"], 1)
                nc.vector.tensor_copy(Bt[:, t, :], ps[:, t % 2, 256:256 + NS]).then_inc(S["copied"], 1)


@scoped
def l3_scan(nc, sp, K, W, dt, a, xs, Bt, BC, CT, Y, NS, NH, HD):
    DI = NH * HD
    after = sp.sb("after", [P, P])
    drow = sp.sb("D", [P, NH])
    state = sp.sb("state", [NS, 2, DI])
    decayed = sp.sb("state_decayed", [NS, DI])
    aU = sp.sb("a_upto", [P, 2, NH, P])
    E = sp.sb("decays", [P, 2, NH, P])
    MT = sp.sb("mixing", [P, 2, NH, P])
    Gm = sp.sb("CB_masked", [P, 2, P])
    ecum = sp.sb("decay_from_start", [P, 2, NH])
    edec = sp.sb("chunk_decay", [NS, 2, NH])
    xdt = sp.sb("x_dt", [P, 2, DI])
    xw = sp.sb("x_dt_to_end", [P, 2, DI])
    off = sp.sb("from_state", [P, 2, DI])
    psE = sp.ps("sums_between", [P, 2, 2, BANK])
    psG = sp.ps("CB_and_sums", [P, BANK])
    psD = sp.ps("within", [P, BANK])
    psO = sp.ps("from_state", [P, BANK])
    psS = sp.ps("state", [P, BANK])
    names = ("loaded after_ready aU_ready xdt_ready skip_ready seg_ready g_ready e_done small_exp gm_ready mt_ready xw_ready within_ready off_ready "
             "state_ready off_scaled off_added within_added decayed updated").split()
    S = {n: sp.sem(n) for n in names}
    heads = "p (h d) -> p h d"
    with nc.Block() as block:
        @block.sync
        def _(sync):
            sync.dma_start(drow[:, :], W["L3_attn_D"].partition_broadcast(P)).then_inc(S["loaded"], 16)
            sync.dma_start(state[:, 0, :], W["L3_attn_init_states"]).then_inc(S["loaded"], 16)

        @block.gpsimd
        def _(pool):
            nc.gpsimd.affine_select(out=after[:, :], in_=K.ones[:, :], compare_op=ALU.is_gt, fill=0.0, base=0, pattern=[[-1, P]],
                                    channel_multiplier=1).then_inc(S["after_ready"], 1)
            pool.wait_ge(S["loaded"], 32)
            for q in range(NT):
                if q >= 2:
                    pool.wait_ge(S["seg_ready"], q - 1)
                nc.gpsimd.tensor_tensor(aU[:, q % 2, :, :], bcast(K.causal_k[:, :].unsqueeze(1), [P, NH, P]), bcast(a[:, q, :].unsqueeze(2), [P, NH, P]),
                                        ALU.mult).then_inc(S["aU_ready"], 1)
                if q >= 2:
                    pool.wait_ge(S["within_ready"], q - 1)
                    pool.wait_ge(S["xw_ready"], q - 1)
                nc.gpsimd.tensor_tensor(xdt[:, q % 2, :].rearrange(heads, h=NH), xs[:, q, :].rearrange(heads, h=NH), bcast(dt[:, q, :].unsqueeze(2), [P, NH, HD]),
                                        ALU.mult).then_inc(S["xdt_ready"], 1)
                nc.gpsimd.tensor_tensor(Y[:, q, :].rearrange(heads, h=NH), xs[:, q, :].rearrange(heads, h=NH), bcast(drow[:, :].unsqueeze(2), [P, NH, HD]),
                                        ALU.mult).then_inc(S["skip_ready"], 1)

        @block.tensor
        def _(pe):
            pe.wait_ge(S["after_ready"], 1)
            pe.wait_ge(S["loaded"], 32)

            def sums(q):
                pe.wait_ge(S["aU_ready"], q + 1)
                if q >= 2:
                    pe.wait_ge(S["e_done"], q - 1)
                for i in range(2):
                    last = nc.tensor.matmul(psE[:, q % 2, i, :], after[:, :], aU[:, q % 2, 4 * i:4 * i + 4, :].rearrange("p h t -> p (h t)"), start=True, stop=True)
                last.then_inc(S["seg_ready"], 1)
                if q >= 1:
                    pe.wait_ge(S["gm_ready"], q)
                    pe.wait_ge(S["small_exp"], 2 * q)
                cols = slice(q * P, (q + 1) * P)
                nc.tensor.matmul(psG[:, 0:P], BC[0:NS, cols], CT[:, cols], start=True, stop=True)
                nc.tensor.matmul(psG[:, P:P + NH], K.causal_k[:, :], a[:, q, :], start=True, stop=True)
                nc.tensor.matmul(psG[0:NS, P + 16:P + 16 + NH], K.ones[:, 0:NS], a[:, q, :], start=True, stop=True).then_inc(S["g_ready"], 1)

            def outputs(q):
                cols = slice(q * P, (q + 1) * P)
                if q >= 1:
                    pe.wait_ge(S["updated"], q)
                    pe.wait_ge(S["off_scaled"], q)
                nc.tensor.matmul(psO[:, 0:DI], CT[:, cols], state[:, q % 2, :], start=True, stop=True).then_inc(S["off_ready"], 1)
                pe.wait_ge(S["xw_ready"], q + 1)
                nc.tensor.matmul(psS[0:NS, 0:DI], Bt[:, q, :], xw[:, q % 2, :], start=True, stop=True).then_inc(S["state_ready"], 1)
                pe.wait_ge(S["mt_ready"], q + 1)
                if q >= 1:
                    pe.wait_ge(S["within_added"], q)
                for h in range(NH):
                    last = nc.tensor.matmul(psD[:, h * HD:(h + 1) * HD], MT[:, q % 2, h, :], xdt[:, q % 2, h * HD:(h + 1) * HD], start=True, stop=True)
                last.then_inc(S["within_ready"], 1)

            for s in range(NT + 1):
                if s < NT:
                    sums(s)
                if s >= 1:
                    outputs(s - 1)

        @block.scalar
        def _(act):
            for q in range(NT):
                act.wait_ge(S["seg_ready"], q + 1)
                if q >= 2:
                    act.wait_ge(S["mt_ready"], q - 1)
                    act.wait_ge(S["xw_ready"], q - 1)
                nc.scalar.activation(E[:, q % 2, :, :].rearrange("p h t -> p (h t)"), psE[:, q % 2, :, :].rearrange("p i n -> p (i n)"), ACT.Exp).then_inc(S["e_done"], 1)
                act.wait_ge(S["g_ready"], q + 1)
                act.wait_ge(S["gm_ready"], q + 1)
                if q >= 2:
                    act.wait_ge(S["off_scaled"], q - 1)
                    act.wait_ge(S["decayed"], q - 1)
                nc.scalar.activation(ecum[:, q % 2, :], psG[:, P:P + NH], ACT.Exp).then_inc(S["small_exp"], 1)
                nc.scalar.activation(edec[:, q % 2, :], psG[0:NS, P + 16:P + 16 + NH], ACT.Exp).then_inc(S["small_exp"], 1)

        @block.vector
        def _(dve):
            for q in range(NT):
                dve.wait_ge(S["g_ready"], q + 1)
                nc.vector.tensor_tensor(Gm[:, q % 2, :], psG[:, 0:P], K.causal_k[:, :], ALU.mult).then_inc(S["gm_ready"], 1)
                dve.wait_ge(S["e_done"], q + 1)
                dve.wait_ge(S["xdt_ready"], q + 1)
                nc.vector.tensor_tensor(xw[:, q % 2, :].rearrange(heads, h=NH), xdt[:, q % 2, :].rearrange(heads, h=NH),
                                        bcast(E[:, q % 2, :, P - 1:P], [P, NH, HD]), ALU.mult).then_inc(S["xw_ready"], 1)
                dve.wait_ge(S["gm_ready"], q + 1)
                if q >= 2:
                    dve.wait_ge(S["within_ready"], q - 1)
                nc.vector.tensor_tensor(MT[:, q % 2, :, :], E[:, q % 2, :, :], bcast(Gm[:, q % 2, :].unsqueeze(1), [P, NH, P]), ALU.mult).then_inc(S["mt_ready"], 1)
                dve.wait_ge(S["small_exp"], 2 * (q + 1))
                nc.vector.tensor_tensor(decayed[:, :].rearrange(heads, h=NH), state[:, q % 2, :].rearrange(heads, h=NH),
                                        bcast(edec[:, q % 2, :].unsqueeze(2), [NS, NH, HD]), ALU.mult).then_inc(S["decayed"], 1)
                dve.wait_ge(S["decayed"], q + 1)
                dve.wait_ge(S["state_ready"], q + 1)
                nc.vector.tensor_tensor(state[:, (q + 1) % 2, :], decayed[:, :], psS[0:NS, 0:DI], ALU.add).then_inc(S["updated"], 1)
                dve.wait_ge(S["off_ready"], q + 1)
                nc.vector.tensor_tensor(off[:, q % 2, :].rearrange(heads, h=NH), psO[:, 0:DI].rearrange(heads, h=NH),
                                        bcast(ecum[:, q % 2, :].unsqueeze(2), [P, NH, HD]), ALU.mult).then_inc(S["off_scaled"], 1)
                dve.wait_ge(S["off_scaled"], q + 1)
                dve.wait_ge(S["skip_ready"], q + 1)
                nc.vector.tensor_tensor(Y[:, q, :], Y[:, q, :], off[:, q % 2, :], ALU.add).then_inc(S["off_added"], 1)
                dve.wait_ge(S["off_added"], q + 1)
                dve.wait_ge(S["within_ready"], q + 1)
                nc.vector.tensor_tensor(Y[:, q, :], Y[:, q, :], psD[:, 0:DI], ALU.add).then_inc(S["within_added"], 1)


@scoped
def l3_out(nc, sp, K, W, Y, Z):
    DI = 256
    wo = sp.sb("w_out", [P, 2, D])
    nw = sp.sb("norm_w", [P, 2])
    sq = sp.sb("squares", [P, 2, DI])
    ms = sp.sb("mean_square", [P, 3, NT])
    yT = sp.sb("yT", [P, 2, 2, P])
    y = sp.sb("y", [P, NT, D])
    q = sp.sb("y_squares", [P, NT * D])
    root = sp.sb("root", [P, NT * D])
    psT = sp.ps("turned", [P, 2, BANK])
    psY = sp.ps("y", [P, 2, BANK])
    S = {n: sp.sem(n) for n in "loaded ms_ready root_ready r_ready turned copied y_ready y_scaled sq_done sqrt_done recip_done".split()}
    with nc.Block() as block:
        @block.sync
        def _(sync):
            sync.dma_start(wo[:, :, :], W["L3_attn_W_out"].rearrange("(c f) n -> f c n", f=P)).then_inc(S["loaded"], 16)
            sync.dma_start(nw[:, :], W["L3_attn_norm_w"]).then_inc(S["loaded"], 16)

        @block.tensor
        def _(pe):
            pe.wait_ge(S["loaded"], 32)

            def out(t):
                pe.wait_ge(S["copied"], 2 * (t + 1))
                if t >= 2:
                    pe.wait_ge(S["y_scaled"], t - 1)
                for c in range(2):
                    last = nc.tensor.matmul(psY[:, t % 2, 0:D], yT[:, t % 2, c, :], wo[:, c, :], start=(c == 0), stop=(c == 1))
                last.then_inc(S["y_ready"], 1)

            for t in range(NT):
                if t >= 2:
                    pe.wait_ge(S["copied"], 2 * (t - 1))
                for c in range(2):
                    last = nc.tensor.transpose(psT[:, t % 2, c * P:(c + 1) * P], Y[:, t, c * P:(c + 1) * P], K.ident[:, :])
                last.then_inc(S["turned"], 1)
                if t >= 1:
                    out(t - 1)
            out(NT - 1)

        @block.scalar
        def _(act):
            for t in range(NT):
                if t >= 2:
                    act.wait_ge(S["ms_ready"], t - 1)
                nc.scalar.activation(sq[:, t % 2, :], Y[:, t, :], ACT.Square, accum_out=ms[:, 0, t:t + 1]).then_inc(S["ms_ready"], 1)
            act.wait_ge(S["ms_ready"], NT)
            nc.scalar.activation(ms[:, 1, :], ms[:, 0, :], ACT.Sqrt, scale=1.0 / DI, bias=K.eps[:, 0:1]).then_inc(S["root_ready"], 1)
            act.wait_ge(S["r_ready"], 1)
            for t in range(NT):
                act.wait_ge(S["y_ready"], t + 1)
                nc.scalar.activation(y[:, t, :], psY[:, t % 2, 0:D], ACT.Copy, scale=ms[:, 2, t:t + 1]).then_inc(S["y_scaled"], 1)
            act.wait_ge(S["y_scaled"], NT)
            nc.scalar.activation(q[:, :], y[:, :, :].rearrange("p t n -> p (t n)"), ACT.Square).then_inc(S["sq_done"], 1)
            act.wait_ge(S["sq_done"], 1)
            nc.scalar.activation(root[:, :], q[:, :], ACT.Sqrt, bias=K.ones[:, 0:1]).then_inc(S["sqrt_done"], 1)

        @block.vector
        def _(dve):
            dve.wait_ge(S["root_ready"], 1)
            nc.vector.reciprocal(ms[:, 2, :], ms[:, 1, :]).then_inc(S["r_ready"], 1)
            dve.wait_ge(S["loaded"], 32)
            for t in range(NT):
                dve.wait_ge(S["turned"], t + 1)
                if t >= 2:
                    dve.wait_ge(S["y_ready"], t - 1)
                for c in range(2):
                    nc.vector.tensor_scalar(yT[:, t % 2, c, :], psT[:, t % 2, c * P:(c + 1) * P], nw[:, c:c + 1], None, ALU.mult).then_inc(S["copied"], 1)
            dve.wait_ge(S["sqrt_done"], 1)
            nc.vector.reciprocal(q[:, :], root[:, :]).then_inc(S["recip_done"], 1)
            dve.wait_ge(S["recip_done"], 1)
            nc.vector.tensor_tensor(Z[:, :, :].rearrange("p t n -> p (t n)"), y[:, :, :].rearrange("p t n -> p (t n)"), q[:, :], ALU.mult)


def by_tile(a):
    return a.reshape(NT, P, -1).transpose(1, 0, 2)


def shape_constants():
    f = np.float32
    pos = np.arange(T, dtype=f)
    inv = f(1.0) / f(10000.0) ** (np.arange(4, dtype=f) / f(4))
    ang = pos[:, None] * inv[None, :]
    rope8 = np.stack([by_tile(np.cos(ang)), by_tile(np.sin(ang))], axis=1)
    rsqrt_t = by_tile(f(1) / np.sqrt(np.arange(1, T + 1, dtype=f)))[:, :, 0]
    half = np.arange(0, 64, 2, dtype=f)
    fr = pos[:, None] * (f(1.0) / f(10000.0) ** (half / f(64)))[None, :]
    base = (half + f(0.4 * 64)) / f(1.4 * 64)
    scale = base[None, :] ** ((pos - f(T // 2)) / f(32))[:, None]
    fr, scale = np.concatenate([fr, fr], 1), np.concatenate([scale, scale], 1)
    sign = np.concatenate([-np.ones(32, f), np.ones(32, f)])
    tabs = [np.stack([by_tile(x * scale * f(8)), by_tile(x / scale)], axis=2) for x in (np.cos(fr), np.sin(fr) * sign)]
    xpos = np.ascontiguousarray(np.stack(tabs, axis=1), dtype=f)
    behind = by_tile(f(T - 1) - pos)[:, :, 0]
    return {"keys_behind": np.ascontiguousarray(behind), "xpos": xpos, "rope8": np.ascontiguousarray(rope8, dtype=f), "rsqrt_t": np.ascontiguousarray(rsqrt_t)}


LAYOUT = {
    "L0_attn_b_Q": lambda a: a.T,
    "L0_attn_b_K": lambda a: a.T,
    "L0_ffn_keys": lambda a: a.transpose(2, 0, 3, 1).reshape(16, 128, 32),
    "L0_ffn_bn_gamma": lambda a: a.reshape(16, P).T,
    "L0_ffn_bn_beta": lambda a: a.reshape(16, P).T,
    "L0_ffn_down_embed": lambda a: a.T,
    "L2_attn_gate": lambda a: np.repeat(a, 64, axis=0).reshape(8, P, 2).transpose(1, 2, 0),
    "L2_attn_freqs": lambda a: a.reshape(8, P).T,
    "L3_attn_conv_b": lambda a: a.reshape(3, P).T,
    "L3_attn_norm_w": lambda a: a.reshape(2, P).T,
    "L3_attn_init_states": lambda a: a.reshape(256, 64).T,
    "L2_ffn_b1": lambda a: np.concatenate([a.reshape(2, 2, 341), np.zeros((2, 2, 43), a.dtype)], axis=2).reshape(2, 2, 3, P).transpose(0, 3, 1, 2),
    "L3_ffn_b1": lambda a: a.reshape(8, 4, P).transpose(2, 1, 0),
    "L3_ffn_b2": lambda a: np.concatenate([a, np.zeros((D - 8, D), a.dtype)]),
}

SUBLAYERS = [l0_attention, l0_experts, l1_attention, l1_experts, l2_attention, l2_transformer, l3_mixer, l3_experts]


class Constants:
    pass


def sem_range(S):
    nums = sorted(s.num for s in S.values())
    assert nums[-1] - nums[0] == len(nums) - 1
    return range(nums[0], nums[-1] + 1)


def build_constants(nc, ctx):
    K = Constants()
    K.ident = ctx.enter_context(nc.sbuf_tensor("ident", [P, P], F32))
    K.ones = ctx.enter_context(nc.sbuf_tensor("ones", [P, P], F32))
    K.causal_q = ctx.enter_context(nc.sbuf_tensor("causal_q", [P, P], F32))
    K.causal_k = ctx.enter_context(nc.sbuf_tensor("causal_k", [P, P], F32))
    K.eps = ctx.enter_context(nc.sbuf_tensor("eps", [P, 1], F32))
    filled = nc.alloc_semaphore("constants_filled")
    with nc.Block() as block:
        @block.gpsimd
        def _(pool):
            nc.gpsimd.memset(K.ident[:, :], 0.0).then_inc(filled, 1)
            nc.gpsimd.memset(K.ones[:, :], 1.0).then_inc(filled, 1)
            nc.gpsimd.memset(K.eps[:, :], LN_EPS).then_inc(filled, 1)
            pool.wait_ge(filled, 3)
            nc.gpsimd.affine_select(out=K.ident[:, :], in_=K.ident[:, :], compare_op=ALU.not_equal, fill=1.0, base=0,
                                    pattern=[[-1, P]], channel_multiplier=1)
            nc.gpsimd.affine_select(out=K.causal_q[:, :], in_=K.ones[:, :], compare_op=ALU.is_ge, fill=0.0, base=0,
                                    pattern=[[-1, P]], channel_multiplier=1)
            nc.gpsimd.affine_select(out=K.causal_k[:, :], in_=K.ones[:, :], compare_op=ALU.is_ge, fill=0.0, base=0,
                                    pattern=[[1, P]], channel_multiplier=-1)
    return K


def program(nc, W, out):
    with ExitStack() as ctx:
        X = ctx.enter_context(nc.sbuf_tensor("X", [P, NT, D], F32))
        K = build_constants(nc, ctx)
        x_moved = nc.alloc_semaphore("x_moved")
        with nc.Block() as block:
            @block.sync
            def _(sync):
                sync.dma_start(X[:, :, :], W["L0_attn_resid_pre"].rearrange("b (t p) d -> p (b t) d", p=P)).then_inc(x_moved, 16)
                sync.wait_ge(x_moved, 16)
        for stage in SUBLAYERS[STAGES[0]:STAGES[1]]:
            stage(nc, X, K, W)
        with nc.Block() as block:
            @block.sync
            def _(sync):
                sync.dma_start(out.rearrange("b (t p) d -> p (b t) d", p=P), X[:, :, :]).then_inc(x_moved, 16)
                sync.wait_ge(x_moved, 32)


def kernel(**inputs):
    import concourse.bacc as _bacc
    from concourse.bass_utils import run_bass_kernel_spmd as _run

    nc = _bacc.Bacc("TRN2", target_bir_lowering=False, num_devices=1)
    arrays, W = {}, {}
    for name in list(inputs):
        a = np.ascontiguousarray(LAYOUT[name](np.asarray(inputs[name])) if name in LAYOUT else inputs[name])
        arrays[f"in_{name}"] = a
        W[name] = nc.dram_tensor(f"in_{name}", a.shape, mybir.dt.from_np(a.dtype), kind="ExternalInput").ap()
    for name, a in shape_constants().items():
        arrays[f"const_{name}"] = a
        W[name] = nc.dram_tensor(f"const_{name}", a.shape, mybir.dt.from_np(a.dtype), kind="ExternalInput").ap()
    ln = np.ascontiguousarray(np.stack([inputs["L2_ffn_ln_g"], inputs["L2_ffn_ln_b"]], axis=2))
    arrays["in_l2_ln"] = ln
    W["l2_ln"] = nc.dram_tensor("in_l2_ln", ln.shape, F32, kind="ExternalInput").ap()
    out = nc.dram_tensor("out_0", (1, T, D), F32, kind="ExternalOutput").ap()
    program(nc, W, out)
    r = _run(nc, [arrays], core_ids=[0])
    return r.results[0]["out_0"]
```

```python
import itertools
from contextlib import ExitStack, contextmanager

import concourse.bass as bass
import concourse.mybir as mybir
import numpy as np

F32 = mybir.dt.float32
BF16 = mybir.dt.bfloat16
I32 = mybir.dt.int32
U32 = mybir.dt.uint32
ALU = mybir.AluOpType
ACT = mybir.ActivationFunctionType
AX_X = mybir.AxisListType.X

P = 128
T = 2048
NT = T // P
D = 128
BANK = 512
NB = T // BANK
TPB = BANK // P
LN_EPS = 1e-5
COUNT = itertools.count()


def bcast(ap, shape):
    return ap.broadcast_to(shape)


@contextmanager
def sublayer(nc):
    sems = []
    with ExitStack() as ctx:
        class Space:
            def sb(self, name, shape, dt=F32):
                return ctx.enter_context(nc.sbuf_tensor(f"{name}_{next(COUNT)}", shape, dt))

            def ps(self, name, shape, dt=F32):
                return ctx.enter_context(nc.psum_tensor(f"{name}_{next(COUNT)}", shape, dt))

            def sem(self, name):
                s = nc.alloc_semaphore(f"{name}_{next(COUNT)}")
                sems.append(s)
                return s
        yield Space()
    nc.clear_and_free_semaphores(sems)
    nc.all_engine_barrier()


def scoped(f):
    def run(nc, *args):
        with sublayer(nc) as sp:
            f(nc, sp, *args)
    return run


def loads_done(nc, sem, count):
    with nc.Block() as block:
        @block.sync
        def _(sync):
            sync.wait_ge(sem, 16 * count)


@scoped
def layernorm(nc, sp, K, src, dst, dstT=None, scale=None, bias=None):
    stats = sp.sb("ln_stats", [P, NT, 6])
    moments = sp.sb("ln_moments", [P, NT, 2])
    std = sp.sb("ln_std", [P, NT])
    rstd = sp.sb("ln_rstd", [P, NT])
    turned = None if dstT is None else sp.ps("ln_turned", [P, NB, BANK])
    stats_ready = sp.sem("ln_stats_ready")
    moments_ready = sp.sem("ln_moments_ready")
    std_ready = sp.sem("ln_std_ready")
    rstd_ready = sp.sem("ln_rstd_ready")
    normed = sp.sem("ln_normed")
    turned_ready = sp.sem("ln_turned_ready")
    with nc.Block() as block:
        @block.vector
        def _(dve):
            for t in range(NT):
                nc.vector.bn_stats(stats[:, t, :], src[:, t, :]).then_inc(stats_ready, 1)
            dve.wait_ge(stats_ready, NT)
            for t in range(NT):
                nc.vector.bn_aggr(moments[:, t, :], stats[:, t, :]).then_inc(moments_ready, 1)
            dve.wait_ge(std_ready, 1)
            nc.vector.reciprocal(rstd[:, :], std[:, :]).then_inc(rstd_ready, 1)
            dve.wait_ge(rstd_ready, 1)
            for t in range(NT):
                nc.vector.tensor_scalar(dst[:, t, :], src[:, t, :], moments[:, t, 0:1], rstd[:, t:t + 1],
                                        ALU.subtract, ALU.mult).then_inc(normed, 1)

        @block.scalar
        def _(act):
            act.wait_ge(moments_ready, NT)
            nc.scalar.activation(std[:, :], moments[:, :, 1], ACT.Sqrt, bias=K.eps[:, 0:1]).then_inc(std_ready, 1)
            for b in range(NB if dstT is not None else 0):
                act.wait_ge(turned_ready, b + 1)
                out = dstT[:, b * BANK:(b + 1) * BANK]
                if scale is None:
                    nc.scalar.copy(out, turned[:, b, :])
                else:
                    nc.scalar.activation(out, turned[:, b, :], ACT.Identity, scale=scale, bias=bias)

        @block.tensor
        def _(pe):
            for b in range(NB if dstT is not None else 0):
                pe.wait_ge(normed, (b + 1) * TPB)
                for j in range(TPB):
                    last = nc.tensor.transpose(turned[:, b, j * P:(j + 1) * P], dst[:, b * TPB + j, :], K.ident[:, :])
                last.then_inc(turned_ready, 1)


@scoped
def transpose_tokens(nc, sp, K, src, dst, scale=None, bias=None):
    turned = sp.ps("turned", [P, 2, BANK])
    turned_ready = sp.sem("turned_ready")
    turned_used = sp.sem("turned_used")
    with nc.Block() as block:
        @block.tensor
        def _(pe):
            for b in range(NB):
                if b >= 2:
                    pe.wait_ge(turned_used, b - 1)
                for j in range(TPB):
                    last = nc.tensor.transpose(turned[:, b % 2, j * P:(j + 1) * P], src[:, b * TPB + j, :], K.ident[:, :])
                last.then_inc(turned_ready, 1)

        @block.vector
        def _(dve):
            for b in range(NB):
                dve.wait_ge(turned_ready, b + 1)
                out = dst[:, b * BANK:(b + 1) * BANK]
                if scale is None:
                    nc.vector.tensor_copy(out, turned[:, b % 2, :]).then_inc(turned_used, 1)
                else:
                    nc.vector.tensor_scalar(out, turned[:, b % 2, :], scale, bias, ALU.mult, ALU.add).then_inc(turned_used, 1)


def l0_attention(nc, X, K, W):
    H, DH = 16, 64
    DA = DH + 1
    PAIRS = H // 2
    items = [(b, h, k) for b in range(NB - 1, -1, -1) for h in range(2) for k in range(TPB * (b + 1))]
    NI = len(items)
    last_of = {(b, h): n for n, (b, h, k) in enumerate(items)}
    outputs = list(last_of)
    on_diagonal = [k >= TPB * b for b, h, k in items]
    masks_to = [sum(on_diagonal[:n + 1]) for n in range(NI)]

    def width(b, k):
        return min(BANK, (b + 1) * BANK - k * P)

    proj = [(kind, b) for b in range(NB) for kind in ("q", "V", "k", "suffix")]
    spread = {"q": {"hi": (0,), "mid": (1,)}, "k": {"hi": (0, 1), "mid": (0, 1)}}
    SPREAD = 2 * NB * sum(len(v["hi"]) for v in spread.values())
    maxi = [[("max", h, t, j) for t in range(NT - 1, -1, -1) for j in range(t // TPB + 1)] for h in range(2)]
    rows_ = [[("row", h)] for h in range(2)]
    next_units = proj + maxi[0] + maxi[1][:6] + rows_[0] + maxi[1][6:] + rows_[1]
    STEPS_A = NI - 8

    def timeline(do_b, do_a):
        if not do_b:
            return [[u] for u in next_units]
        steps = [[] for _ in range(NI + 8)]
        if do_a:
            for i, u in enumerate(next_units):
                steps[i * STEPS_A // len(next_units)].append(u)
        for b in range(NB):
            steps[last_of[b, 1] + 4].append(("turn", b))
            steps[last_of[b, 1] + 6].append(("out", b))
        return steps

    reader = {"q": "mid", "k": "mid", "V": "dve", "suffix": "dve", "max": "dve", "row": "act", "turn": "act", "out": "dve"}

    with sublayer(nc) as sp:
        sufB = sp.sb("suffix_weighed", [P, NT, 2, DA])
        R = sufB[:, :, :, :].rearrange("p t a n -> p (t a n)")[:, 0:NT * D].rearrange("p (t n) -> p t n", t=NT)
        xhat = sp.sb("xhat", [P, NT, D])
        xT = sp.sb("xT", [P, T])
        xsufT = sp.sb("x_suffixT", [P, T])
        wq = sp.sb("wq", [P, H * DH])
        wk = sp.sb("wk", [P, H * DH])
        wv = sp.sb("wv", [P, H * DH])
        wo = sp.sb("wo", [P, PAIRS, D])
        bq = sp.sb("bq", [P, PAIRS])
        bk = sp.sb("bk", [P, PAIRS])
        bv = sp.sb("bv", [P, H * DH])
        behind = sp.sb("keys_behind", [P, NT])
        rows = sp.sb("rows", [P, 5, D])
        loaded = sp.sem("weights_loaded")
        with nc.Block() as block:
            @block.sync
            def _(sync):
                def load(dst, src):
                    sync.dma_start(dst, src).then_inc(loaded, 16)
                for dst, name in ((wq, "L0_attn_W_Q"), (wk, "L0_attn_W_K"), (wv, "L0_attn_W_V")):
                    load(dst[:, :].rearrange("d (h k) -> d h k", k=DH), W[name].rearrange("h d k -> d h k"))
                load(wo[:, :, :], W["L0_attn_W_O"].rearrange("(g a) k n -> (a k) g n", a=2))
                load(bq[:, :], W["L0_attn_b_Q"])
                load(bk[:, :], W["L0_attn_b_K"])
                load(behind[:, :], W["keys_behind"])
                load(bv[:, :], W["L0_attn_b_V"].rearrange("h k -> (h k)").partition_broadcast(P))
                for j, name in enumerate(("L0_attn_b_O", "L0_attn_ln2_w", "L0_attn_ln2_b", "L0_attn_ln1_w", "L0_attn_ln1_b")):
                    load(rows[:, j, :], W[name].partition_broadcast(P))

        layernorm(nc, K, X, R)
        layernorm(nc, K, R, xhat)
        loads_done(nc, loaded, 13)
        acc = xhat
        wqs = sp.sb("wq_pair", [P, P])
        wks = sp.sb("wk_pair", [P, P])
        strict = sp.sb("strict", [P, P])
        qN = sp.sb("q_next", [DA, 2, T])
        kN = sp.sb("k_next", [DH, 2, T])
        hi = sp.sb("block_hi", [P, 2, BANK], BF16)
        mid = sp.sb("block_mid", [P, 2, BANK], BF16)
        q16 = sp.sb("q_hi_mid", [P, 2, T], BF16)
        k16h = sp.sb("k_hi_hi", [P, 2, T], BF16)
        k16m = sp.sb("k_mid_mid", [P, 2, T], BF16)
        VN = sp.sb("v_next", [P, NT, 2, DH])
        sufN = sp.sb("suffix_next", [P, NT, 2, DA])
        qB = sp.sb("q_and_negmax", [DA, 2, T])
        kB = sp.sb("k_and_one", [DA, 2, T])
        VB = sp.sb("v_and_one", [P, NT, 2, DA])
        bmax = sp.sb("bank_max", [P, 2, NT, 1 + NB])
        nmax = sp.sb("neg_max", [P, 2, NT])
        nmaxT = sp.sb("neg_maxT", [NT, 2, P])
        e0 = sp.sb("exp_masked", [P, 2, NT])
        prob = sp.sb("prob", [P, 3, BANK])
        zsum = sp.sb("z_sum", [P, 2, TPB, DA])
        rden = sp.sb("rden", [P, 2, TPB])
        z = sp.sb("z", [P, NT, 2 * DH])
        zT = sp.sb("zT", [P, BANK])
        psS = sp.ps("scores", [P, 3, BANK])
        psO = sp.ps("outs", [P, 2, BANK])
        psR = sp.ps("ring", [P, 3, BANK])
        names = ("w_ready ring_ready dve_used act_used hi_ready hi_spread mid_ready mid_spread masked row_max row_moved "
                 "qk_done exp_done mask_done pv_done z_read rden_ready z_ready "
                 "later_step weighed fin_a fin_b fin_c").split()
        S = {n: sp.sem(n) for n in names}
        x = VN[:, :, :, :].rearrange("p t a n -> p t (a n)")
        later = z
        with nc.Block() as block:
            @block.vector
            def _(dve):
                nc.vector.memset(bmax[:, :, :, :], 0.0).then_inc(S["fin_a"], 1)
                dve.wait_ge(S["fin_a"], 1)
                nc.vector.memset(bmax[:, :, NT - 1, NB:], -3e38)
                nc.vector.memset(VB[:, :, :, :], 1.0)
                nc.vector.memset(kB[:, :, :], 1.0)
                nc.vector.tensor_scalar(bq[:, :], bq[:, :], DH ** -0.5, None, ALU.mult)
                nc.vector.tensor_tensor(strict[:, :], K.ones[:, :], K.causal_k[:, :], ALU.subtract)
                nc.vector.tensor_tensor(x[:, :, :], xhat[:, :, :], bcast(rows[:, 3:4, :], [P, NT, D]), ALU.mult).then_inc(S["fin_b"], 1)
                dve.wait_ge(S["fin_b"], 1)
                nc.vector.tensor_tensor(x[:, :, :], x[:, :, :], bcast(rows[:, 4:5, :], [P, NT, D]), ALU.add)
                nc.vector.tensor_tensor(acc[:, :, :], R[:, :, :], bcast(rows[:, 0:1, :], [P, NT, D]), ALU.add)

            @block.gpsimd
            def _(pool):
                nc.gpsimd.memset(later[:, NT - 1, :], 0.0)
                for h in range(2):
                    nc.gpsimd.tensor_copy(sufN[:, :, h, DH:DA], behind[:, :].unsqueeze(2))

        with nc.Block() as block:
            @block.gpsimd
            def _(pool):
                for i, t in enumerate(range(NT - 2, -1, -1)):
                    if i >= 1:
                        pool.wait_ge(S["later_step"], i)
                    nc.gpsimd.tensor_tensor(later[:, t, :], later[:, t + 1, :], x[:, t + 1, :], ALU.add).then_inc(S["later_step"], 1)

            @block.tensor
            def _(pe):
                for n in range(2 * NB):
                    b = n if n < NB else 2 * NB - 1 - n
                    if n >= 3:
                        pe.wait_ge(S["dve_used"], n - 2)
                    if n >= NB:
                        pe.wait_ge(S["later_step"], NT - 1 - b * TPB)
                    for j in range(TPB):
                        t = b * TPB + j
                        out = psR[:, n % 3, j * P:(j + 1) * P]
                        if n < NB:
                            last = nc.tensor.transpose(out, x[:, t, :], K.ident[:, :])
                        else:
                            nc.tensor.matmul(out, x[:, t, :], strict[:, :], start=True, stop=False)
                            last = nc.tensor.matmul(out, later[:, t, :], K.ones[:, :], start=False, stop=True)
                    last.then_inc(S["ring_ready"], 1)

            @block.vector
            def _(dve):
                for n in range(2 * NB):
                    b = n if n < NB else 2 * NB - 1 - n
                    dve.wait_ge(S["ring_ready"], n + 1)
                    nc.vector.tensor_copy((xT if n < NB else xsufT)[:, b * BANK:(b + 1) * BANK], psR[:, n % 3, :]).then_inc(S["dve_used"], 1)

        def heads_pass(pair, nxt, do_b, do_a):
            steps = timeline(do_b, do_a)
            units = [u for st in steps for u in st]
            number = {u: n for n, u in enumerate(units)}

            def used_to(n, engine):
                return sum(reader[u[0]] == engine for u in units[:n + 1])

            def bank(u):
                return psR[:, number[u] % 3, :]

            def wait_read(eng, u):
                who = reader[u[0]]
                eng.wait_ge(S["mid_ready" if who == "mid" else who + "_used"], used_to(number[u], who))

            def qk_count(u):
                return sum(v[0] in "qk" for v in units[:number[u]])

            def spread_block(copy, u, part, src, done):
                kind, b = u
                to = {("q", "hi"): q16, ("q", "mid"): q16, ("k", "hi"): k16h, ("k", "mid"): k16m}[kind, part]
                for h in range(2):
                    for half in spread[kind][part]:
                        copy(to[half * DH:(half + 1) * DH, h, b * BANK:(b + 1) * BANK], src[h * DH:(h + 1) * DH, :]).then_inc(S[done], 1)

            with nc.Block() as block:
                @block.tensor
                def _(pe):
                    def qk(n):
                        b, h, k = items[n]
                        w = width(b, k)
                        if n >= 3:
                            pe.wait_ge(S["exp_done"], n - 2)
                        nc.tensor.matmul(psS[:, n % 3, 0:w], kB[:, h, k * P:(k + 1) * P], qB[:, h, (b + 1) * BANK - w:(b + 1) * BANK],
                                         start=True, stop=True).then_inc(S["qk_done"], 1)

                    def pv(n):
                        b, h, k = items[n]
                        o = outputs.index((b, h))
                        if k == 0 and o >= 2:
                            pe.wait_ge(S["z_read"], o - 1)
                        if on_diagonal[n]:
                            pe.wait_ge(S["mask_done"], masks_to[n])
                        else:
                            pe.wait_ge(S["exp_done"], n + 1)
                        w = width(b, k)
                        for c in range(w // P):
                            q = TPB - w // P + c
                            last = nc.tensor.matmul(psO[:, o % 2, q * P:q * P + DA], prob[:, n % 3, c * P:(c + 1) * P], VB[:, k, h, :],
                                                    start=(k == 0 and q == 0), stop=(k == TPB * b + q), skip_group_check=True)
                        last.then_inc(S["pv_done"], 1)

                    def unit(u):
                        n, kind, b, ps = number[u], u[0], u[-1], bank(u)
                        if n >= 3:
                            wait_read(pe, units[n - 3])
                        if kind in "qk":
                            if n == 0:
                                pe.wait_ge(S["w_ready"], 2)
                            last = nc.tensor.matmul(ps, (wqs if kind == "q" else wks)[:, :],
                                                    xT[:, b * BANK:(b + 1) * BANK], start=True, stop=True)
                        elif kind in ("V", "suffix"):
                            xs = xT if kind == "V" else xsufT
                            for j in range(TPB):
                                t = b * TPB + j
                                last = nc.tensor.matmul(ps[:, j * P:(j + 1) * P], xs[:, t * P:(t + 1) * P], wv[:, bass.ds(nxt * P, P)],
                                                        start=True, stop=True)
                        elif kind == "max":
                            _, h, t, j = u
                            if h == 0 and j == 0 and t == NT - 1:
                                pe.wait_ge(S["hi_spread"], SPREAD)
                                pe.wait_ge(S["mid_spread"], SPREAD)
                            w = min(BANK, (t + 1) * P - j * BANK)
                            for k16, first in ((k16h, True), (k16m, False)):
                                last = nc.tensor.matmul(ps[:, 0:w], q16[:, h, t * P:(t + 1) * P], k16[:, h, j * BANK:j * BANK + w],
                                                        start=first, stop=not first)
                        elif kind == "row":
                            h = u[1]
                            pe.wait_ge(S["row_max"], h + 1)
                            last = nc.tensor.transpose(ps[0:NT, 0:P], nmax[:, h, :], K.ident[:, :])
                        elif kind == "turn":
                            pe.wait_ge(S["z_ready"], outputs.index((b, 1)) + 1)
                            for j in range(TPB):
                                last = nc.tensor.transpose(ps[:, j * P:(j + 1) * P], z[:, b * TPB + j, :], K.ident[:, :])
                        else:
                            wait_read(pe, ("turn", b))
                            for j in range(TPB):
                                last = nc.tensor.matmul(ps[:, j * P:(j + 1) * P], zT[:, j * P:(j + 1) * P],
                                                        wo[:, bass.ds(pair, 1), :].rearrange("p a n -> p (a n)"), start=True, stop=True)
                        last.then_inc(S["ring_ready"], 1)

                    for s, todo in enumerate(steps):
                        if do_b and s < NI:
                            qk(s)
                        for u in todo:
                            unit(u)
                        if do_b and 0 <= s - 2 < NI:
                            pv(s - 2)

                @block.scalar
                def _(act):
                    if do_a:
                        for ws, w, scale in ((wqs, wq, DH ** -0.5), (wks, wk, 1.0)):
                            nc.scalar.activation(ws[:, :], w[:, bass.ds(nxt * P, P)], ACT.Identity, scale=scale).then_inc(S["w_ready"], 1)

                    def exps(n):
                        b, h, k = items[n]
                        w = width(b, k)
                        act.wait_ge(S["qk_done"], n + 1)
                        if n >= 3:
                            act.wait_ge(S["pv_done"], n - 2)
                        nc.scalar.activation(prob[:, n % 3, 0:w], psS[:, n % 3, 0:w], ACT.Exp).then_inc(S["exp_done"], 1)

                    def copy_out(u):
                        kind, b, ps = u[0], u[-1], bank(u)
                        act.wait_ge(S["ring_ready"], number[u] + 1)
                        if kind in "qk":
                            m = qk_count(u)
                            full, bias = (qN, bq) if kind == "q" else (kN, bk)
                            for h in range(2):
                                r = slice(h * DH, (h + 1) * DH)
                                nc.scalar.activation(full[0:DH, h, b * BANK:(b + 1) * BANK], ps[r, :], ACT.Identity, bias=bias[r, bass.ds(nxt, 1)])
                            if m >= 2:
                                act.wait_ge(S["mid_ready"], m - 1)
                            nc.scalar.activation(hi[:, m % 2, :], ps, ACT.Identity, bias=bias[:, bass.ds(nxt, 1)]).then_inc(S["hi_ready"], 1)
                            act.wait_ge(S["hi_ready"], m + 1)
                            spread_block(nc.scalar.copy, u, "hi", hi[:, m % 2, :], "hi_spread")
                        elif kind == "row":
                            nc.scalar.copy(nmaxT[:, u[1], :], ps[0:NT, 0:P]).then_inc(S["act_used"], 1)
                        else:
                            if b < NB - 1:
                                act.wait_ge(S["ring_ready"], number["out", b + 1] + 1)
                            nc.scalar.copy(zT[:, :], ps).then_inc(S["act_used"], 1)

                    def hand_over():
                        if do_b:
                            act.wait_ge(S["qk_done"], NI)
                        nc.scalar.copy(kB[0:DH, 1, :], kN[:, 1, :])
                        act.wait_ge(S["row_max"], 2)
                        if do_b:
                            act.wait_ge(S["weighed"], 2)
                        nc.scalar.activation(e0[:, :, :], nmax[:, :, :], ACT.Exp)
                        act.wait_ge(S["row_moved"], 32)
                        nc.scalar.copy(qB[:, 1, :], qN[:, 1, :])

                    for s, todo in enumerate(steps):
                        if do_b and s < NI:
                            exps(s)
                        if do_a and do_b and s == NI:
                            hand_over()
                        for u in todo:
                            if reader[u[0]] == "act" or u[0] in "qk":
                                copy_out(u)
                    if do_a and not do_b:
                        hand_over()

                @block.gpsimd
                def _(pool):
                    if do_b:
                        for h in range(2):
                            nc.gpsimd.tensor_tensor(sufB[:, :, h, :], sufN[:, :, h, :], bcast(e0[:, h, :].unsqueeze(2), [P, NT, DA]),
                                                    ALU.mult).then_inc(S["weighed"], 1)

                    for s in range(len(steps)):
                        if do_b and s < NI and on_diagonal[s]:
                            pool.wait_ge(S["exp_done"], s + 1)
                            v = prob[:, s % 3, 0:P]
                            nc.gpsimd.affine_select(out=v, in_=v, compare_op=ALU.is_ge, fill=0.0, base=0, pattern=[[1, P]],
                                                    channel_multiplier=-1).then_inc(S["mask_done"], 1)

                @block.sync
                def _(sync):
                    if do_a:
                        for h in range(2):
                            wait_read(sync, ("row", h))
                            sync.dma_start(qN[DH:DA, h, :], nmaxT[:, h, :]).then_inc(S["row_moved"], 16)

                @block.vector
                def _(dve):
                    def read(u):
                        kind, b, ps = u[0], u[-1], bank(u)
                        dve.wait_ge(S["ring_ready"], number[u] + 1)
                        if kind == "V":
                            nc.vector.tensor_tensor(VN[:, b * TPB:(b + 1) * TPB, :, :].rearrange("p t a n -> p t (a n)"), ps.rearrange("p (t n) -> p t n", n=P),
                                                    bcast(bv[:, bass.ds(nxt * P, P)].unsqueeze(1), [P, TPB, P]), ALU.add).then_inc(S["dve_used"], 1)
                        elif kind == "suffix":
                            if do_b and b == 0:
                                dve.wait_ge(S["weighed"], 2)
                            for j in range(TPB):
                                t = b * TPB + j
                                last = nc.vector.scalar_tensor_tensor(
                                    out=sufN[:, t, :, 0:DH], in0=bv[:, bass.ds(nxt * P, P)].rearrange("p (a n) -> p a n", a=2), scalar=behind[:, t:t + 1],
                                    in1=ps[:, j * P:(j + 1) * P].rearrange("p (a n) -> p a n", a=2), op0=ALU.mult, op1=ALU.add)
                            last.then_inc(S["dve_used"], 1)
                        elif kind in "qk":
                            m = qk_count(u)
                            dve.wait_ge(S["hi_ready"], m + 1)
                            nc.vector.scalar_tensor_tensor(out=mid[:, m % 2, :], in0=ps, scalar=(bq if kind == "q" else bk)[:, bass.ds(nxt, 1)],
                                                           in1=hi[:, m % 2, :], op0=ALU.add, op1=ALU.subtract).then_inc(S["mid_ready"], 1)
                            dve.wait_ge(S["mid_ready"], m + 1)
                            spread_block(nc.vector.tensor_copy, u, "mid", mid[:, m % 2, :], "mid_spread")
                        elif kind == "max":
                            _, h, t, j = u
                            w = min(BANK, (t + 1) * P - j * BANK)
                            if j == t // TPB:
                                diag = ps[:, w - P:w]
                                nc.vector.tensor_tensor(diag, diag, K.causal_q[:, :], ALU.mult).then_inc(S["masked"], 1)
                                dve.wait_ge(S["masked"], h * NT + NT - t)
                            nc.vector.reduce_max(bmax[:, h, t, j:j + 1], ps[:, 0:w], axis=AX_X).then_inc(S["dve_used"], 1)
                            if t == 0:
                                wait_read(dve, u)
                                nc.vector.tensor_reduce(nmax[:, h, :], bmax[:, h, :, :], axis=AX_X, op=ALU.max, negate=True).then_inc(S["row_max"], 1)
                        else:
                            a = acc[:, b * TPB:(b + 1) * TPB, :].rearrange("p t n -> p (t n)")
                            nc.vector.tensor_tensor(a, a, ps, ALU.add).then_inc(S["dve_used"], 1)

                    def finish(o):
                        b, h = outputs[o]
                        ts = slice(b * TPB, (b + 1) * TPB)
                        dve.wait_ge(S["pv_done"], last_of[b, h] + 1)
                        if o < 2:
                            dve.wait_ge(S["weighed"], o + 1)
                        nc.vector.tensor_tensor(zsum[:, o % 2, :, :], psO[:, o % 2, :].rearrange("p (t n) -> p t n", n=P)[:, :, 0:DA], sufB[:, ts, h, :],
                                                ALU.add).then_inc(S["z_read"], 1)
                        dve.wait_ge(S["z_read"], o + 1)
                        nc.vector.reciprocal(rden[:, o % 2, :], zsum[:, o % 2, :, DH]).then_inc(S["rden_ready"], 1)
                        dve.wait_ge(S["rden_ready"], o + 1)
                        nc.vector.tensor_tensor(z[:, ts, h * DH:(h + 1) * DH], zsum[:, o % 2, :, 0:DH], bcast(rden[:, o % 2, :].unsqueeze(2), [P, TPB, DH]),
                                                ALU.mult).then_inc(S["z_ready"], 1)

                    def hand_over():
                        if do_b:
                            dve.wait_ge(S["qk_done"], NI)
                        dve.wait_ge(S["hi_ready"], 2 * NB)
                        nc.vector.tensor_copy(kB[0:DH, 0, :], kN[:, 0, :])
                        dve.wait_ge(S["row_moved"], 32)
                        nc.vector.tensor_copy(qB[:, 0, :], qN[:, 0, :])
                        if do_b:
                            dve.wait_ge(S["pv_done"], NI)
                        wait_read(dve, ("V", NB - 1))
                        nc.vector.tensor_copy(VB[:, :, :, 0:DH], VN[:, :, :, :])

                    for s, todo in enumerate(steps):
                        if do_b:
                            for o in range(len(outputs)):
                                if last_of[outputs[o]] + 3 == s:
                                    finish(o)
                        if do_a and do_b and s == NI + 2:
                            hand_over()
                        for u in todo:
                            if reader[u[0]] in ("dve", "mid"):
                                read(u)
                    if do_a and not do_b:
                        hand_over()

            nc.gpsimd.sem_clear(sem_range(S))
            nc.all_engine_barrier()

        nc.gpsimd.sem_clear(sem_range(S))
        nc.all_engine_barrier()
        heads_pass(None, 0, False, True)
        with nc.Fori(0, PAIRS - 1) as g:
            heads_pass(g, g + 1, True, True)
        heads_pass(PAIRS - 1, None, True, False)
        layernorm(nc, K, acc, R)
        with nc.Block() as block:
            @block.vector
            def _(dve):
                half = NT // 2
                nc.vector.tensor_tensor(R[:, :, :], R[:, :, :], bcast(rows[:, 1:2, :], [P, NT, D]), ALU.mult).then_inc(S["fin_a"], 1)
                nc.vector.tensor_tensor(X[:, :, :], X[:, :, :], acc[:, :, :], ALU.add).then_inc(S["fin_b"], 1)
                dve.wait_ge(S["fin_a"], 1)
                nc.vector.tensor_tensor(R[:, :, :], R[:, :, :], bcast(rows[:, 2:3, :], [P, NT, D]), ALU.add).then_inc(S["fin_c"], 1)
                dve.wait_ge(S["fin_b"], 1)
                dve.wait_ge(S["fin_c"], 1)
                nc.vector.tensor_tensor(X[:, :, :], X[:, :, :], R[:, :, :], ALU.add)


def l0_experts(nc, X, K, W):
    H, KD, NK, TOP = 8, 128, 32, 8
    C = 2 * H
    EC = NK * NK // P
    with sublayer(nc) as sp:
        xn = sp.sb("xn", [P, NT, D])
        xT = sp.sb("xT", [P, T])
        keysT = sp.sb("keysT", [P, C, NK])
        bn = sp.sb("bn", [P, 2, C])
        downT = sp.sb("downT", [P, EC * P])
        up = sp.sb("up", [P, EC, D])
        wq = sp.sb("wq", [P, C * KD])
        G = sp.sb("gelu_hidden", [P, EC, T])
        sim = sp.sb("sim", [P, NT, C, NK])
        loaded = sp.sem("weights_loaded")
        with nc.Block() as block:
            @block.sync
            def _(sync):
                sync.dma_start(keysT[:, :, :], W["L0_ffn_keys"].rearrange("c k n -> k c n")).then_inc(loaded, 16)
                sync.dma_start(bn[:, 0, :], W["L0_ffn_bn_gamma"]).then_inc(loaded, 16)
                sync.dma_start(bn[:, 1, :], W["L0_ffn_bn_beta"]).then_inc(loaded, 16)
                sync.dma_start(downT[:, :], W["L0_ffn_down_embed"]).then_inc(loaded, 16)
                sync.dma_start(up[:, :, :], W["L0_ffn_up_embed"].rearrange("(c e) d -> e c d", e=P)).then_inc(loaded, 16)
                sync.dma_start(wq[:, :], W["L0_ffn_w_q"]).then_inc(loaded, 16)

        layernorm(nc, K, X, xn, xT)
        loads_done(nc, loaded, 6)
        l0_hidden(nc, xT, downT, G, EC)
        l0_queries(nc, K, wq, xT, keysT, bn, sim, C, NK)
        l0_select(nc, X, K, sim, G, up, H, NK, TOP, EC)


@scoped
def l0_hidden(nc, sp, xT, downT, G, EC):
    ps = sp.ps("hidden", [P, 8, BANK])
    hidden_ready = sp.sem("hidden_ready")
    gelu_done = sp.sem("gelu_done")
    with nc.Block() as block:
        @block.tensor
        def _(pe):
            for n in range(EC * NB):
                if n >= 8:
                    pe.wait_ge(gelu_done, n - 7)
                nc.tensor.matmul(ps[:, n % 8, :], downT[:, (n // NB) * P:(n // NB + 1) * P], xT[:, (n % NB) * BANK:(n % NB + 1) * BANK],
                                 start=True, stop=True).then_inc(hidden_ready, 1)

        @block.scalar
        def _(act):
            for n in range(EC * NB):
                act.wait_ge(hidden_ready, n + 1)
                nc.scalar.activation(G[:, n // NB, (n % NB) * BANK:(n % NB + 1) * BANK], ps[:, n % 8, :], ACT.Gelu_apprx_tanh).then_inc(gelu_done, 1)


@scoped
def l0_queries(nc, sp, K, wq_all, xT, keysT, bn, sim, C, NK):
    U = P // NK
    wq = sp.sb("wq_chunks", [P, U * P])
    kw = sp.sb("key_weights", [P, U, P])
    qn = sp.sb("queries", [P, 2, T])
    simF = sp.sb("sims_key_major", [P, NB, BANK])
    stats = sp.sb("bn_stats", [P, 2, NB, 6])
    mv = sp.sb("bn_moments", [P, 2, 2])
    std = sp.sb("bn_std", [P, 2])
    rstd = sp.sb("bn_rstd", [P, 2])
    ab = sp.sb("bn_affine", [P, 2, 3])
    psQ = sp.ps("queries", [P, NB, BANK])
    psK = sp.ps("sims", [P, NB, BANK])
    S = {n: sp.sem(n) for n in ("wq_ready keys_ready q_ready stats_ready mv_ready std_ready rstd_ready a_ready ma_ready b_ready q_normed "
                                "sim_ready sim_copied turned").split()}
    with nc.Block() as block:
        @block.gpsimd
        def _(pool):
            nc.gpsimd.memset(kw[:, :, :], 0.0)

    with nc.Fori(0, C // U) as c4:
        with nc.Block() as block:
            @block.gpsimd
            def _(pool):
                for i in range(U):
                    nc.gpsimd.tensor_copy(wq[:, i * P:(i + 1) * P], wq_all[:, bass.ds(c4 * (U * P) + i * P, P)]).then_inc(S["wq_ready"], 1)
                for i in range(U):
                    nc.gpsimd.tensor_copy(kw[:, i, i * NK:(i + 1) * NK], keysT[:, bass.ds(c4 * U + i, 1), :].rearrange("p a n -> p (a n)")).then_inc(S["keys_ready"], 1)

            @block.tensor
            def _(pe):
                for i in range(U + 1):
                    if i < U:
                        pe.wait_ge(S["wq_ready"], i + 1)
                        for b in range(NB):
                            if i >= 1:
                                pe.wait_ge(S["q_normed"], (i - 1) * NB + b + 1)
                            nc.tensor.matmul(psQ[:, b, :], wq[:, i * P:(i + 1) * P], xT[:, b * BANK:(b + 1) * BANK],
                                             start=True, stop=True).then_inc(S["q_ready"], 1)
                    if i >= 1:
                        pe.wait_ge(S["keys_ready"], i)
                        for b in range(NB):
                            pe.wait_ge(S["q_normed"], (i - 1) * NB + b + 1)
                            nc.tensor.matmul(psK[:, b, :], kw[:, i - 1, :], qn[:, (i - 1) % 2, b * BANK:(b + 1) * BANK],
                                             start=(i == 1), stop=(i == U)).then_inc(S["sim_ready"], 1)
                for b in range(NB):
                    pe.wait_ge(S["sim_copied"], b + 1)
                    for j in range(TPB):
                        last = nc.tensor.transpose(psQ[:, b, j * P:(j + 1) * P], simF[:, b, j * P:(j + 1) * P], K.ident[:, :])
                    last.then_inc(S["turned"], 1)

            @block.scalar
            def _(act):
                for i in range(U):
                    act.wait_ge(S["mv_ready"], i + 1)
                    nc.scalar.activation(std[:, i % 2:i % 2 + 1], mv[:, i % 2, 1:2], ACT.Sqrt, bias=K.eps[:, 0:1]).then_inc(S["std_ready"], 1)
                for b in range(NB):
                    act.wait_ge(S["sim_ready"], (U - 1) * NB + b + 1)
                    nc.scalar.copy(simF[:, b, :], psK[:, b, :]).then_inc(S["sim_copied"], 1)

            @block.vector
            def _(dve):
                for i in range(U):
                    c, w = c4 * U + i, i % 2
                    for b in range(NB):
                        dve.wait_ge(S["q_ready"], i * NB + b + 1)
                        nc.vector.bn_stats(stats[:, w, b, :], psQ[:, b, :]).then_inc(S["stats_ready"], 1)
                    dve.wait_ge(S["stats_ready"], (i + 1) * NB)
                    nc.vector.bn_aggr(mv[:, w, :], stats[:, w, :, :].rearrange("p b s -> p (b s)")).then_inc(S["mv_ready"], 1)
                    dve.wait_ge(S["std_ready"], i + 1)
                    nc.vector.reciprocal(rstd[:, w:w + 1], std[:, w:w + 1]).then_inc(S["rstd_ready"], 1)
                    dve.wait_ge(S["rstd_ready"], i + 1)
                    nc.vector.tensor_tensor(ab[:, w, 0:1], rstd[:, w:w + 1], bn[:, 0, bass.ds(c, 1)], ALU.mult).then_inc(S["a_ready"], 1)
                    dve.wait_ge(S["a_ready"], i + 1)
                    nc.vector.tensor_tensor(ab[:, w, 2:3], mv[:, w, 0:1], ab[:, w, 0:1], ALU.mult).then_inc(S["ma_ready"], 1)
                    dve.wait_ge(S["ma_ready"], i + 1)
                    nc.vector.tensor_tensor(ab[:, w, 1:2], bn[:, 1, bass.ds(c, 1)], ab[:, w, 2:3], ALU.subtract).then_inc(S["b_ready"], 1)
                    dve.wait_ge(S["b_ready"], i + 1)
                    if i >= 2:
                        dve.wait_ge(S["sim_ready"], (i - 1) * NB)
                    for b in range(NB):
                        nc.vector.tensor_scalar(qn[:, w, b * BANK:(b + 1) * BANK], psQ[:, b, :], ab[:, w, 0:1], ab[:, w, 1:2],
                                                ALU.mult, ALU.add).then_inc(S["q_normed"], 1)
                for b in range(NB):
                    dve.wait_ge(S["turned"], b + 1)
                    nc.vector.tensor_copy(sim[:, b * TPB:(b + 1) * TPB, bass.ds(c4 * U, U), :], psQ[:, b, :].rearrange("p (t c n) -> p t c n", c=U, n=NK))
        nc.gpsimd.sem_clear(sem_range(S))
        nc.all_engine_barrier()


@scoped
def l0_select(nc, sp, X, K, sim, G, up, H, NK, TOP, EC):
    U = 8
    RING = 3
    simt = sp.sb("sim_tile", [P, 2, 2 * H, NK])
    top = sp.sb("top_keys", [P, 2 * H, TOP])
    pairs = sp.sb("pair_sums", [P, H, TOP, TOP])
    best = sp.sb("best", [P, 2, H, TOP])
    nmax = sp.sb("neg_best", [P, 2, H])
    shifted = sp.sb("best_shifted", [P, H, TOP])
    expd = sp.sb("best_exp", [P, H, TOP])
    z = sp.sb("z", [P, H])
    rz = sp.sb("one_over_z", [P, 2, H])
    sums = sp.sb("all_sums", [P, RING, NK * NK])
    exps = sp.sb("all_exps", [P, RING, NK * NK])
    picked = sp.sb("picked", [P, RING, NK * NK])
    diag = sp.sb("diag_rz", [P, RING, P])
    weighted = sp.sb("weighted_hidden", [P, EC, P])
    psW = sp.ps("weights", [P, 2, EC // TPB, BANK])
    psY = sp.ps("out", [P, BANK])
    names = ("tile_ready top_ready pairs_ready best_ready shifted_ready exp8_ready z_ready rz_ready diag_ready "
             "sums_ready exps_ready picked_ready added weighted_ready out_ready y_added").split()
    S = {n: sp.sem(n) for n in names}
    with nc.Fori(0, NT // U) as t4:
        with nc.Block() as block:
            @block.gpsimd
            def _(pool):
                for n in range(U * H):
                    u, h = n // H, n % H
                    if h == 0:
                        pool.wait_ge(S["tile_ready"], u + 1)
                    if n >= RING:
                        pool.wait_ge(S["picked_ready"], n - RING + 1)
                    nc.gpsimd.tensor_tensor(sums[:, n % RING, :].rearrange("p (i j) -> p i j", j=NK),
                                            bcast(simt[:, u % 2, h, :].unsqueeze(2), [P, NK, NK]),
                                            bcast(simt[:, u % 2, H + h, :].unsqueeze(1), [P, NK, NK]), ALU.add).then_inc(S["sums_ready"], 1)

            @block.scalar
            def _(act):
                def fetch(u):
                    nc.scalar.copy(simt[:, u % 2, :, :], sim[:, bass.ds(t4 * U + u, 1), :, :].rearrange("p a c n -> p (a c) n")).then_inc(S["tile_ready"], 1)

                def exp_best(u):
                    act.wait_ge(S["shifted_ready"], 2 * (u + 1))
                    nc.scalar.activation(expd[:, :, :], shifted[:, :, :], ACT.Exp).then_inc(S["exp8_ready"], 1)

                fetch(0)
                exp_best(0)
                for n in range(U * H):
                    u, h = n // H, n % H
                    act.wait_ge(S["sums_ready"], n + 1)
                    if n >= RING:
                        act.wait_ge(S["picked_ready"], n - RING + 1)
                    nc.scalar.activation(exps[:, n % RING, :], sums[:, n % RING, :], ACT.Exp, bias=nmax[:, u % 2, h:h + 1]).then_inc(S["exps_ready"], 1)
                    if h == 0:
                        act.wait_ge(S["rz_ready"], u + 1)
                    if n >= RING:
                        act.wait_ge(S["added"], n - RING + 1)
                    nc.scalar.activation(diag[:, n % RING, :], K.ident[:, :], ACT.Identity, scale=rz[:, u % 2, h:h + 1]).then_inc(S["diag_ready"], 1)
                    if u + 1 < U and h == 0:
                        fetch(u + 1)
                    if u + 1 < U and h == 6:
                        exp_best(u + 1)

            @block.vector
            def _(dve):
                def top_keys(u, part):
                    dve.wait_ge(S["tile_ready"], u + 1)
                    for c in range(part * H // 2, (part + 1) * H // 2):
                        nc.vector.max(top[:, c, :], simt[:, u % 2, c, :]).then_inc(S["top_ready"], 1)

                def pair_sums(u):
                    dve.wait_ge(S["top_ready"], 2 * H * (u + 1))
                    nc.vector.tensor_tensor(pairs[:, :, :, :], bcast(top[:, 0:H, :].unsqueeze(3), [P, H, TOP, TOP]),
                                            bcast(top[:, H:2 * H, :].unsqueeze(2), [P, H, TOP, TOP]), ALU.add).then_inc(S["pairs_ready"], 1)

                def best_sums(u):
                    w = u % 2
                    dve.wait_ge(S["pairs_ready"], u + 1)
                    for h in range(H):
                        last = nc.vector.max(best[:, w, h, :], pairs[:, h, :, :].rearrange("p i j -> p (i j)"))
                    last.then_inc(S["best_ready"], 1)
                    dve.wait_ge(S["best_ready"], u + 1)
                    nc.vector.tensor_tensor(shifted[:, :, :], best[:, w, :, :], bcast(best[:, w, :, 0:1], [P, H, TOP]), ALU.subtract).then_inc(S["shifted_ready"], 1)
                    nc.vector.tensor_scalar(nmax[:, w, :], best[:, w, :, 0], -1.0, None, ALU.mult).then_inc(S["shifted_ready"], 1)

                def one_over_sums(u):
                    dve.wait_ge(S["exp8_ready"], u + 1)
                    nc.vector.tensor_reduce(z[:, :], expd[:, :, :], axis=AX_X, op=ALU.add).then_inc(S["z_ready"], 1)
                    dve.wait_ge(S["z_ready"], u + 1)
                    nc.vector.reciprocal(rz[:, u % 2, :], z[:, :]).then_inc(S["rz_ready"], 1)

                def weigh(u):
                    dve.wait_ge(S["added"], (u + 1) * H)
                    nc.vector.tensor_tensor(weighted[:, :, :], psW[:, u % 2, :, :].rearrange("p b (c n) -> p (b c) n", n=P),
                                            G[:, :, bass.ds((t4 * U + u) * P, P)], ALU.mult).then_inc(S["weighted_ready"], 1)

                def add_out(u):
                    dve.wait_ge(S["out_ready"], u + 1)
                    xt = X[:, bass.ds(t4 * U + u, 1), :].rearrange("p a n -> p (a n)")
                    nc.vector.tensor_tensor(xt, xt, psY[:, 0:D], ALU.add).then_inc(S["y_added"], 1)

                for part in range(4):
                    top_keys(0, part)
                pair_sums(0)
                best_sums(0)
                one_over_sums(0)
                for n in range(U * H):
                    u, h = n // H, n % H
                    dve.wait_ge(S["exps_ready"], n + 1)
                    if n >= RING:
                        dve.wait_ge(S["added"], n - RING + 1)
                    nc.vector.scalar_tensor_tensor(out=picked[:, n % RING, :], in0=sums[:, n % RING, :], scalar=best[:, u % 2, h, TOP - 1:TOP],
                                                   in1=exps[:, n % RING, :], op0=ALU.is_ge, op1=ALU.mult).then_inc(S["picked_ready"], 1)
                    if h == 0 and u >= 1:
                        weigh(u - 1)
                    if h == 3 and u >= 1:
                        add_out(u - 1)
                    if u + 1 < U:
                        if h < 4:
                            top_keys(u + 1, h)
                        if h == 4:
                            pair_sums(u + 1)
                        if h == 5:
                            best_sums(u + 1)
                        if h == 7:
                            one_over_sums(u + 1)
                weigh(U - 1)
                add_out(U - 1)

            @block.tensor
            def _(pe):
                def out(u):
                    pe.wait_ge(S["weighted_ready"], u + 1)
                    if u >= 1:
                        pe.wait_ge(S["y_added"], u)
                    for e in range(EC):
                        last = nc.tensor.matmul(psY[:, 0:D], weighted[:, e, :], up[:, e, :], start=(e == 0), stop=(e == EC - 1))
                    last.then_inc(S["out_ready"], 1)

                for n in range(U * H):
                    u, h = n // H, n % H
                    pe.wait_ge(S["diag_ready"], n + 1)
                    pe.wait_ge(S["picked_ready"], n + 1)
                    for e in range(EC):
                        last = nc.tensor.matmul(psW[:, u % 2, e // TPB, (e % TPB) * P:(e % TPB + 1) * P], picked[:, n % RING, e * P:(e + 1) * P],
                                                diag[:, n % RING, :], start=(h == 0 and e % TPB == 0), stop=(h == H - 1), skip_group_check=True)
                    last.then_inc(S["added"], 1)
                    if h == 1 and u >= 1:
                        out(u - 1)
                out(U - 1)
        nc.gpsimd.sem_clear(sem_range(S))
        nc.all_engine_barrier()


def l1_attention(nc, X, K, W):
    H, G, HD = 16, 4, 8
    with sublayer(nc) as sp:
        QS = sp.sb("q_stackT", [72, H, T], BF16)
        KS = sp.sb("k_stackT", [72, G, T], BF16)
        V = sp.sb("v", [P, NT, G, HD])
        xn = sp.sb("xn", [P, NT, D])
        l1_qkv(nc, X, K, W, QS, KS, V, xn, H, G, HD)
        ZT = sp.sb("zT", [H // G * HD, G, T])
        l1_core(nc, QS, KS, V, ZT, K, H, G, HD)
        l1_project(nc, ZT, W, X, G)


@scoped
def project_add(nc, sp, K, Z, w_dram, X):
    w = sp.sb("w", [P, D])
    ZT = sp.sb("ZT", [P, T])
    psY = sp.ps("y", [P, 2, BANK])
    w_loaded = sp.sem("w_loaded")
    y_ready = sp.sem("y_ready")
    y_added = sp.sem("y_added")
    transpose_tokens(nc, K, Z, ZT)
    with nc.Block() as block:
        @block.sync
        def _(sync):
            sync.dma_start(w[:, :], w_dram).then_inc(w_loaded, 16)

        @block.tensor
        def _(pe):
            pe.wait_ge(w_loaded, 16)
            for b in range(NB):
                if b >= 2:
                    pe.wait_ge(y_added, b - 1)
                for j in range(TPB):
                    t = b * TPB + j
                    last = nc.tensor.matmul(psY[:, b % 2, j * D:(j + 1) * D], ZT[:, t * P:(t + 1) * P], w[:, :], start=True, stop=True)
                last.then_inc(y_ready, 1)

        @block.vector
        def _(dve):
            for b in range(NB):
                dve.wait_ge(y_ready, b + 1)
                xb = X[:, b * TPB:(b + 1) * TPB, :].rearrange("p t d -> p (t d)")
                nc.vector.tensor_tensor(xb, xb, psY[:, b % 2, :], ALU.add).then_inc(y_added, 1)


@scoped
def l1_qkv(nc, sp, X, K, W, QS, KS, V, xn, H, G, HD):
    N = H + G
    HALF = HD // 2
    xT = sp.sb("xT", [P, T])
    layernorm(nc, K, X, xn, xT)
    w = sp.sb("w_qkv", [P, (N + G) * HD])
    trig = sp.sb("rope", [P, 2, NT, HALF])
    qk = sp.sb("qk", [P, NT, N, HD])
    sq = sp.sb("squares", [P, NT, N, HD])
    nrm = sp.sb("norms", [P, 2, NT * N])
    rot = sp.sb("rotated", [P, NT, N, HD])
    parts = sp.sb("parts", [P, 3, NT * N, HD], BF16)
    stack = sp.sb("stack", [P, NT * N, 9, HD], BF16)
    tmp = stack[:, 0:2 * NT * N // 9 + 1, :, :].rearrange("p a i d -> p (a i d)")[:, 0:2 * NT * N * HD].bitcast(F32).rearrange(
        "p (t n d) -> p t n d", t=NT, n=N)
    identb = sp.sb("identb", [P, P], BF16)
    psP = sp.ps("qkv", [P, 4, BANK])
    psT = sp.ps("turned", [72, 4, 2 * BANK], BF16)
    names = ("loaded qkv_ready qkv_copied sq_ready ss_ready nrm_ready eps_added rn_ready normed "
             "c_ready s_ready rotated part1 rest1 part2 rest2 part3 stacked identb_ready turned_ready dve_copied act_copied").split()
    S = {n: sp.sem(n) for n in names}
    with nc.Block() as block:
        @block.sync
        def _(sync):
            sync.dma_start(w[:, :], W["L1_attn_w_qkv"]).then_inc(S["loaded"], 16)
            sync.dma_start(trig[:, :, :, :], W["rope8"]).then_inc(S["loaded"], 16)

        @block.tensor
        def _(pe):
            pe.wait_ge(S["loaded"], 32)
            WD = (N + G) * HD
            for n in range(NT // 2):
                if n >= 4:
                    pe.wait_ge(S["qkv_copied"], 2 * (n - 3))
                for j in range(2):
                    t = 2 * n + j
                    last = nc.tensor.matmul(psP[:, n % 4, j * WD:(j + 1) * WD], xT[:, t * P:(t + 1) * P], w[:, :], start=True, stop=True)
                last.then_inc(S["qkv_ready"], 1)
            pe.wait_ge(S["identb_ready"], 1)
            pe.wait_ge(S["stacked"], 3)
            st = stack[:, :, :, :].rearrange("p (t n) i d -> p t n (i d)", n=N)
            for n in range(2 * N):
                if n >= 4:
                    pe.wait_ge(S["dve_copied" if n % 2 == 0 else "act_copied"], (n - 4) // 2 + 1)
                for j in range(8):
                    last = nc.tensor.transpose(psT[:, n % 4, j * P:(j + 1) * P], st[:, (n % 2) * 8 + j, n // 2, :], identb[:, :])
                last.then_inc(S["turned_ready"], 1)

        def stack_out(n):
            h, half = n // 2, n % 2
            return (QS[:, h, half * 1024:(half + 1) * 1024] if h < H else KS[:, h - H, half * 1024:(half + 1) * 1024])

        def stack_views(i, t):
            part = parts[:, i, :, :].rearrange("p (t n) d -> p t n d", n=N)[:, t, :, :]
            to = stack[:, :, :, :].rearrange("p (t n) i d -> p t n i d", n=N)[:, t, :, :, :]
            return ((to[:, 0:H, 3 * i:3 * i + 3, :], bcast(part[:, 0:H, :].unsqueeze(2), [P, H, 3, HD])),
                    (to[:, H:N, i:9:3, :], bcast(part[:, H:N, :].unsqueeze(2), [P, G, 3, HD])))

        @block.scalar
        def _(act):
            for n in range(NT // 2):
                act.wait_ge(S["qkv_ready"], n + 1)
                src = psP[:, n % 4, 0:2 * (N + G) * HD].rearrange("p (t c) -> p t c", t=2)
                nc.scalar.copy(qk[:, 2 * n:2 * n + 2, :, :].rearrange("p t n d -> p t (n d)"), src[:, :, 0:N * HD]).then_inc(S["qkv_copied"], 1)
                nc.scalar.copy(V[:, 2 * n:2 * n + 2, :, :], src[:, :, N * HD:].rearrange("p t (g d) -> p t g d", d=HD)).then_inc(S["qkv_copied"], 1)
            act.wait_ge(S["ss_ready"], 1)
            nc.scalar.activation(nrm[:, 1, :], nrm[:, 0, :], ACT.Sqrt).then_inc(S["nrm_ready"], 1)
            for i, done in ((0, "part1"), (1, "part2")):
                act.wait_ge(S[done], 1)
                for t in range(NT):
                    for out, src in stack_views(i, t):
                        last = nc.scalar.copy(out, src)
                last.then_inc(S["stacked"], 1)
            for n in range(1, 2 * N, 2):
                act.wait_ge(S["turned_ready"], n + 1)
                nc.scalar.copy(stack_out(n), psT[:, n % 4, :]).then_inc(S["act_copied"], 1)

        @block.gpsimd
        def _(pool):
            nc.gpsimd.tensor_copy(identb[:, :], K.ident[:, :]).then_inc(S["identb_ready"], 1)

        @block.vector
        def _(dve):
            dve.wait_ge(S["qkv_copied"], NT)
            flat = "p t n d -> p (t n d)"
            nc.vector.tensor_tensor(sq[:, :, :, :].rearrange(flat), qk[:, :, :, :].rearrange(flat), qk[:, :, :, :].rearrange(flat), ALU.mult).then_inc(S["sq_ready"], 1)
            dve.wait_ge(S["sq_ready"], 1)
            nc.vector.tensor_reduce(nrm[:, 0, :], sq[:, :, :, :].rearrange("p t n d -> p (t n) d"), axis=AX_X, op=ALU.add).then_inc(S["ss_ready"], 1)
            dve.wait_ge(S["nrm_ready"], 1)
            nc.vector.tensor_scalar(nrm[:, 0, :], nrm[:, 1, :], 1e-10, None, ALU.add).then_inc(S["eps_added"], 1)
            dve.wait_ge(S["eps_added"], 1)
            nc.vector.reciprocal(nrm[:, 1, :], nrm[:, 0, :]).then_inc(S["rn_ready"], 1)
            dve.wait_ge(S["rn_ready"], 1)
            nc.vector.tensor_tensor(sq[:, :, :, :].rearrange("p t n d -> p (t n) d"), qk[:, :, :, :].rearrange("p t n d -> p (t n) d"),
                                    bcast(nrm[:, 1, :].unsqueeze(2), [P, NT * N, HD]), ALU.mult).then_inc(S["normed"], 1)
            dve.wait_ge(S["normed"], 1)
            dve.wait_ge(S["loaded"], 32)
            sh = [P, NT, N, HALF]
            cos, sin = (bcast(trig[:, i, :, :].unsqueeze(2), sh) for i in range(2))
            x1, x2 = sq[:, :, :, 0:HALF], sq[:, :, :, HALF:HD]
            nc.vector.tensor_tensor(rot[:, :, :, 0:HALF], x1, cos, ALU.mult).then_inc(S["c_ready"], 1)
            nc.vector.tensor_tensor(rot[:, :, :, HALF:HD], x2, cos, ALU.mult).then_inc(S["c_ready"], 1)
            nc.vector.tensor_tensor(tmp[:, :, :, 0:HALF], x2, sin, ALU.mult).then_inc(S["s_ready"], 1)
            nc.vector.tensor_tensor(tmp[:, :, :, HALF:HD], x1, sin, ALU.mult).then_inc(S["s_ready"], 1)
            dve.wait_ge(S["c_ready"], 2)
            dve.wait_ge(S["s_ready"], 2)
            nc.vector.tensor_tensor(qk[:, :, :, 0:HALF], rot[:, :, :, 0:HALF], tmp[:, :, :, 0:HALF], ALU.subtract).then_inc(S["rotated"], 1)
            nc.vector.tensor_tensor(qk[:, :, :, HALF:HD], rot[:, :, :, HALF:HD], tmp[:, :, :, HALF:HD], ALU.add).then_inc(S["rotated"], 1)
            dve.wait_ge(S["rotated"], 2)
            v, rest = qk[:, :, :, :].rearrange(flat), rot[:, :, :, :].rearrange(flat)
            part = [parts[:, i, :, :].rearrange("p n d -> p (n d)") for i in range(3)]
            nc.vector.tensor_copy(part[0], v).then_inc(S["part1"], 1)
            dve.wait_ge(S["part1"], 1)
            nc.vector.tensor_tensor(rest, v, part[0], ALU.subtract).then_inc(S["rest1"], 1)
            dve.wait_ge(S["rest1"], 1)
            nc.vector.tensor_copy(part[1], rest).then_inc(S["part2"], 1)
            dve.wait_ge(S["part2"], 1)
            nc.vector.tensor_tensor(v, rest, part[1], ALU.subtract).then_inc(S["rest2"], 1)
            dve.wait_ge(S["rest2"], 1)
            nc.vector.tensor_copy(part[2], v).then_inc(S["part3"], 1)
            dve.wait_ge(S["part3"], 1)
            for t in range(NT):
                for out, src in stack_views(2, t):
                    last = nc.vector.tensor_copy(out, src)
            last.then_inc(S["stacked"], 1)
            for n in range(0, 2 * N, 2):
                dve.wait_ge(S["turned_ready"], n + 1)
                nc.vector.tensor_copy(stack_out(n), psT[:, n % 4, :]).then_inc(S["dve_copied"], 1)


@scoped
def l1_core(nc, sp, QS, KS, V, ZT, K, H, G, HD):
    HPG = H // G
    GW = HPG * HD
    prob = sp.sb("prob", [P, 3, 2 * BANK])
    VW = sp.sb("v_weights", [P, NT, HPG, 2 * GW])
    rden = sp.sb("rden", [GW, 2, BANK])
    psS = sp.ps("scores", [P, 3, 2 * BANK])
    psO = sp.ps("outs", [2 * GW, 2, BANK])
    items = []
    for b in range(NB):
        for j in range(HPG):
            for i in range(2 * b):
                items.append((b, j, [(2 * i, 0, BANK), (2 * i + 1, BANK, BANK)]))
            items.append((b, j, [(TPB * b, 0, BANK), (TPB * b + 1, BANK, 3 * P)]))
            items.append((b, j, [(TPB * b + 2, 0, 2 * P), (TPB * b + 3, 2 * P, P)]))
    diagonal = [tiles[0][0] >= TPB * b for b, j, tiles in items]
    masks_to = [sum(diagonal[:n + 1]) for n in range(len(items))]
    last_of = {b: n for n, (b, j, tiles) in enumerate(items)}
    names = "v_set v_placed qk_done exp_done mask_done pv_done rden_ready z_done".split()
    S = {n: sp.sem(n) for n in names}
    with nc.Block() as block:
        @block.gpsimd
        def _(pool):
            nc.gpsimd.memset(VW[:, :, :, :], 0.0).then_inc(S["v_set"], 1)
            pool.wait_ge(S["v_set"], 1)
            for j in range(HPG):
                nc.gpsimd.memset(VW[:, :, j, GW + j * HD:GW + (j + 1) * HD], 1.0)
    with nc.Fori(0, G) as g:
        with nc.Block() as block:
            @block.tensor
            def _(pe):
                def qk(n):
                    b, j, tiles = items[n]
                    if n >= 3:
                        pe.wait_ge(S["exp_done"], n - 2)
                    for t, col, w in tiles:
                        last = nc.tensor.matmul(psS[:, n % 3, col:col + w], KS[:, bass.ds(g, 1), t * P:(t + 1) * P].rearrange("p a n -> p (a n)"),
                                                QS[:, bass.ds(g * HPG + j, 1), (b + 1) * BANK - w:(b + 1) * BANK].rearrange("p a n -> p (a n)"),
                                                start=True, stop=True)
                    last.then_inc(S["qk_done"], 1)

                def pv(n):
                    b, j, tiles = items[n]
                    if n == 0:
                        pe.wait_ge(S["v_placed"], HPG)
                    if j == 0 and tiles[0][0] == 0 and b >= 2:
                        pe.wait_ge(S["z_done"], b - 1)
                    if diagonal[n]:
                        pe.wait_ge(S["mask_done"], masks_to[n])
                    else:
                        pe.wait_ge(S["exp_done"], n + 1)
                    for t, col, w in tiles:
                        last = nc.tensor.matmul(psO[:, b % 2, BANK - w:BANK], VW[:, t, j, :], prob[:, n % 3, col:col + w],
                                                start=(j == 0 and t == 0), stop=(j == HPG - 1 and t == TPB * b + TPB - 1), skip_group_check=True)
                    last.then_inc(S["pv_done"], 1)

                for s in range(len(items) + 2):
                    if s < len(items):
                        qk(s)
                    if s >= 2:
                        pv(s - 2)

            @block.scalar
            def _(act):
                for n, (b, j, tiles) in enumerate(items):
                    act.wait_ge(S["qk_done"], n + 1)
                    if n >= 3:
                        act.wait_ge(S["pv_done"], n - 2)
                    w = tiles[1][1] + tiles[1][2]
                    nc.scalar.activation(prob[:, n % 3, 0:w], psS[:, n % 3, 0:w], ACT.Exp, scale=HD ** -0.5).then_inc(S["exp_done"], 1)

            @block.gpsimd
            def _(pool):
                for n, (b, j, tiles) in enumerate(items):
                    if diagonal[n]:
                        pool.wait_ge(S["exp_done"], n + 1)
                        d = tiles[1][1]
                        v = prob[:, n % 3, 0:2 * d].rearrange("p (a c) -> p a c", a=2)[:, :, 0:P]
                        nc.gpsimd.tensor_tensor(v, v, bcast(K.causal_k[:, :].unsqueeze(1), [P, 2, P]), ALU.mult).then_inc(S["mask_done"], 1)

            @block.vector
            def _(dve):
                for j in range(HPG):
                    nc.vector.tensor_copy(VW[:, :, j, j * HD:(j + 1) * HD], V[:, :, bass.ds(g, 1), :].rearrange("p t a n -> p t (a n)")).then_inc(S["v_placed"], 1)
                for b in range(NB):
                    dve.wait_ge(S["pv_done"], last_of[b] + 1)
                    nc.vector.reciprocal(rden[:, b % 2, :], psO[GW:2 * GW, b % 2, :]).then_inc(S["rden_ready"], 1)
                    dve.wait_ge(S["rden_ready"], b + 1)
                    nc.vector.tensor_tensor(ZT[:, bass.ds(g, 1), b * BANK:(b + 1) * BANK].rearrange("p a n -> p (a n)"), psO[0:GW, b % 2, :], rden[:, b % 2, :],
                                            ALU.mult).then_inc(S["z_done"], 1)
        nc.gpsimd.sem_clear(sem_range(S))
        nc.all_engine_barrier()


@scoped
def l1_project(nc, sp, ZT, W, X, G):
    GW = D // G
    w = sp.sb("w_o", [P, D])
    Z = sp.sb("zT_all", [P, T])
    psY = sp.ps("y", [P, 2, BANK])
    w_loaded = sp.sem("w_loaded")
    z_moved = sp.sem("z_moved")
    y_ready = sp.sem("y_ready")
    y_added = sp.sem("y_added")
    with nc.Block() as block:
        @block.sync
        def _(sync):
            for g in range(G):
                sync.dma_start(Z[g * GW:(g + 1) * GW, :], ZT[:, g, :]).then_inc(z_moved, 16)
            sync.dma_start(w[:, :], W["L1_attn_w_o"]).then_inc(w_loaded, 16)

        @block.tensor
        def _(pe):
            pe.wait_ge(w_loaded, 16)
            pe.wait_ge(z_moved, 16 * G)
            for b in range(NB):
                if b >= 2:
                    pe.wait_ge(y_added, b - 1)
                for j in range(TPB):
                    t = b * TPB + j
                    last = nc.tensor.matmul(psY[:, b % 2, j * D:(j + 1) * D], Z[:, t * P:(t + 1) * P], w[:, :], start=True, stop=True)
                last.then_inc(y_ready, 1)

        @block.vector
        def _(dve):
            for b in range(NB):
                dve.wait_ge(y_ready, b + 1)
                xb = X[:, b * TPB:(b + 1) * TPB, :].rearrange("p t d -> p (t d)")
                nc.vector.tensor_tensor(xb, xb, psY[:, b % 2, :], ALU.add).then_inc(y_added, 1)


@scoped
def route_top2(nc, sp, K, xT, wr_dram, br_dram, E, cw):
    wr = sp.sb("w_router", [P, E])
    br = sp.sb("b_router", [P, E])
    logit = sp.sb("logits", [P, NT, E])
    best = sp.sb("best", [P, NT, 8])
    ex = sp.sb("exp_logits", [P, NT, E])
    zz = sp.sb("z", [P, 2, NT])
    ps = sp.ps("logits", [P, NT, 16])
    S = {n: sp.sem(n) for n in "loaded logits_ready copied best_ready shifted exp_done masked sum_ready rz_ready".split()}
    with nc.Block() as block:
        @block.sync
        def _(sync):
            sync.dma_start(wr[:, :], wr_dram).then_inc(S["loaded"], 16)
            if br_dram is not None:
                sync.dma_start(br[:, :], br_dram.partition_broadcast(P)).then_inc(S["loaded"], 16)

        @block.tensor
        def _(pe):
            pe.wait_ge(S["loaded"], 16 if br_dram is None else 32)
            for t in range(NT):
                last = nc.tensor.matmul(ps[:, t, 0:E], xT[:, t * P:(t + 1) * P], wr[:, :], start=True, stop=True)
            last.then_inc(S["logits_ready"], 1)

        @block.vector
        def _(dve):
            dve.wait_ge(S["logits_ready"], 1)
            if br_dram is None:
                nc.vector.tensor_copy(logit[:, :, :], ps[:, :, 0:E]).then_inc(S["copied"], 1)
            else:
                dve.wait_ge(S["loaded"], 32)
                nc.vector.tensor_tensor(logit[:, :, :], ps[:, :, 0:E], bcast(br[:, :].unsqueeze(1), [P, NT, E]), ALU.add).then_inc(S["copied"], 1)
            dve.wait_ge(S["copied"], 1)
            for t in range(NT):
                nc.vector.max(best[:, t, :], logit[:, t, :]).then_inc(S["best_ready"], 1)
            dve.wait_ge(S["best_ready"], NT)
            nc.vector.tensor_tensor(ex[:, :, :], logit[:, :, :], bcast(best[:, :, 0:1], [P, NT, E]), ALU.subtract).then_inc(S["shifted"], 1)
            nc.vector.tensor_tensor(logit[:, :, :], logit[:, :, :], bcast(best[:, :, 1:2], [P, NT, E]), ALU.is_ge).then_inc(S["shifted"], 1)
            dve.wait_ge(S["shifted"], 2)
            dve.wait_ge(S["exp_done"], 1)
            nc.vector.tensor_tensor(cw[:, :, :], ex[:, :, :], logit[:, :, :], ALU.mult).then_inc(S["masked"], 1)
            dve.wait_ge(S["masked"], 1)
            nc.vector.tensor_reduce(zz[:, 0, :], cw[:, :, :], axis=AX_X, op=ALU.add).then_inc(S["sum_ready"], 1)
            dve.wait_ge(S["sum_ready"], 1)
            nc.vector.reciprocal(zz[:, 1, :], zz[:, 0, :]).then_inc(S["rz_ready"], 1)
            dve.wait_ge(S["rz_ready"], 1)
            nc.vector.tensor_tensor(cw[:, :, :], cw[:, :, :], bcast(zz[:, 1, :].unsqueeze(2), [P, NT, E]), ALU.mult)

        @block.scalar
        def _(act):
            act.wait_ge(S["shifted"], 1)
            nc.scalar.activation(ex[:, :, :], ex[:, :, :], ACT.Exp).then_inc(S["exp_done"], 1)


def load_experts(nc, sp, E, F, up_drams, down_dram, b1_dram=None):
    FC = -(-F // P)
    w1_all = sp.sb("w1_all", [P, len(up_drams), E * F])
    w2_all = sp.sb("w2_all", [P, FC, E, D])
    b1 = None if b1_dram is None else sp.sb("b1", [P, FC, E])
    loaded = sp.sem("experts_loaded")
    with nc.Block() as block:
        @block.sync
        def _(sync):
            for i, w in enumerate(up_drams):
                sync.dma_start(w1_all[:, i, :].rearrange("d (e f) -> d e f", e=E), w.rearrange("e d f -> d e f")).then_inc(loaded, 16)
            for c in range(FC):
                rows = min(P, F - c * P)
                sync.dma_start(w2_all[0:rows, c, :, :], down_dram[:, c * P:c * P + rows, :].rearrange("e f n -> f e n")).then_inc(loaded, 16)
            if b1_dram is not None:
                sync.dma_start(b1[:, :, :], b1_dram).then_inc(loaded, 16)
    return w1_all, w2_all, b1, loaded, len(up_drams) + FC + (b1_dram is not None)


@scoped
def expert_mlps(nc, sp, X, K, xT, cw, E, U, F, weights):
    w1_all, w2_all, b1, loaded, loads = weights
    NW = w1_all.shape[1]
    gated = NW == 2
    FC = -(-F // P)
    rows = [min(P, F - c * P) for c in range(FC)]
    w1 = sp.sb("w1_experts", [P, U, NW, F])
    gate = sp.sb("silu", [P, 2, BANK])
    gate2 = sp.sb("sigmoid", [P, 2, BANK])
    hid = sp.sb("hidden", [P, 2, FC, BANK])
    psG = sp.ps("gate", [P, 2, BANK])
    psU = sp.ps("up", [P, 2, BANK]) if gated else psG
    psY = sp.ps("y", [P, 2, BANK])
    S = {n: sp.sem(n) for n in "w_ready gu_ready silu_done sig_done hid_done y_ready y_added".split()}
    loads_done(nc, loaded, loads)
    n_items = U * NB * FC

    def place(n):
        g = n // FC
        return g // NB, g % NB, g, n % FC

    with nc.Fori(0, E // U) as eu:
        with nc.Block() as block:
            @block.gpsimd
            def _(pool):
                for u in range(U):
                    nc.gpsimd.tensor_copy(w1[:, u, :, :], w1_all[:, :, bass.ds((eu * U + u) * F, F)]).then_inc(S["w_ready"], 1)

            @block.tensor
            def _(pe):
                def hidden(n):
                    u, b, g, c = place(n)
                    if b == 0 and c == 0:
                        pe.wait_ge(S["w_ready"], u + 1)
                    if n >= 2:
                        pe.wait_ge(S["hid_done"], n - 1)
                    for i in range(NW):
                        last = nc.tensor.matmul((psG, psU)[i][0:rows[c], n % 2, :], w1[:, u, i, c * P:c * P + rows[c]], xT[:, b * BANK:(b + 1) * BANK],
                                                start=True, stop=True)
                    last.then_inc(S["gu_ready"], 1)

                def down(g):
                    pe.wait_ge(S["hid_done"], (g + 1) * FC)
                    if g >= 2:
                        pe.wait_ge(S["y_added"], TPB * (g - 1))
                    for j in range(TPB):
                        for c in range(FC):
                            last = nc.tensor.matmul(psY[:, g % 2, j * D:(j + 1) * D], hid[0:rows[c], g % 2, c, j * P:(j + 1) * P],
                                                    w2_all[0:rows[c], c, bass.ds(eu * U + g // NB, 1), :].rearrange("p a n -> p (a n)"),
                                                    start=(c == 0), stop=(c == FC - 1))
                    last.then_inc(S["y_ready"], 1)

                for n in range(n_items):
                    hidden(n)
                    if n % FC == 1 and n > FC:
                        down(n // FC - 1)
                down(U * NB - 1)

            @block.scalar
            def _(act):
                for n in range(n_items):
                    u, b, g, c = place(n)
                    act.wait_ge(S["gu_ready"], n + 1)
                    if gated:
                        if n >= 2:
                            act.wait_ge(S["silu_done"], n - 1)
                        nc.scalar.activation(gate2[0:rows[c], n % 2, :], psG[0:rows[c], n % 2, :], ACT.Sigmoid).then_inc(S["sig_done"], 1)
                    else:
                        if c == 0 and g >= 2:
                            act.wait_ge(S["y_ready"], g - 1)
                        nc.scalar.activation(hid[:, g % 2, c, :], psG[:, n % 2, :], ACT.Relu, bias=b1[:, c, bass.ds(eu * U + u, 1)]).then_inc(S["hid_done"], 1)

            @block.vector
            def _(dve):
                def add(g):
                    dve.wait_ge(S["y_ready"], g + 1)
                    if g >= NB:
                        dve.wait_ge(S["y_added"], TPB * (g - NB + 1))
                    for j in range(TPB):
                        t = g % NB * TPB + j
                        nc.vector.scalar_tensor_tensor(out=X[:, t, :], in0=psY[:, g % 2, j * D:(j + 1) * D], scalar=cw[:, t, bass.ds(eu * U + g // NB, 1)],
                                                       in1=X[:, t, :], op0=ALU.mult, op1=ALU.add).then_inc(S["y_added"], 1)

                for n in range(n_items if gated else 0):
                    u, b, g, c = place(n)
                    dve.wait_ge(S["sig_done"], n + 1)
                    nc.vector.tensor_tensor(gate[0:rows[c], n % 2, :], gate2[0:rows[c], n % 2, :], psG[0:rows[c], n % 2, :], ALU.mult).then_inc(S["silu_done"], 1)
                    dve.wait_ge(S["silu_done"], n + 1)
                    if c == 0 and g >= 2:
                        dve.wait_ge(S["y_ready"], g - 1)
                    nc.vector.tensor_tensor(hid[0:rows[c], g % 2, c, :], gate[0:rows[c], n % 2, :], psU[0:rows[c], n % 2, :], ALU.mult).then_inc(S["hid_done"], 1)
                    if c == FC - 1 and g >= 1:
                        add(g - 1)
                for g in range(U * NB - 1 if gated else 0, U * NB):
                    add(g)
        nc.gpsimd.sem_clear(sem_range(S))
        nc.all_engine_barrier()


def l1_experts(nc, X, K, W):
    E, F = 9, 352
    with sublayer(nc) as sp:
        xn = sp.sb("xn", [P, NT, D])
        xT = sp.sb("xT", [P, T])
        cw = sp.sb("expert_weights", [P, NT, E])
        weights = load_experts(nc, sp, E, F, [W["L1_ffn_Wg"], W["L1_ffn_Wu"]], W["L1_ffn_Wd"])
        layernorm(nc, K, X, xn, xT)
        route_top2(nc, K, xT, W["L1_ffn_Wr"], None, E, cw)
        expert_mlps(nc, X, K, xT, cw, E, 3, F, weights)


def l3_experts(nc, X, K, W):
    E, F = 8, 512
    with sublayer(nc) as sp:
        xn = sp.sb("xn", [P, NT, D])
        xT = sp.sb("xT", [P, T])
        cw = sp.sb("expert_weights", [P, NT, E])
        weights = load_experts(nc, sp, E, F, [W["L3_ffn_W1"]], W["L3_ffn_W2"], W["L3_ffn_b1"])
        layernorm(nc, K, X, xn, xT)
        route_top2(nc, K, xT, W["L3_ffn_W_router"], W["L3_ffn_b_router"], E, cw)
        expert_mlps(nc, X, K, xT, cw, E, 4, F, weights)
        with nc.Block() as block:
            @block.vector
            def _(dve):
                nc.vector.memset(xn[:, :, E:], 0.0)
                nc.vector.tensor_copy(xn[:, :, 0:E], cw[:, :, :])
        project_add(nc, K, xn, W["L3_ffn_b2"], X)


def l2_attention(nc, X, K, W):
    with sublayer(nc) as sp:
        xn = sp.sb("xn", [P, NT, D])
        xT = sp.sb("xT", [P, T])
        layernorm(nc, K, X, xn, xT)
        l2_memories(nc, X, K, W, xT, xn)


@scoped
def l2_memories(nc, sp, X, K, W, xT, Y):
    C = 8
    TWO_PI_HI = 6.28125
    TWO_PI_LO = float(2 * np.pi - TWO_PI_HI)
    ROUND = 12582912.0
    PI = float(np.nextafter(np.float32(np.pi), np.float32(0)))
    PHASE_SCALE = 10.0
    pos = sp.sb("positions", [P, T])
    posi = sp.sb("positions_int", [P, BANK], I32)
    consts = sp.sb("round_and_half_pi", [P, 2])
    gate = sp.sb("gate", [P, 2, C])
    freq = sp.sb("freqs", [P, C])
    rs = sp.sb("rsqrt_t", [P, NT])
    wo = sp.sb("wo", [P, C, D])
    U = 4
    N = U * NB
    wk = sp.sb("wk_chunks", [P, U * P])
    wv = sp.sb("wv_chunks", [P, U * P])
    ang = [sp.sb(n, [P, T]) for n in ("angle_pos", "angle_key")]
    turns = [sp.sb(n, [P, T]) for n in ("turns_pos", "turns_key")]
    v = sp.sb("v", [P, T])
    cs = [[sp.sb(f"{n}_{m}", [P, 1 + T]) for n in ("cos", "sin")] for m in ("pos", "key")]
    prod = [sp.sb(f"prod{i}", [P, T]) for i in range(4)]
    mem = [sp.sb(f"mem{i}", [P, T]) for i in range(4)]
    psK = sp.ps("k", [P, 2, BANK])
    psV = sp.ps("v", [P, 2, BANK])
    psY = sp.ps("y", [P, 4, BANK])
    loaded = sp.sem("loaded")
    setup = sp.sem("setup")
    names = ("w_loaded kv_ready v_copied ang_pos ang_key rounded_pos rounded_key turns_pos turns_key "
             "red1 red2 red3 abs_pos abs_key trig_pos trig_key prods mems finals y_ready").split()
    S = {n: sp.sem(n) for n in names}
    blocks = [slice(b * BANK, (b + 1) * BANK) for b in range(NB)]

    with nc.Block() as block:
        @block.sync
        def _(sync):
            sync.dma_start(gate[:, :, :], W["L2_attn_gate"]).then_inc(loaded, 16)
            sync.dma_start(freq[:, :], W["L2_attn_freqs"]).then_inc(loaded, 16)
            sync.dma_start(rs[:, :], W["rsqrt_t"]).then_inc(loaded, 16)
            sync.dma_start(wo[:, :, :], W["L2_attn_Wo"].rearrange("(c f) n -> f c n", f=P)).then_inc(loaded, 16)
            sync.wait_ge(loaded, 64)

        @block.gpsimd
        def _(pool):
            for b in range(NB):
                if b:
                    pool.wait_ge(setup, 2 * b)
                nc.gpsimd.iota(posi[:, :], pattern=[[1, BANK]], base=b * BANK, channel_multiplier=0).then_inc(setup, 1)
                pool.wait_ge(setup, 2 * b + 1)
                nc.gpsimd.tensor_copy(pos[:, blocks[b]], posi[:, :]).then_inc(setup, 1)

        @block.vector
        def _(dve):
            nc.vector.memset(consts[:, 0:1], ROUND)
            nc.vector.memset(consts[:, 1:2], float(np.pi / 2))
            nc.vector.memset(cs[1][0][:, 0:1], 0.0)
            nc.vector.memset(cs[1][1][:, 0:1], 0.0)
            nc.vector.memset(Y[:, :, :], 0.0)

    def shifted(b):
        return slice(1 + b * BANK, 1 + (b + 1) * BANK)

    with nc.Fori(0, C // U) as cu:
        with nc.Block() as block:
            @block.sync
            def _(sync):
                sync.dma_start(wk[:, :], W["L2_attn_Wk"][:, bass.ds(cu * (U * P), U * P)]).then_inc(S["w_loaded"], 16)
                sync.dma_start(wv[:, :], W["L2_attn_Wv"][:, bass.ds(cu * (U * P), U * P)]).then_inc(S["w_loaded"], 16)

            @block.tensor
            def _(pe):
                pe.wait_ge(S["w_loaded"], 32)
                for s in range(N + 2):
                    if s < N:
                        u, b = s // NB, s % NB
                        if s >= 2:
                            pe.wait_ge(S["ang_key"], s - 1)
                            pe.wait_ge(S["v_copied"], s - 1)
                        nc.tensor.matmul(psK[:, s % 2, :], wk[:, u * P:(u + 1) * P], xT[:, blocks[b]], start=True, stop=True)
                        nc.tensor.matmul(psV[:, s % 2, :], wv[:, u * P:(u + 1) * P], xT[:, blocks[b]], start=True, stop=True).then_inc(S["kv_ready"], 1)
                    if s >= 2:
                        n = s - 2
                        u, b = n // NB, n % NB
                        pe.wait_ge(S["finals"], 4 * (n + 1))
                        for j in range(TPB):
                            t = b * TPB + j
                            for i in range(4):
                                last = nc.tensor.matmul(psY[:, b, j * D:(j + 1) * D], prod[i][:, t * P:(t + 1) * P],
                                                        wo[:, bass.ds(cu * U + u, 1), :].rearrange("p a n -> p (a n)"),
                                                        start=(u == 0 and j == 0 and i == 0), stop=(u == U - 1 and i == 3), skip_group_check=True)
                        last.then_inc(S["y_ready"], 1)

            @block.scalar
            def _(act):
                def angles(n):
                    u, b = n // NB, n % NB
                    nc.scalar.activation(ang[0][:, blocks[b]], pos[:, blocks[b]], ACT.Identity, scale=freq[:, bass.ds(cu * U + u, 1)]).then_inc(S["ang_pos"], 1)
                    act.wait_ge(S["kv_ready"], n + 1)
                    nc.scalar.mul(ang[1][:, blocks[b]], psK[:, n % 2, :], PHASE_SCALE).then_inc(S["ang_key"], 1)
                    if n >= NB:
                        act.wait_ge(S["prods"], 4 * (n - NB + 1))
                    nc.scalar.copy(v[:, blocks[b]], psV[:, n % 2, :]).then_inc(S["v_copied"], 1)
                    for i, (made, done) in enumerate((("ang_pos", "rounded_pos"), ("ang_key", "rounded_key"))):
                        act.wait_ge(S[made], n + 1)
                        nc.scalar.activation(turns[i][:, blocks[b]], ang[i][:, blocks[b]], ACT.Identity, scale=float(1 / (2 * np.pi)),
                                             bias=consts[:, 0:1]).then_inc(S[done], 1)

                def trig(n):
                    b = n % NB
                    if n >= NB:
                        act.wait_ge(S["finals"], 4 * (n - NB + 1))
                        act.wait_ge(S["prods"], 4 * (n - NB + 2))
                    for i, (absd, done) in enumerate((("abs_pos", "trig_pos"), ("abs_key", "trig_key"))):
                        act.wait_ge(S["red3"], 2 * n + i + 1)
                        nc.scalar.activation(turns[i][:, blocks[b]], ang[i][:, blocks[b]], ACT.Abs).then_inc(S[absd], 1)
                        nc.scalar.activation(cs[i][1][:, shifted(b)], ang[i][:, blocks[b]], ACT.Sin).then_inc(S[done], 1)
                        act.wait_ge(S[absd], n + 1)
                        nc.scalar.activation(cs[i][0][:, shifted(b)], turns[i][:, blocks[b]], ACT.Sin, scale=-1.0, bias=consts[:, 1:2]).then_inc(S[done], 1)

                angles(0)
                for n in range(N):
                    if n + 1 < N:
                        angles(n + 1)
                    trig(n)

            @block.gpsimd
            def _(pool):
                def turn(n):
                    b = n % NB
                    for i, (rounded, done) in enumerate((("rounded_pos", "turns_pos"), ("rounded_key", "turns_key"))):
                        pool.wait_ge(S[rounded], n + 1)
                        nc.gpsimd.tensor_scalar(turns[i][:, blocks[b]], turns[i][:, blocks[b]], -ROUND, 1.0, ALU.add, ALU.mult).then_inc(S[done], 1)

                turn(0)
                for n in range(N):
                    b = n % NB
                    if n + 1 < N:
                        turn(n + 1)
                    pool.wait_ge(S["v_copied"], n + 1)
                    if n >= NB:
                        pool.wait_ge(S["y_ready"], n - NB + 1)
                    for i in range(4):
                        if i % 2 == 0:
                            pool.wait_ge(S["trig_pos" if i == 0 else "trig_key"], 2 * (n + 1))
                        src = shifted(b) if i < 2 else blocks[b]
                        nc.gpsimd.tensor_tensor(prod[i][:, blocks[b]], v[:, blocks[b]], cs[i // 2][i % 2][:, src], ALU.mult).then_inc(S["prods"], 1)

            @block.vector
            def _(dve):
                def add(b):
                    dve.wait_ge(S["y_ready"], N - NB + b + 1)
                    yb = Y[:, b * TPB:(b + 1) * TPB, :].rearrange("p t n -> p (t n)")
                    nc.vector.tensor_tensor(yb, yb, psY[:, b, :], ALU.add)

                def reduce(n):
                    b = n % NB
                    for i, made in enumerate(("turns_pos", "turns_key")):
                        dve.wait_ge(S[made], n + 1)
                        a = ang[i][:, blocks[b]]
                        nc.vector.scalar_tensor_tensor(out=a, in0=turns[i][:, blocks[b]], scalar=-TWO_PI_HI, in1=a, op0=ALU.mult, op1=ALU.add).then_inc(S["red1"], 1)
                    for i in range(2):
                        dve.wait_ge(S["red1"], 2 * n + i + 1)
                        a = ang[i][:, blocks[b]]
                        nc.vector.scalar_tensor_tensor(out=a, in0=turns[i][:, blocks[b]], scalar=-TWO_PI_LO, in1=a, op0=ALU.mult, op1=ALU.add).then_inc(S["red2"], 1)
                    for i in range(2):
                        dve.wait_ge(S["red2"], 2 * n + i + 1)
                        a = ang[i][:, blocks[b]]
                        nc.vector.tensor_scalar(a, a, PI, -PI, ALU.min, ALU.max).then_inc(S["red3"], 1)

                reduce(0)
                for n in range(N):
                    u, b = n // NB, n % NB
                    if n + 1 < N:
                        reduce(n + 1)
                    for i in range(4):
                        dve.wait_ge(S["prods"], 4 * n + i + 1)
                        if b:
                            dve.wait_ge(S["mems"], 4 * (n - 1) + i + 1)
                        nc.vector.tensor_tensor_scan(mem[i][:, blocks[b]], bcast(K.ones[:, 0:1], [P, BANK]), prod[i][:, blocks[b]],
                                                     0.0 if b == 0 else mem[i][:, b * BANK - 1:b * BANK], ALU.mult, ALU.add).then_inc(S["mems"], 1)
                    for i in range(4):
                        dve.wait_ge(S["mems"], 4 * n + i + 1)
                        nc.vector.scalar_tensor_tensor(out=prod[i][:, blocks[b]], in0=mem[i][:, blocks[b]], scalar=gate[:, i // 2, bass.ds(cu * U + u, 1)],
                                                       in1=cs[i // 2][i % 2][:, shifted(b)], op0=ALU.mult, op1=ALU.mult).then_inc(S["finals"], 1)
                for b in range(NB):
                    add(b)

        nc.gpsimd.sem_clear(sem_range(S))
        nc.all_engine_barrier()
    with nc.Block() as block:
        @block.vector
        def _(dve):
            for t in range(NT):
                nc.vector.scalar_tensor_tensor(out=X[:, t, :], in0=Y[:, t, :], scalar=rs[:, t:t + 1], in1=X[:, t, :], op0=ALU.mult, op1=ALU.add)


@scoped
def shift_tokens(nc, sp, src, dst):
    HF = D // 2
    zeroed = sp.sem("zeroed")
    shifted = sp.sem("shifted")
    with nc.Block() as block:
        @block.sync
        def _(sync):
            sync.dma_start(dst[1:P, :, HF:D], src[0:P - 1, :, HF:D]).then_inc(shifted, 16)
            sync.dma_start(dst[0:1, 1:NT, HF:D], src[P - 1:P, 0:NT - 1, HF:D]).then_inc(shifted, 16)
            sync.wait_ge(shifted, 32)

        @block.vector
        def _(dve):
            nc.vector.memset(dst[0:1, 0, HF:D], 0.0)

        @block.scalar
        def _(act):
            nc.scalar.copy(dst[:, :, 0:HF], src[:, :, 0:HF])


@scoped
def transpose_shifted(nc, sp, K, src, dst):
    HF = D // 2
    turned = sp.ps("turned", [P, NB, BANK])
    turned_ready = sp.sem("turned_ready")
    with nc.Block() as block:
        @block.tensor
        def _(pe):
            for b in range(NB):
                for j in range(TPB):
                    last = nc.tensor.transpose(turned[:, b, j * P:(j + 1) * P], src[:, b * TPB + j, :], K.ident[:, :])
                last.then_inc(turned_ready, 1)

        @block.vector
        def _(dve):
            nc.vector.memset(dst[HF:D, 0:1], 0.0)
            for b in range(0, NB, 2):
                dve.wait_ge(turned_ready, b + 1)
                nc.vector.tensor_copy(dst[0:HF, b * BANK:(b + 1) * BANK], turned[0:HF, b, :])
                nc.vector.tensor_copy(dst[HF:D, b * BANK + 1:(b + 1) * BANK + 1], turned[HF:D, b, :])

        @block.scalar
        def _(act):
            for b in range(1, NB, 2):
                act.wait_ge(turned_ready, b + 1)
                nc.scalar.copy(dst[0:HF, b * BANK:(b + 1) * BANK], turned[0:HF, b, :])
                nc.scalar.copy(dst[HF:D, b * BANK + 1:(b + 1) * BANK + 1], turned[HF:D, b, :])


def l2_transformer(nc, X, K, W):
    DEPTH = 2
    with sublayer(nc) as sp:
        Y = sp.sb("y", [P, NT, D])
        layernorm(nc, K, X, Y)
        with nc.Fori(0, DEPTH) as l:
            with sublayer(nc) as inner:
                qT = inner.sb("qT", [P, 4, T])
                kT = inner.sb("kT", [P, 4, T])
                V = inner.sb("V", [P, NT, 512])
                rn = inner.sb("rnorm", [P, NT, 16])
                l2_qkv(nc, K, W, l, Y, qT, kT, V, rn)
                l2_window_attention(nc, K, W, l, Y, qT, kT, V, rn)
            l2_geglu(nc, K, W, l, Y)
        with nc.Block() as block:
            @block.vector
            def _(dve):
                nc.vector.tensor_tensor(X[:, :, :], X[:, :, :], Y[:, :, :], ALU.add)


@scoped
def l2_qkv(nc, sp, K, W, l, Y, qT, kT, V, rn):
    DH = 64
    HD2 = DH // 2
    hT = sp.sb("hT", [P, T + 1])
    w = sp.sb("wqkv", [P, 3 * 512])
    tab = sp.sb("rope_tables", [P, 2, NT, 2, DH])
    scl = sp.sb("qk_scales", [P, 2, 2, DH])
    sq = sp.sb("squares", [P, 2, 16, DH])
    ss = sp.sb("sums", [P, 3, 2, 16])
    RING = 3
    m1 = sp.sb("cos_terms", [P, RING, 2, 8, DH])
    m2 = sp.sb("sin_terms", [P, RING, 2, 8, DH])
    names = ("loaded tables_ready qkv_ready sq_ready v_copied ss_ready root_ready clamped rn_ready cos_ready sin_ready "
             "summed k_normed turned_ready q_copied k_copied").split()
    S = {n: sp.sem(n) for n in names}
    with nc.Block() as block:
        @block.sync
        def _(sync):
            sync.dma_start(w[:, :], W["L2_ffn_wqkv"][bass.ds(l, 1), :, :].rearrange("a d n -> (a d) n")).then_inc(S["loaded"], 16)
            sync.dma_start(tab[:, :, :, :, :], W["xpos"]).then_inc(S["loaded"], 16)
            for i, name in enumerate(("L2_ffn_q_scale", "L2_ffn_k_scale")):
                src = W[name][bass.ds(l, 1), :].rearrange("a d -> (a d)")
                sync.dma_start(scl[:, 0, i, :], src.partition_broadcast(P)).then_inc(S["loaded"], 16)
                sync.dma_start(scl[:, 1, i, 0:HD2], src[HD2:DH].partition_broadcast(P)).then_inc(S["loaded"], 16)
                sync.dma_start(scl[:, 1, i, HD2:DH], src[0:HD2].partition_broadcast(P)).then_inc(S["loaded"], 16)

    transpose_shifted(nc, K, Y, hT)
    psA = sp.ps("qkv", [P, 2, 3, BANK])
    psT = sp.ps("turned", [P, 2, BANK])
    with nc.Block() as block:
        @block.tensor
        def _(pe):
            pe.wait_ge(S["loaded"], 16 * 8)
            for t in range(NT + 2):
                if t < NT:
                    if t >= 2:
                        pe.wait_ge(S["sin_ready"], 2 * (t - 1))
                        pe.wait_ge(S["cos_ready"], t - 1)
                        pe.wait_ge(S["sq_ready"], t - 1)
                        pe.wait_ge(S["v_copied"], t - 1)
                    for i in range(3):
                        last = nc.tensor.matmul(psA[:, t % 2, i, :], hT[:, t * P:(t + 1) * P], w[:, i * 512:(i + 1) * 512], start=True, stop=True)
                    last.then_inc(S["qkv_ready"], 1)
                if t >= 2:
                    u = t - 2
                    pe.wait_ge(S["summed"], u + 1)
                    pe.wait_ge(S["k_normed"], u + 1)
                    if u >= 1:
                        pe.wait_ge(S["q_copied"], u)
                        pe.wait_ge(S["k_copied"], u)
                    for i in range(2):
                        for j in range(4):
                            last = nc.tensor.transpose(psT[:, i, j * P:(j + 1) * P], m1[:, u % RING, i, 2 * j:2 * j + 2, :].rearrange("p h d -> p (h d)"), K.ident[:, :])
                    last.then_inc(S["turned_ready"], 1)

        @block.scalar
        def _(act):
            for t in range(NT + 2):
                if t < NT:
                    act.wait_ge(S["qkv_ready"], t + 1)
                    if t >= 2:
                        act.wait_ge(S["ss_ready"], t - 1)
                    nc.scalar.activation(sq[:, t % 2, :, :].rearrange("p h d -> p (h d)"), psA[:, t % 2, 0:2, :].rearrange("p i n -> p (i n)"), ACT.Square).then_inc(S["sq_ready"], 1)
                    nc.scalar.copy(V[:, t, :], psA[:, t % 2, 2, :]).then_inc(S["v_copied"], 1)
                    act.wait_ge(S["ss_ready"], t + 1)
                    nc.scalar.activation(ss[:, 1, t % 2, :], ss[:, 0, t % 2, :], ACT.Sqrt).then_inc(S["root_ready"], 1)
                if t >= 2:
                    act.wait_ge(S["turned_ready"], t - 1)
                    nc.scalar.copy(qT[:, :, (t - 2) * P:(t - 1) * P], psT[:, 0, :].rearrange("p (j n) -> p j n", n=P)).then_inc(S["q_copied"], 1)

        @block.gpsimd
        def _(pool):
            for t in range(NT):
                pool.wait_ge(S["cos_ready"], t + 1)
                pool.wait_ge(S["sin_ready"], 2 * (t + 1))
                a = m1[:, t % RING, :, :, :].rearrange("p i h d -> p (i h d)")
                nc.gpsimd.tensor_tensor(a, a, m2[:, t % RING, :, :, :].rearrange("p i h d -> p (i h d)"), ALU.add).then_inc(S["summed"], 1)
                pool.wait_ge(S["summed"], t + 1)
                pool.wait_ge(S["rn_ready"], t + 1)
                k = m1[:, t % RING, 1, :, :]
                nc.gpsimd.tensor_tensor(k, k, bcast(rn[:, t, 8:16].unsqueeze(2), [P, 8, DH]), ALU.mult).then_inc(S["k_normed"], 1)

        @block.vector
        def _(dve):
            dve.wait_ge(S["loaded"], 16 * 8)
            for i in range(2):
                nc.vector.tensor_tensor(tab[:, i, :, :, :], tab[:, i, :, :, :], bcast(scl[:, i, :, :].unsqueeze(1), [P, NT, 2, DH]), ALU.mult).then_inc(S["tables_ready"], 1)
            dve.wait_ge(S["tables_ready"], 2)
            for t in range(NT + 2):
                if t < NT:
                    dve.wait_ge(S["sq_ready"], t + 1)
                    if t >= 2:
                        dve.wait_ge(S["root_ready"], t - 1)
                    nc.vector.tensor_reduce(ss[:, 0, t % 2, :], sq[:, t % 2, :, :], axis=AX_X, op=ALU.add).then_inc(S["ss_ready"], 1)
                    if t >= RING:
                        dve.wait_ge(S["turned_ready"], t - RING + 1)
                        dve.wait_ge(S["summed"], t - RING + 1)
                    dve.wait_ge(S["v_copied"], t + 1)
                    x = psA[:, t % 2, 0:2, :].rearrange("p i (h d) -> p i h d", d=DH)
                    nc.vector.tensor_tensor(m1[:, t % RING, :, :, :], x, bcast(tab[:, 0, t, :, :].unsqueeze(2), [P, 2, 8, DH]), ALU.mult).then_inc(S["cos_ready"], 1)
                    for o, i in ((0, HD2), (HD2, 0)):
                        nc.vector.tensor_tensor(m2[:, t % RING, :, :, o:o + HD2], x[:, :, :, i:i + HD2],
                                                bcast(tab[:, 1, t, :, o:o + HD2].unsqueeze(2), [P, 2, 8, HD2]), ALU.mult).then_inc(S["sin_ready"], 1)
                    dve.wait_ge(S["root_ready"], t + 1)
                    nc.vector.tensor_scalar(ss[:, 2, t % 2, :], ss[:, 1, t % 2, :], 1e-12, None, ALU.max).then_inc(S["clamped"], 1)
                    dve.wait_ge(S["clamped"], t + 1)
                    nc.vector.reciprocal(rn[:, t, :], ss[:, 2, t % 2, :]).then_inc(S["rn_ready"], 1)
                if t >= 2:
                    dve.wait_ge(S["turned_ready"], t - 1)
                    nc.vector.tensor_copy(kT[:, :, (t - 2) * P:(t - 1) * P], psT[:, 1, :].rearrange("p (j n) -> p j n", n=P)).then_inc(S["k_copied"], 1)


@scoped
def l2_window_attention(nc, sp, K, W, l, Y, qT, kT, V, rn):
    DH, H = 64, 8
    KW = P + 64
    LOW = -3.0e38
    wo = sp.sb("wo", [P, 4, D])
    mask = sp.sb("mask", [P, 2, KW])
    sm = sp.sb("masked_scores", [P, 2, H, KW])
    mx = sp.sb("max", [P, 2, H])
    nb = sp.sb("neg_max", [P, 2, H])
    den = sp.sb("den", [P, 2, H])
    rden = sp.sb("rden", [P, 2, H])
    prob = sp.sb("prob", [P, 2, H, 2 * P])
    probT = sp.sb("probT", [P, 2, 2 * H, P])
    z = sp.sb("z", [P, 2, H, DH])
    zT = sp.sb("zT", [P, 4, P])
    psS = sp.ps("scores", [P, 4, BANK])
    psT = sp.ps("turned", [P, 2, BANK])
    psZ = sp.ps("z", [P, BANK])
    psO = sp.ps("zT_and_out", [P, BANK])
    names = ("loaded mask_ready zeroed qk_done masked max_ready nb_ready exp_done trans_done dve_evac act_evac pv_done rden_ready z_ready "
             "zt_done zt_evac out_done out_added").split()
    S = {n: sp.sem(n) for n in names}
    head = [2 * (m % 4) + m // 4 for m in range(H)]
    with nc.Block() as block:
        @block.sync
        def _(sync):
            sync.dma_start(wo[:, :, :], W["L2_ffn_wo"][bass.ds(l, 1), :, :].rearrange("a (c f) n -> f (a c) n", f=P)).then_inc(S["loaded"], 16)

        @block.gpsimd
        def _(pool):
            nc.gpsimd.memset(mask[:, :, :], 0.0).then_inc(S["zeroed"], 1)
            nc.gpsimd.memset(prob[:, :, :, 0:64], 0.0).then_inc(S["zeroed"], 1)
            pool.wait_ge(S["zeroed"], 2)
            nc.gpsimd.affine_select(out=mask[:, :, :], in_=mask[:, :, :], compare_op=ALU.is_ge, fill=LOW, base=0,
                                    pattern=[[0, 2], [1, KW]], channel_multiplier=-1).then_inc(S["zeroed"], 1)
            pool.wait_ge(S["zeroed"], 3)
            nc.gpsimd.affine_select(out=mask[:, :, :], in_=mask[:, :, :], compare_op=ALU.is_ge, fill=LOW, base=64,
                                    pattern=[[0, 2], [-1, KW]], channel_multiplier=1).then_inc(S["zeroed"], 1)
            pool.wait_ge(S["zeroed"], 4)
            nc.gpsimd.affine_select(out=mask[:, 0, :], in_=mask[:, 0, :], compare_op=ALU.is_ge, fill=LOW, base=-64,
                                    pattern=[[1, KW]], channel_multiplier=0).then_inc(S["mask_ready"], 1)

        @block.tensor
        def _(pe):
            def scores(t):
                if t >= 1:
                    pe.wait_ge(S["masked"], t)
                lo = 64 if t == 0 else 0
                for m in range(H):
                    r = slice((m // 4) * DH, (m // 4) * DH + DH)
                    last = nc.tensor.matmul(psS[:, m // 2, (m % 2) * KW + lo:(m % 2 + 1) * KW], qT[r, m % 4, t * P:(t + 1) * P],
                                            kT[r, m % 4, t * P - 64 + lo:(t + 1) * P], start=True, stop=True)
                last.then_inc(S["qk_done"], 1)

            def trans(t):
                for j in range(4):
                    n = 4 * t + j
                    if n >= 2:
                        pe.wait_ge(S["dve_evac" if n % 2 == 0 else "act_evac"], (n - 2) // 2 + 1)
                    pe.wait_ge(S["exp_done"], H * t + 2 * j + 2)
                    for i in range(4):
                        last = nc.tensor.transpose(psT[:, n % 2, i * P:(i + 1) * P], prob[:, t % 2, 2 * j + i // 2, (i % 2) * P:(i % 2 + 1) * P], K.ident[:, :])
                    last.then_inc(S["trans_done"], 1)

            def pv(t):
                pe.wait_ge(S["dve_evac"], 2 * (t + 1))
                pe.wait_ge(S["act_evac"], 2 * (t + 1))
                if t >= 1:
                    pe.wait_ge(S["z_ready"], t)
                for m in range(H):
                    hs = slice(head[m] * DH, head[m] * DH + DH)
                    if t >= 1:
                        nc.tensor.matmul(psZ[:, hs], probT[:, t % 2, 2 * m, :], V[:, t - 1, hs], start=True, stop=False)
                    last = nc.tensor.matmul(psZ[:, hs], probT[:, t % 2, 2 * m + 1, :], V[:, t, hs], start=(t == 0), stop=True)
                last.then_inc(S["pv_done"], 1)

            def turn_z(t):
                pe.wait_ge(S["z_ready"], t + 1)
                if t >= 1:
                    pe.wait_ge(S["out_added"], t)
                for j in range(4):
                    last = nc.tensor.transpose(psO[:, j * P:(j + 1) * P], z[:, t % 2, 2 * j:2 * j + 2, :].rearrange("p h d -> p (h d)"), K.ident[:, :])
                last.then_inc(S["zt_done"], 1)

            def project(t):
                pe.wait_ge(S["zt_evac"], t + 1)
                for j in range(4):
                    last = nc.tensor.matmul(psO[:, 0:D], zT[:, j, :], wo[:, j, :], start=(j == 0), stop=(j == 3))
                last.then_inc(S["out_done"], 1)

            pe.wait_ge(S["loaded"], 16)
            for s in range(NT + 3):
                if s < NT:
                    scores(s)
                if 0 <= s - 3 < NT:
                    turn_z(s - 3)
                if 0 <= s - 1 < NT:
                    trans(s - 1)
                if 0 <= s - 3 < NT:
                    project(s - 3)
                if 0 <= s - 2 < NT:
                    pv(s - 2)

        @block.scalar
        def _(act):
            for s in range(NT + 3):
                if 0 <= s - 3 < NT:
                    act.wait_ge(S["zt_done"], s - 2)
                    nc.scalar.copy(zT[:, :, :].rearrange("p j n -> p (j n)"), psO[:, :]).then_inc(S["zt_evac"], 1)
                if 0 <= s - 1 < NT:
                    t = s - 1
                    for j in (1, 3):
                        if t >= 2 and j == 1:
                            act.wait_ge(S["pv_done"], t - 1)
                        act.wait_ge(S["trans_done"], 4 * t + j + 1)
                        nc.scalar.copy(probT[:, t % 2, 4 * j:4 * j + 4, :].rearrange("p a n -> p (a n)"), psT[:, j % 2, :]).then_inc(S["act_evac"], 1)
                if s < NT:
                    act.wait_ge(S["nb_ready"], s + 1)
                    if s >= 2:
                        act.wait_ge(S["trans_done"], 4 * (s - 1))
                        act.wait_ge(S["rden_ready"], s - 1)
                    if s < 2:
                        act.wait_ge(S["zeroed"], 2)
                    for m in range(H):
                        nc.scalar.activation(prob[:, s % 2, m, 64:2 * P], sm[:, s % 2, m, :], ACT.Exp, scale=rn[:, s, head[m]:head[m] + 1],
                                             bias=nb[:, s % 2, m:m + 1], accum_out=den[:, s % 2, m:m + 1]).then_inc(S["exp_done"], 1)

        @block.vector
        def _(dve):
            def mask_scores(s):
                dve.wait_ge(S["qk_done"], s + 1)
                if s >= 2:
                    dve.wait_ge(S["exp_done"], H * (s - 1))
                smv = sm[:, s % 2, :, :].rearrange("p (b a) k -> p b a k", a=2)
                lo = 64 if s == 0 else 0
                if s == 0:
                    nc.vector.tensor_copy(sm[:, 0, :, 0:64], bcast(mask[:, 0:1, 0:64], [P, H, 64]))
                nc.vector.tensor_tensor(smv[:, :, :, lo:], psS[:, :, 0:2 * KW].rearrange("p b (a k) -> p b a k", a=2)[:, :, :, lo:],
                                        bcast(mask[:, min(s, 1), lo:].unsqueeze(1).unsqueeze(1), [P, 4, 2, KW - lo]), ALU.add).then_inc(S["masked"], 1)

            def maxima(s):
                dve.wait_ge(S["masked"], s + 1)
                nc.vector.tensor_reduce(mx[:, s % 2, :], sm[:, s % 2, :, :], axis=AX_X, op=ALU.max).then_inc(S["max_ready"], 1)
                dve.wait_ge(S["max_ready"], s + 1)
                nc.vector.scalar_tensor_tensor(out=nb[:, s % 2, :].rearrange("p (o a) -> p o a", o=2), in0=mx[:, s % 2, :].rearrange("p (o a) -> p o a", o=2),
                                               scalar=-1.0, in1=rn[:, s, 0:H].rearrange("p (a o) -> p o a", o=2), op0=ALU.mult, op1=ALU.mult).then_inc(S["nb_ready"], 1)

            def evacuate(t, j):
                if t >= 2 and j == 0:
                    dve.wait_ge(S["pv_done"], t - 1)
                dve.wait_ge(S["trans_done"], 4 * t + j + 1)
                nc.vector.tensor_copy(probT[:, t % 2, 4 * j:4 * j + 4, :].rearrange("p a n -> p (a n)"), psT[:, j % 2, :]).then_inc(S["dve_evac"], 1)

            dve.wait_ge(S["mask_ready"], 1)
            for s in range(NT + 3):
                if s < NT:
                    mask_scores(s)
                if 0 <= s - 1 < NT:
                    evacuate(s - 1, 0)
                if s < NT:
                    maxima(s)
                if 0 <= s - 1 < NT:
                    evacuate(s - 1, 2)
                if 0 <= s - 3 < NT:
                    t = s - 3
                    dve.wait_ge(S["out_done"], t + 1)
                    nc.vector.tensor_tensor(Y[:, t, :], Y[:, t, :], psO[:, 0:D], ALU.add).then_inc(S["out_added"], 1)
                if 0 <= s - 2 < NT:
                    t = s - 2
                    dve.wait_ge(S["exp_done"], H * (t + 1))
                    nc.vector.reciprocal(rden[:, t % 2, :].rearrange("p (a o) -> p o a", o=2), den[:, t % 2, :].rearrange("p (o a) -> p o a", o=2)).then_inc(S["rden_ready"], 1)
                    dve.wait_ge(S["rden_ready"], t + 1)
                    dve.wait_ge(S["pv_done"], t + 1)
                    if t >= 2:
                        dve.wait_ge(S["zt_done"], t - 1)
                    nc.vector.tensor_tensor(z[:, t % 2, :, :], psZ[:, :].rearrange("p (h d) -> p h d", d=DH), bcast(rden[:, t % 2, :].unsqueeze(2), [P, H, DH]),
                                            ALU.mult).then_inc(S["z_ready"], 1)


@scoped
def l2_geglu(nc, sp, K, W, l, Y):
    HID = 341
    FC = 3
    rows = [min(P, HID - c * P) for c in range(FC)]
    h = sp.sb("shifted", [P, NT, D])
    hn = sp.sb("normed", [P, NT, D])
    hT = sp.sb("hT", [P, T])
    w1 = sp.sb("w1", [P, 2 * HID])
    w2 = sp.sb("w2", [P, FC, D])
    b1 = sp.sb("b1", [P, 2, FC])
    b2 = sp.sb("b2", [P, D])
    ln = sp.sb("ln", [P, 2])
    g = sp.sb("gelu", [P, 2, BANK])
    hid = sp.sb("hidden", [P, 2, FC, BANK])
    loaded = sp.sem("loaded")
    with nc.Block() as block:
        @block.sync
        def _(sync):
            sync.dma_start(w1[:, :], W["L2_ffn_w1"][bass.ds(l, 1), :, :].rearrange("a d n -> (a d) n")).then_inc(loaded, 16)
            for c in range(FC):
                sync.dma_start(w2[0:rows[c], c, :], W["L2_ffn_w2"][bass.ds(l, 1), c * P:c * P + rows[c], :].rearrange("a f n -> (a f) n")).then_inc(loaded, 16)
            sync.dma_start(b1[:, :, :], W["L2_ffn_b1"][bass.ds(l, 1), :, :, :].rearrange("a p g c -> (a p) g c")).then_inc(loaded, 16)
            sync.dma_start(b2[:, :], W["L2_ffn_b2"][bass.ds(l, 1), :].rearrange("a d -> (a d)").partition_broadcast(P)).then_inc(loaded, 16)
            sync.dma_start(ln[:, :], W["l2_ln"][bass.ds(l, 1), :, :].rearrange("a d g -> (a d) g")).then_inc(loaded, 16)

    shift_tokens(nc, Y, h)
    loads_done(nc, loaded, 7)
    layernorm(nc, K, h, hn, hT, ln[:, 0:1], ln[:, 1:2])
    psA = sp.ps("a", [P, 2, BANK])
    psG = sp.ps("g", [P, 2, BANK])
    psY = sp.ps("y", [P, 2, BANK])
    S = {n: sp.sem(n) for n in "ag_ready gelu_done hid_done y_ready b2_added y_added".split()}
    n_items = NB * FC
    with nc.Block() as block:
        @block.tensor
        def _(pe):
            def down(b):
                pe.wait_ge(S["hid_done"], (b + 1) * FC)
                if b >= 2:
                    pe.wait_ge(S["y_added"], b - 1)
                for j in range(TPB):
                    for c in range(FC):
                        last = nc.tensor.matmul(psY[:, b % 2, j * D:(j + 1) * D], hid[0:rows[c], b % 2, c, j * P:(j + 1) * P], w2[0:rows[c], c, :],
                                                start=(c == 0), stop=(c == FC - 1))
                last.then_inc(S["y_ready"], 1)

            for n in range(n_items):
                b, c = n // FC, n % FC
                if n >= 2:
                    pe.wait_ge(S["hid_done"], n - 1)
                for i, ps in enumerate((psA, psG)):
                    last = nc.tensor.matmul(ps[0:rows[c], n % 2, :], w1[:, i * HID + c * P:i * HID + c * P + rows[c]], hT[:, b * BANK:(b + 1) * BANK],
                                            start=True, stop=True)
                last.then_inc(S["ag_ready"], 1)
                if c == 0 and b >= 1:
                    down(b - 1)
            down(NB - 1)

        @block.scalar
        def _(act):
            for n in range(n_items):
                c = n % FC
                act.wait_ge(S["ag_ready"], n + 1)
                if n >= 2:
                    act.wait_ge(S["hid_done"], n - 1)
                nc.scalar.activation(g[0:rows[c], n % 2, :], psG[0:rows[c], n % 2, :], ACT.Gelu, bias=b1[0:rows[c], 1, c:c + 1]).then_inc(S["gelu_done"], 1)

        @block.vector
        def _(dve):
            def add(b):
                yb = Y[:, b * TPB:(b + 1) * TPB, :]
                nc.vector.tensor_tensor(yb, yb, bcast(b2[:, :].unsqueeze(1), [P, TPB, D]), ALU.add).then_inc(S["b2_added"], 1)
                dve.wait_ge(S["b2_added"], b + 1)
                dve.wait_ge(S["y_ready"], b + 1)
                nc.vector.tensor_tensor(yb, yb, psY[:, b % 2, :].rearrange("p (t n) -> p t n", n=D), ALU.add).then_inc(S["y_added"], 1)

            for n in range(n_items):
                b, c = n // FC, n % FC
                dve.wait_ge(S["gelu_done"], n + 1)
                if c == 0 and b >= 2:
                    dve.wait_ge(S["y_ready"], b - 1)
                nc.vector.scalar_tensor_tensor(out=hid[0:rows[c], b % 2, c, :], in0=psA[0:rows[c], n % 2, :], scalar=b1[0:rows[c], 0, c:c + 1],
                                               in1=g[0:rows[c], n % 2, :], op0=ALU.add, op1=ALU.mult).then_inc(S["hid_done"], 1)
                if c == 0 and b >= 1:
                    add(b - 1)
            add(NB - 1)


def l3_mixer(nc, X, K, W):
    DI, NS, NH, HD = 256, 64, 8, 32
    with sublayer(nc) as sp:
        xn = sp.sb("xn", [P, NT, D])
        Yo = sp.sb("mixed", [P, NT, DI])
        with sublayer(nc) as inner:
            xT = inner.sb("xT", [P, T])
            w_in = inner.sb("w_in", [P, 648])
            layernorm(nc, K, X, xn, xT)
            gate = inner.sb("silu_z", [P, NT, DI])
            dt = inner.sb("dt", [P, NT, NH])
            a = inner.sb("log_decay", [P, NT, NH])
            xs = inner.sb("x_tokens", [P, NT, DI])
            Bt = inner.sb("B_tokens", [P, NT, NS])
            BC = inner.sb("BC", [P, T])
            CT = inner.sb("CT", [NS, T])
            l3_gate_dt(nc, K, W, xT, w_in, gate, dt, a, NH)
            with sublayer(nc) as conv:
                xc = [conv.sb(f"x_conv{i}", [P, T]) for i in range(2)] + [BC]
                l3_conv(nc, K, W, xT, w_in, xc)
                l3_turn(nc, K, xc, xs, Bt, CT)
            l3_scan(nc, K, W, dt, a, xs, Bt, BC, CT, Yo, NS, NH, HD)
            with nc.Block() as block:
                @block.vector
                def _(dve):
                    nc.vector.tensor_tensor(Yo[:, 0:NT // 2, :], Yo[:, 0:NT // 2, :], gate[:, 0:NT // 2, :], ALU.mult)

                @block.gpsimd
                def _(pool):
                    nc.gpsimd.tensor_tensor(Yo[:, NT // 2:, :], Yo[:, NT // 2:, :], gate[:, NT // 2:, :], ALU.mult)
        Z = sp.sb("squashed", [P, NT, D])
        l3_out(nc, K, W, Yo, Z)
        rows = sp.sb("b_nl", [P, D])
        loaded = sp.sem("b_loaded")
        added = sp.sem("x_added")
        with nc.Block() as block:
            @block.sync
            def _(sync):
                sync.dma_start(rows[:, :], W["L3_attn_b_nl"].partition_broadcast(P)).then_inc(loaded, 16)

            @block.vector
            def _(dve):
                nc.vector.tensor_tensor(X[:, :, :], X[:, :, :], xn[:, :, :], ALU.add).then_inc(added, 1)
                dve.wait_ge(added, 1)
                dve.wait_ge(loaded, 16)
                nc.vector.tensor_tensor(X[:, :, :], X[:, :, :], bcast(rows[:, :].unsqueeze(1), [P, NT, D]), ALU.add)
        project_add(nc, K, Z, W["L3_attn_W_nl"], X)


@scoped
def l3_gate_dt(nc, sp, K, W, xT, w_in, gate, dt, a, NH):
    SERIES = [1.0 / (2 * i + 1) for i in range(8)]
    rows = sp.sb("bias_and_alog", [P, 2, NH])
    nexpA = sp.sb("exp_A_log", [P, NH])
    N = NT * NH
    d = {n: sp.sb(n, [P, N]) for n in "raw absd u den rden z z2 acc lin pos".split()}
    sig = sp.sb("sigmoid", [P, 2, 2, 256])
    psZ = sp.ps("z", [P, 2, BANK])
    psD = sp.ps("dt", [P, BANK])
    S = {n: sp.sem(n) for n in "loaded z_ready sig_done gate_done d_ready raw_ready abs_done u_done expA_done step".split()}
    with nc.Block() as block:
        @block.sync
        def _(sync):
            sync.dma_start(w_in[:, :], W["L3_attn_W_in"]).then_inc(S["loaded"], 16)
            sync.dma_start(rows[:, 0, :], W["L3_attn_dt_bias"].partition_broadcast(P)).then_inc(S["loaded"], 16)
            sync.dma_start(rows[:, 1, :], W["L3_attn_A_log"].partition_broadcast(P)).then_inc(S["loaded"], 16)

        @block.tensor
        def _(pe):
            pe.wait_ge(S["loaded"], 48)
            for t in range(NT):
                last = nc.tensor.matmul(psD[:, t * NH:(t + 1) * NH], xT[:, t * P:(t + 1) * P], w_in[:, 640:648], start=True, stop=True)
            last.then_inc(S["d_ready"], 1)
            for n in range(NT // 2):
                if n >= 2:
                    pe.wait_ge(S["gate_done"], n - 1)
                for j in range(2):
                    t = 2 * n + j
                    last = nc.tensor.matmul(psZ[:, n % 2, j * 256:(j + 1) * 256], xT[:, t * P:(t + 1) * P], w_in[:, 0:256], start=True, stop=True)
                last.then_inc(S["z_ready"], 1)

        @block.scalar
        def _(act):
            act.wait_ge(S["loaded"], 48)
            nc.scalar.activation(nexpA[:, :], rows[:, 1, :], ACT.Exp).then_inc(S["expA_done"], 1)
            act.wait_ge(S["raw_ready"], 1)
            nc.scalar.activation(d["absd"][:, :], d["raw"][:, :], ACT.Abs).then_inc(S["abs_done"], 1)
            act.wait_ge(S["abs_done"], 1)
            nc.scalar.activation(d["u"][:, :], d["absd"][:, :], ACT.Exp, scale=-1.0).then_inc(S["u_done"], 1)
            for n in range(NT // 2):
                act.wait_ge(S["z_ready"], n + 1)
                if n >= 2:
                    act.wait_ge(S["gate_done"], n - 1)
                nc.scalar.activation(sig[:, n % 2, :, :].rearrange("p t n -> p (t n)"), psZ[:, n % 2, :], ACT.Sigmoid).then_inc(S["sig_done"], 1)

        @block.vector
        def _(dve):
            steps = [0]

            def done(ins):
                steps[0] += 1
                ins.then_inc(S["step"], 1)
                dve.wait_ge(S["step"], steps[0])

            V = nc.vector
            dve.wait_ge(S["d_ready"], 1)
            dve.wait_ge(S["loaded"], 48)
            V.tensor_tensor(d["raw"][:, :].rearrange("p (t h) -> p t h", h=NH), psD[:, 0:N].rearrange("p (t h) -> p t h", h=NH),
                            bcast(rows[:, 0:1, :], [P, NT, NH]), ALU.add).then_inc(S["raw_ready"], 1)
            dve.wait_ge(S["u_done"], 1)
            done(V.tensor_scalar(d["den"][:, :], d["u"][:, :], 2.0, None, ALU.add))
            done(V.reciprocal(d["rden"][:, :], d["den"][:, :]))
            done(V.tensor_tensor(d["z"][:, :], d["u"][:, :], d["rden"][:, :], ALU.mult))
            done(V.tensor_tensor(d["z2"][:, :], d["z"][:, :], d["z"][:, :], ALU.mult))
            done(V.tensor_scalar(d["acc"][:, :], d["z2"][:, :], SERIES[7], SERIES[6], ALU.mult, ALU.add))
            for c in SERIES[5::-1]:
                done(V.tensor_tensor(d["lin"][:, :], d["acc"][:, :], d["z2"][:, :], ALU.mult))
                done(V.tensor_scalar(d["acc"][:, :], d["lin"][:, :], c, None, ALU.add))
            done(V.scalar_tensor_tensor(out=d["lin"][:, :], in0=d["acc"][:, :], scalar=2.0, in1=d["z"][:, :], op0=ALU.mult, op1=ALU.mult))
            done(V.tensor_scalar(d["pos"][:, :], d["raw"][:, :], 0.0, None, ALU.max))
            flat = dt[:, :, :].rearrange("p t h -> p (t h)")
            done(V.tensor_tensor(flat, d["pos"][:, :], d["lin"][:, :], ALU.add))
            dve.wait_ge(S["expA_done"], 1)
            V.scalar_tensor_tensor(out=a[:, :, :], in0=dt[:, :, :], scalar=-1.0, in1=bcast(nexpA[:, :].unsqueeze(1), [P, NT, NH]), op0=ALU.mult, op1=ALU.mult)
            for n in range(NT // 2):
                dve.wait_ge(S["sig_done"], n + 1)
                V.tensor_tensor(gate[:, 2 * n:2 * n + 2, :].rearrange("p t n -> p (t n)"), sig[:, n % 2, :, :].rearrange("p t n -> p (t n)"), psZ[:, n % 2, :],
                                ALU.mult).then_inc(S["gate_done"], 1)


@scoped
def l3_conv(nc, sp, K, W, xT, w_in, xc):
    TAPS = 16
    PAD = TAPS - 1
    cw = sp.sb("conv_w", [P, 3, TAPS])
    cb = sp.sb("conv_b", [P, 3])
    diag = sp.sb("tap_diagonals", [P, 2, TAPS, P])
    xp = [sp.sb(f"padded{c}", [P, PAD + T]) for c in range(3)]
    PE1 = 1
    CUT = PE1 * BANK
    acc = sp.sb("acc", [P, 2, T])
    acc1 = sp.sb("acc_chunk1", [P, 2, T - CUT])
    sig1 = acc1[:, TAPS % 2, :]
    pe_items = [(0, b) for b in range(NB)] + [(1, b) for b in range(PE1)]
    sig = sp.sb("sigmoid", [P, 2, BANK])
    sig2 = acc[:, TAPS % 2, :]
    psP = sp.ps("proj", [P, 4, BANK])
    psC = sp.ps("conv", [P, 4, BANK])
    S = {n: sp.sem(n) for n in "loaded padded proj_ready act_copied dve_copied diag_ready conv_ready sig_done silu_done tap bc_sig c1_sig".split()}
    order = [2, 0, 1]
    with nc.Block() as block:
        @block.sync
        def _(sync):
            sync.dma_start(cw[:, :, :], W["L3_attn_conv_w"].rearrange("(c p) k -> p c k", p=P)).then_inc(S["loaded"], 16)
            sync.dma_start(cb[:, :], W["L3_attn_conv_b"]).then_inc(S["loaded"], 16)

        @block.tensor
        def _(pe):
            for n in range(3 * NB):
                c, b = order[n // NB], n % NB
                if n >= 4:
                    pe.wait_ge(S["act_copied"], n - 3)
                nc.tensor.matmul(psP[:, n % 4, :], w_in[:, 256 + c * P:256 + (c + 1) * P], xT[:, b * BANK:(b + 1) * BANK], start=True, stop=True).then_inc(S["proj_ready"], 1)
            for n, (c, b) in enumerate(pe_items):
                pe.wait_ge(S["act_copied"], NB + n + 1)
                pe.wait_ge(S["diag_ready"], TAPS * (c + 1))
                if n >= 4:
                    pe.wait_ge(S["silu_done"], n - 3)
                for k in range(TAPS):
                    last = nc.tensor.matmul(psC[:, n % 4, :], diag[:, c, k, :], xp[c][:, k + b * BANK:k + (b + 1) * BANK], start=(k == 0), stop=(k == TAPS - 1))
                last.then_inc(S["conv_ready"], 1)

        @block.gpsimd
        def _(pool):
            for c in range(3):
                last = nc.gpsimd.memset(xp[c][:, 0:PAD], 0.0)
            last.then_inc(S["padded"], 1)
            pool.wait_ge(S["loaded"], 32)
            for c in range(2):
                for k in range(TAPS):
                    nc.gpsimd.tensor_scalar(diag[:, c, k, :], K.ident[:, :], cw[:, c, k:k + 1], 1.0, ALU.mult, ALU.mult).then_inc(S["diag_ready"], 1)

        @block.scalar
        def _(act):
            act.wait_ge(S["padded"], 1)
            for n in range(3 * NB):
                c, b = order[n // NB], n % NB
                act.wait_ge(S["proj_ready"], n + 1)
                nc.scalar.copy(xp[c][:, PAD + b * BANK:PAD + (b + 1) * BANK], psP[:, n % 4, :]).then_inc(S["act_copied"], 1)
            act.wait_ge(S["loaded"], 32)
            for n, (c, b) in enumerate(pe_items):
                if n == 2:
                    act.wait_ge(S["tap"], TAPS)
                    nc.scalar.activation(sig2, acc[:, (TAPS - 1) % 2, :], ACT.Sigmoid, bias=cb[:, 2:3]).then_inc(S["bc_sig"], 1)
                act.wait_ge(S["conv_ready"], n + 1)
                if n >= 2:
                    act.wait_ge(S["silu_done"], n - 1)
                nc.scalar.activation(sig[:, n % 2, :], psC[:, n % 4, :], ACT.Sigmoid, bias=cb[:, c:c + 1]).then_inc(S["sig_done"], 1)
            act.wait_ge(S["tap"], 2 * TAPS)
            nc.scalar.activation(sig1, acc1[:, (TAPS - 1) % 2, :], ACT.Sigmoid, bias=cb[:, 1:2]).then_inc(S["c1_sig"], 1)

        @block.vector
        def _(dve):
            def taps(c, a, start, before):
                for k in range(TAPS):
                    src = xp[c][:, start + k:k + T]
                    if k == 0:
                        nc.vector.tensor_scalar(a[:, 0, :], src, cw[:, c, 0:1], None, ALU.mult).then_inc(S["tap"], 1)
                    else:
                        dve.wait_ge(S["tap"], before + k)
                        nc.vector.scalar_tensor_tensor(out=a[:, k % 2, :], in0=src, scalar=cw[:, c, k:k + 1], in1=a[:, (k - 1) % 2, :],
                                                       op0=ALU.mult, op1=ALU.add).then_inc(S["tap"], 1)

            def silu(n):
                c, b = pe_items[n]
                dve.wait_ge(S["sig_done"], n + 1)
                nc.vector.scalar_tensor_tensor(out=xc[c][:, b * BANK:(b + 1) * BANK], in0=psC[:, n % 4, :], scalar=cb[:, c:c + 1], in1=sig[:, n % 2, :],
                                               op0=ALU.add, op1=ALU.mult).then_inc(S["silu_done"], 1)

            dve.wait_ge(S["loaded"], 32)
            dve.wait_ge(S["act_copied"], NB)
            taps(2, acc, 0, 0)
            silu(0)
            silu(1)
            dve.wait_ge(S["bc_sig"], 1)
            nc.vector.scalar_tensor_tensor(out=xc[2][:, :], in0=acc[:, (TAPS - 1) % 2, :], scalar=cb[:, 2:3], in1=sig2, op0=ALU.add, op1=ALU.mult)
            dve.wait_ge(S["act_copied"], 3 * NB)
            taps(1, acc1, CUT, TAPS)
            for n in range(2, len(pe_items)):
                silu(n)
            dve.wait_ge(S["c1_sig"], 1)
            nc.vector.scalar_tensor_tensor(out=xc[1][:, CUT:], in0=acc1[:, (TAPS - 1) % 2, :], scalar=cb[:, 1:2], in1=sig1, op0=ALU.add, op1=ALU.mult)


@scoped
def l3_turn(nc, sp, K, xc, xs, Bt, CT):
    NS = 64
    ps = sp.ps("turned", [P, 2, BANK])
    S = {n: sp.sem(n) for n in "c_moved turned copied".split()}
    with nc.Block() as block:
        @block.sync
        def _(sync):
            sync.dma_start(CT[:, :], xc[2][NS:P, :]).then_inc(S["c_moved"], 16)
            sync.wait_ge(S["c_moved"], 16)

        @block.tensor
        def _(pe):
            for t in range(NT):
                if t >= 2:
                    pe.wait_ge(S["copied"], 2 * (t - 1))
                for c in range(3):
                    last = nc.tensor.transpose(ps[:, t % 2, c * P:(c + 1) * P], xc[c][:, t * P:(t + 1) * P], K.ident[:, :])
                last.then_inc(S["turned"], 1)

        @block.vector
        def _(dve):
            for t in range(NT):
                dve.wait_ge(S["turned"], t + 1)
                nc.vector.tensor_copy(xs[:, t, :], ps[:, t % 2, 0:256]).then_inc(S["copied"], 1)
                nc.vector.tensor_copy(Bt[:, t, :], ps[:, t % 2, 256:256 + NS]).then_inc(S["copied"], 1)


@scoped
def l3_scan(nc, sp, K, W, dt, a, xs, Bt, BC, CT, Y, NS, NH, HD):
    DI = NH * HD
    after = sp.sb("after", [P, P])
    drow = sp.sb("D", [P, NH])
    state = sp.sb("state", [NS, 2, DI])
    decayed = sp.sb("state_decayed", [NS, DI])
    aU = sp.sb("a_upto", [P, 2, NH, P])
    E = sp.sb("decays", [P, 2, NH, P])
    MT = sp.sb("mixing", [P, 2, NH, P])
    Gm = sp.sb("CB_masked", [P, 2, P])
    ecum = sp.sb("decay_from_start", [P, 2, NH])
    edec = sp.sb("chunk_decay", [NS, 2, NH])
    xdt = sp.sb("x_dt", [P, 2, DI])
    xw = sp.sb("x_dt_to_end", [P, 2, DI])
    off = sp.sb("from_state", [P, 2, DI])
    psE = sp.ps("sums_between", [P, 2, 2, BANK])
    psG = sp.ps("CB_and_sums", [P, BANK])
    psD = sp.ps("within", [P, BANK])
    psO = sp.ps("from_state", [P, BANK])
    psS = sp.ps("state", [P, BANK])
    names = ("loaded after_ready aU_ready xdt_ready skip_ready seg_ready g_ready e_done small_exp gm_ready mt_ready xw_ready within_ready off_ready "
             "state_ready off_scaled off_added within_added decayed updated").split()
    S = {n: sp.sem(n) for n in names}
    heads = "p (h d) -> p h d"
    with nc.Block() as block:
        @block.sync
        def _(sync):
            sync.dma_start(drow[:, :], W["L3_attn_D"].partition_broadcast(P)).then_inc(S["loaded"], 16)
            sync.dma_start(state[:, 0, :], W["L3_attn_init_states"]).then_inc(S["loaded"], 16)

        @block.gpsimd
        def _(pool):
            nc.gpsimd.affine_select(out=after[:, :], in_=K.ones[:, :], compare_op=ALU.is_gt, fill=0.0, base=0, pattern=[[-1, P]],
                                    channel_multiplier=1).then_inc(S["after_ready"], 1)
            pool.wait_ge(S["loaded"], 32)
            for q in range(NT):
                if q >= 2:
                    pool.wait_ge(S["seg_ready"], q - 1)
                nc.gpsimd.tensor_tensor(aU[:, q % 2, :, :], bcast(K.causal_k[:, :].unsqueeze(1), [P, NH, P]), bcast(a[:, q, :].unsqueeze(2), [P, NH, P]),
                                        ALU.mult).then_inc(S["aU_ready"], 1)
                if q >= 2:
                    pool.wait_ge(S["within_ready"], q - 1)
                    pool.wait_ge(S["xw_ready"], q - 1)
                nc.gpsimd.tensor_tensor(xdt[:, q % 2, :].rearrange(heads, h=NH), xs[:, q, :].rearrange(heads, h=NH), bcast(dt[:, q, :].unsqueeze(2), [P, NH, HD]),
                                        ALU.mult).then_inc(S["xdt_ready"], 1)
                nc.gpsimd.tensor_tensor(Y[:, q, :].rearrange(heads, h=NH), xs[:, q, :].rearrange(heads, h=NH), bcast(drow[:, :].unsqueeze(2), [P, NH, HD]),
                                        ALU.mult).then_inc(S["skip_ready"], 1)

        @block.tensor
        def _(pe):
            pe.wait_ge(S["after_ready"], 1)
            pe.wait_ge(S["loaded"], 32)

            def sums(q):
                pe.wait_ge(S["aU_ready"], q + 1)
                if q >= 2:
                    pe.wait_ge(S["e_done"], q - 1)
                for i in range(2):
                    last = nc.tensor.matmul(psE[:, q % 2, i, :], after[:, :], aU[:, q % 2, 4 * i:4 * i + 4, :].rearrange("p h t -> p (h t)"), start=True, stop=True)
                last.then_inc(S["seg_ready"], 1)
                if q >= 1:
                    pe.wait_ge(S["gm_ready"], q)
                    pe.wait_ge(S["small_exp"], 2 * q)
                cols = slice(q * P, (q + 1) * P)
                nc.tensor.matmul(psG[:, 0:P], BC[0:NS, cols], CT[:, cols], start=True, stop=True)
                nc.tensor.matmul(psG[:, P:P + NH], K.causal_k[:, :], a[:, q, :], start=True, stop=True)
                nc.tensor.matmul(psG[0:NS, P + 16:P + 16 + NH], K.ones[:, 0:NS], a[:, q, :], start=True, stop=True).then_inc(S["g_ready"], 1)

            def outputs(q):
                cols = slice(q * P, (q + 1) * P)
                if q >= 1:
                    pe.wait_ge(S["updated"], q)
                    pe.wait_ge(S["off_scaled"], q)
                nc.tensor.matmul(psO[:, 0:DI], CT[:, cols], state[:, q % 2, :], start=True, stop=True).then_inc(S["off_ready"], 1)
                pe.wait_ge(S["xw_ready"], q + 1)
                nc.tensor.matmul(psS[0:NS, 0:DI], Bt[:, q, :], xw[:, q % 2, :], start=True, stop=True).then_inc(S["state_ready"], 1)
                pe.wait_ge(S["mt_ready"], q + 1)
                if q >= 1:
                    pe.wait_ge(S["within_added"], q)
                for h in range(NH):
                    last = nc.tensor.matmul(psD[:, h * HD:(h + 1) * HD], MT[:, q % 2, h, :], xdt[:, q % 2, h * HD:(h + 1) * HD], start=True, stop=True)
                last.then_inc(S["within_ready"], 1)

            for s in range(NT + 1):
                if s < NT:
                    sums(s)
                if s >= 1:
                    outputs(s - 1)

        @block.scalar
        def _(act):
            for q in range(NT):
                act.wait_ge(S["seg_ready"], q + 1)
                if q >= 2:
                    act.wait_ge(S["mt_ready"], q - 1)
                    act.wait_ge(S["xw_ready"], q - 1)
                nc.scalar.activation(E[:, q % 2, :, :].rearrange("p h t -> p (h t)"), psE[:, q % 2, :, :].rearrange("p i n -> p (i n)"), ACT.Exp).then_inc(S["e_done"], 1)
                act.wait_ge(S["g_ready"], q + 1)
                act.wait_ge(S["gm_ready"], q + 1)
                if q >= 2:
                    act.wait_ge(S["off_scaled"], q - 1)
                    act.wait_ge(S["decayed"], q - 1)
                nc.scalar.activation(ecum[:, q % 2, :], psG[:, P:P + NH], ACT.Exp).then_inc(S["small_exp"], 1)
                nc.scalar.activation(edec[:, q % 2, :], psG[0:NS, P + 16:P + 16 + NH], ACT.Exp).then_inc(S["small_exp"], 1)

        @block.vector
        def _(dve):
            for q in range(NT):
                dve.wait_ge(S["g_ready"], q + 1)
                nc.vector.tensor_tensor(Gm[:, q % 2, :], psG[:, 0:P], K.causal_k[:, :], ALU.mult).then_inc(S["gm_ready"], 1)
                dve.wait_ge(S["e_done"], q + 1)
                dve.wait_ge(S["xdt_ready"], q + 1)
                nc.vector.tensor_tensor(xw[:, q % 2, :].rearrange(heads, h=NH), xdt[:, q % 2, :].rearrange(heads, h=NH),
                                        bcast(E[:, q % 2, :, P - 1:P], [P, NH, HD]), ALU.mult).then_inc(S["xw_ready"], 1)
                dve.wait_ge(S["gm_ready"], q + 1)
                if q >= 2:
                    dve.wait_ge(S["within_ready"], q - 1)
                nc.vector.tensor_tensor(MT[:, q % 2, :, :], E[:, q % 2, :, :], bcast(Gm[:, q % 2, :].unsqueeze(1), [P, NH, P]), ALU.mult).then_inc(S["mt_ready"], 1)
                dve.wait_ge(S["small_exp"], 2 * (q + 1))
                nc.vector.tensor_tensor(decayed[:, :].rearrange(heads, h=NH), state[:, q % 2, :].rearrange(heads, h=NH),
                                        bcast(edec[:, q % 2, :].unsqueeze(2), [NS, NH, HD]), ALU.mult).then_inc(S["decayed"], 1)
                dve.wait_ge(S["decayed"], q + 1)
                dve.wait_ge(S["state_ready"], q + 1)
                nc.vector.tensor_tensor(state[:, (q + 1) % 2, :], decayed[:, :], psS[0:NS, 0:DI], ALU.add).then_inc(S["updated"], 1)
                dve.wait_ge(S["off_ready"], q + 1)
                nc.vector.tensor_tensor(off[:, q % 2, :].rearrange(heads, h=NH), psO[:, 0:DI].rearrange(heads, h=NH),
                                        bcast(ecum[:, q % 2, :].unsqueeze(2), [P, NH, HD]), ALU.mult).then_inc(S["off_scaled"], 1)
                dve.wait_ge(S["off_scaled"], q + 1)
                dve.wait_ge(S["skip_ready"], q + 1)
                nc.vector.tensor_tensor(Y[:, q, :], Y[:, q, :], off[:, q % 2, :], ALU.add).then_inc(S["off_added"], 1)
                dve.wait_ge(S["off_added"], q + 1)
                dve.wait_ge(S["within_ready"], q + 1)
                nc.vector.tensor_tensor(Y[:, q, :], Y[:, q, :], psD[:, 0:DI], ALU.add).then_inc(S["within_added"], 1)


@scoped
def l3_out(nc, sp, K, W, Y, Z):
    DI = 256
    wo = sp.sb("w_out", [P, 2, D])
    nw = sp.sb("norm_w", [P, 2])
    sq = sp.sb("squares", [P, 2, DI])
    ms = sp.sb("mean_square", [P, 3, NT])
    yT = sp.sb("yT", [P, 2, 2, P])
    y = sp.sb("y", [P, NT, D])
    q = sp.sb("y_squares", [P, NT * D])
    root = sp.sb("root", [P, NT * D])
    psT = sp.ps("turned", [P, 2, BANK])
    psY = sp.ps("y", [P, 2, BANK])

    def block_of(b):
        return slice(b * BANK, (b + 1) * BANK)

    S = {n: sp.sem(n) for n in "loaded ms_ready root_ready r_ready turned copied y_ready y_scaled sq_done sqrt_done recip_done".split()}
    with nc.Block() as block:
        @block.sync
        def _(sync):
            sync.dma_start(wo[:, :, :], W["L3_attn_W_out"].rearrange("(c f) n -> f c n", f=P)).then_inc(S["loaded"], 16)
            sync.dma_start(nw[:, :], W["L3_attn_norm_w"]).then_inc(S["loaded"], 16)

        @block.tensor
        def _(pe):
            pe.wait_ge(S["loaded"], 32)

            def out(t):
                pe.wait_ge(S["copied"], 2 * (t + 1))
                if t >= 2:
                    pe.wait_ge(S["y_scaled"], t - 1)
                for c in range(2):
                    last = nc.tensor.matmul(psY[:, t % 2, 0:D], yT[:, t % 2, c, :], wo[:, c, :], start=(c == 0), stop=(c == 1))
                last.then_inc(S["y_ready"], 1)

            for t in range(NT):
                if t >= 2:
                    pe.wait_ge(S["copied"], 2 * (t - 1))
                for c in range(2):
                    last = nc.tensor.transpose(psT[:, t % 2, c * P:(c + 1) * P], Y[:, t, c * P:(c + 1) * P], K.ident[:, :])
                last.then_inc(S["turned"], 1)
                if t >= 1:
                    out(t - 1)
            out(NT - 1)

        @block.scalar
        def _(act):
            for t in range(NT):
                if t >= 2:
                    act.wait_ge(S["ms_ready"], t - 1)
                nc.scalar.activation(sq[:, t % 2, :], Y[:, t, :], ACT.Square, accum_out=ms[:, 0, t:t + 1]).then_inc(S["ms_ready"], 1)
            act.wait_ge(S["ms_ready"], NT)
            nc.scalar.activation(ms[:, 1, :], ms[:, 0, :], ACT.Sqrt, scale=1.0 / DI, bias=K.eps[:, 0:1]).then_inc(S["root_ready"], 1)
            act.wait_ge(S["r_ready"], 1)
            for t in range(NT):
                act.wait_ge(S["y_ready"], t + 1)
                nc.scalar.activation(y[:, t, :], psY[:, t % 2, 0:D], ACT.Copy, scale=ms[:, 2, t:t + 1]).then_inc(S["y_scaled"], 1)
                if t % TPB == TPB - 1:
                    b = t // TPB
                    act.wait_ge(S["y_scaled"], t + 1)
                    nc.scalar.activation(q[:, block_of(b)], y[:, b * TPB:(b + 1) * TPB, :].rearrange("p t n -> p (t n)"), ACT.Square).then_inc(S["sq_done"], 1)
                    act.wait_ge(S["sq_done"], b + 1)
                    nc.scalar.activation(root[:, block_of(b)], q[:, block_of(b)], ACT.Sqrt, bias=K.ones[:, 0:1]).then_inc(S["sqrt_done"], 1)

        @block.vector
        def _(dve):
            def squash(b):
                dve.wait_ge(S["sqrt_done"], b + 1)
                nc.vector.reciprocal(q[:, block_of(b)], root[:, block_of(b)]).then_inc(S["recip_done"], 1)
                dve.wait_ge(S["recip_done"], b + 1)
                tiles = slice(b * TPB, (b + 1) * TPB)
                nc.vector.tensor_tensor(Z[:, tiles, :].rearrange("p t n -> p (t n)"), y[:, tiles, :].rearrange("p t n -> p (t n)"), q[:, block_of(b)], ALU.mult)

            dve.wait_ge(S["root_ready"], 1)
            nc.vector.reciprocal(ms[:, 2, :], ms[:, 1, :]).then_inc(S["r_ready"], 1)
            dve.wait_ge(S["loaded"], 32)
            for t in range(NT):
                dve.wait_ge(S["turned"], t + 1)
                if t >= 2:
                    dve.wait_ge(S["y_ready"], t - 1)
                for c in range(2):
                    nc.vector.tensor_scalar(yT[:, t % 2, c, :], psT[:, t % 2, c * P:(c + 1) * P], nw[:, c:c + 1], None, ALU.mult).then_inc(S["copied"], 1)
                if t % TPB == 2 and t > TPB:
                    squash(t // TPB - 1)
            squash(NB - 1)


def by_tile(a):
    return a.reshape(NT, P, -1).transpose(1, 0, 2)


def shape_constants():
    f = np.float32
    pos = np.arange(T, dtype=f)
    inv = f(1.0) / f(10000.0) ** (np.arange(4, dtype=f) / f(4))
    ang = pos[:, None] * inv[None, :]
    rope8 = np.stack([by_tile(np.cos(ang)), by_tile(np.sin(ang))], axis=1)
    rsqrt_t = by_tile(f(1) / np.sqrt(np.arange(1, T + 1, dtype=f)))[:, :, 0]
    half = np.arange(0, 64, 2, dtype=f)
    fr = pos[:, None] * (f(1.0) / f(10000.0) ** (half / f(64)))[None, :]
    base = (half + f(0.4 * 64)) / f(1.4 * 64)
    scale = base[None, :] ** ((pos - f(T // 2)) / f(32))[:, None]
    fr, scale = np.concatenate([fr, fr], 1), np.concatenate([scale, scale], 1)
    sign = np.concatenate([-np.ones(32, f), np.ones(32, f)])
    tabs = [np.stack([by_tile(x * scale * f(8)), by_tile(x / scale)], axis=2) for x in (np.cos(fr), np.sin(fr) * sign)]
    xpos = np.ascontiguousarray(np.stack(tabs, axis=1), dtype=f)
    behind = by_tile(f(T - 1) - pos)[:, :, 0]
    return {"keys_behind": np.ascontiguousarray(behind), "xpos": xpos, "rope8": np.ascontiguousarray(rope8, dtype=f), "rsqrt_t": np.ascontiguousarray(rsqrt_t)}


LAYOUT = {
    "L0_attn_b_Q": lambda a: a.reshape(8, P).T,
    "L0_attn_b_K": lambda a: a.reshape(8, P).T,
    "L0_ffn_keys": lambda a: a.transpose(2, 0, 3, 1).reshape(16, 128, 32),
    "L0_ffn_bn_gamma": lambda a: a.reshape(16, P).T,
    "L0_ffn_bn_beta": lambda a: a.reshape(16, P).T,
    "L0_ffn_down_embed": lambda a: a.T,
    "L2_attn_gate": lambda a: np.repeat(a, 64, axis=0).reshape(8, P, 2).transpose(1, 2, 0),
    "L2_attn_freqs": lambda a: a.reshape(8, P).T,
    "L3_attn_conv_b": lambda a: a.reshape(3, P).T,
    "L3_attn_norm_w": lambda a: a.reshape(2, P).T,
    "L3_attn_init_states": lambda a: a.reshape(256, 64).T,
    "L2_ffn_b1": lambda a: np.concatenate([a.reshape(2, 2, 341), np.zeros((2, 2, 43), a.dtype)], axis=2).reshape(2, 2, 3, P).transpose(0, 3, 1, 2),
    "L3_ffn_b1": lambda a: a.reshape(8, 4, P).transpose(2, 1, 0),
    "L3_ffn_b2": lambda a: np.concatenate([a, np.zeros((D - 8, D), a.dtype)]),
}

SUBLAYERS = [l0_attention, l0_experts, l1_attention, l1_experts, l2_attention, l2_transformer, l3_mixer, l3_experts]


class Constants:
    pass


def sem_range(S):
    nums = sorted(s.num for s in S.values())
    assert nums[-1] - nums[0] == len(nums) - 1
    return range(nums[0], nums[-1] + 1)


def build_constants(nc, ctx):
    K = Constants()
    K.ident = ctx.enter_context(nc.sbuf_tensor("ident", [P, P], F32))
    K.ones = ctx.enter_context(nc.sbuf_tensor("ones", [P, P], F32))
    K.causal_q = ctx.enter_context(nc.sbuf_tensor("causal_q", [P, P], F32))
    K.causal_k = ctx.enter_context(nc.sbuf_tensor("causal_k", [P, P], F32))
    K.eps = ctx.enter_context(nc.sbuf_tensor("eps", [P, 1], F32))
    filled = nc.alloc_semaphore("constants_filled")
    with nc.Block() as block:
        @block.gpsimd
        def _(pool):
            nc.gpsimd.memset(K.ident[:, :], 0.0).then_inc(filled, 1)
            nc.gpsimd.memset(K.ones[:, :], 1.0).then_inc(filled, 1)
            nc.gpsimd.memset(K.eps[:, :], LN_EPS).then_inc(filled, 1)
            pool.wait_ge(filled, 3)
            nc.gpsimd.affine_select(out=K.ident[:, :], in_=K.ident[:, :], compare_op=ALU.not_equal, fill=1.0, base=0,
                                    pattern=[[-1, P]], channel_multiplier=1)
            nc.gpsimd.affine_select(out=K.causal_q[:, :], in_=K.ones[:, :], compare_op=ALU.is_ge, fill=0.0, base=0,
                                    pattern=[[-1, P]], channel_multiplier=1)
            nc.gpsimd.affine_select(out=K.causal_k[:, :], in_=K.ones[:, :], compare_op=ALU.is_ge, fill=0.0, base=0,
                                    pattern=[[1, P]], channel_multiplier=-1)
    return K


def program(nc, W, out):
    with ExitStack() as ctx:
        X = ctx.enter_context(nc.sbuf_tensor("X", [P, NT, D], F32))
        K = build_constants(nc, ctx)
        x_moved = nc.alloc_semaphore("x_moved")
        with nc.Block() as block:
            @block.sync
            def _(sync):
                sync.dma_start(X[:, :, :], W["L0_attn_resid_pre"].rearrange("b (t p) d -> p (b t) d", p=P)).then_inc(x_moved, 16)
                sync.wait_ge(x_moved, 16)
        for stage in SUBLAYERS:
            stage(nc, X, K, W)
        with nc.Block() as block:
            @block.sync
            def _(sync):
                sync.dma_start(out.rearrange("b (t p) d -> p (b t) d", p=P), X[:, :, :]).then_inc(x_moved, 16)
                sync.wait_ge(x_moved, 32)


def kernel(**inputs):
    import concourse.bacc as _bacc
    from concourse.bass_utils import run_bass_kernel_spmd as _run

    nc = _bacc.Bacc("TRN2", target_bir_lowering=False, num_devices=1)
    arrays, W = {}, {}
    for name in list(inputs):
        a = np.ascontiguousarray(LAYOUT[name](np.asarray(inputs[name])) if name in LAYOUT else inputs[name])
        arrays[f"in_{name}"] = a
        W[name] = nc.dram_tensor(f"in_{name}", a.shape, mybir.dt.from_np(a.dtype), kind="ExternalInput").ap()
    for name, a in shape_constants().items():
        arrays[f"const_{name}"] = a
        W[name] = nc.dram_tensor(f"const_{name}", a.shape, mybir.dt.from_np(a.dtype), kind="ExternalInput").ap()
    ln = np.ascontiguousarray(np.stack([inputs["L2_ffn_ln_g"], inputs["L2_ffn_ln_b"]], axis=2))
    arrays["in_l2_ln"] = ln
    W["l2_ln"] = nc.dram_tensor("in_l2_ln", ln.shape, F32, kind="ExternalInput").ap()
    out = nc.dram_tensor("out_0", (1, T, D), F32, kind="ExternalOutput").ap()
    program(nc, W, out)
    r = _run(nc, [arrays], core_ids=[0])
    return r.results[0]["out_0"]
```
